# Optimizing a Trainium2 kernel written in Bass

```python
import numpy as np
import jax
import jax.numpy as jnp

def _softmax(x, axis=-1):
    return jax.nn.softmax(x, axis=axis)

def _gelu(x):
    return jax.nn.gelu(x, approximate=True)

def _silu(x):
    return jax.nn.silu(x)

def _sigmoid(x):
    return jax.nn.sigmoid(x)

def _layernorm(x, axis=-1, eps=1e-05):
    m = jnp.mean(x, axis=axis, keepdims=True)
    v = jnp.var(x, axis=axis, keepdims=True)
    return (x - m) / jnp.sqrt(v + eps)

def _scatter_add(tgt, idx, src, axis=0):
    return tgt.at[idx].add(src)

def _segment_sum(src, seg, n):
    return jax.ops.segment_sum(src, seg, n)
kernel_name = 'mk_decoder_preln_d4_seqx_r4_610c40'

def setup_inputs(seed: int=0):
    np.random.seed(seed)
    _w = jnp.asarray

    def _rec_inputs():
        import jax
        import jax.numpy as jnp
        _rk = jax.random.key(seed)
        x = 7.22e-05 + 1 * jax.random.normal(jax.random.fold_in(_rk, 1), (8, 256, 256), jnp.float32)
        _lenS = 256 - jax.random.randint(jax.random.fold_in(_rk, 7), (8,), 0, max(1, 256 // 4) + 1, jnp.int32)
        _lenS2 = 256 - jax.random.randint(jax.random.fold_in(_rk, 8), (8,), 0, max(1, 256 // 4) + 1, jnp.int32)
        _ctx_1024P = jax.random.normal(jax.random.fold_in(_rk, 11), (8, 16, 256), jnp.float32)
        _ctx_1024c = jax.random.dirichlet(jax.random.fold_in(_rk, 511), 0.3 * jnp.ones((16,), jnp.float32), (8, 256))
        _ctx_1024t = jnp.einsum('bsk,bkd->bsd', _ctx_1024c, _ctx_1024P)
        _ctx_1024t = _ctx_1024t * jax.lax.rsqrt(jnp.mean(jnp.square(_ctx_1024t)) + 1e-12) * 0.953939
        ctx_1024 = 4.13588e-05 + 0.999923 * (_ctx_1024t + 0.3 * jax.random.normal(jax.random.fold_in(_rk, 611), (8, 256, 256), jnp.float32))
        _validS = jnp.arange(256)[None, :] < _lenS[:, None]
        _validS2 = jnp.arange(256)[None, :] < _lenS2[:, None]
        _causal = jnp.tril(jnp.ones((256, 256), dtype=bool))
        mask_Bx1xSxS2_ik0 = jnp.where(jnp.broadcast_to(_validS2[:, None, None, :], (8, 1, 256, 256)), 0, 1).astype(jnp.int32)
        mask_Bx1xS2_ik0 = jnp.where(jnp.broadcast_to(_validS2[:, None, :], (8, 1, 256)), 0, 1).astype(jnp.int32)
        mask_BxS2_bk1 = jnp.broadcast_to(_validS2[:, :], (8, 256))
        return (x, ctx_1024, mask_Bx1xSxS2_ik0, mask_Bx1xS2_ik0, mask_BxS2_bk1)
    x, ctx_1024, mask_Bx1xSxS2_ik0, mask_Bx1xS2_ik0, mask_BxS2_bk1 = _rec_inputs()

    def _L0_attn_setup():
        import jax, jax.numpy as jnp
        import numpy as np
        H, HEADDIM, HIDDEN, DSTATE, G, K, NL = (32, 64, 256, 128, 1, 4, 15)
        DIM = H * HEADDIM
        CONV_DIM = DIM + 2 * G * DSTATE
        PROJ = DIM + CONV_DIM + H * (NL + 1)
        EPS = 1e-05

        def fenwick_level_map(T, num_levels):
            t = np.arange(T)[:, None]
            s = np.arange(T)[None, :]
            lvl = np.zeros((T, T), np.int32)
            for k in range(num_levels - 1):
                lo = t >> k + 1 << k + 1
                hi = t >> k << k
                m = (t >> k & 1 == 1) & (s >= lo) & (s < hi)
                lvl = np.where(m, k + 1, lvl)
            return jnp.asarray(lvl)
        key = jax.random.key(seed)
        ks = jax.random.split(key, 6)
        B, T = (1, 256)
        return {'hidden_states': jax.random.normal(ks[0], (B, T, HIDDEN), jnp.float32), 'in_proj_w': jax.random.normal(ks[1], (PROJ, HIDDEN), jnp.float32) / np.sqrt(HIDDEN).astype(np.float32), 'in_proj_b': jax.random.normal(ks[2], (PROJ,), jnp.float32) * 0.02, 'conv_w': jax.random.normal(ks[3], (CONV_DIM, K), jnp.float32) / np.sqrt(K).astype(np.float32), 'dt_bias': jnp.ones((H,), jnp.float32), 'A_log': jnp.log(jnp.arange(1, H + 1, dtype=jnp.float32)), 'L': jnp.ones((H, NL), jnp.float32), 'D': jnp.ones((H,), jnp.float32), 'norm_w': jnp.ones((DIM,), jnp.float32), 'out_proj_w': jax.random.normal(ks[4], (HIDDEN, DIM), jnp.float32) / np.sqrt(DIM).astype(np.float32), 'out_proj_b': jnp.zeros((HIDDEN,), jnp.float32)}
    _L0_attn_all = _L0_attn_setup()
    _L0_attn_in = {k: v for k, v in _L0_attn_all.items() if k in ('in_proj_w', 'in_proj_b', 'conv_w', 'dt_bias', 'A_log', 'L', 'D', 'norm_w', 'out_proj_w', 'out_proj_b')}
    del _L0_attn_all

    def _L0_xattn_setup():
        import jax, jax.numpy as jnp
        import numpy as np
        D_MODEL = 256
        N_HEADS = 16
        HEAD_D = D_MODEL // N_HEADS
        B, L = (4, 512)
        EPS_CAUSAL = 1e-06

        def _feat(x):
            return jax.nn.elu(x) + 1.0

        def _causal_linear_attn(qs, ks, vs):

            def step(carry, xs):
                Si, Zi = carry
                q, k, v = xs
                Si = Si + jnp.einsum('bhd,bhk->bhdk', k, v)
                Zi = Zi + k
                num = jnp.einsum('bhd,bhkd->bhk', q, Si)
                Vi = num / (q * Zi + EPS_CAUSAL)
                return ((Si, Zi), Vi)
            Bn, Ln, H, D = qs.shape
            K = vs.shape[-1]
            Si0 = jnp.zeros((Bn, H, D, K), qs.dtype)
            Zi0 = jnp.zeros((Bn, H, D), qs.dtype)
            xs = (jnp.swapaxes(qs, 0, 1), jnp.swapaxes(ks, 0, 1), jnp.swapaxes(vs, 0, 1))
            _, out = jax.lax.scan(step, (Si0, Zi0), xs)
            return jnp.swapaxes(out, 0, 1)
        key = jax.random.key(seed)
        ks = jax.random.split(key, 11)
        s = 1.0 / np.sqrt(D_MODEL)
        inp = {'queries': jax.random.normal(ks[0], (B, L, D_MODEL), jnp.float32), 'keys': jax.random.normal(ks[1], (B, L, D_MODEL), jnp.float32), 'values': jax.random.normal(ks[2], (B, L, D_MODEL), jnp.float32), 'Wq': jax.random.uniform(ks[3], (D_MODEL, N_HEADS * HEAD_D), jnp.float32, -s, s), 'bq': jax.random.uniform(ks[4], (N_HEADS * HEAD_D,), jnp.float32, -s, s), 'Wk': jax.random.uniform(ks[5], (D_MODEL, N_HEADS * HEAD_D), jnp.float32, -s, s), 'bk': jax.random.uniform(ks[6], (N_HEADS * HEAD_D,), jnp.float32, -s, s), 'Wv': jax.random.uniform(ks[7], (D_MODEL, N_HEADS * HEAD_D), jnp.float32, -s, s), 'bv': jax.random.uniform(ks[8], (N_HEADS * HEAD_D,), jnp.float32, -s, s), 'Wo': jax.random.uniform(ks[9], (D_MODEL, D_MODEL), jnp.float32, -s, s), 'bo': jax.random.uniform(ks[10], (D_MODEL,), jnp.float32, -s, s)}
        return inp
    _L0_xattn_all = _L0_xattn_setup()
    _L0_xattn_in = {k: v for k, v in _L0_xattn_all.items() if k in ('Wq', 'bq', 'Wk', 'bk', 'Wv', 'bv', 'Wo', 'bo')}
    del _L0_xattn_all

    def _L0_ffn_setup():
        import jax, jax.numpy as jnp
        import numpy as np
        DIM = 256
        INTER = 256
        E = 8
        TOPK = 2
        ROUTE_SCALE = 1.0
        SHARED_INTER = 512
        B, S = (4, 512)

        def _moe_forward(x, gate_w, gate_b, w1, b1, w3, b3, w2, b2, ws1, bs1, ws3, bs3, ws2, bs2):
            Bq, Sq, D = x.shape
            xt = x.reshape(-1, D)
            logits = (xt @ gate_w.T + gate_b).astype(jnp.float32)
            scores = jax.nn.softmax(logits, axis=-1)
            top_w, top_i = jax.lax.top_k(scores, TOPK)
            weights = (top_w * ROUTE_SCALE).astype(x.dtype)
            gate_dense = jnp.sum(jax.nn.one_hot(top_i, E, dtype=x.dtype) * weights[..., None], axis=1)

            def expert(w1e, b1e, w3e, b3e, w2e, b2e):
                h = jax.nn.silu(xt @ w1e.T + b1e) * (xt @ w3e.T + b3e)
                return h @ w2e.T + b2e
            outs = jax.vmap(expert)(w1, b1, w3, b3, w2, b2)
            y = jnp.einsum('etd,te->td', outs, gate_dense)
            z = jax.nn.silu(xt @ ws1.T + bs1) * (xt @ ws3.T + bs3) @ ws2.T + bs2
            return (y + z).reshape(Bq, Sq, D)
        key = jax.random.key(seed)
        ks = jax.random.split(key, 10)

        def w(k, shape, scale=0.02):
            return jax.random.normal(k, shape, jnp.float32) * scale
        return {'x': jax.random.normal(ks[0], (B, S, DIM), jnp.float32), 'gate_w': w(ks[1], (E, DIM)), 'gate_b': jnp.zeros((E,), jnp.float32), 'w1': w(ks[2], (E, INTER, DIM)), 'b1': jnp.zeros((E, INTER), jnp.float32), 'w3': w(ks[3], (E, INTER, DIM)), 'b3': jnp.zeros((E, INTER), jnp.float32), 'w2': w(ks[4], (E, DIM, INTER)), 'b2': jnp.zeros((E, DIM), jnp.float32), 'ws1': w(ks[5], (SHARED_INTER, DIM)), 'bs1': jnp.zeros((SHARED_INTER,), jnp.float32), 'ws3': w(ks[6], (SHARED_INTER, DIM)), 'bs3': jnp.zeros((SHARED_INTER,), jnp.float32), 'ws2': w(ks[7], (DIM, SHARED_INTER)), 'bs2': jnp.zeros((DIM,), jnp.float32)}
    _L0_ffn_all = _L0_ffn_setup()
    _L0_ffn_in = {k: v for k, v in _L0_ffn_all.items() if k in ('gate_w', 'gate_b', 'w1', 'b1', 'w3', 'b3', 'w2', 'b2', 'ws1', 'bs1', 'ws3', 'bs3', 'ws2', 'bs2')}
    del _L0_ffn_all

    def _L1_attn_setup():
        import jax, jax.numpy as jnp
        import numpy as np
        B, N, D_IN, D_OUT, H = (2, 512, 256, 256, 16)
        HEAD_DIM = D_OUT // H
        key = jax.random.key(seed)
        ks = jax.random.split(key, 8)
        s = 0.02
        return {'x': jax.random.normal(ks[0], (B, N, D_IN), dtype=jnp.float32), 'Wq': jax.random.normal(ks[1], (D_IN, D_OUT), dtype=jnp.float32) * s, 'Wk': jax.random.normal(ks[2], (D_IN, D_OUT), dtype=jnp.float32) * s, 'Wv': jax.random.normal(ks[3], (D_IN, D_OUT), dtype=jnp.float32) * s, 'Wo': jax.random.normal(ks[4], (D_OUT, D_OUT), dtype=jnp.float32) * s, 'bo': jnp.zeros((D_OUT,), dtype=jnp.float32), 'w': jax.random.uniform(ks[5], (H,), dtype=jnp.float32), 'v': jax.random.uniform(ks[6], (H,), dtype=jnp.float32)}
    _L1_attn_all = _L1_attn_setup()
    _L1_attn_in = {k: v for k, v in _L1_attn_all.items() if k in ('Wq', 'Wk', 'Wv', 'Wo', 'bo', 'w', 'v')}
    del _L1_attn_all

    def _L1_xattn_setup():
        import jax, jax.numpy as jnp
        import numpy as np
        N, L, E, H = (2, 512, 256, 16)
        D = E // H
        key = jax.random.key(seed)
        ks = jax.random.split(key, 8)
        s = 0.02
        values = jax.random.normal(ks[0], (N, L, E), jnp.float32)
        keys_t = jax.random.normal(ks[1], (N, L, E), jnp.float32)
        query = jax.random.normal(ks[2], (N, L, E), jnp.float32)
        mask = jnp.tril(jnp.ones((L, L), jnp.int32))[None, None].repeat(N, axis=0)
        Wv = jax.random.normal(ks[3], (E, E), jnp.float32) * s
        Wk = jax.random.normal(ks[4], (E, E), jnp.float32) * s
        Wq = jax.random.normal(ks[5], (E, E), jnp.float32) * s
        Wo = jax.random.normal(ks[6], (E, E), jnp.float32) * s
        bo = jnp.zeros((E,), jnp.float32)
        return {'values': values, 'keys': keys_t, 'query': query, 'mask': mask, 'Wv': Wv, 'Wk': Wk, 'Wq': Wq, 'Wo': Wo, 'bo': bo}
    _L1_xattn_all = _L1_xattn_setup()
    _L1_xattn_in = {k: v for k, v in _L1_xattn_all.items() if k in ('Wv', 'Wk', 'Wq', 'Wo', 'bo')}
    del _L1_xattn_all

    def _L1_ffn_setup():
        import jax, jax.numpy as jnp
        import numpy as np
        BLOCK = 32
        W_BITS = 4
        ACT_BITS = 16

        def act_qdq(x):
            qmax = 2.0 ** (ACT_BITS - 1) - 1.0
            scale = jnp.maximum(jnp.max(jnp.abs(x)) / qmax, 1e-12)
            return jnp.clip(jnp.round(x / scale), -qmax - 1.0, qmax) * scale

        def fixed_qdq_u16(x):
            scale = 1.0 / 65536.0
            return jnp.clip(jnp.round(x / scale), 0.0, 65535.0) * scale

        def lpbq_dequant(w):
            O, I = w.shape
            qmax = 2.0 ** (W_BITS - 1) - 1.0
            wb = w.reshape(O, I // BLOCK, BLOCK)
            s = jnp.maximum(jnp.max(jnp.abs(wb), axis=-1, keepdims=True) / qmax, 1e-12)
            wq = jnp.clip(jnp.round(wb / s), -qmax - 1.0, qmax) * s
            return wq.reshape(O, I)
        key = jax.random.key(seed)
        k1, k2, k3, k4 = jax.random.split(key, 4)
        B, S, H, I = (2, 1024, 256, 768)
        x = jax.random.normal(k1, (B, S, H), jnp.float32)
        w_gate = jax.random.normal(k2, (I, H), jnp.float32) * 0.02
        w_up = jax.random.normal(k3, (I, H), jnp.float32) * 0.02
        w_down = jax.random.normal(k4, (H, I), jnp.float32) * 0.02
        return {'x': x, 'w_gate': w_gate, 'w_up': w_up, 'w_down': w_down}
    _L1_ffn_all = _L1_ffn_setup()
    _L1_ffn_in = {k: v for k, v in _L1_ffn_all.items() if k in ('w_gate', 'w_up', 'w_down')}
    del _L1_ffn_all

    def _L2_attn_setup():
        import jax, jax.numpy as jnp
        import numpy as np
        B_SZ, SEQ, D_MODEL, D_STATE, KSIZE = (8, 1024, 256, 64, 64)
        DT_MIN, DT_MAX = (0.001, 0.1)
        key = jax.random.key(seed)
        k1, k2, k3, k4 = jax.random.split(key, 4)
        u = jax.random.normal(k1, (B_SZ, SEQ, D_MODEL), dtype=jnp.float32)
        A = -(jnp.arange(D_STATE, dtype=jnp.float32) + 1.0)
        Bp = 0.01 * jax.random.normal(k2, (D_STATE, D_MODEL), dtype=jnp.float32)
        Cp = 0.01 * jax.random.normal(k3, (D_MODEL, D_STATE), dtype=jnp.float32)
        Dp = jnp.ones((D_MODEL,), dtype=jnp.float32)
        log_dt = jnp.log(jax.random.uniform(k4, (D_MODEL,), dtype=jnp.float32, minval=DT_MIN, maxval=DT_MAX))
        return {'u': u, 'A': A, 'B': Bp, 'C': Cp, 'D': Dp, 'log_dt': log_dt}
    _L2_attn_all = _L2_attn_setup()
    _L2_attn_in = {k: v for k, v in _L2_attn_all.items() if k in ('A', 'B', 'C', 'D', 'log_dt')}
    del _L2_attn_all

    def _L2_xattn_setup():
        import jax, jax.numpy as jnp
        import numpy as np
        D_MODEL = 256
        NEG_BIG = -1000000000.0
        key = jax.random.key(seed)
        kq, kk, kv, km = jax.random.split(key, 4)
        B, S, D = (4, 512, D_MODEL)
        q = jax.random.normal(kq, (B, S, D), dtype=jnp.float32)
        k = jax.random.normal(kk, (B, S, D), dtype=jnp.float32)
        v = jax.random.normal(kv, (B, S, D), dtype=jnp.float32)
        mask = jax.random.randint(km, (B, 1, S), 0, 2, dtype=jnp.int32)
        return {'q': q, 'k': k, 'v': v, 'mask': mask}
    _L2_xattn_all = _L2_xattn_setup()
    _L2_xattn_in = {k: v for k, v in _L2_xattn_all.items() if k in ()}
    del _L2_xattn_all

    def _L2_ffn_setup():
        import jax, jax.numpy as jnp
        import numpy as np
        B, S, D = (4, 512, 256)
        E, F = (8, 1024)
        key = jax.random.key(seed)
        ks = jax.random.split(key, 5)
        x = jax.random.normal(ks[0], (B, S, D), dtype=jnp.float32)
        switch_w = jax.random.normal(ks[1], (D, E), dtype=jnp.float32) * D ** (-0.5)
        switch_b = jnp.zeros((E,), dtype=jnp.float32)
        w1 = jax.random.normal(ks[2], (E, D, F), dtype=jnp.float32) * D ** (-0.5)
        b1 = jnp.zeros((E, F), dtype=jnp.float32)
        w2 = jax.random.normal(ks[3], (E, F, D), dtype=jnp.float32) * F ** (-0.5)
        b2 = jnp.zeros((E, D), dtype=jnp.float32)
        return {'x': x, 'switch_w': switch_w, 'switch_b': switch_b, 'w1': w1, 'b1': b1, 'w2': w2, 'b2': b2}
    _L2_ffn_all = _L2_ffn_setup()
    _L2_ffn_in = {k: v for k, v in _L2_ffn_all.items() if k in ('switch_w', 'switch_b', 'w1', 'b1', 'w2', 'b2')}
    del _L2_ffn_all

    def _L3_attn_setup():
        import jax, jax.numpy as jnp
        import numpy as np
        HEADS = 16
        THETA = 10000.0

        def _rope(x):
            b, n, d = x.shape
            half = d // 2
            inv_freq = 1.0 / THETA ** (jnp.arange(0, d, 2, dtype=jnp.float32) / d)
            ang = jnp.arange(n, dtype=jnp.float32)[:, None] * inv_freq
            cos, sin = (jnp.cos(ang), jnp.sin(ang))
            xp = x.reshape(b, n, half, 2)
            x1, x2 = (xp[..., 0], xp[..., 1])
            out = jnp.stack([x1 * cos - x2 * sin, x2 * cos + x1 * sin], axis=-1)
            return out.reshape(b, n, d)
        key = jax.random.key(seed)
        ks = jax.random.split(key, 8)
        B, N, C = (8, 512, 256)
        s = C ** (-0.5)
        return {'x': jax.random.normal(ks[0], (B, N, C), jnp.float32), 'Wq': jax.random.normal(ks[1], (C, C), jnp.float32) * s, 'bq': jax.random.normal(ks[2], (C,), jnp.float32) * 0.01, 'Wk': jax.random.normal(ks[3], (C, C), jnp.float32) * s, 'bk': jax.random.normal(ks[4], (C,), jnp.float32) * 0.01, 'Wv': jax.random.normal(ks[5], (C, C), jnp.float32) * s, 'bv': jax.random.normal(ks[6], (C,), jnp.float32) * 0.01, 'gamma': jnp.ones((C,), jnp.float32), 'beta': jnp.zeros((C,), jnp.float32)}
    _L3_attn_all = _L3_attn_setup()
    _L3_attn_in = {k: v for k, v in _L3_attn_all.items() if k in ('Wq', 'bq', 'Wk', 'bk', 'Wv', 'bv', 'gamma', 'beta')}
    del _L3_attn_all

    def _L3_xattn_setup():
        import jax, jax.numpy as jnp
        import numpy as np
        DIM = 256
        DIM_HEAD = 64
        HEADS = 8
        INNER = DIM_HEAD * HEADS
        EPS = 1e-05

        def layernorm(x, g, b):
            mu = jnp.mean(x, axis=-1, keepdims=True)
            var = jnp.var(x, axis=-1, keepdims=True)
            return (x - mu) * jax.lax.rsqrt(var + EPS) * g + b
        key = jax.random.key(seed)
        ks = jax.random.split(key, 8)
        b, n, m = (8, 1024, 64)
        x = jax.random.normal(ks[0], (b, n, DIM), dtype=jnp.float32)
        latents = jax.random.normal(ks[1], (b, m, DIM), dtype=jnp.float32)
        mask = jax.random.bernoulli(ks[2], 0.9, (b, n))
        s = DIM ** (-0.5)
        Wq = jax.random.normal(ks[3], (DIM, INNER), dtype=jnp.float32) * s
        Wkv = jax.random.normal(ks[4], (DIM, 2 * INNER), dtype=jnp.float32) * s
        Wo = jax.random.normal(ks[5], (INNER, DIM), dtype=jnp.float32) * INNER ** (-0.5)
        ln_x_g = jnp.ones((DIM,), jnp.float32)
        ln_x_b = jnp.zeros((DIM,), jnp.float32)
        ln_l_g = jnp.ones((DIM,), jnp.float32)
        ln_l_b = jnp.zeros((DIM,), jnp.float32)
        ln_o_g = jnp.ones((DIM,), jnp.float32)
        ln_o_b = jnp.zeros((DIM,), jnp.float32)
        return {'x': x, 'latents': latents, 'mask': mask, 'Wq': Wq, 'Wkv': Wkv, 'Wo': Wo, 'ln_x_g': ln_x_g, 'ln_x_b': ln_x_b, 'ln_l_g': ln_l_g, 'ln_l_b': ln_l_b, 'ln_o_g': ln_o_g, 'ln_o_b': ln_o_b}
    _L3_xattn_all = _L3_xattn_setup()
    _L3_xattn_in = {k: v for k, v in _L3_xattn_all.items() if k in ('Wq', 'Wkv', 'Wo', 'ln_x_g', 'ln_x_b', 'ln_l_g', 'ln_l_b', 'ln_o_g', 'ln_o_b')}
    del _L3_xattn_all

    def _L3_ffn_setup():
        import math
        import jax, jax.numpy as jnp
        import numpy as np
        B, S, H = (4, 512, 256)
        E, K, I = (8, 2, 256)
        NSH = 2
        CF, RSF = (1.25, 1.0)
        key = jax.random.key(seed)
        ks = jax.random.split(key, 8)
        w = lambda k, sh: jax.random.normal(k, sh, dtype=jnp.float32) * 0.02
        return {'hidden_states': jax.random.normal(ks[0], (B, S, H), dtype=jnp.float32), 'gate_w': w(ks[1], (E, H)), 'we_gate': w(ks[2], (E, I, H)), 'we_up': w(ks[3], (E, I, H)), 'we_down': w(ks[4], (E, H, I)), 'ws_gate': w(ks[5], (NSH * I, H)), 'ws_up': w(ks[6], (NSH * I, H)), 'ws_down': w(ks[7], (H, NSH * I))}
    _L3_ffn_all = _L3_ffn_setup()
    _L3_ffn_in = {k: v for k, v in _L3_ffn_all.items() if k in ('gate_w', 'we_gate', 'we_up', 'we_down', 'ws_gate', 'ws_up', 'ws_down')}
    del _L3_ffn_all
    return {'x': x, 'ctx_1024': ctx_1024, 'mask_Bx1xSxS2_ik0': mask_Bx1xSxS2_ik0, 'mask_Bx1xS2_ik0': mask_Bx1xS2_ik0, 'mask_BxS2_bk1': mask_BxS2_bk1, 'L0_attn_in_proj_w': _L0_attn_in['in_proj_w'], 'L0_attn_in_proj_b': _L0_attn_in['in_proj_b'], 'L0_attn_conv_w': _L0_attn_in['conv_w'], 'L0_attn_dt_bias': _L0_attn_in['dt_bias'], 'L0_attn_A_log': _L0_attn_in['A_log'], 'L0_attn_L': _L0_attn_in['L'], 'L0_attn_D': _L0_attn_in['D'], 'L0_attn_norm_w': _L0_attn_in['norm_w'], 'L0_attn_out_proj_w': _L0_attn_in['out_proj_w'], 'L0_attn_out_proj_b': _L0_attn_in['out_proj_b'], 'L0_xattn_Wq': _L0_xattn_in['Wq'], 'L0_xattn_bq': _L0_xattn_in['bq'], 'L0_xattn_Wk': _L0_xattn_in['Wk'], 'L0_xattn_bk': _L0_xattn_in['bk'], 'L0_xattn_Wv': _L0_xattn_in['Wv'], 'L0_xattn_bv': _L0_xattn_in['bv'], 'L0_xattn_Wo': _L0_xattn_in['Wo'], 'L0_xattn_bo': _L0_xattn_in['bo'], 'L0_ffn_gate_w': _L0_ffn_in['gate_w'], 'L0_ffn_gate_b': _L0_ffn_in['gate_b'], 'L0_ffn_w1': _L0_ffn_in['w1'], 'L0_ffn_b1': _L0_ffn_in['b1'], 'L0_ffn_w3': _L0_ffn_in['w3'], 'L0_ffn_b3': _L0_ffn_in['b3'], 'L0_ffn_w2': _L0_ffn_in['w2'], 'L0_ffn_b2': _L0_ffn_in['b2'], 'L0_ffn_ws1': _L0_ffn_in['ws1'], 'L0_ffn_bs1': _L0_ffn_in['bs1'], 'L0_ffn_ws3': _L0_ffn_in['ws3'], 'L0_ffn_bs3': _L0_ffn_in['bs3'], 'L0_ffn_ws2': _L0_ffn_in['ws2'], 'L0_ffn_bs2': _L0_ffn_in['bs2'], 'L1_attn_Wq': _L1_attn_in['Wq'], 'L1_attn_Wk': _L1_attn_in['Wk'], 'L1_attn_Wv': _L1_attn_in['Wv'], 'L1_attn_Wo': _L1_attn_in['Wo'], 'L1_attn_bo': _L1_attn_in['bo'], 'L1_attn_w': _L1_attn_in['w'], 'L1_attn_v': _L1_attn_in['v'], 'L1_xattn_Wv': _L1_xattn_in['Wv'], 'L1_xattn_Wk': _L1_xattn_in['Wk'], 'L1_xattn_Wq': _L1_xattn_in['Wq'], 'L1_xattn_Wo': _L1_xattn_in['Wo'], 'L1_xattn_bo': _L1_xattn_in['bo'], 'L1_ffn_w_gate': _L1_ffn_in['w_gate'], 'L1_ffn_w_up': _L1_ffn_in['w_up'], 'L1_ffn_w_down': _L1_ffn_in['w_down'], 'L2_attn_A': _L2_attn_in['A'], 'L2_attn_B': _L2_attn_in['B'], 'L2_attn_C': _L2_attn_in['C'], 'L2_attn_D': _L2_attn_in['D'], 'L2_attn_log_dt': _L2_attn_in['log_dt'], 'L2_ffn_switch_w': _L2_ffn_in['switch_w'], 'L2_ffn_switch_b': _L2_ffn_in['switch_b'], 'L2_ffn_w1': _L2_ffn_in['w1'], 'L2_ffn_b1': _L2_ffn_in['b1'], 'L2_ffn_w2': _L2_ffn_in['w2'], 'L2_ffn_b2': _L2_ffn_in['b2'], 'L3_attn_Wq': _L3_attn_in['Wq'], 'L3_attn_bq': _L3_attn_in['bq'], 'L3_attn_Wk': _L3_attn_in['Wk'], 'L3_attn_bk': _L3_attn_in['bk'], 'L3_attn_Wv': _L3_attn_in['Wv'], 'L3_attn_bv': _L3_attn_in['bv'], 'L3_attn_gamma': _L3_attn_in['gamma'], 'L3_attn_beta': _L3_attn_in['beta'], 'L3_xattn_Wq': _L3_xattn_in['Wq'], 'L3_xattn_Wkv': _L3_xattn_in['Wkv'], 'L3_xattn_Wo': _L3_xattn_in['Wo'], 'L3_xattn_ln_x_g': _L3_xattn_in['ln_x_g'], 'L3_xattn_ln_x_b': _L3_xattn_in['ln_x_b'], 'L3_xattn_ln_l_g': _L3_xattn_in['ln_l_g'], 'L3_xattn_ln_l_b': _L3_xattn_in['ln_l_b'], 'L3_xattn_ln_o_g': _L3_xattn_in['ln_o_g'], 'L3_xattn_ln_o_b': _L3_xattn_in['ln_o_b'], 'L3_ffn_gate_w': _L3_ffn_in['gate_w'], 'L3_ffn_we_gate': _L3_ffn_in['we_gate'], 'L3_ffn_we_up': _L3_ffn_in['we_up'], 'L3_ffn_we_down': _L3_ffn_in['we_down'], 'L3_ffn_ws_gate': _L3_ffn_in['ws_gate'], 'L3_ffn_ws_up': _L3_ffn_in['ws_up'], 'L3_ffn_ws_down': _L3_ffn_in['ws_down']}

def reference(x, ctx_1024, mask_Bx1xSxS2_ik0, mask_Bx1xS2_ik0, mask_BxS2_bk1, L0_attn_in_proj_w, L0_attn_in_proj_b, L0_attn_conv_w, L0_attn_dt_bias, L0_attn_A_log, L0_attn_L, L0_attn_D, L0_attn_norm_w, L0_attn_out_proj_w, L0_attn_out_proj_b, L0_xattn_Wq, L0_xattn_bq, L0_xattn_Wk, L0_xattn_bk, L0_xattn_Wv, L0_xattn_bv, L0_xattn_Wo, L0_xattn_bo, L0_ffn_gate_w, L0_ffn_gate_b, L0_ffn_w1, L0_ffn_b1, L0_ffn_w3, L0_ffn_b3, L0_ffn_w2, L0_ffn_b2, L0_ffn_ws1, L0_ffn_bs1, L0_ffn_ws3, L0_ffn_bs3, L0_ffn_ws2, L0_ffn_bs2, L1_attn_Wq, L1_attn_Wk, L1_attn_Wv, L1_attn_Wo, L1_attn_bo, L1_attn_w, L1_attn_v, L1_xattn_Wv, L1_xattn_Wk, L1_xattn_Wq, L1_xattn_Wo, L1_xattn_bo, L1_ffn_w_gate, L1_ffn_w_up, L1_ffn_w_down, L2_attn_A, L2_attn_B, L2_attn_C, L2_attn_D, L2_attn_log_dt, L2_ffn_switch_w, L2_ffn_switch_b, L2_ffn_w1, L2_ffn_b1, L2_ffn_w2, L2_ffn_b2, L3_attn_Wq, L3_attn_bq, L3_attn_Wk, L3_attn_bk, L3_attn_Wv, L3_attn_bv, L3_attn_gamma, L3_attn_beta, L3_xattn_Wq, L3_xattn_Wkv, L3_xattn_Wo, L3_xattn_ln_x_g, L3_xattn_ln_x_b, L3_xattn_ln_l_g, L3_xattn_ln_l_b, L3_xattn_ln_o_g, L3_xattn_ln_o_b, L3_ffn_gate_w, L3_ffn_we_gate, L3_ffn_we_up, L3_ffn_we_down, L3_ffn_ws_gate, L3_ffn_ws_up, L3_ffn_ws_down):
    import jax
    import jax.numpy as jnp

    def _L0_attn_ref(hidden_states, in_proj_w, in_proj_b, conv_w, dt_bias, A_log, L, D, norm_w, out_proj_w, out_proj_b):
        import jax, jax.numpy as jnp
        import numpy as np
        H, HEADDIM, HIDDEN, DSTATE, G, K, NL = (32, 64, 256, 128, 1, 4, 15)
        DIM = H * HEADDIM
        CONV_DIM = DIM + 2 * G * DSTATE
        PROJ = DIM + CONV_DIM + H * (NL + 1)
        EPS = 1e-05

        def fenwick_level_map(T, num_levels):
            t = np.arange(T)[:, None]
            s = np.arange(T)[None, :]
            lvl = np.zeros((T, T), np.int32)
            for k in range(num_levels - 1):
                lo = t >> k + 1 << k + 1
                hi = t >> k << k
                m = (t >> k & 1 == 1) & (s >= lo) & (s < hi)
                lvl = np.where(m, k + 1, lvl)
            return jnp.asarray(lvl)
        B, T, _ = hidden_states.shape
        zxbcdtdl = hidden_states @ in_proj_w.T + in_proj_b
        z = zxbcdtdl[..., :DIM]
        xBC = zxbcdtdl[..., DIM:DIM + CONV_DIM]
        dt = zxbcdtdl[..., DIM + CONV_DIM:DIM + CONV_DIM + H]
        dl = zxbcdtdl[..., DIM + CONV_DIM + H:].reshape(B, T, H, NL)
        xp = jnp.pad(xBC, ((0, 0), (K - 1, 0), (0, 0)))
        xBC = sum((xp[:, i:i + T, :] * conv_w[:, i] for i in range(K)))
        xBC = jax.nn.silu(xBC)
        x = xBC[..., :DIM].reshape(B, T, H, HEADDIM)
        Bm = xBC[..., DIM:DIM + G * DSTATE].reshape(B, T, G, DSTATE)
        Cm = xBC[..., DIM + G * DSTATE:].reshape(B, T, G, DSTATE)
        dt = jax.nn.softplus(dt + dt_bias)
        D_res = x * D[None, None, :, None]
        v = x * dt[..., None]
        g = -jnp.exp(A_log)[None, None, :] * dt
        lam = jax.nn.softplus(L[None, None] * dl)
        gc = jnp.cumsum(g, axis=1).transpose(0, 2, 1)
        causal = jnp.tril(jnp.ones((T, T), bool))
        diff = jnp.where(causal, gc[:, :, :, None] - gc[:, :, None, :], -jnp.inf)
        decay = jnp.exp(diff)
        lvl = fenwick_level_map(T, NL)
        lam_ts = jnp.take_along_axis(lam.transpose(0, 2, 1, 3), lvl[None, None], axis=3)
        qk = jnp.einsum('btgn,bsgn->bgts', Cm, Bm)
        qk = jnp.repeat(qk, H // G, axis=1)
        att = qk * decay * lam_ts
        y = jnp.einsum('bhts,bshp->bthp', att, v) + D_res
        y = y.reshape(B, T, DIM)
        yz = y * jax.nn.silu(z)
        y = yz * jax.lax.rsqrt(jnp.mean(yz * yz, axis=-1, keepdims=True) + EPS) * norm_w
        return y @ out_proj_w.T + out_proj_b

    def _L0_xattn_ref(queries, keys, values, Wq, bq, Wk, bk, Wv, bv, Wo, bo):
        import jax, jax.numpy as jnp
        import numpy as np
        D_MODEL = 256
        N_HEADS = 16
        HEAD_D = D_MODEL // N_HEADS
        B, L = (4, 512)
        EPS_CAUSAL = 1e-06

        def _feat(x):
            return jax.nn.elu(x) + 1.0

        def _causal_linear_attn(qs, ks, vs):

            def step(carry, xs):
                Si, Zi = carry
                q, k, v = xs
                Si = Si + jnp.einsum('bhd,bhk->bhdk', k, v)
                Zi = Zi + k
                num = jnp.einsum('bhd,bhkd->bhk', q, Si)
                Vi = num / (q * Zi + EPS_CAUSAL)
                return ((Si, Zi), Vi)
            Bn, Ln, H, D = qs.shape
            K = vs.shape[-1]
            Si0 = jnp.zeros((Bn, H, D, K), qs.dtype)
            Zi0 = jnp.zeros((Bn, H, D), qs.dtype)
            xs = (jnp.swapaxes(qs, 0, 1), jnp.swapaxes(ks, 0, 1), jnp.swapaxes(vs, 0, 1))
            _, out = jax.lax.scan(step, (Si0, Zi0), xs)
            return jnp.swapaxes(out, 0, 1)
        N, Lq, _ = queries.shape
        H = N_HEADS
        Q = (queries @ Wq + bq).reshape(N, Lq, H, -1)
        Kp = (keys @ Wk + bk).reshape(N, keys.shape[1], H, -1)
        V = (values @ Wv + bv).reshape(N, values.shape[1], H, -1)
        Q_lin = _feat(Q)
        K_lin = _feat(Kp)
        V_lin = _causal_linear_attn(Q_lin, K_lin, V)
        new_values = V_lin.reshape(N, Lq, -1)
        return new_values @ Wo + bo

    def _L0_ffn_ref(x, gate_w, gate_b, w1, b1, w3, b3, w2, b2, ws1, bs1, ws3, bs3, ws2, bs2):
        import jax, jax.numpy as jnp
        import numpy as np
        DIM = 256
        INTER = 256
        E = 8
        TOPK = 2
        ROUTE_SCALE = 1.0
        SHARED_INTER = 512
        B, S = (4, 512)

        def _moe_forward(x, gate_w, gate_b, w1, b1, w3, b3, w2, b2, ws1, bs1, ws3, bs3, ws2, bs2):
            Bq, Sq, D = x.shape
            xt = x.reshape(-1, D)
            logits = (xt @ gate_w.T + gate_b).astype(jnp.float32)
            scores = jax.nn.softmax(logits, axis=-1)
            top_w, top_i = jax.lax.top_k(scores, TOPK)
            weights = (top_w * ROUTE_SCALE).astype(x.dtype)
            gate_dense = jnp.sum(jax.nn.one_hot(top_i, E, dtype=x.dtype) * weights[..., None], axis=1)

            def expert(w1e, b1e, w3e, b3e, w2e, b2e):
                h = jax.nn.silu(xt @ w1e.T + b1e) * (xt @ w3e.T + b3e)
                return h @ w2e.T + b2e
            outs = jax.vmap(expert)(w1, b1, w3, b3, w2, b2)
            y = jnp.einsum('etd,te->td', outs, gate_dense)
            z = jax.nn.silu(xt @ ws1.T + bs1) * (xt @ ws3.T + bs3) @ ws2.T + bs2
            return (y + z).reshape(Bq, Sq, D)
        return _moe_forward(x, gate_w, gate_b, w1, b1, w3, b3, w2, b2, ws1, bs1, ws3, bs3, ws2, bs2)

    def _L1_attn_ref(x, Wq, Wk, Wv, Wo, bo, w, v):
        import jax, jax.numpy as jnp
        import numpy as np
        B, N, D_IN, D_OUT, H = (2, 512, 256, 256, 16)
        HEAD_DIM = D_OUT // H
        b, n, _ = x.shape
        h = w.shape[0]
        hd = Wq.shape[1] // h

        def proj(W):
            return (x @ W).reshape(b, n, h, hd).transpose(0, 2, 1, 3)
        q, k, val = (proj(Wq), proj(Wk), proj(Wv))
        pos = jnp.arange(n)
        R = jnp.abs(pos[:, None] - pos[None, :]).astype(x.dtype)
        wv = w[:, None, None]
        vv = v[:, None, None]
        R_hat = (1.0 + jnp.exp(vv)) / (1.0 + jnp.exp(vv - wv * R))
        scores = jax.nn.relu(jnp.einsum('bhqd,bhkd->bhqk', q, k)) * R_hat[None]
        causal = jnp.triu(jnp.ones((n, n), dtype=bool), k=1)
        scores = jnp.where(causal[None, None], -jnp.inf, scores)
        attn = jax.nn.softmax(scores / np.sqrt(hd).astype(x.dtype), axis=-1)
        ctx = jnp.einsum('bhqk,bhkd->bhqd', attn, val)
        ctx = ctx.transpose(0, 2, 1, 3).reshape(b, n, h * hd)
        return ctx @ Wo + bo

    def _L1_xattn_ref(values, keys, query, mask, Wv, Wk, Wq, Wo, bo):
        import jax, jax.numpy as jnp
        import numpy as np
        N, L, E, H = (2, 512, 256, 16)
        D = E // H
        n, lq, e = query.shape
        v = (values @ Wv.T).reshape(n, -1, H, D)
        k = (keys @ Wk.T).reshape(n, -1, H, D)
        q = (query @ Wq.T).reshape(n, lq, H, D)
        score = jnp.einsum('nqhd,nkhd->nhqk', q, k)
        score = jnp.where(mask == 0, jnp.float32(-1e+20), score)
        attn = jax.nn.softmax(score / jnp.sqrt(jnp.float32(D)), axis=-1)
        out = jnp.einsum('nhqk,nkhd->nqhd', attn, v).reshape(n, lq, H * D)
        return out @ Wo.T + bo

    def _L1_ffn_ref(x, w_gate, w_up, w_down):
        import jax, jax.numpy as jnp
        import numpy as np
        BLOCK = 32
        W_BITS = 4
        ACT_BITS = 16

        def act_qdq(x):
            qmax = 2.0 ** (ACT_BITS - 1) - 1.0
            scale = jnp.maximum(jnp.max(jnp.abs(x)) / qmax, 1e-12)
            return jnp.clip(jnp.round(x / scale), -qmax - 1.0, qmax) * scale

        def fixed_qdq_u16(x):
            scale = 1.0 / 65536.0
            return jnp.clip(jnp.round(x / scale), 0.0, 65535.0) * scale

        def lpbq_dequant(w):
            O, I = w.shape
            qmax = 2.0 ** (W_BITS - 1) - 1.0
            wb = w.reshape(O, I // BLOCK, BLOCK)
            s = jnp.maximum(jnp.max(jnp.abs(wb), axis=-1, keepdims=True) / qmax, 1e-12)
            wq = jnp.clip(jnp.round(wb / s), -qmax - 1.0, qmax) * s
            return wq.reshape(O, I)
        x = act_qdq(x)
        up = act_qdq(x @ lpbq_dequant(w_up).T)
        gate = act_qdq(x @ lpbq_dequant(w_gate).T)
        sig = fixed_qdq_u16(jax.nn.sigmoid(gate))
        gate = act_qdq(gate * sig)
        o = act_qdq(gate * up)
        return o @ lpbq_dequant(w_down).T

    def _L2_attn_ref(u, A, B, C, D, log_dt):
        import jax, jax.numpy as jnp
        import numpy as np
        B_SZ, SEQ, D_MODEL, D_STATE, KSIZE = (8, 1024, 256, 64, 64)
        DT_MIN, DT_MAX = (0.001, 0.1)
        batch, seq_len, d_model = u.shape
        L = min(seq_len, KSIZE)
        dt = jnp.exp(log_dt)
        A_bar = jnp.exp(A[:, None] * dt[None, :])
        powers = jnp.arange(L)[:, None, None]
        A_powers = A_bar[None, :, :] ** powers
        K = jnp.einsum('md,ldk,dk->lk', C, A_powers, B)
        n = seq_len + L - 1
        Uf = jnp.fft.rfft(u, n=n, axis=1)
        Kf = jnp.fft.rfft(K, n=n, axis=0)
        conv_full = jnp.fft.irfft(Uf * Kf[None], n=n, axis=1)
        start = (L - 1) // 2
        y = conv_full[:, start:start + seq_len, :]
        y = y + D[None, None, :] * u
        return y

    def _L2_xattn_ref(q, k, v, mask):
        import jax, jax.numpy as jnp
        import numpy as np
        D_MODEL = 256
        NEG_BIG = -1000000000.0
        scale = jnp.asarray(D_MODEL, q.dtype) ** (-0.5)
        logits = jnp.einsum('bqd,bkd->bqk', q, k) * scale
        logits = logits + mask.astype(q.dtype) * NEG_BIG
        weights = jax.nn.softmax(logits, axis=-1)
        return jnp.einsum('bqk,bkd->bqd', weights, v)

    def _L2_ffn_ref(x, switch_w, switch_b, w1, b1, w2, b2):
        import jax, jax.numpy as jnp
        import numpy as np
        B, S, D = (4, 512, 256)
        E, F = (8, 1024)
        b, s, d = x.shape
        t = x.reshape(-1, d)
        logits = t @ switch_w + switch_b
        route_prob = jax.nn.softmax(logits, axis=-1)
        route_prob_max = jnp.max(route_prob, axis=-1)
        routes = jnp.argmax(route_prob, axis=-1)
        out = jnp.zeros_like(t)
        n_experts = w1.shape[0]
        for e in range(n_experts):
            h = jax.nn.gelu(t @ w1[e] + b1[e])
            y = h @ w2[e] + b2[e]
            mask = (routes == e)[:, None]
            out = jnp.where(mask, y, out)
        out = out * route_prob_max[:, None]
        return out.reshape(b, s, d)

    def _L3_attn_ref(x, Wq, bq, Wk, bk, Wv, bv, gamma, beta):
        import jax, jax.numpy as jnp
        import numpy as np
        HEADS = 16
        THETA = 10000.0

        def _rope(x):
            b, n, d = x.shape
            half = d // 2
            inv_freq = 1.0 / THETA ** (jnp.arange(0, d, 2, dtype=jnp.float32) / d)
            ang = jnp.arange(n, dtype=jnp.float32)[:, None] * inv_freq
            cos, sin = (jnp.cos(ang), jnp.sin(ang))
            xp = x.reshape(b, n, half, 2)
            x1, x2 = (xp[..., 0], xp[..., 1])
            out = jnp.stack([x1 * cos - x2 * sin, x2 * cos + x1 * sin], axis=-1)
            return out.reshape(b, n, d)
        b, n, c = x.shape
        h = HEADS
        d = c // h
        gelu = lambda t: jax.nn.gelu(t, approximate=False)
        q = gelu(x @ Wq.T + bq) + 0.21
        k = gelu(x @ Wk.T + bk) + 0.21
        v = x @ Wv.T + bv
        q_r = _rope(q)
        k_r = _rope(k)
        split = lambda t: t.reshape(b, n, h, d).transpose(0, 2, 1, 3)
        qh, kh, vh, qrh, krh = (split(q), split(k), split(v), split(q_r), split(k_r))
        z = 1.0 / (jnp.einsum('bhnd,bhd->bhn', qh, kh.mean(axis=2)) + 1e-06)
        scale = n ** (-0.5)
        kv = jnp.einsum('bhnd,bhne->bhde', krh * scale, vh * scale)
        out = jnp.einsum('bhnd,bhde->bhne', qrh, kv) * z[..., None]
        out = out.transpose(0, 2, 1, 3).reshape(b, n, c)
        res = out + x
        mu = res.mean(-1, keepdims=True)
        var = res.var(-1, keepdims=True)
        return (res - mu) / jnp.sqrt(var + 1e-12) * gamma + beta

    def _L3_xattn_ref(x, latents, mask, Wq, Wkv, Wo, ln_x_g, ln_x_b, ln_l_g, ln_l_b, ln_o_g, ln_o_b):
        import jax, jax.numpy as jnp
        import numpy as np
        DIM = 256
        DIM_HEAD = 64
        HEADS = 8
        INNER = DIM_HEAD * HEADS
        EPS = 1e-05

        def layernorm(x, g, b):
            mu = jnp.mean(x, axis=-1, keepdims=True)
            var = jnp.var(x, axis=-1, keepdims=True)
            return (x - mu) * jax.lax.rsqrt(var + EPS) * g + b
        scale = DIM_HEAD ** (-0.5)
        b, m = (latents.shape[0], latents.shape[1])
        xn = layernorm(x, ln_x_g, ln_x_b)
        ln = layernorm(latents, ln_l_g, ln_l_b)
        q = ln @ Wq
        kv_in = jnp.concatenate([xn, ln], axis=1)
        kv = kv_in @ Wkv
        k, v = jnp.split(kv, 2, axis=-1)
        q = q.reshape(b, m, HEADS, DIM_HEAD).transpose(0, 2, 1, 3)
        k = k.reshape(b, k.shape[1], HEADS, DIM_HEAD).transpose(0, 2, 1, 3)
        v = v.reshape(b, v.shape[1], HEADS, DIM_HEAD).transpose(0, 2, 1, 3)
        sim = jnp.einsum('bhid,bhjd->bhij', q * scale, k) * scale
        full_mask = jnp.concatenate([mask, jnp.ones((b, m), dtype=bool)], axis=1)
        max_neg = -jnp.finfo(sim.dtype).max
        sim = jnp.where(full_mask[:, None, None, :], sim, max_neg)
        attn = jax.nn.softmax(sim.astype(jnp.float32), axis=-1).astype(sim.dtype)
        out = jnp.einsum('bhij,bhjd->bhid', attn, v)
        out = out.transpose(0, 2, 1, 3).reshape(b, m, INNER)
        out = out @ Wo
        return layernorm(out, ln_o_g, ln_o_b)

    def _L3_ffn_ref(hidden_states, gate_w, we_gate, we_up, we_down, ws_gate, ws_up, ws_down):
        import math
        import jax, jax.numpy as jnp
        import numpy as np
        B, S, H = (4, 512, 256)
        E, K, I = (8, 2, 256)
        NSH = 2
        CF, RSF = (1.25, 1.0)
        orig_shape = hidden_states.shape
        x = hidden_states.reshape(-1, H)
        N = x.shape[0]
        logits = x.astype(jnp.float32) @ gate_w.astype(jnp.float32).T
        scores = jax.nn.softmax(logits, axis=-1)
        topk_w, topk_idx = jax.lax.top_k(scores, K)
        topk_w = topk_w / (topk_w.sum(-1, keepdims=True) + 1e-20) * RSF
        capacity = math.ceil(CF * N * K / E)
        flat = topk_idx.reshape(-1)
        one_hot = jax.nn.one_hot(flat, E, dtype=jnp.int32)
        pos = jnp.cumsum(one_hot, axis=0) - 1
        pos_tok = jnp.take_along_axis(pos, flat[:, None], axis=1)[:, 0]
        keep = (pos_tok < capacity).reshape(N, K)
        topk_w = topk_w * keep.astype(topk_w.dtype)
        comb = jnp.zeros((N, E), jnp.float32).at[jnp.arange(N)[:, None], topk_idx].add(topk_w)
        g = jnp.einsum('nh,eih->nei', x, we_gate)
        u = jnp.einsum('nh,eih->nei', x, we_up)
        eo = jnp.einsum('nei,ehi->neh', jax.nn.silu(g) * u, we_down)
        y = jnp.einsum('neh,ne->nh', eo, comb)
        sh = jax.nn.silu(x @ ws_gate.T) * (x @ ws_up.T) @ ws_down.T
        return (y + sh).reshape(orig_shape)
    x = x + _L0_attn_ref(_layernorm(x, axis=-1), L0_attn_in_proj_w, L0_attn_in_proj_b, L0_attn_conv_w, L0_attn_dt_bias, L0_attn_A_log, L0_attn_L, L0_attn_D, L0_attn_norm_w, L0_attn_out_proj_w, L0_attn_out_proj_b)
    x = x + _L0_xattn_ref(_layernorm(x, axis=-1), ctx_1024, ctx_1024, L0_xattn_Wq, L0_xattn_bq, L0_xattn_Wk, L0_xattn_bk, L0_xattn_Wv, L0_xattn_bv, L0_xattn_Wo, L0_xattn_bo)
    x = x + _L0_ffn_ref(_layernorm(x, axis=-1), L0_ffn_gate_w, L0_ffn_gate_b, L0_ffn_w1, L0_ffn_b1, L0_ffn_w3, L0_ffn_b3, L0_ffn_w2, L0_ffn_b2, L0_ffn_ws1, L0_ffn_bs1, L0_ffn_ws3, L0_ffn_bs3, L0_ffn_ws2, L0_ffn_bs2)
    x = x + _L1_attn_ref(_layernorm(x, axis=-1), L1_attn_Wq, L1_attn_Wk, L1_attn_Wv, L1_attn_Wo, L1_attn_bo, L1_attn_w, L1_attn_v)
    x = x + _L1_xattn_ref(ctx_1024, ctx_1024, _layernorm(x, axis=-1), mask_Bx1xSxS2_ik0, L1_xattn_Wv, L1_xattn_Wk, L1_xattn_Wq, L1_xattn_Wo, L1_xattn_bo)
    x = x + _L1_ffn_ref(_layernorm(x, axis=-1), L1_ffn_w_gate, L1_ffn_w_up, L1_ffn_w_down)
    x = x + _L2_attn_ref(_layernorm(x, axis=-1), L2_attn_A, L2_attn_B, L2_attn_C, L2_attn_D, L2_attn_log_dt)
    x = x + _L2_xattn_ref(_layernorm(x, axis=-1), ctx_1024, ctx_1024, mask_Bx1xS2_ik0)
    x = x + _L2_ffn_ref(_layernorm(x, axis=-1), L2_ffn_switch_w, L2_ffn_switch_b, L2_ffn_w1, L2_ffn_b1, L2_ffn_w2, L2_ffn_b2)
    x = x + _L3_attn_ref(_layernorm(x, axis=-1), L3_attn_Wq, L3_attn_bq, L3_attn_Wk, L3_attn_bk, L3_attn_Wv, L3_attn_bv, L3_attn_gamma, L3_attn_beta)
    x = x + _L3_xattn_ref(ctx_1024, _layernorm(x, axis=-1), mask_BxS2_bk1, L3_xattn_Wq, L3_xattn_Wkv, L3_xattn_Wo, L3_xattn_ln_x_g, L3_xattn_ln_x_b, L3_xattn_ln_l_g, L3_xattn_ln_l_b, L3_xattn_ln_o_g, L3_xattn_ln_o_b)
    x = x + _L3_ffn_ref(_layernorm(x, axis=-1), L3_ffn_gate_w, L3_ffn_we_gate, L3_ffn_we_up, L3_ffn_we_down, L3_ffn_ws_gate, L3_ffn_ws_up, L3_ffn_ws_down)
    return x

_drawn_inputs = setup_inputs


def setup_inputs(seed=0):
    import zlib

    import numpy as np

    out = dict(_drawn_inputs(seed))
    spreads = {'L0_attn_dt_bias': (1.0, 0.2),
     'L0_attn_L': (1.0, 0.2),
     'L0_attn_D': (1.0, 0.2),
     'L0_attn_norm_w': (1.0, 0.2),
     'L0_attn_out_proj_b': (0.0, 0.1),
     'L0_ffn_gate_b': (0.0, 0.8),
     'L0_ffn_b1': (0.0, 0.8),
     'L0_ffn_b3': (0.0, 0.8),
     'L0_ffn_b2': (0.0, 0.51),
     'L0_ffn_bs1': (0.0, 0.8),
     'L0_ffn_bs3': (0.0, 0.8),
     'L0_ffn_bs2': (0.0, 0.1),
     'L1_attn_bo': (0.0, 0.1),
     'L1_xattn_bo': (0.0, 0.1),
     'L2_attn_D': (1.0, 0.2),
     'L2_ffn_switch_b': (0.0, 0.42),
     'L2_ffn_b1': (0.0, 0.8),
     'L2_ffn_b2': (0.0, 0.604),
     'L3_attn_gamma': (1.0, 0.2),
     'L3_attn_beta': (0.0, 0.298),
     'L3_xattn_ln_x_g': (1.0, 0.536),
     'L3_xattn_ln_x_b': (0.0, 0.1),
     'L3_xattn_ln_l_g': (1.0, 0.2),
     'L3_xattn_ln_l_b': (0.0, 0.268),
     'L3_xattn_ln_o_g': (1.0, 0.2),
     'L3_xattn_ln_o_b': (0.0, 0.337)}
    factors = {'L0_xattn_bk': 8.0,
     'L0_ffn_gate_w': 4.274,
     'L0_ffn_w1': 8.0,
     'L0_ffn_w3': 8.0,
     'L0_ffn_w2': 8.0,
     'L0_ffn_ws1': 3.775,
     'L0_ffn_ws3': 3.725,
     'L0_ffn_ws2': 3.572,
     'L1_attn_Wq': 8.0,
     'L1_attn_Wk': 8.0,
     'L1_attn_w': 22.956,
     'L1_attn_v': 30.186,
     'L1_xattn_Wk': 8.0,
     'L1_xattn_Wq': 8.0,
     'L1_ffn_w_gate': 3.299,
     'L1_ffn_w_up': 3.219,
     'L1_ffn_w_down': 3.142,
     'L2_attn_A': 59.088,
     'L2_attn_B': 5.395,
     'L2_attn_C': 4.307,
     'L2_attn_log_dt': 57.008,
     'L3_attn_Wq': 18.672,
     'L3_attn_bq': 55.295,
     'L3_attn_Wk': 29.227,
     'L3_attn_bk': 64.0,
     'L3_attn_bv': 21.813,
     'L3_xattn_Wq': 4.615,
     'L3_ffn_gate_w': 8.0,
     'L3_ffn_we_gate': 8.0,
     'L3_ffn_we_up': 8.0,
     'L3_ffn_we_down': 8.0,
     'L3_ffn_ws_gate': 8.0,
     'L3_ffn_ws_up': 8.0,
     'L3_ffn_ws_down': 8.0}
    for name, (base, spread) in spreads.items():
        noise = np.random.default_rng([zlib.crc32(name.encode()), seed]).standard_normal(out[name].shape)
        drawn = base * np.exp(spread * noise) if base else spread * noise
        out[name] = jnp.asarray(drawn.astype(out[name].dtype))
    for name, factor in factors.items():
        out[name] = (out[name] * factor).astype(out[name].dtype)
    return out
```

```python
from contextlib import ExitStack

import numpy as np

import concourse.bass as bass
from concourse import mybir

P = 128
B, T, D = 8, 256, 256
N = B * T
NT = N // P
KD = D // P
TB = T // P
BLK = 512
NBLK = N // BLK

F32 = mybir.dt.float32
I32 = mybir.dt.int32
BF16 = mybir.dt.bfloat16
U8 = mybir.dt.uint8
ACT = mybir.ActivationFunctionType
ALU = mybir.AluOpType
AX = mybir.AxisListType
ROUND = 12582912.0


class Signals:

    def __init__(self, nc, tag):
        self.nc, self.tag, self.ctx, self.by_name = nc, tag, ExitStack(), {}

    def __call__(self, name):
        if name not in self.by_name:
            self.by_name[name] = self.ctx.enter_context(self.nc.semaphore(f"{self.tag}_{name}"))
        return self.by_name[name]

    def clear(self):
        for s in self.by_name.values():
            self.nc.sync.sem_clear(s)
        self.nc.all_engine_barrier()

    def close(self):
        self.ctx.close()


class Ring:

    def __init__(self, sig, name, bufs):
        self.filled, self.emptied, self.bufs = sig(name + "_filled"), sig(name + "_emptied"), bufs
        self.n_in = self.n_out = 0

    def claim(self, eng):
        if self.n_in >= len(self.bufs):
            eng.wait_ge(self.emptied, self.n_in - len(self.bufs) + 1)
        self.n_in += 1
        return self.bufs[(self.n_in - 1) % len(self.bufs)]

    def fill(self, ins):
        ins.then_inc(self.filled, 1)

    def take(self, eng):
        self.n_out += 1
        eng.wait_ge(self.filled, self.n_out)
        return self.bufs[(self.n_out - 1) % len(self.bufs)]

    def empty(self, ins):
        ins.then_inc(self.emptied, 1)


class Chain:

    def __init__(self, eng, sem):
        self.eng, self.sem, self.n = eng, sem, 0

    def link(self, ins):
        self.n += 1
        ins.then_inc(self.sem, 1)
        self.eng.wait_ge(self.sem, self.n)


class Core:

    def __init__(self, nc, ctx, dram):
        self.nc, self.dram = nc, dram
        sb = lambda name, shape, dt=F32: ctx.enter_context(nc.sbuf_tensor(name, shape, dt))
        self.x = sb("x_res", [P, NT, D])
        self.ctx = sb("ctx_tok", [P, NT, D])
        self.ctxT = sb("ctx_feat", [P, KD, N])
        self.xT = sb("x_feat", [P, KD, N])
        self.ident = sb("ident", [P, P])
        self.banks = [ctx.enter_context(nc.psum_tensor(f"bank{i}", [P, BLK], F32)) for i in range(8)]

    def tiles(self, stack, tag):
        return lambda name, shape, dt=F32: stack.enter_context(self.nc.sbuf_tensor(f"{tag}_{name}", shape, dt))

    def load(self, tag, pairs):
        nc, sig = self.nc, Signals(self.nc, tag)
        with nc.Block() as block:

            @block.sync
            def _(sp):
                for dst, src in pairs[0::2]:
                    sp.dma_start(dst, src).then_inc(sig("loaded_sp"), 16)
                sp.wait_ge(sig("loaded_sp"), 16 * len(pairs[0::2]))

            @block.scalar
            def _(act):
                for dst, src in pairs[1::2]:
                    act.dma_start(dst, src).then_inc(sig("loaded_act"), 16)
                if len(pairs) > 1:
                    act.wait_ge(sig("loaded_act"), 16 * len(pairs[1::2]))
        sig.clear()
        sig.close()


def transpose_tokens(c, tag, src, dstT):
    nc = c.nc
    sig = Signals(nc, tag)
    with ExitStack() as stack:
        xs = c.tiles(stack, tag)("xs", [P, 4, D])
        with nc.Fori(0, NT // 4) as t:
            with nc.Block() as block:
                @block.vector
                def _(dve):
                    nc.vector.tensor_copy(xs[:], src[:, bass.ts(t, 4), :]).then_inc(sig("copied"), 1)

                @block.tensor
                def _(pe):
                    pe.wait_ge(sig("copied"), 1)
                    for k in range(KD):
                        for j in range(4):
                            last = nc.tensor.transpose(c.banks[k][:, j * P:(j + 1) * P],
                                                       xs[:, j, k * P:(k + 1) * P], c.ident[:])
                        last.then_inc(sig("transposed"), 1)

                @block.scalar
                def _(act):
                    for k in range(KD):
                        act.wait_ge(sig("transposed"), k + 1)
                        nc.scalar.activation(dstT[:, k, bass.ts(t, BLK)], c.banks[k][:], ACT.Copy)
            sig.clear()
    sig.close()


def normalise(c, tag, src, dst=None, dstT=None, gain=None, shift=None, eps=1e-5):
    nc = c.nc
    sig = Signals(nc, tag)
    with ExitStack() as stack:
        sb = c.tiles(stack, tag)
        stats = sb("stats", [P, 4, 6])
        mv = sb("mv", [P, 4, 2])
        rstd = sb("rstd", [P, 4, 3])
        xs = sb("xs", [P, 4, D])
        with nc.Fori(0, NT // 4) as t:
            with nc.Block() as block:
                @block.vector
                def _(dve):
                    for j in range(4):
                        last = nc.vector.bn_stats(stats[:, j, :], src[:, t * 4 + j, :])
                    last.then_inc(sig("stats"), 1)
                    dve.wait_ge(sig("stats"), 1)
                    for j in range(4):
                        last = nc.vector.bn_aggr(mv[:, j, :], stats[:, j, :])
                    last.then_inc(sig("mean_var"), 1)
                    dve.wait_ge(sig("mean_var"), 1)
                    nc.vector.tensor_scalar_add(rstd[:, :, 0], mv[:, :, 1], eps).then_inc(sig("var_eps"), 1)
                    dve.wait_ge(sig("std"), 1)
                    nc.vector.reciprocal(rstd[:, :, 2], rstd[:, :, 1]).then_inc(sig("rstd"), 1)
                    dve.wait_ge(sig("rstd"), 1)
                    for j in range(4):
                        nc.vector.tensor_scalar(xs[:, j, :], src[:, t * 4 + j, :], mv[:, j, 0:1], rstd[:, j, 2:3],
                                                ALU.subtract, ALU.mult).then_inc(sig("normed"), 1)
                    if dst is not None:
                        dve.wait_ge(sig("normed"), 4)
                        nc.vector.tensor_copy(dst[:, bass.ts(t, 4), :], xs[:])

                @block.tensor
                def _(pe):
                    if dstT is not None:
                        pe.wait_ge(sig("normed"), 4)
                        for k in range(KD):
                            for j in range(4):
                                last = nc.tensor.transpose(c.banks[k][:, j * P:(j + 1) * P],
                                                           xs[:, j, k * P:(k + 1) * P], c.ident[:])
                            last.then_inc(sig("transposed"), 1)

                @block.scalar
                def _(act):
                    act.wait_ge(sig("var_eps"), 1)
                    nc.scalar.activation(rstd[:, :, 1], rstd[:, :, 0], ACT.Sqrt).then_inc(sig("std"), 1)
                    if dstT is not None:
                        for k in range(KD):
                            act.wait_ge(sig("transposed"), k + 1)
                            if gain is None:
                                nc.scalar.activation(dstT[:, k, bass.ts(t, BLK)], c.banks[k][:], ACT.Copy)
                            else:
                                nc.scalar.activation(dstT[:, k, bass.ts(t, BLK)], c.banks[k][:], ACT.Identity,
                                                     bias=shift[:, k:k + 1], scale=gain[:, k:k + 1])
            sig.clear()
    sig.close()


def mixture(c, tag, n_routed, n_shared, M, gated, top, biases, renorm=False, capacity=None):
    nc = c.nc
    E = n_routed + n_shared
    R = n_routed
    w = c.dram
    F = M * P
    act_fn = ACT.Silu if gated else ACT.Gelu_apprx_tanh
    with ExitStack() as stack:
        sb = c.tiles(stack, tag)
        comb = sb("comb", [P, E, NT])
        combT = sb("combT", [E, NT, P])
        down_b = sb("down_b", [E, D])
        with ExitStack() as inner:
            sc = c.tiles(inner, tag)
            gate = sc("gate", [P, KD, R])
            gate_b = sc("gate_b", [P, R])
            iota = sc("iota", [P, R])
            trist = sc("trist", [P, 2, P])
            pairs = [(gate[:], w[f"{tag}_gate"]), (iota[:], w["iota8"])]
            if biases:
                pairs += [(gate_b[:], w[f"{tag}_gate_b"].rearrange("(a n) -> a n", a=1).to_broadcast([P, R])),
                          (down_b[:], w[f"{tag}_down_b"])]
            if capacity:
                pairs += [(trist[:], w["tri_strict_ones"])]
            c.load(tag + "_ldg", pairs)
            prob = sc("prob", [P, NT, R])
            tmp = sc("tmp", [P, NT, R])
            onehot = sc("onehot", [P, NT, R])
            assigned = sc("assigned", [P, NT, R])
            dense = sc("dense", [P, NT, R])
            count = sc("count", [P, NT, R])
            best = sc("best", [P, NT])
            wsum = sc("wsum", [P, NT])
            sig = Signals(nc, tag + "_gt")
            with nc.Block() as block:
                def bc(t2):
                    return t2[:].unsqueeze(2).to_broadcast([P, NT, R])

                def ie():
                    return iota[:].unsqueeze(1).to_broadcast([P, NT, R])

                logits = c.banks[0][:, 0:NT * R].rearrange("p (t e) -> p t e", t=NT)
                inside = c.banks[1][:, 0:NT * R].rearrange("p (t e) -> p t e", t=NT)
                totals = c.banks[2][:, 0:NT * R].rearrange("p (t e) -> p t e", t=NT)

                @block.tensor
                def _(pe):
                    for t in range(NT):
                        for k in range(KD):
                            last = nc.tensor.matmul(logits[:, t, :], c.xT[:, k, t * P:(t + 1) * P], gate[:, k, :],
                                                    start=(k == 0), stop=(k == KD - 1))
                    last.then_inc(sig("logits"), 1)
                    if capacity:
                        pe.wait_ge(sig("assigned"), 1)
                        nc.tensor.matmul(c.banks[1][:, 0:NT * R], trist[:, 0, :], assigned[:].rearrange("p t e -> p (t e)"),
                                         start=True, stop=True)
                        nc.tensor.matmul(c.banks[2][:, 0:NT * R], trist[:, 1, :], assigned[:].rearrange("p t e -> p (t e)"),
                                         start=True, stop=True).then_inc(sig("counted"), 1)
                    pe.wait_ge(sig("comb"), 1)
                    if biases:
                        for t in range(NT):
                            bank = c.banks[3 + t // 4]
                            last = nc.tensor.transpose(bank[0:E, (t % 4) * P:(t % 4 + 1) * P], comb[:, :, t], c.ident[:])
                        last.then_inc(sig("combT"), 1)

                @block.scalar
                def _(act):
                    act.wait_ge(sig("centred"), 1)
                    nc.scalar.activation(prob[:], prob[:], ACT.Exp).then_inc(sig("exp"), 1)
                    if biases:
                        act.wait_ge(sig("combT"), 1)
                        for i in range(4):
                            nc.scalar.activation(combT[:, 4 * i:4 * i + 4, :].rearrange("e t p -> e (t p)"),
                                                 c.banks[3 + i][0:E, :], ACT.Copy)

                @block.vector
                def _(dve):
                    ch = Chain(dve, sig("dve_chain"))
                    v = nc.vector
                    dve.wait_ge(sig("logits"), 1)
                    if biases:
                        ch.link(v.tensor_tensor(prob[:], logits, gate_b[:].unsqueeze(1).to_broadcast([P, NT, R]), ALU.add))
                    else:
                        ch.link(v.tensor_copy(prob[:], logits))
                    ch.link(v.tensor_reduce(best[:], prob[:], AX.X, ALU.max))
                    v.tensor_tensor(prob[:], prob[:], bc(best), ALU.subtract).then_inc(sig("centred"), 1)
                    dve.wait_ge(sig("exp"), 1)
                    ch.link(v.tensor_reduce(wsum[:], prob[:], AX.X, ALU.add))
                    ch.link(v.reciprocal(wsum[:], wsum[:]))
                    ch.link(v.tensor_tensor(prob[:], prob[:], bc(wsum), ALU.mult))
                    ch.link(v.memset(assigned[:], 0.0))
                    ch.link(v.memset(dense[:], 0.0))
                    for r in range(top):
                        ch.link(v.tensor_reduce(best[:], prob[:], AX.X, ALU.max))
                        ch.link(v.tensor_tensor(onehot[:], prob[:], bc(best), ALU.is_equal))
                        ch.link(v.tensor_scalar(onehot[:], onehot[:], -64.0, 64.0, ALU.mult, ALU.add))
                        ch.link(v.tensor_tensor(onehot[:], onehot[:], ie(), ALU.add))
                        ch.link(v.tensor_reduce(wsum[:], onehot[:], AX.X, ALU.min))
                        ch.link(v.tensor_tensor(onehot[:], bc(wsum), ie(), ALU.is_equal))
                        ch.link(v.tensor_tensor(assigned[:], assigned[:], onehot[:], ALU.add))
                        ch.link(v.tensor_tensor(tmp[:], onehot[:], bc(best), ALU.mult))
                        ch.link(v.tensor_tensor(dense[:], dense[:], tmp[:], ALU.add))
                        if r + 1 < top:
                            ch.link(v.tensor_scalar(onehot[:], onehot[:], -2.0, None, ALU.mult))
                            ch.link(v.tensor_tensor(prob[:], prob[:], onehot[:], ALU.add))
                    if renorm:
                        ch.link(v.tensor_reduce(wsum[:], dense[:], AX.X, ALU.add))
                        ch.link(v.tensor_scalar_add(wsum[:], wsum[:], 1e-20))
                        ch.link(v.reciprocal(wsum[:], wsum[:]))
                        ch.link(v.tensor_tensor(dense[:], dense[:], bc(wsum), ALU.mult))
                    if capacity:
                        v.tensor_copy(tmp[:], assigned[:]).then_inc(sig("assigned"), 1)
                        dve.wait_ge(sig("counted"), 1)
                        ch.link(v.memset(count[:, 0, :], 0.0))
                        for t in range(1, NT):
                            ch.link(v.tensor_tensor(count[:, t, :], count[:, t - 1, :], totals[:, t - 1, :], ALU.add))
                        ch.link(v.tensor_tensor(count[:], count[:], inside, ALU.add))
                        ch.link(v.tensor_scalar(count[:], count[:], float(capacity), None, ALU.is_lt))
                        ch.link(v.tensor_tensor(dense[:], dense[:], count[:], ALU.mult))
                    if n_shared:
                        ch.link(v.memset(comb[:, R:E, :], 1.0))
                    v.tensor_copy(comb[:, 0:R, :].rearrange("p e t -> p t e"), dense[:]).then_inc(sig("comb"), 1)
            sig.clear()
            sig.close()
        up = [sb(f"up{i}", [P, KD, F]) for i in range(2)]
        lin = [sb(f"lin{i}", [P, KD, F]) for i in range(2)] if gated else None
        down = [sb(f"down{i}", [P, M, D]) for i in range(2)]
        bup = sb("bup", [P, 2, 2, M])
        hT = [sb(f"hT{i}", [P, M, BLK]) for i in range(2)]
        silu = [sb(f"silu{i}", [P, BLK]) for i in range(2)] if gated else None
        comb2 = sb("comb2", [P, 2, NT])
        if biases:
            sig = Signals(nc, tag + "_ob")
            with nc.Block() as block:
                ring = Ring(sig, "bias", c.banks[0:4])

                @block.tensor
                def _(pe):
                    for t in range(NT):
                        ring.fill(nc.tensor.matmul(ring.claim(pe)[:, 0:D], combT[:, t, :], down_b[:], start=True, stop=True))

                @block.vector
                def _(dve):
                    for t in range(NT):
                        bank = ring.take(dve)
                        ring.empty(nc.vector.tensor_tensor(c.x[:, t, :], bank[:, 0:D], c.x[:, t, :], ALU.add))
            sig.clear()
            sig.close()
        sig = Signals(nc, tag + "_ex")
        with nc.Fori(0, E // 2) as pair:
            with nc.Block() as block:
                up_ring = Ring(sig, "up", c.banks[0:3])
                lin_ring = Ring(sig, "lin", c.banks[3:5])
                out_ring = Ring(sig, "out", c.banks[5:8])
                silu_ring = Ring(sig, "silu", silu) if gated else None
                steps = [(i, n) for i in range(2) for n in range(NBLK)]

                @block.sync
                def _(sp):
                    for i in range(2):
                        e = pair * 2 + i
                        sp.dma_start(up[i][:], w[f"{tag}_up"][e]).then_inc(sig(f"w_up{i}"), 16)
                        if gated:
                            sp.dma_start(lin[i][:], w[f"{tag}_lin"][e]).then_inc(sig(f"w_up{i}"), 16)
                        if biases:
                            sp.dma_start(bup[:, i, 0, :], w[f"{tag}_up_b"][e]).then_inc(sig(f"w_up{i}"), 16)
                            if gated:
                                sp.dma_start(bup[:, i, 1, :], w[f"{tag}_lin_b"][e]).then_inc(sig(f"w_up{i}"), 16)
                        sp.dma_start(down[i][:], w[f"{tag}_down"][e]).then_inc(sig(f"w_down{i}"), 16)

                n_up = 16 * (1 + gated) * (1 + biases)

                @block.tensor
                def _(pe):
                    def rise(i, n):
                        if n == 0:
                            pe.wait_ge(sig(f"w_up{i}"), n_up)
                        for m in range(M):
                            for weights, ring in ((up, up_ring), (lin, lin_ring)) if gated else ((up, up_ring),):
                                bank = ring.claim(pe)
                                for k in range(KD):
                                    last = nc.tensor.matmul(bank[:], weights[i][:, k, m * P:(m + 1) * P],
                                                            c.xT[:, k, n * BLK:(n + 1) * BLK],
                                                            start=(k == 0), stop=(k == KD - 1))
                                ring.fill(last)

                    def fall(s):
                        i, n = steps[s]
                        if n == 0:
                            pe.wait_ge(sig(f"w_down{i}"), 16)
                        pe.wait_ge(sig("h"), M * (s + 1))
                        for half in range(2):
                            bank = out_ring.claim(pe)
                            for j in range(2):
                                tok = (2 * half + j) * P
                                for m in range(M):
                                    last = nc.tensor.matmul(bank[:, j * D:(j + 1) * D], hT[s % 2][:, m, tok:tok + P],
                                                            down[i][:, m, :], start=(m == 0), stop=(m == M - 1))
                            out_ring.fill(last)

                    for s, (i, n) in enumerate(steps):
                        rise(i, n)
                        if s:
                            fall(s - 1)
                    fall(len(steps) - 1)

                @block.scalar
                def _(act):
                    for s, (i, n) in enumerate(steps):
                        if biases and n == 0:
                            act.wait_ge(sig(f"w_up{i}"), n_up)
                        for m in range(M):
                            bank = up_ring.take(act)
                            if gated:
                                dst = silu_ring.claim(act)[:]
                            else:
                                dst = hT[s % 2][:, m, :]
                                if s >= 2 and m == 0:
                                    act.wait_ge(out_ring.filled, 2 * (s - 1))
                            ins = nc.scalar.activation(dst, bank[:], act_fn, bias=bup[:, i, 0, m:m + 1] if biases else 0.0)
                            ins.then_inc(up_ring.emptied, 1)
                            act.wait_ge(up_ring.emptied, up_ring.n_out)
                            nc.scalar.sem_inc(silu_ring.filled if gated else sig("h"), 1)

                @block.vector
                def _(dve):
                    nc.vector.tensor_copy(comb2[:], comb[:, bass.ts(pair, 2), :]).then_inc(sig("comb2"), 1)
                    dve.wait_ge(sig("comb2"), 1)

                    def gate_h(s):
                        i, n = steps[s]
                        for m in range(M):
                            sv = silu_ring.take(dve)
                            bank = lin_ring.take(dve)
                            if biases and n == 0 and m == 0:
                                dve.wait_ge(sig(f"w_up{i}"), n_up)
                            if s >= 2 and m == 0:
                                dve.wait_ge(out_ring.filled, 2 * (s - 1))
                            ins = nc.vector.scalar_tensor_tensor(out=hT[s % 2][:, m, :], in0=bank[:],
                                                                 scalar=bup[:, i, 1, m:m + 1] if biases else 0.0,
                                                                 in1=sv[:], op0=ALU.add, op1=ALU.mult)
                            ins.then_inc(sig("h"), 1)
                            dve.wait_ge(sig("h"), M * s + m + 1)
                            nc.vector.sem_inc(silu_ring.emptied, 1)
                            nc.vector.sem_inc(lin_ring.emptied, 1)

                    def add_out(s):
                        i, n = steps[s]
                        for half in range(2):
                            bank = out_ring.take(dve)
                            if s and half == 0:
                                dve.wait_ge(out_ring.emptied, 2 * s)
                            for j in range(2):
                                t = 4 * n + 2 * half + j
                                last = nc.vector.scalar_tensor_tensor(out=c.x[:, t, :], in0=bank[:, j * D:(j + 1) * D],
                                                                      scalar=comb2[:, i, t:t + 1], in1=c.x[:, t, :],
                                                                      op0=ALU.mult, op1=ALU.add)
                            out_ring.empty(last)

                    for s in range(len(steps)):
                        if gated:
                            gate_h(s)
                        if s:
                            add_out(s - 1)
                    add_out(len(steps) - 1)
            sig.clear()
        sig.close()


def layer0_ffn(c):
    normalise(c, "n0f", c.x, dstT=c.xT)
    mixture(c, "L0f", 8, 2, 2, gated=True, top=2, biases=True)


def layer2_ffn(c):
    normalise(c, "n2f", c.x, dstT=c.xT)
    mixture(c, "L2f", 8, 0, 8, gated=False, top=1, biases=True)


def layer3_ffn(c):
    normalise(c, "n3f", c.x, dstT=c.xT)
    mixture(c, "L3f", 8, 2, 2, gated=True, top=2, biases=False, renorm=True, capacity=640)

def out_tail(c, sig, ring, C, heads_out, cT, wo, out_bank):
    KC = C // P

    def on_tensor(pe, evacuated):
        for t in range(TB):
            pe.wait_ge(sig("heads_out"), t + 1)
            bank = ring.claim(pe)
            for k in range(KC):
                last = c.nc.tensor.transpose(bank[:, k * P:(k + 1) * P], heads_out[:, t, k * P:(k + 1) * P], c.ident[:])
            ring.fill(last)
        for t in range(TB):
            pe.wait_ge(ring.emptied, evacuated + t + 1)
            for k in range(KC):
                last = c.nc.tensor.matmul(out_bank[:, t * D:(t + 1) * D], cT[:, k, t * P:(t + 1) * P], wo[:, k, :],
                                          start=(k == 0), stop=(k == KC - 1))
        last.then_inc(sig("projected"), 1)

    def on_scalar(act):
        for t in range(TB):
            bank = ring.take(act)
            ring.empty(c.nc.scalar.activation(cT[:, :, t * P:(t + 1) * P],
                                              bank[:, 0:C].rearrange("p (k t) -> p k t", k=KC), ACT.Copy))

    return on_tensor, on_scalar


def softmax_attention(c, tag, H, rows, MQ, KT, DV, kind, scale, final_norm=False):
    nc, w = c.nc, c.dram
    NK, C = KT * P, H * DV
    plain = kind == "plain"
    per_tile = MQ * P // max(rows, 1)
    step = P * MQ // H if not plain else P
    with ExitStack() as stack:
        sb = c.tiles(stack, tag)
        xb = sb("xb", [P, KD, T])
        cb = sb("cb", [P, KD, T])
        qT = xb if plain else sb("qT", [P, MQ, T])
        kT = cb if plain else sb("kT", [P, MQ, NK])
        v = sb("v", [P, KT, C])
        s_sb = [sb(f"s{i}", [P, NK]) for i in range(3)]
        p_sb = [sb(f"p{i}", [P, NK]) for i in range(3)]
        pT = [sb(f"pT{i}", [P, NK]) for i in range(3)]
        nmax = sb("nmax", [P, TB * H])
        rsum = sb("rsum", [P, TB, H])
        heads_out = sb("heads_out", [P, TB, C])
        bias = sb("bias", [P, TB if kind == "pairs" else 1, NK])
        pairs = []
        if not plain:
            wq, wk = sb("wq", [P, KD, MQ * P]), sb("wk", [P, KD, MQ * P])
            wv, wo = sb("wv", [P, KD, C]), sb("wo", [P, C // P, D])
            cT = sb("cT", [P, C // P, T])
            bo = sb("bo", [P, D])
            y = sb("y", [P, TB, D])
            pairs += [(wq[:], w[f"{tag}_wq"]), (wk[:], w[f"{tag}_wk"]), (wv[:], w[f"{tag}_wv"]), (wo[:], w[f"{tag}_wo"])]
            if kind != "latent":
                pairs += [(bo[:], w[f"{tag}_bo"].rearrange("(a n) -> a n", a=1).to_broadcast([P, D]))]
        if kind == "pairs":
            mask = sb("mask", [P, TB, NK], I32)
        if kind == "plain":
            mask = sb("mask", [P, 1, NK], I32)
        if kind == "latent":
            mask = sb("mask", [P, 1, T], U8)
            xb2 = cb
            og, ob = sb("og", [P, D]), sb("ob", [P, D])
            stats, mv, rstd = sb("stats", [P, TB, 6]), sb("mv", [P, TB, 2]), sb("rstd", [P, TB, 3])
            pairs += [(og[:], w[f"{tag}_og"].rearrange("(a n) -> a n", a=1).to_broadcast([P, D])),
                      (ob[:], w[f"{tag}_ob"].rearrange("(a n) -> a n", a=1).to_broadcast([P, D]))]
        if kind == "decay":
            rhat = sb("rhat", [P, H, 3 * P])
            dist = sb("dist", [P, 3 * P])
            future = sb("future", [P, P])
            wh, vh, ev = sb("wh", [P, H]), sb("vh", [P, H]), sb("ev", [P, H])
            pairs += [(dist[:], w["distance"]), (future[:], w["future_neg"]),
                      (wh[:], w[f"{tag}_w"].rearrange("(a n) -> a n", a=1).to_broadcast([P, H])),
                      (vh[:], w[f"{tag}_v"].rearrange("(a n) -> a n", a=1).to_broadcast([P, H]))]
        if pairs:
            c.load(tag + "_ld", pairs)
        if kind == "decay":
            sig = Signals(nc, tag + "_rh")
            with nc.Block() as block:
                @block.vector
                def _(dve):
                    for h in range(H):
                        last = nc.vector.tensor_scalar(rhat[:, h, :], dist[:], wh[:, h:h + 1], -1.0, ALU.mult, ALU.mult)
                    last.then_inc(sig("minus_wr"), 1)
                    dve.wait_ge(sig("exped"), H + 1)
                    ch = Chain(dve, sig("dve_chain"))
                    ch.link(nc.vector.tensor_scalar(rhat[:], rhat[:], 1.0, None, ALU.add))
                    ch.link(nc.vector.reciprocal(rhat[:], rhat[:]))
                    ch.link(nc.vector.tensor_scalar(ev[:], ev[:], 1.0, scale, ALU.add, ALU.mult))
                    for h in range(H):
                        last = nc.vector.tensor_scalar(rhat[:, h, :], rhat[:, h, :], ev[:, h:h + 1], None, ALU.mult)

                @block.scalar
                def _(act):
                    nc.scalar.activation(ev[:], vh[:], ACT.Exp).then_inc(sig("exped"), 1)
                    act.wait_ge(sig("minus_wr"), 1)
                    for h in range(H):
                        nc.scalar.activation(rhat[:, h, :], rhat[:, h, :], ACT.Exp,
                                             bias=vh[:, h:h + 1]).then_inc(sig("exped"), 1)
            sig.clear()
            sig.close()

        sig = Signals(nc, tag)
        with nc.Fori(0, B) as b:
            with nc.Block() as block:
                s_ring = Ring(sig, "s", c.banks[0:3])
                t_ring = Ring(sig, "t", c.banks[3:5])
                acc = c.banks[5:7]
                out_bank = c.banks[7]
                items = [(t, h) for t in range(TB) for h in range(H)]
                n = len(items)
                causal = kind == "decay"
                keys = lambda t: (t + 1) * P if causal else NK
                wo_ = None if plain else wo
                tail_pe, tail_act = (None, None) if plain else out_tail(c, sig, t_ring, C, heads_out, cT, wo_, out_bank)
                q_banks = 0 if plain else (MQ + 1) // 2
                k_banks = 0 if plain else MQ * (NK // T) // 2
                v_banks = 0 if plain else KT

                def source(i):
                    return (cb, i) if kind in ("pairs",) else (xb, i) if kind == "decay" else ((cb, i) if i < TB else (xb, i - TB))

                def parts(h):
                    if plain:
                        return [(k, slice(0, P)) for k in range(KD)]
                    p0 = h * step
                    return [(p0 // P, slice(p0 % P, p0 % P + rows))]

                @block.sync
                def _(sp):
                    if kind == "pairs":
                        sp.dma_start(mask[:], w["mask_pairs"][b]).then_inc(sig("mask"), 16)
                    if kind == "plain":
                        sp.dma_start(mask[:, 0, :], w["mask_keys"][b].to_broadcast([P, NK])).then_inc(sig("mask"), 16)
                    if kind == "latent":
                        sp.dma_start(mask[:, 0, :], w["mask_bool"][b].to_broadcast([P, T])).then_inc(sig("mask"), 16)

                @block.tensor
                def _(pe):
                    if not plain:
                        pe.wait_ge(sig("sliced"), 2)
                        for i in range(0, MQ, 2):
                            bank = t_ring.claim(pe)
                            for m in range(i, min(i + 2, MQ)):
                                for k in range(KD):
                                    last = nc.tensor.matmul(bank[:, (m - i) * T:(m - i + 1) * T], wq[:, k, m * P:(m + 1) * P],
                                                            xb[:, k, :], start=(k == 0), stop=(k == KD - 1))
                            t_ring.fill(last)
                        for i in range(0, MQ * (NK // T), 2):
                            bank = s_ring.claim(pe)
                            for j in (i, i + 1):
                                m, part = j % MQ, j // MQ
                                src = source(part * TB)[0]
                                for k in range(KD):
                                    last = nc.tensor.matmul(bank[:, (j - i) * T:(j - i + 1) * T], wk[:, k, m * P:(m + 1) * P],
                                                            src[:, k, :], start=(k == 0), stop=(k == KD - 1))
                            s_ring.fill(last)
                        for i in range(KT):
                            bank = t_ring.claim(pe)
                            src, j = source(i)
                            for k in range(KD):
                                last = nc.tensor.matmul(bank[:, 0:C], src[:, k, j * P:(j + 1) * P], wv[:, k, :],
                                                        start=(k == 0), stop=(k == KD - 1))
                            t_ring.fill(last)
                        pe.wait_ge(t_ring.emptied, q_banks)
                        pe.wait_ge(s_ring.emptied, k_banks)
                    else:
                        pe.wait_ge(sig("sliced"), 3)
                    for i in range(n + 3):
                        if i < n:
                            t, h = items[i]
                            bank = s_ring.claim(pe)
                            pp = parts(h)
                            for j, (m, ps) in enumerate(pp):
                                last = nc.tensor.matmul(bank[:, 0:keys(t)], qT[ps, m, t * P:(t + 1) * P], kT[ps, m, 0:keys(t)],
                                                        start=(j == 0), stop=(j == len(pp) - 1))
                            s_ring.fill(last)
                        if 2 <= i < n + 2:
                            j = i - 2
                            bank = t_ring.claim(pe)
                            pe.wait_ge(sig("exp"), j + 1)
                            for kt in range(keys(items[j][0]) // P):
                                last = nc.tensor.transpose(bank[:, kt * P:(kt + 1) * P], p_sb[j % 3][:, kt * P:(kt + 1) * P], c.ident[:])
                            t_ring.fill(last)
                        if i >= 3:
                            j = i - 3
                            t, h = items[j]
                            pe.wait_ge(t_ring.emptied, q_banks + v_banks + j + 1)
                            nkt = keys(t) // P
                            for kt in range(nkt):
                                last = nc.tensor.matmul(acc[t][:, h * DV:(h + 1) * DV], pT[j % 3][:, kt * P:(kt + 1) * P],
                                                        v[:, kt, h * DV:(h + 1) * DV], start=(kt == 0), stop=(kt == nkt - 1))
                            last.then_inc(sig("weighted"), 1)
                    if not plain:
                        tail_pe(pe, q_banks + v_banks + n)

                @block.scalar
                def _(act):
                    nc.scalar.activation(xb[:], c.xT[:, :, bass.ts(b, T)], ACT.Copy).then_inc(sig("sliced"), 1)
                    if plain:
                        nc.scalar.activation(v[:], c.ctx[:, bass.ts(b, TB), :], ACT.Copy).then_inc(sig("sliced"), 1)
                    else:
                        for i in range(0, MQ, 2):
                            bank = t_ring.take(act)
                            t_ring.empty(nc.scalar.activation(qT[:, i:i + 2, :], bank[:].rearrange("p (m t) -> p m t", m=2), ACT.Copy))
                        for i in range(KT):
                            bank = t_ring.take(act)
                            t_ring.empty(nc.scalar.activation(v[:, i, :], bank[:, 0:C], ACT.Copy))
                    for i in range(n + 1):
                        if i < n:
                            nk = keys(items[i][0])
                            act.wait_ge(s_ring.emptied, k_banks + i + 1)
                            nc.scalar.activation(p_sb[i % 3][:, 0:nk], s_sb[i % 3][:, 0:nk], ACT.Exp, bias=nmax[:, i:i + 1],
                                                 accum_out=rsum[:, items[i][0], items[i][1]:items[i][1] + 1]).then_inc(sig("exp"), 1)
                        if i >= 1:
                            j = i - 1
                            nk = keys(items[j][0])
                            if j >= 3:
                                act.wait_ge(sig("weighted"), j - 2)
                            bank = t_ring.take(act)
                            t_ring.empty(nc.scalar.activation(pT[j % 3][:, 0:nk], bank[:, 0:nk], ACT.Copy))
                    if not plain:
                        tail_act(act)
                    if kind == "latent":
                        act.wait_ge(sig("var_eps"), 1)
                        nc.scalar.activation(rstd[:, :, 1], rstd[:, :, 0], ACT.Sqrt).then_inc(sig("std"), 1)

                @block.vector
                def _(dve):
                    ch = Chain(dve, sig("dve_chain"))
                    vec = nc.vector
                    if kind == "latent":
                        vec.tensor_copy(cb[:], c.ctxn[:, :, bass.ts(b, T)]).then_inc(sig("sliced"), 1)
                    else:
                        vec.tensor_copy(cb[:], c.ctxT[:, :, bass.ts(b, T)]).then_inc(sig("sliced"), 1)
                    if kind == "pairs":
                        dve.wait_ge(sig("mask"), 16)
                        ch.link(vec.tensor_scalar(bias[:], mask[:], 0.0, -1.0, ALU.not_equal, ALU.add))
                        ch.link(vec.tensor_scalar(bias[:], bias[:], 1e20 * scale, None, ALU.mult))
                    if kind == "plain":
                        dve.wait_ge(sig("mask"), 16)
                        ch.link(vec.tensor_scalar(bias[:], mask[:], -1e9, None, ALU.mult))
                    if kind == "latent":
                        dve.wait_ge(sig("mask"), 16)
                        ch.link(vec.tensor_scalar(bias[:, :, 0:T], mask[:], 0.0, -1.0, ALU.not_equal, ALU.add))
                        ch.link(vec.tensor_scalar(bias[:, :, 0:T], bias[:, :, 0:T], 3e38, None, ALU.mult))
                        ch.link(vec.memset(bias[:, :, T:NK], 0.0))
                    if not plain:
                        for i in range(0, MQ * (NK // T), 2):
                            bank = s_ring.take(dve)
                            m, part = i % MQ, i // MQ
                            s_ring.empty(vec.tensor_copy(kT[:, m:m + 2, part * T:(part + 1) * T],
                                                         bank[:].rearrange("p (m t) -> p m t", m=2)))
                    for i, (t, h) in enumerate(items):
                        bank = s_ring.take(dve)
                        nk = keys(t)
                        s = s_sb[i % 3]
                        if i >= 3:
                            dve.wait_ge(sig("exp"), i - 2)
                        if kind == "decay":
                            f = rhat[:, h, 0:P] if t == 0 else rhat[:, h, P:3 * P]
                            ch.link(vec.scalar_tensor_tensor(out=s[:, 0:nk], in0=bank[:, 0:nk], scalar=0.0, in1=f,
                                                             op0=ALU.max, op1=ALU.mult))
                            ch.link(vec.tensor_tensor(s[:, nk - P:nk], s[:, nk - P:nk], future[:], ALU.add))
                        else:
                            ch.link(vec.scalar_tensor_tensor(out=s[:], in0=bank[:], scalar=scale, in1=bias[:, t if kind == "pairs" else 0, :],
                                                             op0=ALU.mult, op1=ALU.add) if NK == BLK else
                                    vec.scalar_tensor_tensor(out=s[:], in0=bank[:, 0:NK], scalar=scale,
                                                             in1=bias[:, t if kind == "pairs" else 0, :], op0=ALU.mult, op1=ALU.add))
                        s_ring.empty(vec.tensor_reduce(nmax[:, i:i + 1], s[:, 0:nk], AX.X, ALU.max, negate=True))
                    for t in range(TB):
                        dve.wait_ge(sig("weighted"), H * (t + 1))
                        ch.link(vec.reciprocal(rsum[:, t, :], rsum[:, t, :]))
                        vec.tensor_tensor(heads_out[:, t, :].rearrange("p (h d) -> p h d", h=H),
                                          acc[t][:, 0:C].rearrange("p (h d) -> p h d", h=H),
                                          rsum[:, t, :].unsqueeze(2).to_broadcast([P, H, DV]), ALU.mult).then_inc(sig("heads_out"), 1)
                    if plain:
                        dve.wait_ge(sig("heads_out"), TB)
                        vec.tensor_tensor(c.x[:, bass.ts(b, TB), :], c.x[:, bass.ts(b, TB), :], heads_out[:], ALU.add)
                        return
                    dve.wait_ge(sig("projected"), 1)
                    proj = out_bank[:].rearrange("p (t d) -> p t d", t=TB)
                    rowwise = lambda a: a[:].unsqueeze(1).to_broadcast([P, TB, D])
                    if kind == "latent":
                        for t in range(TB):
                            last = vec.bn_stats(stats[:, t, :], proj[:, t, :])
                        ch.link(last)
                        for t in range(TB):
                            last = vec.bn_aggr(mv[:, t, :], stats[:, t, :])
                        ch.link(last)
                        vec.tensor_scalar_add(rstd[:, :, 0], mv[:, :, 1], 1e-5).then_inc(sig("var_eps"), 1)
                        dve.wait_ge(sig("std"), 1)
                        ch.link(vec.reciprocal(rstd[:, :, 2], rstd[:, :, 1]))
                        for t in range(TB):
                            last = vec.tensor_scalar(y[:, t, :], proj[:, t, :], mv[:, t, 0:1], rstd[:, t, 2:3], ALU.subtract, ALU.mult)
                        ch.link(last)
                        ch.link(vec.tensor_tensor(y[:], y[:], rowwise(og), ALU.mult))
                        ch.link(vec.tensor_tensor(y[:], y[:], rowwise(ob), ALU.add))
                    else:
                        ch.link(vec.tensor_tensor(y[:], proj, rowwise(bo), ALU.add))
                    vec.tensor_tensor(c.x[:, bass.ts(b, TB), :], c.x[:, bass.ts(b, TB), :], y[:], ALU.add)
            sig.clear()
        sig.close()


def layer1_attn(c):
    normalise(c, "n1a", c.x, dstT=c.xT)
    softmax_attention(c, "L1a", 16, 16, 4, 2, 16, "decay", 0.25)


def layer1_xattn(c):
    normalise(c, "n1x", c.x, dstT=c.xT)
    softmax_attention(c, "L1x", 16, 16, 4, 2, 16, "pairs", 0.25)


def layer2_xattn(c):
    normalise(c, "n2x", c.x, dstT=c.xT)
    softmax_attention(c, "L2x", 1, 0, 2, 2, 256, "plain", 1.0 / 16.0)


def layer3_xattn(c):
    with ExitStack() as stack:
        sb = c.tiles(stack, "L3xn")
        c.ctxn = sb("ctxn", [P, KD, N])
        xn = sb("xn", [P, NT, D])
        affine = sb("affine", [P, 4, KD])
        c.load("L3xn_ld", [(affine[:], c.dram["L3x_ln"])])
        normalise(c, "n3x", c.x, dst=xn)
        normalise(c, "n3y", xn, dstT=c.xT, gain=affine[:, 0, :], shift=affine[:, 1, :])
        normalise(c, "n3z", c.ctx, dstT=c.ctxn, gain=affine[:, 2, :], shift=affine[:, 3, :])
        softmax_attention(c, "L3x", 8, 64, 4, 4, 64, "latent", 1.0 / 64.0)


def layer1_ffn(c):
    nc, w = c.nc, c.dram
    I = 768
    MI = I // P
    QMAX = 32767.0
    normalise(c, "n1f", c.x, dstT=c.xT)
    with ExitStack() as stack:
        sb = c.tiles(stack, "L1f")
        up, gate = sb("up", [P, MI, N]), sb("gate", [P, MI, N])
        wT = {"up": sb("wT_up", [P, KD, I]), "gate": sb("wT_gate", [P, KD, I]), "down": sb("wT_down", [P, MI, D])}
        s = {n: sb("s_" + n, [P, 4]) for n in ("x", "up", "gate", "mix", "out")}

        def scale_of(ch, vec, t, factor=None):
            if factor is not None:
                ch.link(vec.tensor_tensor(t[:, 1:2], t[:, 0:1], factor, ALU.mult))
                ch.link(vec.tensor_scalar(t[:, 1:2], t[:, 1:2], 1.0 / QMAX, 1e-12, ALU.mult, ALU.max))
                ch.link(vec.reciprocal(t[:, 2:3], t[:, 1:2]))
                ch.link(vec.tensor_tensor(t[:, 3:4], t[:, 2:3], factor, ALU.mult))
            else:
                ch.link(vec.tensor_scalar(t[:, 1:2], t[:, 0:1], 1.0 / QMAX, 1e-12, ALU.mult, ALU.max))
                ch.link(vec.reciprocal(t[:, 2:3], t[:, 1:2]))
                ch.link(vec.tensor_copy(t[:, 3:4], t[:, 2:3]))

        def quantise(ch, vec, a, t, low=True):
            ch.link(vec.tensor_scalar(a, a, t[:, 3:4], ROUND, ALU.mult, ALU.add))
            ch.link(vec.tensor_scalar(a, a, -ROUND, QMAX, ALU.add, ALU.min))
            if low:
                ch.link(vec.tensor_scalar(a, a, -QMAX - 1.0, None, ALU.max))

        with ExitStack() as inner:
            sw = c.tiles(inner, "L1f")
            nat = {"up": sw("nat_up", [P, MI, D]), "gate": sw("nat_gate", [P, MI, D]), "down": sw("nat_down", [P, KD, I])}
            bs, binv = sw("block_scale", [P, 48]), sw("block_inv", [P, 48])
            c.load("L1f_ld", [(nat[n][:], w[f"L1f_{n}"]) for n in ("up", "gate", "down")])
            sig = Signals(nc, "L1f_w")
            with nc.Block() as block:
                order = ("up", "gate", "down")
                ring = Ring(sig, "wt", c.banks[0:4])

                @block.vector
                def _(dve):
                    ch = Chain(dve, sig("dve_chain"))
                    vec = nc.vector
                    for n in order:
                        a = nat[n][:].rearrange("p a b -> p (a b)").rearrange("p (g i) -> p g i", i=32)
                        wide = lambda t: t[:].unsqueeze(2).to_broadcast([P, 48, 32])
                        ch.link(vec.tensor_reduce(bs[:], a, AX.X, ALU.max, apply_absolute_value=True))
                        ch.link(vec.tensor_scalar(bs[:], bs[:], 1.0 / 7.0, 1e-12, ALU.mult, ALU.max))
                        ch.link(vec.reciprocal(binv[:], bs[:]))
                        ch.link(vec.tensor_tensor(a, a, wide(binv), ALU.mult))
                        ch.link(vec.tensor_scalar(a, a, ROUND, None, ALU.add))
                        ch.link(vec.tensor_scalar(a, a, -ROUND, 7.0, ALU.add, ALU.min))
                        ch.link(vec.tensor_scalar(a, a, -8.0, None, ALU.max))
                        ch.link(vec.tensor_tensor(a, a, wide(bs), ALU.mult))
                        vec.sem_inc(sig("dequantised"), 1)
                    vec.tensor_reduce(s["x"][:, 0:1], c.xT[:].rearrange("p k n -> p (k n)"), AX.X, ALU.max,
                                      apply_absolute_value=True).then_inc(sig("x_max"), 1)
                    dve.wait_ge(sig("x_all"), 1)
                    scale_of(ch, vec, s["x"])
                    quantise(ch, vec, c.xT[:], s["x"])

                @block.gpsimd
                def _(pool):
                    pool.wait_ge(sig("x_max"), 1)
                    nc.gpsimd.partition_all_reduce(s["x"][:, 0:1], s["x"][:, 0:1], P, bass.bass_isa.ReduceOp.max).then_inc(sig("x_all"), 1)

                @block.tensor
                def _(pe):
                    for q, n in enumerate(order):
                        pe.wait_ge(sig("dequantised"), q + 1)
                        outer, inner_ = (MI, KD) if n != "down" else (KD, MI)
                        for i in range(inner_):
                            for o0 in range(0, outer, 4):
                                bank = ring.claim(pe)
                                for o in range(o0, min(o0 + 4, outer)):
                                    last = nc.tensor.transpose(bank[:, (o - o0) * P:(o - o0 + 1) * P],
                                                               nat[n][:, o, i * P:(i + 1) * P], c.ident[:])
                                ring.fill(last)

                @block.scalar
                def _(act):
                    for n in order:
                        outer, inner_ = (MI, KD) if n != "down" else (KD, MI)
                        for i in range(inner_):
                            for o0 in range(0, outer, 4):
                                bank = ring.take(act)
                                cnt = min(4, outer - o0) * P
                                ring.empty(nc.scalar.activation(wT[n][:, i, o0 * P:o0 * P + cnt], bank[:, 0:cnt], ACT.Copy))
            sig.clear()
            sig.close()

        sig = Signals(nc, "L1f_u")
        with nc.Fori(0, NBLK) as t:
            with nc.Block() as block:
                u_ring = Ring(sig, "u", c.banks[0:4])
                g_ring = Ring(sig, "g", c.banks[4:8])

                @block.tensor
                def _(pe):
                    for m in range(MI):
                        for n, ring in (("up", u_ring), ("gate", g_ring)):
                            bank = ring.claim(pe)
                            for k in range(KD):
                                last = nc.tensor.matmul(bank[:], wT[n][:, k, m * P:(m + 1) * P], c.xT[:, k, bass.ts(t, BLK)],
                                                        start=(k == 0), stop=(k == KD - 1))
                            ring.fill(last)

                @block.scalar
                def _(act):
                    for m in range(MI):
                        bank = u_ring.take(act)
                        u_ring.empty(nc.scalar.activation(up[:, m, bass.ts(t, BLK)], bank[:], ACT.Copy, scale=s["x"][:, 1:2]))

                @block.vector
                def _(dve):
                    for m in range(MI):
                        bank = g_ring.take(dve)
                        g_ring.empty(nc.vector.tensor_scalar(gate[:, m, bass.ts(t, BLK)], bank[:], s["x"][:, 1:2], None, ALU.mult))
            sig.clear()
        sig.close()

        with ExitStack() as inner:
            sw = c.tiles(inner, "L1f")
            sg = [sw(f"sigmoid{i}", [P, N]) for i in range(2)]
            mx = sw("chunk_max", [P, 4, MI])
            sig = Signals(nc, "L1f_g")
            with nc.Block() as block:
                @block.vector
                def _(dve):
                    ch = Chain(dve, sig("dve_chain"))
                    vec = nc.vector
                    absmax = lambda o, a: vec.tensor_reduce(o, a, AX.X, ALU.max, apply_absolute_value=True)
                    for m in range(MI):
                        vec_last = absmax(mx[:, 0, m:m + 1], up[:, m, :])
                    ch.link(vec_last)
                    vec.tensor_reduce(s["up"][:, 0:1], mx[:, 0, :], AX.X, ALU.max).then_inc(sig("maxima"), 1)
                    for m in range(MI):
                        vec_last = absmax(mx[:, 1, m:m + 1], gate[:, m, :])
                    ch.link(vec_last)
                    vec.tensor_reduce(s["gate"][:, 0:1], mx[:, 1, :], AX.X, ALU.max).then_inc(sig("maxima"), 1)
                    dve.wait_ge(sig("reduced"), 1)
                    scale_of(ch, vec, s["up"])
                    vec.sem_inc(sig("up_scaled"), 1)
                    dve.wait_ge(sig("reduced"), 2)
                    scale_of(ch, vec, s["gate"])

                    def weigh(m):
                        dve.wait_ge(sig("sigmoid"), m + 1)
                        a = sg[m % 2][:]
                        ch.link(vec.tensor_scalar(a, a, 65536.0, ROUND, ALU.mult, ALU.add))
                        ch.link(vec.tensor_scalar(a, a, -ROUND, 65535.0, ALU.add, ALU.min))
                        ch.link(vec.scalar_tensor_tensor(out=gate[:, m, :], in0=a, scalar=0.0, in1=gate[:, m, :],
                                                         op0=ALU.max, op1=ALU.mult))
                        ch.link(absmax(mx[:, 2, m:m + 1], gate[:, m, :]))
                        vec.sem_inc(sig("weighed"), 1)

                    for m in range(MI):
                        quantise(ch, vec, gate[:, m, :], s["gate"])
                        vec.sem_inc(sig("gate_q"), 1)
                        if m:
                            weigh(m - 1)
                    weigh(MI - 1)
                    ch.link(vec.tensor_scalar(s["gate"][:, 0:1], s["gate"][:, 1:2], 1.0 / 65536.0, None, ALU.mult))
                    vec.tensor_reduce(s["mix"][:, 0:1], mx[:, 2, :], AX.X, ALU.max).then_inc(sig("maxima"), 1)
                    dve.wait_ge(sig("reduced"), 3)
                    scale_of(ch, vec, s["mix"], factor=s["gate"][:, 0:1])
                    ch.link(vec.tensor_tensor(s["up"][:, 0:1], s["up"][:, 1:2], s["mix"][:, 1:2], ALU.mult))
                    for m in range(MI):
                        quantise(ch, vec, gate[:, m, :], s["mix"], low=False)
                        dve.wait_ge(sig("up_q"), m + 1)
                        ch.link(vec.scalar_tensor_tensor(out=gate[:, m, :], in0=gate[:, m, :], scalar=-QMAX - 1.0, in1=up[:, m, :],
                                                         op0=ALU.max, op1=ALU.mult))
                        ch.link(absmax(mx[:, 3, m:m + 1], gate[:, m, :]))
                    vec.tensor_reduce(s["out"][:, 0:1], mx[:, 3, :], AX.X, ALU.max).then_inc(sig("maxima"), 1)
                    dve.wait_ge(sig("reduced"), 4)
                    scale_of(ch, vec, s["out"], factor=s["up"][:, 0:1])
                    for m in range(MI):
                        quantise(ch, vec, gate[:, m, :], s["out"])

                @block.gpsimd
                def _(pool):
                    for i, n in enumerate(("up", "gate")):
                        pool.wait_ge(sig("maxima"), i + 1)
                        nc.gpsimd.partition_all_reduce(s[n][:, 0:1], s[n][:, 0:1], P, bass.bass_isa.ReduceOp.max).then_inc(sig("reduced"), 1)
                    pool.wait_ge(sig("up_scaled"), 1)
                    for m in range(MI):
                        a = up[:, m, :]
                        nc.gpsimd.tensor_scalar(a, a, s["up"][:, 3:4], ROUND, ALU.mult, ALU.add).then_inc(sig("up_steps"), 1)
                        pool.wait_ge(sig("up_steps"), 3 * m + 1)
                        nc.gpsimd.tensor_scalar(a, a, -ROUND, QMAX, ALU.add, ALU.min).then_inc(sig("up_steps"), 1)
                        pool.wait_ge(sig("up_steps"), 3 * m + 2)
                        nc.gpsimd.tensor_scalar(a, a, -QMAX - 1.0, None, ALU.max).then_inc(sig("up_steps"), 1)
                        pool.wait_ge(sig("up_steps"), 3 * m + 3)
                        nc.gpsimd.sem_inc(sig("up_q"), 1)
                    for i, n in enumerate(("mix", "out")):
                        pool.wait_ge(sig("maxima"), i + 3)
                        nc.gpsimd.partition_all_reduce(s[n][:, 0:1], s[n][:, 0:1], P, bass.bass_isa.ReduceOp.max).then_inc(sig("reduced"), 1)

                @block.scalar
                def _(act):
                    for m in range(MI):
                        act.wait_ge(sig("gate_q"), m + 1)
                        if m >= 2:
                            act.wait_ge(sig("weighed"), m - 1)
                        nc.scalar.activation(sg[m % 2][:], gate[:, m, :], ACT.Sigmoid, scale=s["gate"][:, 1:2]).then_inc(sig("sigmoid"), 1)
            sig.clear()
            sig.close()

        sig = Signals(nc, "L1f_d")
        with nc.Block() as block:
            ring = Ring(sig, "y", c.banks)

            @block.tensor
            def _(pe):
                for t in range(0, NT, 2):
                    bank = ring.claim(pe)
                    for j in range(2):
                        for m in range(MI):
                            last = nc.tensor.matmul(bank[:, j * D:(j + 1) * D], gate[:, m, (t + j) * P:(t + j + 1) * P], wT["down"][:, m, :],
                                                    start=(m == 0), stop=(m == MI - 1))
                    ring.fill(last)

            @block.vector
            def _(dve):
                for t in range(0, NT, 2):
                    bank = ring.take(dve)
                    xs = c.x[:, t:t + 2, :].rearrange("p t d -> p (t d)")
                    ring.empty(nc.vector.scalar_tensor_tensor(out=xs, in0=bank[:], scalar=s["out"][:, 1:2], in1=xs,
                                                              op0=ALU.mult, op1=ALU.add))
        sig.clear()
        sig.close()


def layer2_attn(c):
    nc, w = c.nc, c.dram
    L, S = 64, 64
    START = (L - 1) // 2
    PAD = L - START - 1
    W = PAD + T + START + 1
    ON_TENSOR = list(range(0, 26))
    ON_VECTOR = [l for l in range(L) if l not in ON_TENSOR]
    normalise(c, "n2a", c.x, dstT=c.xT)
    with ExitStack() as stack:
        sb = c.tiles(stack, "L2a")
        taps = sb("taps", [P, KD, L])
        u = sb("u", [P, KD, B, W])
        with ExitStack() as inner:
            sw = c.tiles(inner, "L2a")
            cm, bm = sw("cm", [P, KD, S]), sw("bm", [P, KD, S])
            am, dvec, ldt = sw("am", [P, S]), sw("dvec", [P, KD]), sw("ldt", [P, KD])
            power, ones = sw("power", [P, L]), sw("ones", [P, P])
            la = sw("la", [P, L, S])
            ex = [sw(f"ex{k}", [P, L, S]) for k in range(KD)]
            c.load("L2a_ld", [(cm[:], w["L2a_c"]), (bm[:], w["L2a_b"]), (dvec[:], w["L2a_d"]), (ldt[:], w["L2a_ldt"]),
                              (power[:], w["iota64"]), (ones[:], w["tri_strict_ones"][:, 1, :]), (am[:], w["L2a_a"].rearrange("(a n) -> a n", a=1).to_broadcast([P, S]))])
            sig = Signals(nc, "L2a_k")
            with nc.Block() as block:
                @block.gpsimd
                def _(pool):
                    nc.gpsimd.memset(u[:], 0.0).then_inc(sig("zeroed"), 1)

                @block.tensor
                def _(pe):
                    for k in range(KD):
                        last = nc.tensor.matmul(c.banks[0][:, 0:S], ones[:], cm[:, k, :], start=(k == 0), stop=(k == KD - 1))
                    last.then_inc(sig("c_sum"), 1)

                @block.vector
                def _(dve):
                    ch = Chain(dve, sig("dve_chain"))
                    vec = nc.vector
                    vec.tensor_tensor(la[:], power[:].unsqueeze(2).to_broadcast([P, L, S]),
                                      am[:].unsqueeze(1).to_broadcast([P, L, S]), ALU.mult).then_inc(sig("exponents"), 1)
                    dve.wait_ge(sig("c_sum"), 1)
                    ch.link(vec.tensor_tensor(cm[:], c.banks[0][:, 0:S].unsqueeze(1).to_broadcast([P, KD, S]), bm[:], ALU.mult))
                    for k in range(KD):
                        dve.wait_ge(sig("powers"), k + 1)
                        ch.link(vec.tensor_tensor(ex[k][:], ex[k][:], cm[:, k, :].unsqueeze(1).to_broadcast([P, L, S]), ALU.mult))
                        ch.link(vec.tensor_reduce(taps[:, k, :], ex[k][:], AX.X, ALU.add))
                    vec.tensor_tensor(taps[:, :, START], taps[:, :, START], dvec[:], ALU.add)

                @block.scalar
                def _(act):
                    nc.scalar.activation(ldt[:], ldt[:], ACT.Exp).then_inc(sig("dt"), 1)
                    act.wait_ge(sig("dt"), 1)
                    act.wait_ge(sig("exponents"), 1)
                    for k in range(KD):
                        nc.scalar.activation(ex[k][:], la[:], ACT.Exp, scale=ldt[:, k:k + 1]).then_inc(sig("powers"), 1)
                    act.wait_ge(sig("zeroed"), 1)
                    for k in range(KD):
                        nc.scalar.activation(u[:, k, :, PAD:PAD + T], c.xT[:, k, :].rearrange("p (b t) -> p b t", b=B), ACT.Copy)
            sig.clear()
            sig.close()
        acc = sb("acc", [P, KD, B, T])
        diag = sb("diag", [P, KD, len(ON_TENSOR), P])
        sig = Signals(nc, "L2a")
        with nc.Block() as block:
            shifted = lambda k, l: u[:, k, :, PAD + START - l:PAD + START - l + T]
            y_ring_banks = c.banks

            @block.scalar
            def _(act):
                for k in range(KD):
                    for i, l in enumerate(ON_TENSOR):
                        nc.scalar.activation(diag[:, k, i, :], c.ident[:], ACT.Copy, scale=taps[:, k, l:l + 1]).then_inc(sig("diagonal"), 1)

            @block.tensor
            def _(pe):
                for k in range(KD):
                    for i, l in enumerate(ON_TENSOR):
                        pe.wait_ge(sig("diagonal"), k * len(ON_TENSOR) + i + 1)
                        for q in range(NBLK):
                            last = nc.tensor.matmul(c.banks[k * NBLK + q][:], diag[:, k, i, :],
                                                    shifted(k, l)[:, q * TB:(q + 1) * TB, :],
                                                    start=(i == 0), stop=(i == len(ON_TENSOR) - 1))
                    last.then_inc(sig("tensor_taps"), 1)
                pe.wait_ge(sig("summed"), 1)
                for t in range(0, NT, 2):
                    bank = c.banks[t // 2]
                    for j in range(2):
                        for k in range(KD):
                            tt = t + j
                            last = nc.tensor.transpose(bank[:, j * D + k * P:j * D + (k + 1) * P],
                                                       acc[:, k, tt // TB, (tt % TB) * P:(tt % TB + 1) * P], c.ident[:])
                    last.then_inc(sig("turned"), 1)

            @block.vector
            def _(dve):
                ch = Chain(dve, sig("dve_chain"))
                vec = nc.vector
                for k in range(KD):
                    for i, l in enumerate(ON_VECTOR):
                        if i == 0:
                            ch.link(vec.tensor_scalar(acc[:, k], shifted(k, l), taps[:, k, l:l + 1], None, ALU.mult))
                        else:
                            ch.link(vec.scalar_tensor_tensor(out=acc[:, k], in0=shifted(k, l), scalar=taps[:, k, l:l + 1], in1=acc[:, k],
                                                             op0=ALU.mult, op1=ALU.add))
                for k in range(KD):
                    dve.wait_ge(sig("tensor_taps"), k + 1)
                    for q in range(NBLK):
                        part = acc[:, k, q * TB:(q + 1) * TB, :].rearrange("p b t -> p (b t)")
                        last = vec.tensor_tensor(part, part, c.banks[k * NBLK + q][:], ALU.add)
                last.then_inc(sig("summed"), 1)
                for t in range(0, NT, 2):
                    dve.wait_ge(sig("turned"), t // 2 + 1)
                    xs = c.x[:, t:t + 2, :].rearrange("p t d -> p (t d)")
                    vec.tensor_tensor(xs, xs, c.banks[t // 2][:], ALU.add)
        sig.clear()
        sig.close()


def layer3_attn(c):
    nc, w = c.nc, c.dram
    H, DH = 16, 16
    with ExitStack() as stack:
        sb = c.tiles(stack, "L3a")
        xn = sb("xn", [P, NT, D])
        normalise(c, "n3a", c.x, dst=xn, dstT=c.xT)
        wqk, wv = sb("wqk", [P, KD, 2 * D]), sb("wv", [P, KD, D])
        bqk, bv, gamma, beta = sb("bqk", [P, 2 * D]), sb("bv", [P, D]), sb("gamma", [P, D]), sb("beta", [P, D])
        cos, sin = sb("cos", [P, TB, D]), sb("sin", [P, TB, D])
        ones, diag = sb("ones", [P, P]), sb("blockdiag", [P, P])
        xb = sb("xb", [P, KD, T])
        qk, rot, tmp = sb("qk", [P, TB, 2, D]), sb("rot", [P, TB, 2, D]), sb("tmp", [P, TB, 2, D])
        v = sb("v", [P, TB, D])
        kv = sb("kv", [P, KD, P])
        qrT = sb("qrT", [P, KD, T])
        z = sb("z", [P, TB, H])
        res = sb("res", [P, TB, D])
        stats, mv, rstd = sb("stats", [P, TB, 6]), sb("mv", [P, TB, 2]), sb("rstd", [P, TB, 3])
        row = lambda n: w[n].rearrange("(a n) -> a n", a=1)
        c.load("L3a_ld", [(wqk[:], w["L3a_wqk"]), (wv[:], w["L3a_wv"]), (bqk[:], row("L3a_bqk").to_broadcast([P, 2 * D])),
                          (bv[:], row("L3a_bv").to_broadcast([P, D])), (gamma[:], row("L3a_gamma").to_broadcast([P, D])),
                          (beta[:], row("L3a_beta").to_broadcast([P, D])), (cos[:], w["rope_cos"]), (sin[:], w["rope_sin"]),
                          (ones[:], w["tri_strict_ones"][:, 1, :]), (diag[:], w["blockdiag16"])])
        sig = Signals(nc, "L3a")
        with nc.Fori(0, B) as b:
            with nc.Block() as block:
                qk_bank, v_bank, sum_bank, kv_bank, turn_bank, out_bank = c.banks[0:2], c.banks[2], c.banks[3], c.banks[4], c.banks[5], c.banks[6]

                @block.scalar
                def _(act):
                    nc.scalar.activation(xb[:], c.xT[:, :, bass.ts(b, T)], ACT.Copy).then_inc(sig("sliced"), 1)
                    for t in range(TB):
                        act.wait_ge(sig("biased"), t + 1)
                        nc.scalar.activation(qk[:, t], qk[:, t], ACT.Gelu).then_inc(sig("gelu"), 1)
                    act.wait_ge(sig("turned"), 1)
                    nc.scalar.activation(qrT[:], turn_bank[:].rearrange("p (k t) -> p k t", k=KD), ACT.Copy).then_inc(sig("q_feat"), 1)
                    act.wait_ge(sig("var_eps"), 1)
                    nc.scalar.activation(rstd[:, :, 1], rstd[:, :, 0], ACT.Sqrt).then_inc(sig("std"), 1)

                @block.tensor
                def _(pe):
                    pe.wait_ge(sig("sliced"), 1)
                    for t in range(TB):
                        for k in range(KD):
                            last = nc.tensor.matmul(qk_bank[t][:], xb[:, k, t * P:(t + 1) * P], wqk[:, k, :], start=(k == 0), stop=(k == KD - 1))
                        last.then_inc(sig("qk"), 1)
                    for t in range(TB):
                        for k in range(KD):
                            last = nc.tensor.matmul(v_bank[:, t * D:(t + 1) * D], xb[:, k, t * P:(t + 1) * P], wv[:, k, :],
                                                    start=(k == 0), stop=(k == KD - 1))
                    last.then_inc(sig("v_raw"), 1)
                    pe.wait_ge(sig("shifted"), 1)
                    for t in range(TB):
                        last = nc.tensor.matmul(sum_bank[:, 0:D], ones[:], qk[:, t, 1, :], start=(t == 0), stop=(t == TB - 1))
                    last.then_inc(sig("k_sum"), 1)
                    pe.wait_ge(sig("rotated"), 1)
                    for m in range(KD):
                        for t in range(TB):
                            last = nc.tensor.transpose(turn_bank[:, m * T + t * P:m * T + (t + 1) * P], rot[:, t, 0, m * P:(m + 1) * P], c.ident[:])
                    last.then_inc(sig("turned"), 1)
                    for m in range(KD):
                        for t in range(TB):
                            last = nc.tensor.matmul(kv_bank[:, m * P:(m + 1) * P], rot[:, t, 1, m * P:(m + 1) * P],
                                                    v[:, t, m * P:(m + 1) * P], start=(t == 0), stop=(t == TB - 1))
                    last.then_inc(sig("kv"), 1)
                    pe.wait_ge(sig("q_feat"), 1)
                    pe.wait_ge(sig("kv_heads"), 1)
                    for t in range(TB):
                        for m in range(KD):
                            last = nc.tensor.matmul(out_bank[:, t * D + m * P:t * D + (m + 1) * P], qrT[:, m, t * P:(t + 1) * P], kv[:, m, :],
                                                    start=True, stop=True)
                    last.then_inc(sig("attended"), 1)

                @block.vector
                def _(dve):
                    ch = Chain(dve, sig("dve_chain"))
                    vec = nc.vector
                    for t in range(TB):
                        dve.wait_ge(sig("qk"), t + 1)
                        vec.tensor_tensor(qk[:, t].rearrange("p a d -> p (a d)"), qk_bank[t][:], bqk[:], ALU.add).then_inc(sig("biased"), 1)
                    dve.wait_ge(sig("v_raw"), 1)
                    vec.tensor_tensor(v[:], v_bank[:].rearrange("p (t d) -> p t d", t=TB), bv[:].unsqueeze(1).to_broadcast([P, TB, D]), ALU.add)
                    dve.wait_ge(sig("gelu"), TB)
                    vec.tensor_scalar(qk[:], qk[:], 0.21, None, ALU.add).then_inc(sig("shifted"), 1)
                    dve.wait_ge(sig("shifted"), 1)
                    for t in range(TB):
                        both = lambda a: a[:, t].unsqueeze(1).to_broadcast([P, 2, D])
                        even = lambda a: a.rearrange("p a (d two) -> p a d two", two=2)[:, :, :, 0]
                        odd = lambda a: a.rearrange("p a (d two) -> p a d two", two=2)[:, :, :, 1]
                        vec.tensor_tensor(even(tmp[:, t]), odd(qk[:, t]), even(both(sin)), ALU.mult)
                        vec.tensor_tensor(odd(tmp[:, t]), even(qk[:, t]), odd(both(sin)), ALU.mult)
                        ch.link(vec.tensor_tensor(rot[:, t], qk[:, t], both(cos), ALU.mult))
                    vec.tensor_tensor(rot[:], rot[:], tmp[:], ALU.add).then_inc(sig("rotated"), 1)
                    dve.wait_ge(sig("k_sum"), 1)
                    dve.wait_ge(sig("rotated"), 1)
                    ch.link(vec.tensor_tensor(tmp[:, :, 0, :], qk[:, :, 0, :], sum_bank[:, 0:D].unsqueeze(1).to_broadcast([P, TB, D]), ALU.mult))
                    for t in range(TB):
                        last = vec.tensor_reduce(z[:, t, :], tmp[:, t, 0, :].rearrange("p (h d) -> p h d", h=H), AX.X, ALU.add)
                    ch.link(last)
                    ch.link(vec.tensor_scalar(z[:], z[:], 1.0 / T, 1e-6, ALU.mult, ALU.add))
                    ch.link(vec.reciprocal(z[:], z[:]))
                    dve.wait_ge(sig("kv"), 1)
                    vec.tensor_tensor(kv[:], kv_bank[:, 0:T].rearrange("p (m e) -> p m e", m=KD),
                                      diag[:].unsqueeze(1).to_broadcast([P, KD, P]), ALU.mult).then_inc(sig("kv_heads"), 1)
                    dve.wait_ge(sig("attended"), 1)
                    for t in range(TB):
                        last = vec.tensor_tensor(res[:, t, :].rearrange("p (h d) -> p h d", h=H),
                                                 out_bank[:, t * D:(t + 1) * D].rearrange("p (h d) -> p h d", h=H),
                                                 z[:, t, :].unsqueeze(2).to_broadcast([P, H, DH]), ALU.mult)
                    ch.link(last)
                    ch.link(vec.tensor_tensor(res[:], res[:], xn[:, bass.ts(b, TB), :], ALU.add))
                    for t in range(TB):
                        last = vec.bn_stats(stats[:, t, :], res[:, t, :])
                    ch.link(last)
                    for t in range(TB):
                        last = vec.bn_aggr(mv[:, t, :], stats[:, t, :])
                    ch.link(last)
                    vec.tensor_scalar_add(rstd[:, :, 0], mv[:, :, 1], 1e-12).then_inc(sig("var_eps"), 1)
                    dve.wait_ge(sig("std"), 1)
                    ch.link(vec.reciprocal(rstd[:, :, 2], rstd[:, :, 1]))
                    for t in range(TB):
                        last = vec.tensor_scalar(res[:, t, :], res[:, t, :], mv[:, t, 0:1], rstd[:, t, 2:3], ALU.subtract, ALU.mult)
                    ch.link(last)
                    rowwise = lambda a: a[:].unsqueeze(1).to_broadcast([P, TB, D])
                    ch.link(vec.tensor_tensor(res[:], res[:], rowwise(gamma), ALU.mult))
                    ch.link(vec.tensor_tensor(res[:], res[:], rowwise(beta), ALU.add))
                    vec.tensor_tensor(c.x[:, bass.ts(b, TB), :], c.x[:, bass.ts(b, TB), :], res[:], ALU.add)
            sig.clear()
        sig.close()


def layer0_xattn(c):
    nc, w = c.nc, c.dram
    H, DH, MQ = 16, 16, 4
    normalise(c, "n0x", c.x, dstT=c.xT)
    with ExitStack() as stack:
        sb = c.tiles(stack, "L0x")
        wf = sb("wf", [P, 2, KD, MQ * P])
        bf = sb("bf", [P, 2, MQ])
        wt = sb("wt", [P, 2, KD, D])
        bt = sb("bt", [P, 2, D])
        wo, bo = sb("wo", [P, KD, D]), sb("bo", [P, D])
        causal = sb("causal", [P, 3 * P])
        ones = sb("ones", [P, P])
        src = [sb("xb", [P, KD, T]), sb("cb", [P, KD, T])]
        fT, eT = sb("fT", [P, 2, MQ, T]), sb("eT", [P, MQ, T])
        ft, et = sb("ft", [P, 2, TB, D]), sb("et", [P, 2, TB, D])
        att = [sb(f"att{i}", [P, 3 * P]) for i in range(3)]
        heads_out, cT, y = sb("heads_out", [P, TB, D]), sb("cT", [P, KD, T]), sb("y", [P, TB, D])
        row = lambda n: w[n].rearrange("(a n) -> a n", a=1)
        c.load("L0x_ld", [(wf[:, i], w[f"L0x_wf{i}"]) for i in range(2)] + [(wt[:, i], w[f"L0x_wt{i}"]) for i in range(2)]
               + [(bt[:, i, :], row(f"L0x_bt{i}").to_broadcast([P, D])) for i in range(2)]
               + [(bf[:], w["L0x_bf"]), (wo[:], w["L0x_wo"]), (bo[:], row("L0x_bo").to_broadcast([P, D])),
                  (causal[:], w["causal"]), (ones[:], w["tri_strict_ones"][:, 1, :])])
        sig = Signals(nc, "L0x")
        with nc.Fori(0, B) as b:
            with nc.Block() as block:
                s_ring = Ring(sig, "s", c.banks[0:3])
                z_bank, acc_bank, out_bank = c.banks[3], c.banks[4], c.banks[5]
                t_ring = Ring(sig, "t", [c.banks[6]])
                tail_pe, tail_act = out_tail(c, sig, t_ring, D, heads_out, cT, wo, out_bank)

                @block.tensor
                def _(pe):
                    pe.wait_ge(sig("sliced"), 2)
                    for i in range(2):
                        for m in range(MQ):
                            bank = c.banks[2 * i + m // 2]
                            for k in range(KD):
                                last = nc.tensor.matmul(bank[:, (m % 2) * T:(m % 2 + 1) * T], wf[:, i, k, m * P:(m + 1) * P], src[i][:, k, :],
                                                        start=(k == 0), stop=(k == KD - 1))
                        last.then_inc(sig("by_feature"), 1)
                    for i in range(2):
                        for t in range(TB):
                            for k in range(KD):
                                last = nc.tensor.matmul(c.banks[4 + i][:, t * D:(t + 1) * D], src[i][:, k, t * P:(t + 1) * P], wt[:, i, k, :],
                                                        start=(k == 0), stop=(k == KD - 1))
                        last.then_inc(sig("by_token"), 1)
                    pe.wait_ge(sig("features"), 1)
                    for i in range(H + 2):
                        if i < H:
                            bank = s_ring.claim(pe)
                            ps = slice(32 * (i % 4), 32 * (i % 4) + DH)
                            nc.tensor.matmul(bank[:, 0:T], fT[ps, 1, i // 4, 0:P], fT[ps, 0, i // 4, :], start=True, stop=True)
                            s_ring.fill(nc.tensor.matmul(bank[:, T:3 * P], fT[ps, 1, i // 4, P:T], fT[ps, 0, i // 4, P:T], start=True, stop=True))
                        if i == 1:
                            pe.wait_ge(sig("token_features"), 1)
                            tri = causal[:, 0:P]
                            nc.tensor.matmul(z_bank[:, 0:D], tri, ft[:, 1, 0, :], start=True, stop=True)
                            nc.tensor.matmul(z_bank[:, D:2 * D], ones[:], ft[:, 1, 0, :], start=True, stop=False)
                            nc.tensor.matmul(z_bank[:, D:2 * D], tri, ft[:, 1, 1, :], start=False, stop=True).then_inc(sig("k_running"), 1)
                        if i >= 2:
                            h = i - 2
                            hs = slice(h * DH, (h + 1) * DH)
                            pe.wait_ge(s_ring.emptied, h + 1)
                            a = att[h % 3]
                            nc.tensor.matmul(acc_bank[:, hs], a[:, 0:P], ft[:, 1, 0, hs], start=True, stop=True)
                            late = slice(D + h * DH, D + (h + 1) * DH)
                            nc.tensor.matmul(acc_bank[:, late], a[:, P:2 * P], ft[:, 1, 0, hs], start=True, stop=False)
                            nc.tensor.matmul(acc_bank[:, late], a[:, 2 * P:3 * P], ft[:, 1, 1, hs], start=False, stop=True).then_inc(sig("weighted"), 1)
                    tail_pe(pe, 0)

                @block.scalar
                def _(act):
                    nc.scalar.activation(src[0][:], c.xT[:, :, bass.ts(b, T)], ACT.Copy).then_inc(sig("sliced"), 1)
                    act.wait_ge(sig("negative"), 1)
                    nc.scalar.activation(eT[:], eT[:], ACT.Exp).then_inc(sig("exp"), 1)
                    act.wait_ge(sig("negative"), 2)
                    nc.scalar.activation(et[:], et[:], ACT.Exp).then_inc(sig("exp"), 1)
                    tail_act(act)

                @block.vector
                def _(dve):
                    ch = Chain(dve, sig("dve_chain"))
                    vec = nc.vector
                    vec.tensor_copy(src[1][:], c.ctxT[:, :, bass.ts(b, T)]).then_inc(sig("sliced"), 1)
                    part = lambda i, m: c.banks[2 * i + m // 2][:, (m % 2) * T:(m % 2 + 1) * T]
                    dve.wait_ge(sig("by_feature"), 1)
                    for m in range(MQ):
                        last = vec.tensor_scalar(eT[:, m, :], part(0, m), bf[:, 0, m:m + 1], 0.0, ALU.add, ALU.min)
                    last.then_inc(sig("negative"), 1)
                    for m in range(MQ):
                        last = vec.tensor_scalar(fT[:, 0, m, :], part(0, m), bf[:, 0, m:m + 1], 0.0, ALU.add, ALU.max)
                    ch.link(last)
                    dve.wait_ge(sig("by_feature"), 2)
                    for m in range(MQ):
                        last = vec.tensor_scalar(fT[:, 1, m, :], part(1, m), bf[:, 1, m:m + 1], None, ALU.add)
                    dve.wait_ge(sig("exp"), 1)
                    vec.tensor_tensor(fT[:, 0], fT[:, 0], eT[:], ALU.add).then_inc(sig("features"), 1)
                    wide = lambda a: a.unsqueeze(1).to_broadcast([P, TB, D])
                    for i in range(2):
                        dve.wait_ge(sig("by_token"), i + 1)
                        last = vec.tensor_tensor(ft[:, i], c.banks[4 + i][:].rearrange("p (t d) -> p t d", t=TB), wide(bt[:, i, :]), ALU.add)
                    ch.link(last)
                    vec.tensor_scalar(et[:], ft[:], 0.0, None, ALU.min).then_inc(sig("negative"), 1)
                    dve.wait_ge(sig("exp"), 2)
                    flat4 = lambda a: a[:].rearrange("p a t d -> p (a t d)")
                    vec.scalar_tensor_tensor(out=flat4(ft), in0=flat4(ft), scalar=0.0, in1=flat4(et),
                                             op0=ALU.max, op1=ALU.add).then_inc(sig("token_features"), 1)
                    for h in range(H):
                        bank = s_ring.take(dve)
                        if h >= 3:
                            dve.wait_ge(sig("weighted"), h - 2)
                        s_ring.empty(vec.tensor_tensor(att[h % 3][:], bank[:, 0:3 * P], causal[:], ALU.mult))
                    dve.wait_ge(sig("k_running"), 1)
                    flat = lambda a: a.rearrange("p t d -> p (t d)")
                    ch.link(vec.tensor_tensor(flat(y[:]), flat(ft[:, 0]), z_bank[:], ALU.mult))
                    ch.link(vec.tensor_scalar(y[:], y[:], 1e-6, None, ALU.add))
                    ch.link(vec.reciprocal(y[:], y[:]))
                    dve.wait_ge(sig("weighted"), H)
                    for t in range(TB):
                        vec.tensor_tensor(heads_out[:, t, :], acc_bank[:, t * D:(t + 1) * D], y[:, t, :], ALU.mult).then_inc(sig("heads_out"), 1)
                    dve.wait_ge(sig("heads_out"), TB)
                    dve.wait_ge(sig("projected"), 1)
                    ch.link(vec.tensor_tensor(y[:], out_bank[:].rearrange("p (t d) -> p t d", t=TB), wide(bo[:]), ALU.add))
                    vec.tensor_tensor(c.x[:, bass.ts(b, TB), :], c.x[:, bass.ts(b, TB), :], y[:], ALU.add)
            sig.clear()
        sig.close()


def layer0_attn(c):
    nc, w = c.nc, c.dram
    H, HD, DI, KC = 32, 64, 2048, 4
    MH = H * 16 // P
    MX = 18
    NG, GC = 4, BLK
    normalise(c, "n0a", c.x, dstT=c.xT)
    xt = c.ctxT[:].rearrange("p k n -> p (k n)").rearrange("p (t e) -> p t e", t=TB)
    v = c.ctx[:].rearrange("p a d -> p (a d)").rearrange("p (t e) -> p t e", t=TB)
    yzT = c.ctx[:].rearrange("p a d -> p (a d)").rearrange("p (k t) -> p k t", t=T)
    with ExitStack() as stack:
        sb = c.tiles(stack, "L0a")
        wz, wx, wd = sb("wz", [P, KD, DI]), sb("wx", [P, KD, MX * P]), sb("wd", [P, 2, KD, MH * P])
        wout, norm = sb("wout", [P, DI // P, D]), sb("norm", [P, DI // P])
        bz, bx, bd = sb("bz", [P, DI]), sb("bx", [P, MX]), sb("bd", [P, 2, MH])
        conv = sb("conv", [P, MX, KC])
        lcol, nega, dtb = sb("lcol", [P, MH]), sb("nega", [P, MH]), sb("dtb", [P, MH])
        dh, bo = sb("dh", [P, H]), sb("bo", [P, D])
        pick = sb("pick", [P, 8, P])
        um, vm, tri, last_row = sb("um", [P, T]), sb("vm", [P, P]), sb("tri", [P, P]), sb("last_row", [P, P])
        ones = sb("ones", [P, P])
        row = lambda n: w[n].rearrange("(a n) -> a n", a=1)
        c.load("L0a_ld", [(wz[:], w["L0a_wz"]), (wx[:], w["L0a_wx"]), (wd[:, 0], w["L0a_wdl"]), (wd[:, 1], w["L0a_wdt"]),
                          (wout[:], w["L0a_wout"]), (norm[:], w["L0a_norm"]), (bz[:], row("L0a_bz").to_broadcast([P, DI])),
                          (bx[:], w["L0a_bx"]), (bd[:], w["L0a_bd"]), (conv[:], w["L0a_conv"]), (lcol[:], w["L0a_l"]),
                          (nega[:], w["L0a_alog"]), (dtb[:], w["L0a_dtb"]), (dh[:], row("L0a_d").to_broadcast([P, H])),
                          (bo[:], row("L0a_bo").to_broadcast([P, D])), (pick[:], w["L0a_pick"]), (um[:], w["L0a_u"]),
                          (vm[:], w["L0a_v"]), (tri[:], w["tri_strict_ones"][:, 0, :]), (last_row[:], w["last_row"]),
                          (ones[:], w["tri_strict_ones"][:, 1, :])])
        xb = sb("xb", [P, KD, T])
        xc = [sb(f"xc{i}", [P, 2, KC - 1 + T]) for i in range(3)]
        xf = [sb(f"xf{i}", [P, 2, T]) for i in range(3)]
        bc = sb("bc", [P, 2, T])
        pre, sp, ex1 = sb("pre", [P, 2, MH, T]), sb("sp", [P, 2, MH, T]), sb("soft", [P, 2, MH, T])
        gcT, g, R = sb("gcT", [P, MH, T]), ex1[:, 0], ex1[:, 1]
        dt, gc, lam0, lam8 = (sb(n, [P, TB, H]) for n in ("dt", "gc", "lam0", "lam8"))
        ngc, coef = sb("ngc", [P, TB, H]), sb("coef", [P, TB, H])
        sfac, tfac = sb("sfac", [P, H]), sb("tfac", [P, H])
        qkd, qko, qdiag = sb("qkd", [P, TB, P]), sb("qko", [P, P]), sb("qdiag", [P, TB])
        wv = sb("wv", [P, DI])
        dtmp = wv[:, 0:T].rearrange("p (t s) -> p t s", t=TB)
        ident16, never16 = sb("ident16", [P, P], BF16), sb("never16", [P, P], BF16)
        ru = [sb(f"ru{i}", [P, 2, T]) for i in range(2)]
        ex = [sb(f"ex{i}", [P, 2, T]) for i in range(2)]
        att = [sb(f"att{i}", [P, 2, T]) for i in range(2)]
        spare = pre[:].rearrange("p i m t -> p (i m t)")
        tmp, y = spare[:, 0:GC], spare[:, GC:2 * GC].rearrange("p (t d) -> p t d", t=TB)
        zb = [spare[:, 2 * GC:3 * GC], spare[:, 3 * GC:4 * GC]]
        ss = sb("ss", [P, TB, 4])

        sig = Signals(nc, "L0a_c")
        with nc.Block() as block:
            @block.scalar
            def _(act):
                nc.scalar.activation(nega[:], nega[:], ACT.Exp).then_inc(sig("a"), 1)

            @block.vector
            def _(dve):
                vec = nc.vector
                dve.wait_ge(sig("a"), 1)
                vec.tensor_scalar(nega[:], nega[:], -1.0, None, ALU.mult)
                vec.tensor_tensor(bd[:, 0, :], bd[:, 0, :], lcol[:], ALU.mult)
                vec.tensor_tensor(bd[:, 1, :], bd[:, 1, :], dtb[:], ALU.add)
                for i in range(3):
                    vec.memset(xc[i][:], 0.0)
                vec.tensor_copy(ident16[:], c.ident[:])
                vec.tensor_scalar(never16[:], tri[:], -1.0, 1e30, ALU.add, ALU.mult)
                for k in range(DI // P):
                    vec.tensor_scalar(wout[:, k, :], wout[:, k, :], norm[:, k:k + 1], None, ALU.mult)
        sig.clear()
        sig.close()

        sig = Signals(nc, "L0a")
        with nc.Fori(0, B) as b:
            with nc.Block() as block:
                ra = Ring(sig, "ra", c.banks[0:2])
                rv = Ring(sig, "rv", c.banks[2:4])
                qk_bank, y_bank, off_bank = c.banks[4], c.banks[5:7], c.banks[7]
                NPX = MX // 2
                NPH = H // 2
                A_EXP = 4 + NPX

                @block.tensor
                def _(pe):
                    mm, tp = nc.tensor.matmul, nc.tensor.transpose

                    def project(p):
                        bank = ra.claim(pe)
                        for j in range(2):
                            for k in range(KD):
                                last = mm(bank[:, j * T:(j + 1) * T], wx[:, k, (2 * p + j) * P:(2 * p + j + 1) * P], xb[:, k, :],
                                          start=(k == 0), stop=(k == KD - 1))
                        ra.fill(last)

                    def turn(p):
                        pe.wait_ge(sig("silu"), p + 1)
                        bank = rv.claim(pe)
                        for t in range(TB):
                            for j in range(2):
                                last = tp(bank[:, t * T + j * P:t * T + (j + 1) * P], xf[p % 3][:, j, t * P:(t + 1) * P], c.ident[:])
                        rv.fill(last)

                    pe.wait_ge(sig("sliced"), 1)
                    for i in range(2):
                        for m in range(0, MH, 2):
                            bank = ra.claim(pe)
                            for j in range(2):
                                for k in range(KD):
                                    last = mm(bank[:, j * T:(j + 1) * T], wd[:, i, k, (m + j) * P:(m + j + 1) * P], xb[:, k, :],
                                              start=(k == 0), stop=(k == KD - 1))
                            ra.fill(last)
                    for p in range(3):
                        project(p)
                    pe.wait_ge(sig("silu"), 1)
                    mm(qk_bank[:, 0:T], bc[:, 0, 0:P], bc[:, 1, :], start=True, stop=True)
                    mm(qk_bank[:, T:T + P], bc[:, 0, P:T], bc[:, 1, P:T], start=True, stop=True).then_inc(sig("qk"), 1)
                    for n, a in enumerate((sp[:, 1], sp[:, 0], gcT)):
                        pe.wait_ge(sig("rows"), (1, 1, 2)[n])
                        for t in range(TB):
                            bank = rv.claim(pe)
                            for m in range(MH):
                                last = tp(bank[:, m * P:(m + 1) * P], a[:, m, t * P:(t + 1) * P], c.ident[:])
                            rv.fill(last)
                    for p in range(3, NPX):
                        project(p)
                        turn(p - 2)
                    pe.wait_ge(sig("gc_tok"), 1)
                    mm(off_bank[:, 0:H], last_row[:], gc[:, 0, :], start=True, stop=True).then_inc(sig("total"), 1)
                    turn(NPX - 2)
                    turn(NPX - 1)
                    pe.wait_ge(sig("R"), 1)
                    for i in range(NPH + 2):
                        if i < NPH:
                            bank = rv.claim(pe)
                            for j in range(2):
                                h = 2 * i + j
                                last = mm(bank[:, j * T:(j + 1) * T], pick[:, h % 8, :], R[:, h // 8, :], start=True, stop=True)
                            rv.fill(last)
                        if 1 <= i <= NPH:
                            bank = ra.claim(pe)
                            pe.wait_ge(sig("ru"), i)
                            mm(bank[:], vm[:], ru[(i - 1) % 2][:].rearrange("p j t -> p (j t)"), start=True, stop=False)
                            ra.fill(mm(bank[:].rearrange("p (j t) -> p j t", t=P), ident16[:],
                                       never16[:].unsqueeze(1).to_broadcast([P, 4, P]), start=False, stop=True))
                        if i >= 2:
                            q = i - 2
                            if q % 4 == 0:
                                gi = q // 4
                                if gi == 0:
                                    pe.wait_ge(sig("wv"), 1)
                                else:
                                    pe.wait_ge(sig("combined"), gi)
                                mm(off_bank[:], qko[:], wv[:, gi * GC:(gi + 1) * GC], start=True, stop=True)
                            pe.wait_ge(sig("att"), q + 1)
                            for j in range(2):
                                h = 2 * q + j
                                for t in range(TB):
                                    last = mm(y_bank[t][:, (h % 8) * HD:(h % 8 + 1) * HD], att[q % 2][:, j, t * P:(t + 1) * P],
                                              v[:, t, h * HD:(h + 1) * HD], start=True, stop=True)
                            last.then_inc(sig("weighted"), 1)
                    for gi in range(NG):
                        for t in range(TB):
                            bank = rv.claim(pe)
                            for k in range(KD):
                                last = mm(bank[:], xb[:, k, t * P:(t + 1) * P], wz[:, k, gi * GC:(gi + 1) * GC], start=(k == 0), stop=(k == KD - 1))
                            rv.fill(last)
                    for k in range(0, DI // P, 2):
                        bank = ra.claim(pe)
                        pe.wait_ge(sig("gated"), 2 * (k // 4) + 2)
                        for j in range(2):
                            for t in range(TB):
                                last = tp(bank[:, j * T + t * P:j * T + (t + 1) * P], xt[:, t, (k + j) * P:(k + j + 1) * P], c.ident[:])
                        ra.fill(last)
                    pe.wait_ge(ra.emptied, A_EXP + NPH + DI // P // 2)
                    for t in range(TB):
                        for k in range(DI // P):
                            last = mm(off_bank[:, t * D:(t + 1) * D], yzT[:, k, t * P:(t + 1) * P], wout[:, k, :],
                                      start=(k == 0), stop=(k == DI // P - 1))
                    last.then_inc(sig("projected"), 1)

                @block.scalar
                def _(act):
                    a = nc.scalar.activation
                    ch = Chain(act, sig("act_chain"))

                    def biased(p):
                        bank = ra.take(act)
                        if p >= 3:
                            act.wait_ge(sig("conv"), p - 2)
                        for j in range(2):
                            last = a(xc[p % 3][:, j, KC - 1:], bank[:, j * T:(j + 1) * T], ACT.Identity, bias=bx[:, 2 * p + j:2 * p + j + 1])
                        ra.empty(last)

                    def silu(p):
                        act.wait_ge(sig("conv"), p + 1)
                        a((bc if p == 0 else xf[p % 3])[:], xf[p % 3][:], ACT.Silu).then_inc(sig("silu"), 1)

                    a(xb[:], c.xT[:, :, bass.ts(b, T)], ACT.Copy).then_inc(sig("sliced"), 1)
                    for i in range(2):
                        for m in range(0, MH, 2):
                            bank = ra.take(act)
                            for j in range(2):
                                last = a(pre[:, i, m + j, :], bank[:, j * T:(j + 1) * T], ACT.Identity, bias=bd[:, i, m + j:m + j + 1],
                                         scale=lcol[:, m + j:m + j + 1] if i == 0 else 1.0)
                            ra.empty(last)
                    act.wait_ge(ra.emptied, 4)
                    ch.link(a(ex1[:], pre[:], ACT.Abs))
                    ch.link(a(ex1[:], ex1[:], ACT.Exp, scale=-1.0))
                    a(ex1[:], ex1[:], ACT.Ln, bias=1.0).then_inc(sig("log1p"), 1)
                    biased(0)
                    biased(1)
                    act.wait_ge(sig("lam_floor"), 1)
                    a(R, R, ACT.Ln).then_inc(sig("lnlam"), 1)
                    silu(0)
                    biased(2)
                    silu(1)
                    silu(2)
                    for p in range(3, NPX):
                        biased(p)
                        silu(p)
                    act.wait_ge(sig("total_diff"), 1)
                    a(sfac[:], sfac[:], ACT.Exp).then_inc(sig("factors"), 1)
                    a(tfac[:], tfac[:], ACT.Exp).then_inc(sig("factors"), 1)
                    for i in range(NPH):
                        bank = ra.take(act)
                        if i >= 2:
                            act.wait_ge(sig("att"), i - 1)
                        for j in range(2):
                            for t in range(TB):
                                last = a(ex[i % 2][:, j, t * P:(t + 1) * P], bank[:, j * T + t * P:j * T + (t + 1) * P], ACT.Exp,
                                         bias=ngc[:, t, 2 * i + j:2 * i + j + 1])
                        ra.empty(last)
                    for i in range(NG * TB):
                        act.wait_ge(sig("zb"), i + 1)
                        a(zb[i % 2], zb[i % 2], ACT.Silu).then_inc(sig("z_silu"), 1)
                    act.wait_ge(sig("gated"), NG * TB)
                    for k in range(0, DI // P, 2):
                        bank = ra.take(act)
                        ra.empty(a(yzT[:, k:k + 2, :], bank[:].rearrange("p (k t) -> p k t", k=2), ACT.Copy))
                    for t in range(TB):
                        a(wv[:], xt[:, t, :], ACT.Square, accum_out=ss[:, t, 0:1]).then_inc(sig("squares"), 1)
                        act.wait_ge(sig("squares"), t + 1)
                    act.wait_ge(sig("mean_sq"), 1)
                    a(ss[:, :, 2], ss[:, :, 1], ACT.Sqrt).then_inc(sig("rms"), 1)

                @block.vector
                def _(dve):
                    ch = Chain(dve, sig("dve_chain"))
                    vec = nc.vector

                    def convolve(p):
                        dve.wait_ge(ra.emptied, 4 + p + 1)
                        if p >= 4:
                            dve.wait_ge(rv.filled, 6 + p - 3)
                        elif p == 3:
                            dve.wait_ge(sig("silu"), 1)
                        for j in range(2):
                            m = 2 * p + j
                            ch.link(vec.tensor_scalar(xf[p % 3][:, j, :], xc[p % 3][:, j, 0:T], conv[:, m, 0:1], None, ALU.mult))
                            for i in range(1, KC):
                                ins = vec.scalar_tensor_tensor(out=xf[p % 3][:, j, :], in0=xc[p % 3][:, j, i:i + T], scalar=conv[:, m, i:i + 1],
                                                               in1=xf[p % 3][:, j, :], op0=ALU.mult, op1=ALU.add)
                                if j == 1 and i == KC - 1:
                                    ins.then_inc(sig("conv"), 1)
                                else:
                                    ch.link(ins)

                    def take_x(p):
                        bank = rv.take(dve)
                        cs = slice((p - 1) * T, p * T)
                        vec.tensor_copy(xt[:, :, cs], bank[:].rearrange("p (t e) -> p t e", t=TB))
                        for t in range(TB):
                            hs = slice((p - 1) * 4, p * 4)
                            last = vec.tensor_tensor(v[:, t, cs].rearrange("p (h d) -> p h d", h=4),
                                                     bank[:, t * T:(t + 1) * T].rearrange("p (h d) -> p h d", h=4),
                                                     dt[:, t, hs].unsqueeze(2).to_broadcast([P, 4, HD]), ALU.mult)
                        rv.empty(last)

                    dve.wait_ge(sig("log1p"), 1)
                    f = lambda a: a.rearrange("p i m t -> p (i m t)")
                    vec.scalar_tensor_tensor(out=f(sp[:]), in0=f(pre[:]), scalar=0.0, in1=f(ex1[:]), op0=ALU.max, op1=ALU.add).then_inc(sig("rows"), 1)
                    dve.wait_ge(sig("rows"), 1)
                    vec.tensor_scalar(R, sp[:, 0], 1e-9, None, ALU.max).then_inc(sig("lam_floor"), 1)
                    for m in range(MH):
                        last = vec.tensor_scalar(g[:, m, :], sp[:, 1, m, :], nega[:, m:m + 1], None, ALU.mult)
                    ch.link(last)
                    for m in range(MH):
                        for t in range(TB):
                            ts = slice(t * P, (t + 1) * P)
                            last = vec.tensor_tensor_scan(gcT[:, m, ts], ones[:], g[:, m, ts], 0.0, ALU.mult, ALU.add)
                    last.then_inc(sig("rows"), 1)
                    convolve(0)
                    convolve(1)
                    dve.wait_ge(sig("lnlam"), 1)
                    dve.wait_ge(sig("rows"), 2)
                    ch.link(vec.tensor_tensor(R, R, pre[:, 0], ALU.min))
                    vec.tensor_tensor(R, R, gcT[:], ALU.add).then_inc(sig("R"), 1)
                    convolve(2)
                    heads = lambda bank, j: bank[:].rearrange("p (h j) -> p h j", j=16)[:, :, j]
                    for t in range(TB):
                        bank = rv.take(dve)
                        rv.empty(vec.tensor_copy(dt[:, t, :], heads(bank, 0)))
                    for t in range(TB):
                        bank = rv.take(dve)
                        vec.tensor_copy(lam0[:, t, :], heads(bank, 0))
                        rv.empty(vec.tensor_copy(lam8[:, t, :], heads(bank, 8)))
                    for t in range(TB):
                        bank = rv.take(dve)
                        rv.empty(vec.tensor_copy(gc[:, t, :], heads(bank, 0)))
                    dve.wait_ge(rv.emptied, 6)
                    vec.sem_inc(sig("gc_tok"), 1)
                    vec.tensor_scalar(ngc[:], gc[:], -1.0, None, ALU.mult)
                    dve.wait_ge(sig("qk"), 1)
                    idw = c.ident[:]
                    vec.tensor_tensor(dtmp[:, 0, :], qk_bank[:, 0:P], idw, ALU.mult)
                    ch.link(vec.tensor_tensor(dtmp[:, 1, :], qk_bank[:, T:T + P], idw, ALU.mult))
                    ch.link(vec.tensor_reduce(qdiag[:], dtmp, AX.X, ALU.add))
                    vec.tensor_copy(qkd[:, 0, :], qk_bank[:, 0:P])
                    vec.tensor_copy(qkd[:, 1, :], qk_bank[:, T:T + P])
                    vec.tensor_copy(qko[:], qk_bank[:, P:T])
                    ch.link(vec.tensor_tensor(coef[:], dt[:], lam0[:], ALU.mult))
                    ch.link(vec.tensor_tensor(coef[:], coef[:], qdiag[:].unsqueeze(2).to_broadcast([P, TB, H]), ALU.mult))
                    ch.link(vec.tensor_tensor(coef[:], coef[:], dh[:].unsqueeze(1).to_broadcast([P, TB, H]), ALU.add))
                    for p in range(3, NPX):
                        convolve(p)
                        take_x(p - 2)
                    take_x(NPX - 2)
                    take_x(NPX - 1)
                    dve.wait_ge(sig("total"), 1)
                    vec.tensor_tensor(sfac[:], off_bank[:, 0:H], gc[:, 0, :], ALU.subtract)
                    vec.tensor_copy(tfac[:], gc[:, 1, :]).then_inc(sig("total_diff"), 1)
                    dve.wait_ge(sig("factors"), 2)
                    ch.link(vec.tensor_tensor(tfac[:], tfac[:], lam8[:, 1, :], ALU.mult))
                    dve.wait_ge(rv.emptied, 6 + NPX - 1)
                    vec.tensor_tensor(wv[:].rearrange("p (h d) -> p h d", h=H), v[:, 0, :].rearrange("p (h d) -> p h d", h=H),
                                      sfac[:].unsqueeze(2).to_broadcast([P, H, HD]), ALU.mult).then_inc(sig("wv"), 1)

                    def combine(gi):
                        dve.wait_ge(sig("weighted"), 4 * gi + 4)
                        cs, hs = slice(gi * GC, (gi + 1) * GC), slice(gi * 8, gi * 8 + 8)
                        by_head = lambda a: a.rearrange("p (h d) -> p h d", h=8)
                        for t in range(TB):
                            last = vec.tensor_tensor(by_head(xt[:, t, cs]), by_head(xt[:, t, cs]), coef[:, t, hs].unsqueeze(2).to_broadcast([P, 8, HD]), ALU.mult)
                        ch.link(last)
                        vec.tensor_tensor(by_head(tmp), by_head(off_bank[:]), tfac[:, hs].unsqueeze(2).to_broadcast([P, 8, HD]), ALU.mult)
                        for t in range(TB):
                            last = vec.tensor_tensor(xt[:, t, cs], xt[:, t, cs], y_bank[t][:], ALU.add)
                        last.then_inc(sig("combined"), 1)
                        dve.wait_ge(sig("combined"), gi + 1)
                        ch.link(vec.tensor_tensor(xt[:, 1, cs], xt[:, 1, cs], tmp, ALU.add))

                    for i in range(NPH + 1):
                        if i < NPH:
                            bank = rv.take(dve)
                            if i >= 2:
                                dve.wait_ge(ra.filled, A_EXP + i - 1)
                            ins = vec.tensor_tensor(ru[i % 2][:], bank[:].rearrange("p (j t) -> p j t", j=2),
                                                    um[:].unsqueeze(1).to_broadcast([P, 2, T]), ALU.mult)
                            ins.then_inc(sig("ru"), 1)
                            dve.wait_ge(sig("ru"), i + 1)
                            vec.sem_inc(rv.emptied, 1)
                        if i >= 1:
                            q = i - 1
                            dve.wait_ge(ra.emptied, A_EXP + q + 1)
                            if q >= 2:
                                dve.wait_ge(sig("weighted"), q - 1)
                            vec.tensor_tensor(att[q % 2][:], ex[q % 2][:], qkd[:].rearrange("p t s -> p (t s)").unsqueeze(1).to_broadcast([P, 2, T]),
                                              ALU.mult).then_inc(sig("att"), 1)
                            if q % 4 == 3:
                                combine(q // 4)
                    n = 0
                    for gi in range(NG):
                        for t in range(TB):
                            bank = rv.take(dve)
                            cs = slice(gi * GC, (gi + 1) * GC)
                            ins = vec.tensor_tensor(zb[n % 2], bank[:], bz[:, cs], ALU.add)
                            ins.then_inc(sig("zb"), 1)
                            dve.wait_ge(sig("zb"), n + 1)
                            vec.sem_inc(rv.emptied, 1)
                            dve.wait_ge(sig("z_silu"), n + 1)
                            vec.tensor_tensor(xt[:, t, cs], xt[:, t, cs], zb[n % 2], ALU.mult).then_inc(sig("gated"), 1)
                            n += 1
                    dve.wait_ge(sig("squares"), TB)
                    vec.tensor_scalar(ss[:, :, 1], ss[:, :, 0], 1.0 / DI, 1e-5, ALU.mult, ALU.add).then_inc(sig("mean_sq"), 1)
                    dve.wait_ge(sig("rms"), 1)
                    ch.link(vec.reciprocal(ss[:, :, 3], ss[:, :, 2]))
                    dve.wait_ge(sig("projected"), 1)
                    for t in range(TB):
                        last = vec.scalar_tensor_tensor(out=y[:, t, :], in0=off_bank[:, t * D:(t + 1) * D], scalar=ss[:, t, 3:4], in1=bo[:],
                                                        op0=ALU.mult, op1=ALU.add)
                    ch.link(last)
                    vec.tensor_tensor(c.x[:, bass.ts(b, TB), :], c.x[:, bass.ts(b, TB), :], y, ALU.add)
            sig.clear()
        sig.close()


def pack(inputs):
    i = {k: np.asarray(v) for k, v in inputs.items()}
    a = {}

    def rows(w):
        s = w.shape
        return np.ascontiguousarray(np.moveaxis(w.reshape(*s[:-2], s[-2] // P, P, s[-1]), -3, -2))

    def cols(v):
        return np.ascontiguousarray(np.swapaxes(v.reshape(*v.shape[:-1], v.shape[-1] // P, P), -1, -2))

    tok = lambda v: np.ascontiguousarray(v.reshape(NT, P, D).transpose(1, 0, 2))
    tr = lambda v: np.swapaxes(v, -1, -2)
    a["x"], a["ctx"] = tok(i["x"]), tok(i["ctx_1024"])
    a["ident"] = np.eye(P, dtype=np.float32)
    a["iota8"] = np.broadcast_to(np.arange(8, dtype=np.float32), (P, 8)).copy()
    earlier = (np.arange(P)[:, None] < np.arange(P)[None, :]).astype(np.float32)
    a["tri_strict_ones"] = np.stack([earlier, np.ones((P, P), np.float32)], 1)

    def experts(tag, gate, ups, lins, downs):
        a[f"{tag}_gate"] = rows(gate)
        a[f"{tag}_up"] = rows(np.concatenate(ups))
        if lins:
            a[f"{tag}_lin"] = rows(np.concatenate(lins))
        a[f"{tag}_down"] = rows(np.concatenate(downs))

    halves = lambda w: w.reshape(2, 256, D)
    experts("L0f", i["L0_ffn_gate_w"].T, [tr(i["L0_ffn_w1"]), tr(halves(i["L0_ffn_ws1"]))],
            [tr(i["L0_ffn_w3"]), tr(halves(i["L0_ffn_ws3"]))],
            [tr(i["L0_ffn_w2"]), i["L0_ffn_ws2"].T.reshape(2, 256, D)])
    a["L0f_gate_b"] = i["L0_ffn_gate_b"]
    a["L0f_up_b"] = cols(np.concatenate([i["L0_ffn_b1"], i["L0_ffn_bs1"].reshape(2, 256)]))
    a["L0f_lin_b"] = cols(np.concatenate([i["L0_ffn_b3"], i["L0_ffn_bs3"].reshape(2, 256)]))
    a["L0f_down_b"] = np.concatenate([i["L0_ffn_b2"], i["L0_ffn_bs2"][None], np.zeros((1, D), np.float32)])
    experts("L2f", i["L2_ffn_switch_w"], [i["L2_ffn_w1"]], None, [i["L2_ffn_w2"]])
    a["L2f_gate_b"] = i["L2_ffn_switch_b"]
    a["L2f_up_b"] = cols(i["L2_ffn_b1"])
    a["L2f_down_b"] = i["L2_ffn_b2"]
    experts("L3f", i["L3_ffn_gate_w"].T, [tr(i["L3_ffn_we_gate"]), tr(halves(i["L3_ffn_ws_gate"]))],
            [tr(i["L3_ffn_we_up"]), tr(halves(i["L3_ffn_ws_up"]))],
            [tr(i["L3_ffn_we_down"]), i["L3_ffn_ws_down"].T.reshape(2, 256, D)])
    pack_attention(i, a, rows, cols, tr)
    return {k: np.ascontiguousarray(v) for k, v in a.items()}


def pack_attention(i, a, rows, cols, tr):
    def spread(w):
        return np.concatenate([w.reshape(D, 16, 16), np.zeros((D, 16, 16), w.dtype)], -1).reshape(D, 512)

    t = np.arange(P)
    dist = np.abs(t[:, None] - t[None, :])
    dist1 = np.abs(P + t[:, None] - np.arange(T)[None, :])
    a["distance"] = np.concatenate([dist, dist1], 1).astype(np.float32)
    a["future_neg"] = np.where(t[None, :] > t[:, None], -1e30, 0.0).astype(np.float32)
    a["L1a_wq"], a["L1a_wk"] = rows(spread(i["L1_attn_Wq"])), rows(spread(i["L1_attn_Wk"]))
    a["L1a_wv"], a["L1a_wo"] = rows(i["L1_attn_Wv"]), rows(i["L1_attn_Wo"])
    a["L1a_bo"], a["L1a_w"], a["L1a_v"] = i["L1_attn_bo"], i["L1_attn_w"], i["L1_attn_v"]
    a["L1x_wq"], a["L1x_wk"] = rows(spread(i["L1_xattn_Wq"].T)), rows(spread(i["L1_xattn_Wk"].T))
    a["L1x_wv"], a["L1x_wo"] = rows(i["L1_xattn_Wv"].T), rows(i["L1_xattn_Wo"].T)
    a["L1x_bo"] = i["L1_xattn_bo"]
    a["mask_pairs"] = i["mask_Bx1xSxS2_ik0"].reshape(B, TB, P, T).transpose(0, 2, 1, 3)
    a["mask_keys"] = i["mask_Bx1xS2_ik0"]
    a["mask_bool"] = i["mask_BxS2_bk1"].reshape(B, 1, T)
    a["L3x_wq"], a["L3x_wo"] = rows(i["L3_xattn_Wq"]), rows(i["L3_xattn_Wo"])
    a["L3x_wk"], a["L3x_wv"] = rows(i["L3_xattn_Wkv"][:, :512]), rows(i["L3_xattn_Wkv"][:, 512:])
    a["L3x_ln"] = np.stack([cols(i[f"L3_xattn_ln_{n}"]) for n in ("l_g", "l_b", "x_g", "x_b")], 1)
    a["L3x_og"], a["L3x_ob"] = i["L3_xattn_ln_o_g"], i["L3_xattn_ln_o_b"]
    for n in ("up", "gate", "down"):
        o, k = i[f"L1_ffn_w_{n}"].shape
        a[f"L1f_{n}"] = i[f"L1_ffn_w_{n}"].reshape(o // P, P, k).transpose(1, 0, 2)
    a["L2a_c"] = i["L2_attn_C"].reshape(KD, P, 64).transpose(1, 0, 2)
    a["L2a_b"] = i["L2_attn_B"].T.reshape(KD, P, 64).transpose(1, 0, 2)
    a["L2a_a"], a["L2a_d"], a["L2a_ldt"] = i["L2_attn_A"], cols(i["L2_attn_D"]), cols(i["L2_attn_log_dt"])
    a["iota64"] = np.broadcast_to(np.arange(64, dtype=np.float32), (P, 64))
    a["L3a_wqk"] = rows(np.concatenate([i["L3_attn_Wq"].T, i["L3_attn_Wk"].T], 1))
    a["L3a_wv"], a["L3a_bv"] = rows(i["L3_attn_Wv"].T), i["L3_attn_bv"]
    a["L3a_bqk"] = np.concatenate([i["L3_attn_bq"], i["L3_attn_bk"]])
    a["L3a_gamma"], a["L3a_beta"] = i["L3_attn_gamma"], i["L3_attn_beta"]
    freq = (1.0 / 10000.0 ** (np.arange(0, D, 2, dtype=np.float32) / D)).astype(np.float32)
    ang = np.arange(T, dtype=np.float32)[:, None] * freq
    paired = lambda e, o: np.stack([e, o], -1).reshape(TB, P, D).transpose(1, 0, 2).astype(np.float32)
    a["rope_cos"], a["rope_sin"] = paired(np.cos(ang), np.cos(ang)), paired(-np.sin(ang), np.sin(ang))
    a["blockdiag16"] = np.where(t[:, None] // 16 == t[None, :] // 16, 1.0 / T, 0.0).astype(np.float32)
    upto = (t[:, None] <= t[None, :]).astype(np.float32)
    a["causal"] = np.concatenate([upto, np.ones((P, P), np.float32), upto], 1)
    for j, n in enumerate(("q", "k")):
        a[f"L0x_wt{j}"], a[f"L0x_bt{j}"] = rows(i[f"L0_xattn_W{n}"]), i[f"L0_xattn_b{n}"]
    for j, n in enumerate(("q", "v")):
        a[f"L0x_wf{j}"] = rows(spread(i[f"L0_xattn_W{n}"]))
    wide = lambda v: np.concatenate([v.reshape(16, 16), np.zeros((16, 16), v.dtype)], -1).reshape(512)
    a["L0x_bf"] = np.stack([cols(wide(i["L0_xattn_bq"])), cols(wide(i["L0_xattn_bv"]))], 1)
    a["L0x_wo"], a["L0x_bo"] = rows(i["L0_xattn_Wo"]), i["L0_xattn_bo"]

    wi, bi = i["L0_attn_in_proj_w"], i["L0_attn_in_proj_b"]
    order = np.concatenate([np.arange(4096, 4352), np.arange(2048, 4096)])
    a["L0a_wz"], a["L0a_bz"] = rows(wi[:2048].T), bi[:2048]
    a["L0a_wx"], a["L0a_bx"] = rows(wi[order].T), cols(bi[order])
    a["L0a_conv"] = i["L0_attn_conv_w"][order - 2048].reshape(18, P, 4).transpose(1, 0, 2)
    padded = lambda m: np.concatenate([m.reshape(32, 15, -1), np.zeros((32, 1, m.size // 480), m.dtype)], 1).reshape(512, -1)
    per_head = lambda m: np.repeat(m, 16, axis=0)
    a["L0a_wdl"], a["L0a_wdt"] = rows(padded(wi[4384:]).T), rows(per_head(wi[4352:4384]).T)
    a["L0a_bd"] = np.stack([cols(padded(bi[4384:])[:, 0]), cols(per_head(bi[4352:4384]))], 1)
    a["L0a_l"] = cols(padded(i["L0_attn_L"].reshape(480))[:, 0])
    a["L0a_alog"], a["L0a_dtb"] = cols(per_head(i["L0_attn_A_log"])), cols(per_head(i["L0_attn_dt_bias"]))
    a["L0a_d"], a["L0a_norm"] = i["L0_attn_D"], cols(i["L0_attn_norm_w"])
    a["L0a_wout"], a["L0a_bo"] = rows(i["L0_attn_out_proj_w"].T), i["L0_attn_out_proj_b"]
    pick, u, v = np.zeros((P, 8, P), np.float32), np.zeros((P, P), np.float32), np.zeros((P, P), np.float32)
    n = 0
    for k in range(7):
        for j in range(P >> (k + 1)):
            start, half = j << (k + 1), 1 << k
            v[n, start:start + half] = 1.0
            u[n, start + half:start + 2 * half] = 1.0
            for h in range(8):
                pick[h * 16 + k + 1, h, n] = 1.0
            n += 1
    a["L0a_pick"], a["L0a_u"], a["L0a_v"] = pick, np.concatenate([u, u], 1), v
    last_row = np.zeros((P, P), np.float32)
    last_row[P - 1] = 1.0
    a["last_row"] = last_row


LAYERS = {1: layer0_attn, 2: layer0_xattn, 3: layer0_ffn, 4: layer1_attn, 5: layer1_xattn, 6: layer1_ffn, 7: layer2_attn, 8: layer2_xattn, 9: layer2_ffn, 10: layer3_attn, 11: layer3_xattn, 12: layer3_ffn}


def program(nc, dram, out, layers):
    with ExitStack() as ctx:
        c = Core(nc, ctx, dram)
        c.load("first", [(c.x[:], dram["x"]), (c.ident[:], dram["ident"])])
        if layers[0] == 1:
            layer0_attn(c)
            layers = layers[1:]
        c.load("context", [(c.ctx[:], dram["ctx"])])
        transpose_tokens(c, "ctxT", c.ctx, c.ctxT)
        for n in layers:
            LAYERS[n](c)
        sig = Signals(nc, "last")
        with nc.Block() as block:
            @block.sync
            def _(sp):
                sp.dma_start(out, c.x[:]).then_inc(sig("stored"), 16)
                sp.wait_ge(sig("stored"), 16)
        sig.close()


def kernel(**inputs):
    import concourse.bacc as bacc
    from concourse.bass_utils import run_bass_kernel_spmd

    arrays = pack(inputs)
    nc = bacc.Bacc("TRN2", target_bir_lowering=False, num_devices=1)
    dram = {k: nc.dram_tensor(f"in_{k}", v.shape, mybir.dt.from_np(v.dtype), kind="ExternalInput").ap()
            for k, v in arrays.items()}
    out = nc.dram_tensor("out_x", (P, NT, D), F32, kind="ExternalOutput").ap()
    program(nc, dram, out, sorted(LAYERS))
    r = run_bass_kernel_spmd(nc, [{f"in_{k}": v for k, v in arrays.items()}], core_ids=[0])
    got = r.results[0]["out_x"]
    return np.ascontiguousarray(got.transpose(1, 0, 2)).reshape(B, T, D)
```

```python
from contextlib import ExitStack

import numpy as np

import concourse.bass as bass
from concourse import mybir

P = 128
B, T, D = 8, 256, 256
N = B * T
NT = N // P
KD = D // P
TB = T // P
BLK = 512
NBLK = N // BLK

F32 = mybir.dt.float32
I32 = mybir.dt.int32
BF16 = mybir.dt.bfloat16
F32R = mybir.dt.float32r
U8 = mybir.dt.uint8
ACT = mybir.ActivationFunctionType
ALU = mybir.AluOpType
AX = mybir.AxisListType
ROWS = 4
ROUND = 12582912.0


class Signals:

    def __init__(self, nc, tag):
        self.nc, self.tag, self.ctx, self.by_name = nc, tag, ExitStack(), {}

    def __call__(self, name):
        if name not in self.by_name:
            self.by_name[name] = self.ctx.enter_context(self.nc.semaphore(f"{self.tag}_{name}"))
        return self.by_name[name]

    def clear(self):
        for s in self.by_name.values():
            self.nc.sync.sem_clear(s)
        self.nc.all_engine_barrier()

    def close(self):
        self.ctx.close()


class Ring:

    def __init__(self, sig, name, bufs):
        self.filled, self.emptied, self.bufs = sig(name + "_filled"), sig(name + "_emptied"), bufs
        self.n_in = self.n_out = 0

    def claim(self, eng):
        if self.n_in >= len(self.bufs):
            eng.wait_ge(self.emptied, self.n_in - len(self.bufs) + 1)
        self.n_in += 1
        return self.bufs[(self.n_in - 1) % len(self.bufs)]

    def fill(self, ins):
        ins.then_inc(self.filled, 1)

    def take(self, eng):
        self.n_out += 1
        eng.wait_ge(self.filled, self.n_out)
        return self.bufs[(self.n_out - 1) % len(self.bufs)]

    def empty(self, ins):
        ins.then_inc(self.emptied, 1)


class Chain:

    def __init__(self, eng, sem):
        self.eng, self.sem, self.n = eng, sem, 0

    def link(self, ins):
        self.n += 1
        ins.then_inc(self.sem, 1)
        self.eng.wait_ge(self.sem, self.n)


class Core:

    def __init__(self, nc, ctx, dram):
        self.nc, self.dram = nc, dram
        sb = lambda name, shape, dt=F32: ctx.enter_context(nc.sbuf_tensor(name, shape, dt))
        self.x = sb("x_res", [P, NT, D])
        self.ctx = sb("ctx_tok", [P, NT, D])
        self.ctxT = sb("ctx_feat", [P, KD, N])
        self.xT = sb("x_feat", [P, KD, N])
        self.ident = sb("ident", [P, P])
        self.banks = [ctx.enter_context(nc.psum_tensor(f"bank{i}", [P, BLK], F32)) for i in range(8)]

    def tiles(self, stack, tag):
        return lambda name, shape, dt=F32: stack.enter_context(self.nc.sbuf_tensor(f"{tag}_{name}", shape, dt))

    def load(self, tag, pairs):
        nc, sig = self.nc, Signals(self.nc, tag)
        with nc.Block() as block:

            @block.sync
            def _(sp):
                for dst, src in pairs[0::2]:
                    sp.dma_start(dst, src).then_inc(sig("loaded_sp"), 16)
                sp.wait_ge(sig("loaded_sp"), 16 * len(pairs[0::2]))

            @block.scalar
            def _(act):
                for dst, src in pairs[1::2]:
                    act.dma_start(dst, src).then_inc(sig("loaded_act"), 16)
                if len(pairs) > 1:
                    act.wait_ge(sig("loaded_act"), 16 * len(pairs[1::2]))
        sig.clear()
        sig.close()


def transpose_tokens(c, tag, src, dstT):
    nc = c.nc
    sig = Signals(nc, tag)
    with nc.Block() as block:
        ring = Ring(sig, "turned", c.banks)

        @block.tensor
        def _(pe):
            for n in range(NBLK):
                for k in range(KD):
                    bank = ring.claim(pe)
                    for j in range(4):
                        last = nc.tensor.transpose(bank[:, j * P:(j + 1) * P], src[:, 4 * n + j, k * P:(k + 1) * P], c.ident[:])
                    ring.fill(last)

        @block.scalar
        def _(act):
            for n in range(NBLK):
                for k in range(KD):
                    bank = ring.take(act)
                    ring.empty(nc.scalar.activation(dstT[:, k, n * BLK:(n + 1) * BLK], bank[:], ACT.Copy))
    sig.clear()
    sig.close()


def normalise(c, tag, src, dst=None, dstT=None, gain=None, shift=None, eps=1e-5, loads=()):
    nc = c.nc
    sig = Signals(nc, tag)
    with ExitStack() as stack:
        sb = c.tiles(stack, tag)
        stats = sb("stats", [P, NT, 6])
        mv = sb("mv", [P, NT, 2])
        rstd = sb("rstd", [P, NT, 3])
        xs = None if dst is not None else [sb(f"xs{i}", [P, 4, D]) for i in range(2)]
        rows_of = lambda n: dst[:, 4 * n:4 * n + 4, :] if dst is not None else xs[n % 2][:]
        with nc.Block() as block:
            @block.sync
            def _(sp):
                for to, come_from in loads:
                    sp.dma_start(to, come_from).then_inc(sig("loaded"), 16)
                if loads:
                    sp.wait_ge(sig("loaded"), 16 * len(loads))

            @block.vector
            def _(dve):
                for t in range(NT):
                    last = nc.vector.bn_stats(stats[:, t, :], src[:, t, :])
                last.then_inc(sig("stats"), 1)
                dve.wait_ge(sig("stats"), 1)
                for t in range(NT):
                    last = nc.vector.bn_aggr(mv[:, t, :], stats[:, t, :])
                last.then_inc(sig("mean_var"), 1)
                dve.wait_ge(sig("mean_var"), 1)
                nc.vector.tensor_scalar_add(rstd[:, :, 0], mv[:, :, 1], eps).then_inc(sig("var_eps"), 1)
                dve.wait_ge(sig("std"), 1)
                nc.vector.reciprocal(rstd[:, :, 2], rstd[:, :, 1]).then_inc(sig("rstd"), 1)
                dve.wait_ge(sig("rstd"), 1)
                for n in range(NBLK):
                    if dst is None and n >= 2:
                        dve.wait_ge(sig("transposed"), KD * (n - 1))
                    for j in range(4):
                        t = 4 * n + j
                        last = nc.vector.tensor_scalar(rows_of(n)[:, j, :], src[:, t, :], mv[:, t, 0:1], rstd[:, t, 2:3],
                                                       ALU.subtract, ALU.mult)
                    last.then_inc(sig("normed"), 1)

            @block.tensor
            def _(pe):
                if dstT is not None:
                    for n in range(NBLK):
                        pe.wait_ge(sig("normed"), n + 1)
                        for k in range(KD):
                            bank = c.banks[2 * n + k]
                            for j in range(4):
                                last = nc.tensor.transpose(bank[:, j * P:(j + 1) * P], rows_of(n)[:, j, k * P:(k + 1) * P], c.ident[:])
                            last.then_inc(sig("transposed"), 1)

            @block.scalar
            def _(act):
                act.wait_ge(sig("var_eps"), 1)
                nc.scalar.activation(rstd[:, :, 1], rstd[:, :, 0], ACT.Sqrt).then_inc(sig("std"), 1)
                if dstT is not None:
                    for n in range(NBLK):
                        for k in range(KD):
                            act.wait_ge(sig("transposed"), KD * n + k + 1)
                            out, bank = dstT[:, k, n * BLK:(n + 1) * BLK], c.banks[2 * n + k]
                            if gain is None:
                                nc.scalar.activation(out, bank[:], ACT.Copy)
                            else:
                                nc.scalar.activation(out, bank[:], ACT.Identity, bias=shift[:, k:k + 1], scale=gain[:, k:k + 1])
        sig.clear()
    sig.close()


def mixture(c, tag, n_routed, n_shared, M, gated, top, biases, renorm=False, capacity=None, parts=1):
    nc = c.nc
    E = n_routed * parts + n_shared
    R = n_routed
    w = c.dram
    F = M * P
    act_fn = ACT.Silu if gated else ACT.Gelu_apprx_tanh
    with ExitStack() as stack:
        sb = c.tiles(stack, tag)
        comb = sb("comb", [P, E, NT])
        combT = sb("combT", [E, NT, P])
        down_b = sb("down_b", [E, D])
        xh, xl = sb("xh", [P, KD, N], F32R), sb("xl", [P, KD, N], F32R)
        b_all = sb("b_all", [P, 1 + gated, E, M])
        n_kinds = 2 + gated
        raw = [sb(f"raw{i}", [P, n_kinds, KD * F]) for i in range(2)]
        wh = [sb(f"wh{i}", [P, n_kinds, KD * F], F32R) for i in range(2)]
        wl = [sb(f"wl{i}", [P, n_kinds, KD * F], F32R) for i in range(2)]
        rising = lambda a, kind: a[:, kind, :].rearrange("p (k f) -> p k f", k=KD)
        falling = lambda a: a[:, n_kinds - 1, :].rearrange("p (m d) -> p m d", m=M)
        h = [sb(f"h{i}", [P, BLK]) for i in range(2)]
        hh = [sb(f"hh{i}", [P, M, BLK], F32R) for i in range(2)]
        hl = [sb(f"hl{i}", [P, M, BLK], F32R) for i in range(2)]
        silu = [sb(f"silu{i}", [P, BLK]) for i in range(2)] if gated else None
        comb2 = sb("comb2", [P, 2, NT])
        b2 = sb("b2", [P, 1 + gated, 2, M])
        kinds = ("up", "lin", "down") if gated else ("up", "down")

        def fetch(sp, i, e, sem):
            for j, kind in enumerate(kinds):
                sp.dma_start(raw[i][:, j, :], w[f"{tag}_{kind}"][e].rearrange("p a b -> p (a b)")).then_inc(sem, 16)

        def split(pool, i, high, sem):
            nc.gpsimd.tensor_copy(wh[i][:], raw[i][:]).then_inc(high, 1)
            pool.wait_ge(high, 1)
            nc.gpsimd.tensor_tensor(wl[i][:], raw[i][:], wh[i][:].bitcast(F32), ALU.subtract).then_inc(sem, 1)

        with ExitStack() as inner:
            sc = c.tiles(inner, tag)
            gate = sc("gate", [P, KD, R])
            gate_b = sc("gate_b", [P, R])
            iota = sc("iota", [P, R])
            trist = sc("trist", [P, 2, P])
            pairs = [(gate[:], w[f"{tag}_gate"]), (iota[:], w["iota8"])]
            if biases:
                pairs += [(gate_b[:], w[f"{tag}_gate_b"].rearrange("(a n) -> a n", a=1).to_broadcast([P, R])),
                          (down_b[:], w[f"{tag}_down_b"]), (b_all[:, 0], w[f"{tag}_up_b"])]
                if gated:
                    pairs += [(b_all[:, 1], w[f"{tag}_lin_b"])]
            if capacity:
                pairs += [(trist[:], w["tri_strict_ones"])]
            normalise(c, tag + "_n", c.x, dstT=c.xT, loads=pairs)
            prob = sc("prob", [P, NT, R])
            tmp = sc("tmp", [P, NT, R])
            onehot = sc("onehot", [P, NT, R])
            assigned = sc("assigned", [P, NT, R])
            dense = sc("dense", [P, NT, R])
            count = sc("count", [P, NT, R])
            best = sc("best", [P, NT])
            wsum = sc("wsum", [P, NT])
            sig = Signals(nc, tag + "_gt")
            with nc.Block() as block:
                def bc(t2):
                    return t2[:].unsqueeze(2).to_broadcast([P, NT, R])

                def ie():
                    return iota[:].unsqueeze(1).to_broadcast([P, NT, R])

                logits = c.banks[0][:, 0:NT * R].rearrange("p (t e) -> p t e", t=NT)
                inside = c.banks[1][:, 0:NT * R].rearrange("p (t e) -> p t e", t=NT)
                totals = c.banks[2][:, 0:NT * R].rearrange("p (t e) -> p t e", t=NT)

                @block.tensor
                def _(pe):
                    for t in range(NT):
                        for k in range(KD):
                            last = nc.tensor.matmul(logits[:, t, :], c.xT[:, k, t * P:(t + 1) * P], gate[:, k, :],
                                                    start=(k == 0), stop=(k == KD - 1))
                    last.then_inc(sig("logits"), 1)
                    if capacity:
                        pe.wait_ge(sig("assigned"), 1)
                        nc.tensor.matmul(c.banks[1][:, 0:NT * R], trist[:, 0, :], assigned[:].rearrange("p t e -> p (t e)"),
                                         start=True, stop=True)
                        nc.tensor.matmul(c.banks[2][:, 0:NT * R], trist[:, 1, :], assigned[:].rearrange("p t e -> p (t e)"),
                                         start=True, stop=True).then_inc(sig("counted"), 1)
                    pe.wait_ge(sig("comb"), 1)
                    if biases:
                        for t in range(NT):
                            bank = c.banks[3 + t // 4]
                            last = nc.tensor.transpose(bank[0:E, (t % 4) * P:(t % 4 + 1) * P], comb[:, :, t], c.ident[:])
                        last.then_inc(sig("combT"), 1)

                @block.sync
                def _(sp):
                    fetch(sp, 0, 0, sig("raw0"))
                    fetch(sp, 1, 1, sig("raw1"))
                    sp.wait_ge(sig("raw1"), 16 * n_kinds)

                @block.gpsimd
                def _(pool):
                    pool.wait_ge(sig("raw0"), 16 * n_kinds)
                    split(pool, 0, sig("wh0"), sig("split0"))
                    for n in range(NBLK):
                        pool.wait_ge(sig("xh"), n + 1)
                        cols = slice(n * BLK, (n + 1) * BLK)
                        nc.gpsimd.tensor_tensor(xl[:, :, cols], c.xT[:, :, cols], xh[:, :, cols].bitcast(F32), ALU.subtract)

                @block.scalar
                def _(act):
                    for n in range(NBLK):
                        cols = slice(n * BLK, (n + 1) * BLK)
                        nc.scalar.activation(xh[:, :, cols], c.xT[:, :, cols], ACT.Copy).then_inc(sig("xh"), 1)
                    act.wait_ge(sig("centred"), 1)
                    nc.scalar.activation(prob[:], prob[:], ACT.Exp).then_inc(sig("exp"), 1)
                    if biases:
                        act.wait_ge(sig("combT"), 1)
                        for i in range(4):
                            nc.scalar.activation(combT[:, 4 * i:4 * i + 4, :].rearrange("e t p -> e (t p)"),
                                                 c.banks[3 + i][0:E, :], ACT.Copy)

                @block.vector
                def _(dve):
                    ch = Chain(dve, sig("dve_chain"))
                    v = nc.vector
                    dve.wait_ge(sig("logits"), 1)
                    if biases:
                        ch.link(v.tensor_tensor(prob[:], logits, gate_b[:].unsqueeze(1).to_broadcast([P, NT, R]), ALU.add))
                    else:
                        ch.link(v.tensor_copy(prob[:], logits))
                    ch.link(v.tensor_reduce(best[:], prob[:], AX.X, ALU.max))
                    v.tensor_tensor(prob[:], prob[:], bc(best), ALU.subtract).then_inc(sig("centred"), 1)
                    dve.wait_ge(sig("exp"), 1)
                    ch.link(v.tensor_reduce(wsum[:], prob[:], AX.X, ALU.add))
                    ch.link(v.reciprocal(wsum[:], wsum[:]))
                    ch.link(v.tensor_tensor(prob[:], prob[:], bc(wsum), ALU.mult))
                    ch.link(v.memset(assigned[:], 0.0))
                    ch.link(v.memset(dense[:], 0.0))
                    for r in range(top):
                        ch.link(v.tensor_reduce(best[:], prob[:], AX.X, ALU.max))
                        ch.link(v.tensor_tensor(onehot[:], prob[:], bc(best), ALU.is_equal))
                        ch.link(v.tensor_scalar(onehot[:], onehot[:], -64.0, 64.0, ALU.mult, ALU.add))
                        ch.link(v.tensor_tensor(onehot[:], onehot[:], ie(), ALU.add))
                        ch.link(v.tensor_reduce(wsum[:], onehot[:], AX.X, ALU.min))
                        ch.link(v.tensor_tensor(onehot[:], bc(wsum), ie(), ALU.is_equal))
                        ch.link(v.tensor_tensor(assigned[:], assigned[:], onehot[:], ALU.add))
                        ch.link(v.tensor_tensor(tmp[:], onehot[:], bc(best), ALU.mult))
                        ch.link(v.tensor_tensor(dense[:], dense[:], tmp[:], ALU.add))
                        if r + 1 < top:
                            ch.link(v.tensor_scalar(onehot[:], onehot[:], -2.0, None, ALU.mult))
                            ch.link(v.tensor_tensor(prob[:], prob[:], onehot[:], ALU.add))
                    if renorm:
                        ch.link(v.tensor_reduce(wsum[:], dense[:], AX.X, ALU.add))
                        ch.link(v.tensor_scalar_add(wsum[:], wsum[:], 1e-20))
                        ch.link(v.reciprocal(wsum[:], wsum[:]))
                        ch.link(v.tensor_tensor(dense[:], dense[:], bc(wsum), ALU.mult))
                    if capacity:
                        v.tensor_copy(tmp[:], assigned[:]).then_inc(sig("assigned"), 1)
                        dve.wait_ge(sig("counted"), 1)
                        ch.link(v.memset(count[:, 0, :], 0.0))
                        for t in range(1, NT):
                            ch.link(v.tensor_tensor(count[:, t, :], count[:, t - 1, :], totals[:, t - 1, :], ALU.add))
                        ch.link(v.tensor_tensor(count[:], count[:], inside, ALU.add))
                        ch.link(v.tensor_scalar(count[:], count[:], float(capacity), None, ALU.is_lt))
                        ch.link(v.tensor_tensor(dense[:], dense[:], count[:], ALU.mult))
                    if n_shared:
                        ch.link(v.memset(comb[:, R * parts:E, :], 1.0))
                    for part in range(parts):
                        last = v.tensor_copy(comb[:, 0:R * parts, :].rearrange("p (e u) t -> p t e u", u=parts)[:, :, :, part], dense[:])
                    last.then_inc(sig("comb"), 1)
            sig.clear()
            sig.close()
        if biases:
            sig = Signals(nc, tag + "_ob")
            with nc.Block() as block:
                ring = Ring(sig, "bias", c.banks[0:4])

                @block.tensor
                def _(pe):
                    for t in range(NT):
                        ring.fill(nc.tensor.matmul(ring.claim(pe)[:, 0:D], combT[:, t, :], down_b[:], start=True, stop=True))

                @block.vector
                def _(dve):
                    for t in range(NT):
                        bank = ring.take(dve)
                        ring.empty(nc.vector.tensor_tensor(c.x[:, t, :], bank[:, 0:D], c.x[:, t, :], ALU.add))
            sig.clear()
            sig.close()
        sig = Signals(nc, tag + "_ex")
        steps = [(i, n) for i in range(2) for n in range(NBLK)]
        passes = ((0, 0), (0, 1), (1, 0))

        def turn(pair, more):
            with nc.Block() as block:
                up_ring = Ring(sig, "up", c.banks[0:3])
                lin_ring = Ring(sig, "lin", c.banks[3:5])
                out_ring = Ring(sig, "out", c.banks[5:8])

                @block.sync
                def _(sp):
                    if more:
                        fetch(sp, 0, pair * 2 + 2, sig("raw0"))
                        sp.wait_ge(sig("split1"), 1)
                        fetch(sp, 1, pair * 2 + 3, sig("raw1"))
                        sp.wait_ge(sig("raw1"), 16 * n_kinds)

                @block.tensor
                def _(pe):
                    def rise(i, n):
                        if i == 1 and n == 0:
                            pe.wait_ge(sig("split1"), 1)
                        for m in range(M):
                            for kind, ring in enumerate((up_ring, lin_ring) if gated else (up_ring,)):
                                bank = ring.claim(pe)
                                for k in range(KD):
                                    for a, b in passes:
                                        last = nc.tensor.matmul(bank[:], rising((wh, wl)[a][i], kind)[:, k, m * P:(m + 1) * P],
                                                                (xh, xl)[b][:, k, n * BLK:(n + 1) * BLK],
                                                                start=(k == 0 and (a, b) == passes[0]),
                                                                stop=(k == KD - 1 and (a, b) == passes[-1]))
                                ring.fill(last)

                    def fall(s):
                        i, n = steps[s]
                        pe.wait_ge(sig("hl"), M * (s + 1))
                        for half in range(2):
                            bank = out_ring.claim(pe)
                            for j in range(2):
                                tok = (2 * half + j) * P
                                for m in range(M):
                                    for a, b in passes:
                                        last = nc.tensor.matmul(bank[:, j * D:(j + 1) * D], (hh, hl)[a][s % 2][:, m, tok:tok + P],
                                                                falling((wh, wl)[b][i])[:, m, :],
                                                                start=(m == 0 and (a, b) == passes[0]),
                                                                stop=(m == M - 1 and (a, b) == passes[-1]))
                            out_ring.fill(last)

                    for s, (i, n) in enumerate(steps):
                        rise(i, n)
                        if s:
                            fall(s - 1)
                    fall(len(steps) - 1)

                @block.scalar
                def _(act):
                    if biases:
                        act.wait_ge(sig("b2"), 1)
                    for s, (i, n) in enumerate(steps):
                        for m in range(M):
                            q = s * M + m
                            if q >= 2:
                                act.wait_ge(lin_ring.emptied if gated else sig("hl"), q - 1)
                            bank = up_ring.take(act)
                            up_ring.empty(nc.scalar.activation((silu if gated else h)[q % 2][:], bank[:], act_fn,
                                                               bias=b2[:, 0, i, m:m + 1] if biases else 0.0))

                @block.gpsimd
                def _(pool):
                    for s in range(len(steps)):
                        for m in range(M):
                            q = s * M + m
                            pool.wait_ge(sig("hh"), q + 1)
                            nc.gpsimd.tensor_tensor(hl[s % 2][:, m, :], h[q % 2][:], hh[s % 2][:, m, :].bitcast(F32),
                                                    ALU.subtract).then_inc(sig("hl"), 1)
                        if s == 0:
                            split(pool, 1, sig("wh1"), sig("split1"))
                        if s == NBLK + 1 and more:
                            pool.wait_ge(sig("raw0"), 16 * n_kinds)
                            pool.wait_ge(out_ring.filled, 2 * NBLK)
                            split(pool, 0, sig("wh0"), sig("split0"))

                @block.vector
                def _(dve):
                    if biases:
                        nc.vector.tensor_copy(b2[:], b_all[:, :, bass.ts(pair, 2), :]).then_inc(sig("b2"), 1)
                        dve.wait_ge(sig("b2"), 1)
                    nc.vector.tensor_copy(comb2[:], comb[:, bass.ts(pair, 2), :]).then_inc(sig("comb2"), 1)
                    dve.wait_ge(sig("comb2"), 1)

                    def high(s):
                        i, n = steps[s]
                        for m in range(M):
                            q = s * M + m
                            if gated:
                                dve.wait_ge(up_ring.emptied, q + 1)
                                if q >= 2:
                                    dve.wait_ge(sig("hl"), q - 1)
                                bank = lin_ring.take(dve)
                                lin_ring.empty(nc.vector.scalar_tensor_tensor(out=h[q % 2][:], in0=bank[:],
                                                                              scalar=b2[:, 1, i, m:m + 1] if biases else 0.0,
                                                                              in1=silu[q % 2][:], op0=ALU.add, op1=ALU.mult))
                                dve.wait_ge(lin_ring.emptied, q + 1)
                            else:
                                dve.wait_ge(up_ring.emptied, q + 1)
                            if s >= 2 and m == 0:
                                dve.wait_ge(out_ring.filled, 2 * (s - 1))
                            nc.vector.tensor_copy(hh[s % 2][:, m, :], h[q % 2][:]).then_inc(sig("hh"), 1)

                    def add_out(s):
                        i, n = steps[s]
                        for half in range(2):
                            bank = out_ring.take(dve)
                            if s and half == 0:
                                dve.wait_ge(out_ring.emptied, 2 * s)
                            for j in range(2):
                                t = 4 * n + 2 * half + j
                                last = nc.vector.scalar_tensor_tensor(out=c.x[:, t, :], in0=bank[:, j * D:(j + 1) * D],
                                                                      scalar=comb2[:, i, t:t + 1], in1=c.x[:, t, :],
                                                                      op0=ALU.mult, op1=ALU.add)
                            out_ring.empty(last)

                    for s in range(len(steps)):
                        high(s)
                        if s:
                            add_out(s - 1)
                    add_out(len(steps) - 1)
            sig.clear()

        with nc.Fori(0, E // 2 - 1) as pair:
            turn(pair, more=True)
        turn(E // 2 - 1, more=False)
        sig.close()


def layer0_ffn(c):
    mixture(c, "L0f", 8, 2, 2, gated=True, top=2, biases=True)


def layer2_ffn(c):
    mixture(c, "L2f", 8, 0, 4, gated=False, top=1, biases=True, parts=2)


def layer3_ffn(c):
    mixture(c, "L3f", 8, 2, 2, gated=True, top=2, biases=False, renorm=True, capacity=640)

def out_tail(c, sig, ring, C, heads_out, cT, wo, out_bank):
    KC = C // P

    def on_tensor(pe, evacuated):
        for t in range(TB):
            pe.wait_ge(sig("heads_out"), t + 1)
            bank = ring.claim(pe)
            for k in range(KC):
                last = c.nc.tensor.transpose(bank[:, k * P:(k + 1) * P], heads_out[:, t, k * P:(k + 1) * P], c.ident[:])
            ring.fill(last)
        for t in range(TB):
            pe.wait_ge(ring.emptied, evacuated + t + 1)
            for k in range(KC):
                last = c.nc.tensor.matmul(out_bank[:, t * D:(t + 1) * D], cT[:, k, t * P:(t + 1) * P], wo[:, k, :],
                                          start=(k == 0), stop=(k == KC - 1))
        last.then_inc(sig("projected"), 1)

    def on_scalar(act):
        for t in range(TB):
            bank = ring.take(act)
            ring.empty(c.nc.scalar.activation(cT[:, :, t * P:(t + 1) * P],
                                              bank[:, 0:C].rearrange("p (k t) -> p k t", k=KC), ACT.Copy))

    return on_tensor, on_scalar


def plain_attention(c, tag, H, rows, MQ, KT, DV, kind, scale):
    nc, w = c.nc, c.dram
    NK, C = KT * P, H * DV
    plain = kind == "plain"
    per_tile = MQ * P // max(rows, 1)
    step = P * MQ // H if not plain else P
    with ExitStack() as stack:
        sb = c.tiles(stack, tag)
        xb = [sb(f"xb{i}", [P, KD, T]) for i in range(2)]
        cb = [sb(f"cb{i}", [P, KD, T]) for i in range(2)]
        qT = None if plain else [sb(f"qT{i}", [P, MQ, T]) for i in range(2)]
        kT = None if plain else [sb(f"kT{i}", [P, MQ, NK]) for i in range(2)]
        v = [sb(f"v{i}", [P, KT, C]) for i in range(2)]
        s_sb = [sb(f"s{i}", [P, NK]) for i in range(3)]
        p_sb = [sb(f"p{i}", [P, NK]) for i in range(3)]
        pT = [sb(f"pT{i}", [P, NK]) for i in range(3)]
        nmax = [sb(f"nmax{i}", [P, TB * H]) for i in range(2)]
        rsum = [sb(f"rsum{i}", [P, TB, H]) for i in range(2)]
        heads_out = sb("heads_out", [P, TB, C])
        bias = [sb(f"bias{i}", [P, TB if kind == "pairs" else 1, NK]) for i in range(2)]
        pairs = []
        if not plain:
            wq, wk = sb("wq", [P, KD, MQ * P]), sb("wk", [P, KD, MQ * P])
            wv, wo = sb("wv", [P, KD, C]), sb("wo", [P, C // P, D])
            cT = sb("cT", [P, C // P, T])
            bo = sb("bo", [P, D])
            y = sb("y", [P, TB, D])
            pairs += [(wq[:], w[f"{tag}_wq"]), (wk[:], w[f"{tag}_wk"]), (wv[:], w[f"{tag}_wv"]), (wo[:], w[f"{tag}_wo"])]
            if kind != "latent":
                pairs += [(bo[:], w[f"{tag}_bo"].rearrange("(a n) -> a n", a=1).to_broadcast([P, D]))]
        if kind == "pairs":
            mask = [sb(f"mask{i}", [P, TB, NK], I32) for i in range(2)]
        if kind == "plain":
            mask = [sb(f"mask{i}", [P, 1, NK], I32) for i in range(2)]
        if kind == "latent":
            mask = [sb(f"mask{i}", [P, 1, T], U8) for i in range(2)]
            og, ob = sb("og", [P, D]), sb("ob", [P, D])
            stats, mv, rstd = sb("stats", [P, TB, 6]), sb("mv", [P, TB, 2]), sb("rstd", [P, TB, 3])
            pairs += [(og[:], w[f"{tag}_og"].rearrange("(a n) -> a n", a=1).to_broadcast([P, D])),
                      (ob[:], w[f"{tag}_ob"].rearrange("(a n) -> a n", a=1).to_broadcast([P, D]))]
        if kind == "decay":
            rhat = sb("rhat", [P, H, 3 * P])
            dist = sb("dist", [P, 3 * P])
            future = sb("future", [P, P])
            wh, vh, ev = sb("wh", [P, H]), sb("vh", [P, H]), sb("ev", [P, H])
            pairs += [(dist[:], w["distance"]), (future[:], w["future_neg"]),
                      (wh[:], w[f"{tag}_w"].rearrange("(a n) -> a n", a=1).to_broadcast([P, H])),
                      (vh[:], w[f"{tag}_v"].rearrange("(a n) -> a n", a=1).to_broadcast([P, H]))]
        if pairs:
            c.load(tag + "_ld", pairs)
        if kind == "decay":
            sig = Signals(nc, tag + "_rh")
            with nc.Block() as block:
                @block.vector
                def _(dve):
                    for h in range(H):
                        last = nc.vector.tensor_scalar(rhat[:, h, :], dist[:], wh[:, h:h + 1], -1.0, ALU.mult, ALU.mult)
                    last.then_inc(sig("minus_wr"), 1)
                    dve.wait_ge(sig("exped"), H + 1)
                    ch = Chain(dve, sig("dve_chain"))
                    ch.link(nc.vector.tensor_scalar(rhat[:], rhat[:], 1.0, None, ALU.add))
                    ch.link(nc.vector.reciprocal(rhat[:], rhat[:]))
                    ch.link(nc.vector.tensor_scalar(ev[:], ev[:], 1.0, scale, ALU.add, ALU.mult))
                    for h in range(H):
                        last = nc.vector.tensor_scalar(rhat[:, h, :], rhat[:, h, :], ev[:, h:h + 1], None, ALU.mult)

                @block.scalar
                def _(act):
                    nc.scalar.activation(ev[:], vh[:], ACT.Exp).then_inc(sig("exped"), 1)
                    act.wait_ge(sig("minus_wr"), 1)
                    for h in range(H):
                        nc.scalar.activation(rhat[:, h, :], rhat[:, h, :], ACT.Exp,
                                             bias=vh[:, h:h + 1]).then_inc(sig("exped"), 1)
            sig.clear()
            sig.close()

        sig = Signals(nc, tag)
        with nc.Fori(0, B // ROWS) as turn:
            with nc.Block() as block:
                s_ring = Ring(sig, "s", c.banks[0:3])
                t_ring = Ring(sig, "t", c.banks[3:5])
                acc = c.banks[5:7]
                out_bank = c.banks[7]
                items = [(t, h) for t in range(TB) for h in range(H)]
                n = len(items)
                causal = kind == "decay"
                keys = lambda t: (t + 1) * P if causal else NK
                row_of = lambda r: turn * ROWS + r
                q_banks = 0 if plain else MQ // 2
                k_banks = 0 if plain else MQ * (NK // T) // 2
                v_banks = 0 if plain else KT
                KC = C // P

                stages = []
                for r in range(ROWS):
                    stages += [("project", r)] if r == 0 else []
                    stages += [("attend", r)] + ([("project", r + 1)] if r + 1 < ROWS else []) + [("output", r)]

                def counts(project, attend, output):
                    before, at = 0, {}
                    for stage in stages:
                        at[stage] = before
                        before += {"project": project, "attend": attend, "output": output}[stage[0]]
                    return at

                t_at = counts(q_banks + v_banks, n, 0 if plain else TB)
                s_at = counts(k_banks, n, 0)

                def source(i, r):
                    x_, c_ = xb[r % 2], cb[r % 2]
                    return (c_, i) if kind == "pairs" else (x_, i) if kind == "decay" else ((c_, i) if i < TB else (x_, i - TB))

                def parts(h):
                    if plain:
                        return [(k, slice(0, P)) for k in range(KD)]
                    p0 = h * step
                    return [(p0 // P, slice(p0 % P, p0 % P + rows))]

                @block.sync
                def _(sp):
                    for r in range(ROWS if kind != "decay" else 0):
                        if r >= 2:
                            sp.wait_ge(sig("bias"), r - 1)
                        if kind == "pairs":
                            sp.dma_start(mask[r % 2][:], w["mask_pairs"][row_of(r)]).then_inc(sig(f"mask{r % 2}"), 16)
                        if kind == "plain":
                            sp.dma_start(mask[r % 2][:, 0, :], w["mask_keys"][row_of(r)].to_broadcast([P, NK])).then_inc(sig(f"mask{r % 2}"), 16)
                        if kind == "latent":
                            sp.dma_start(mask[r % 2][:, 0, :], w["mask_bool"][row_of(r)].to_broadcast([P, T])).then_inc(sig(f"mask{r % 2}"), 16)

                @block.tensor
                def _(pe):
                    def project(r):
                        pe.wait_ge(sig("sliced_x"), r + 1)
                        pe.wait_ge(sig("sliced_c"), r + 1)
                        if plain:
                            return
                        for i in range(0, MQ, 2):
                            bank = t_ring.claim(pe)
                            for m in range(i, i + 2):
                                for k in range(KD):
                                    last = nc.tensor.matmul(bank[:, (m - i) * T:(m - i + 1) * T], wq[:, k, m * P:(m + 1) * P],
                                                            xb[r % 2][:, k, :], start=(k == 0), stop=(k == KD - 1))
                            t_ring.fill(last)
                        for i in range(0, MQ * (NK // T), 2):
                            bank = s_ring.claim(pe)
                            for j in (i, i + 1):
                                m, part = j % MQ, j // MQ
                                src = source(part * TB, r)[0]
                                for k in range(KD):
                                    last = nc.tensor.matmul(bank[:, (j - i) * T:(j - i + 1) * T], wk[:, k, m * P:(m + 1) * P],
                                                            src[:, k, :], start=(k == 0), stop=(k == KD - 1))
                            s_ring.fill(last)
                        for i in range(KT):
                            bank = t_ring.claim(pe)
                            src, j = source(i, r)
                            for k in range(KD):
                                last = nc.tensor.matmul(bank[:, 0:C], src[:, k, j * P:(j + 1) * P], wv[:, k, :],
                                                        start=(k == 0), stop=(k == KD - 1))
                            t_ring.fill(last)

                    def attend(r):
                        qT_, kT_, v_ = (xb[r % 2], cb[r % 2], v[r % 2]) if plain else (qT[r % 2], kT[r % 2], v[r % 2])
                        if plain:
                            pe.wait_ge(sig("sliced_v"), r + 1)
                        else:
                            pe.wait_ge(t_ring.emptied, t_at["project", r] + q_banks)
                            pe.wait_ge(s_ring.emptied, s_at["project", r] + k_banks)
                        for i in range(n + 3):
                            if i < n:
                                t, h = items[i]
                                bank = s_ring.claim(pe)
                                pp = parts(h)
                                for j, (m, ps) in enumerate(pp):
                                    last = nc.tensor.matmul(bank[:, 0:keys(t)], qT_[ps, m, t * P:(t + 1) * P], kT_[ps, m, 0:keys(t)],
                                                            start=(j == 0), stop=(j == len(pp) - 1))
                                s_ring.fill(last)
                            if 2 <= i < n + 2:
                                j = i - 2
                                bank = t_ring.claim(pe)
                                pe.wait_ge(sig("exp"), r * n + j + 1)
                                p_ = p_sb[(r * n + j) % 3]
                                for kt in range(keys(items[j][0]) // P):
                                    last = nc.tensor.transpose(bank[:, kt * P:(kt + 1) * P], p_[:, kt * P:(kt + 1) * P], c.ident[:])
                                t_ring.fill(last)
                            if i >= 3:
                                j = i - 3
                                t, h = items[j]
                                if h == 0 and r:
                                    pe.wait_ge(sig("heads_out"), TB * (r - 1) + t + 1)
                                pe.wait_ge(t_ring.emptied, t_at["attend", r] + j + 1)
                                nkt = keys(t) // P
                                for kt in range(nkt):
                                    last = nc.tensor.matmul(acc[t][:, h * DV:(h + 1) * DV], pT[(r * n + j) % 3][:, kt * P:(kt + 1) * P],
                                                            v_[:, kt, h * DV:(h + 1) * DV], start=(kt == 0), stop=(kt == nkt - 1))
                                last.then_inc(sig("weighted"), 1)

                    def output(r):
                        if plain:
                            return
                        for t in range(TB):
                            pe.wait_ge(sig("heads_out"), TB * r + t + 1)
                            bank = t_ring.claim(pe)
                            for k in range(KC):
                                last = nc.tensor.transpose(bank[:, k * P:(k + 1) * P], heads_out[:, t, k * P:(k + 1) * P], c.ident[:])
                            t_ring.fill(last)
                        if r:
                            pe.wait_ge(sig("out_read"), r)
                        for t in range(TB):
                            pe.wait_ge(t_ring.emptied, t_at["output", r] + t + 1)
                            for k in range(KC):
                                last = nc.tensor.matmul(out_bank[:, t * D:(t + 1) * D], cT[:, k, t * P:(t + 1) * P], wo[:, k, :],
                                                        start=(k == 0), stop=(k == KC - 1))
                        last.then_inc(sig("projected"), 1)

                    for stage, r in stages:
                        {"project": project, "attend": attend, "output": output}[stage](r)

                @block.scalar
                def _(act):
                    def project(r):
                        nc.scalar.activation(xb[r % 2][:], c.xT[:, :, bass.ts(row_of(r), T)], ACT.Copy).then_inc(sig("sliced_x"), 1)
                        if plain:
                            nc.scalar.activation(v[r % 2][:], c.ctx[:, bass.ts(row_of(r), TB), :], ACT.Copy).then_inc(sig("sliced_v"), 1)
                            return
                        for i in range(0, MQ, 2):
                            bank = t_ring.take(act)
                            t_ring.empty(nc.scalar.activation(qT[r % 2][:, i:i + 2, :], bank[:].rearrange("p (m t) -> p m t", m=2), ACT.Copy))
                        for i in range(KT):
                            bank = t_ring.take(act)
                            t_ring.empty(nc.scalar.activation(v[r % 2][:, i, :], bank[:, 0:C], ACT.Copy))

                    def attend(r):
                        for i in range(n + 1):
                            if i < n:
                                t, h = items[i]
                                nk, g = keys(t), r * n + i
                                act.wait_ge(s_ring.emptied, s_at["attend", r] + i + 1)
                                nc.scalar.activation(p_sb[g % 3][:, 0:nk], s_sb[g % 3][:, 0:nk], ACT.Exp, bias=nmax[r % 2][:, i:i + 1],
                                                     accum_out=rsum[r % 2][:, t, h:h + 1]).then_inc(sig("exp"), 1)
                            if i >= 1:
                                j = i - 1
                                nk, g = keys(items[j][0]), r * n + j
                                if g >= 3:
                                    act.wait_ge(sig("weighted"), g - 2)
                                bank = t_ring.take(act)
                                t_ring.empty(nc.scalar.activation(pT[g % 3][:, 0:nk], bank[:, 0:nk], ACT.Copy))

                    def output(r):
                        if plain:
                            return
                        for t in range(TB):
                            bank = t_ring.take(act)
                            t_ring.empty(nc.scalar.activation(cT[:, :, t * P:(t + 1) * P],
                                                              bank[:, 0:C].rearrange("p (k t) -> p k t", k=KC), ACT.Copy))
                        if kind == "latent":
                            act.wait_ge(sig("var_eps"), r + 1)
                            nc.scalar.activation(rstd[:, :, 1], rstd[:, :, 0], ACT.Sqrt).then_inc(sig("std"), 1)

                    for stage, r in stages:
                        {"project": project, "attend": attend, "output": output}[stage](r)

                @block.vector
                def _(dve):
                    ch = Chain(dve, sig("dve_chain"))
                    vec = nc.vector

                    def project(r):
                        src = c.ctxn if kind == "latent" else c.ctxT
                        vec.tensor_copy(cb[r % 2][:], src[:, :, bass.ts(row_of(r), T)]).then_inc(sig("sliced_c"), 1)
                        if kind != "decay":
                            dve.wait_ge(sig(f"mask{r % 2}"), 16 * (r // 2 + 1))
                        b_, m_ = bias[r % 2], mask[r % 2] if kind != "decay" else None
                        if kind == "pairs":
                            ch.link(vec.tensor_scalar(b_[:], m_[:], 0.0, -1.0, ALU.not_equal, ALU.add))
                            vec.tensor_scalar(b_[:], b_[:], 1e20 * scale, None, ALU.mult).then_inc(sig("bias"), 1)
                            dve.wait_ge(sig("bias"), r + 1)
                        if kind == "plain":
                            vec.tensor_scalar(b_[:], m_[:], -1e9, None, ALU.mult).then_inc(sig("bias"), 1)
                            dve.wait_ge(sig("bias"), r + 1)
                        if kind == "latent":
                            vec.memset(b_[:, :, T:NK], 0.0)
                            ch.link(vec.tensor_scalar(b_[:, :, 0:T], m_[:], 0.0, -1.0, ALU.not_equal, ALU.add))
                            vec.tensor_scalar(b_[:, :, 0:T], b_[:, :, 0:T], 3e38, None, ALU.mult).then_inc(sig("bias"), 1)
                            dve.wait_ge(sig("bias"), r + 1)
                        if not plain:
                            for i in range(0, MQ * (NK // T), 2):
                                bank = s_ring.take(dve)
                                m, part = i % MQ, i // MQ
                                s_ring.empty(vec.tensor_copy(kT[r % 2][:, m:m + 2, part * T:(part + 1) * T],
                                                             bank[:].rearrange("p (m t) -> p m t", m=2)))

                    def attend(r):
                        for i, (t, h) in enumerate(items):
                            bank = s_ring.take(dve)
                            nk, g = keys(t), r * n + i
                            s = s_sb[g % 3]
                            if g >= 3:
                                dve.wait_ge(sig("exp"), g - 2)
                            if kind == "decay":
                                f = rhat[:, h, 0:P] if t == 0 else rhat[:, h, P:3 * P]
                                ch.link(vec.scalar_tensor_tensor(out=s[:, 0:nk], in0=bank[:, 0:nk], scalar=0.0, in1=f,
                                                                 op0=ALU.max, op1=ALU.mult))
                                ch.link(vec.tensor_tensor(s[:, nk - P:nk], s[:, nk - P:nk], future[:], ALU.add))
                            else:
                                ch.link(vec.scalar_tensor_tensor(out=s[:], in0=bank[:, 0:NK], scalar=scale,
                                                                 in1=bias[r % 2][:, t if kind == "pairs" else 0, :], op0=ALU.mult, op1=ALU.add))
                            s_ring.empty(vec.tensor_reduce(nmax[r % 2][:, i:i + 1], s[:, 0:nk], AX.X, ALU.max, negate=True))

                    def output(r):
                        rs = rsum[r % 2]
                        if plain and r:
                            dve.wait_ge(sig("added"), r)
                        for t in range(TB):
                            dve.wait_ge(sig("weighted"), r * n + H * (t + 1))
                            ch.link(vec.reciprocal(rs[:, t, :], rs[:, t, :]))
                            vec.tensor_tensor(heads_out[:, t, :].rearrange("p (h d) -> p h d", h=H),
                                              acc[t][:, 0:C].rearrange("p (h d) -> p h d", h=H),
                                              rs[:, t, :].unsqueeze(2).to_broadcast([P, H, DV]), ALU.mult).then_inc(sig("heads_out"), 1)
                        xr = c.x[:, bass.ts(row_of(r), TB), :]
                        if plain:
                            dve.wait_ge(sig("heads_out"), TB * (r + 1))
                            vec.tensor_tensor(xr, xr, heads_out[:], ALU.add).then_inc(sig("added"), 1)
                            return
                        dve.wait_ge(sig("projected"), r + 1)
                        if r:
                            dve.wait_ge(sig("added"), r)
                        proj = out_bank[:].rearrange("p (t d) -> p t d", t=TB)
                        rowwise = lambda a: a[:].unsqueeze(1).to_broadcast([P, TB, D])
                        if kind == "latent":
                            for t in range(TB):
                                last = vec.bn_stats(stats[:, t, :], proj[:, t, :])
                            ch.link(last)
                            for t in range(TB):
                                last = vec.bn_aggr(mv[:, t, :], stats[:, t, :])
                            ch.link(last)
                            vec.tensor_scalar_add(rstd[:, :, 0], mv[:, :, 1], 1e-5).then_inc(sig("var_eps"), 1)
                            dve.wait_ge(sig("std"), r + 1)
                            ch.link(vec.reciprocal(rstd[:, :, 2], rstd[:, :, 1]))
                            for t in range(TB):
                                last = vec.tensor_scalar(y[:, t, :], proj[:, t, :], mv[:, t, 0:1], rstd[:, t, 2:3], ALU.subtract, ALU.mult)
                            last.then_inc(sig("out_read"), 1)
                            dve.wait_ge(sig("out_read"), r + 1)
                            ch.link(vec.tensor_tensor(y[:], y[:], rowwise(og), ALU.mult))
                            ch.link(vec.tensor_tensor(y[:], y[:], rowwise(ob), ALU.add))
                        else:
                            vec.tensor_tensor(y[:], proj, rowwise(bo), ALU.add).then_inc(sig("out_read"), 1)
                            dve.wait_ge(sig("out_read"), r + 1)
                        vec.tensor_tensor(xr, xr, y[:], ALU.add).then_inc(sig("added"), 1)

                    for stage, r in stages:
                        {"project": project, "attend": attend, "output": output}[stage](r)
            sig.clear()
        sig.close()


def softmax_attention(c, tag, H, rows, MQ, KT, DV, kind, scale, norm=None):
    nc, w = c.nc, c.dram
    NK, C = KT * P, H * DV
    causal = kind == "decay"
    twins = 2 if rows == 16 else 1
    DS = DV * twins
    HT = P // DS
    KC = C // P
    if causal:
        items = [(h, [(0, 0, P), (1, P, 2 * P)]) for h in range(H)]
    elif NK == T:
        items = [(h, [(0, 0, NK), (1, NK, NK)]) for h in range(H)]
    else:
        items = [(h, [(t, 0, NK)]) for h in range(H) for t in range(TB)]
    n, S = len(items), len(items[0][1])
    W = sum(nk for _, _, nk in items[0][1])
    LAG = 4 + twins
    BEHIND = LAG - 2 - causal
    with ExitStack() as stack:
        sb = c.tiles(stack, tag)
        xb = [sb(f"xb{i}", [P, KD, T]) for i in range(2)]
        cb = [sb(f"cb{i}", [P, KD, T]) for i in range(2)]
        qT = [sb(f"qT{i}", [P, MQ, T]) for i in range(2)]
        kT = [sb(f"kT{i}", [P, twins * MQ, NK]) for i in range(2)]
        v = [sb(f"v{i}", [P, KT, twins * C]) for i in range(2)]
        s_sb = [sb(f"s{i}", [P, W]) for i in range(4)]
        p_sb = [sb(f"p{i}", [P, W]) for i in range(LAG)]
        pT = [sb(f"pT{i}", [P, W]) for i in range(3)]
        nmax = [sb(f"nmax{i}", [P, n, S]) for i in range(2)]
        rsum = [sb(f"rsum{i}", [P, n, S]) for i in range(2)]
        bias = [sb(f"bias{i}", [P, TB if kind == "pairs" else 1, NK]) for i in range(2)]
        pairs = []
        wq, wk = sb("wq", [P, KD, MQ * P]), sb("wk", [P, KD, MQ * P])
        wv, wo = sb("wv", [P, KD, C]), sb("wo", [P, KC, D])
        cT = sb("cT", [P, KC, T])
        bo = sb("bo", [P, D])
        y = sb("y", [P, TB, D])
        pairs += [(wq[:], w[f"{tag}_wq"]), (wk[:], w[f"{tag}_wk"]), (wv[:], w[f"{tag}_wv"]), (wo[:], w[f"{tag}_wo"])]
        if twins == 2:
            twin = sb("twin", [P, 2])
            pairs += [(twin[:], w["twin"])]
        if kind != "latent":
            pairs += [(bo[:], w[f"{tag}_bo"].rearrange("(a n) -> a n", a=1).to_broadcast([P, D]))]
        if kind == "pairs":
            mask = [sb(f"mask{i}", [P, TB, NK], I32) for i in range(2)]
        if kind == "latent":
            mask = [sb(f"mask{i}", [P, 1, T], U8) for i in range(2)]
            og, ob = sb("og", [P, D]), sb("ob", [P, D])
            stats, mv, rstd = sb("stats", [P, TB, 6]), sb("mv", [P, TB, 2]), sb("rstd", [P, TB, 3])
            pairs += [(og[:], w[f"{tag}_og"].rearrange("(a n) -> a n", a=1).to_broadcast([P, D])),
                      (ob[:], w[f"{tag}_ob"].rearrange("(a n) -> a n", a=1).to_broadcast([P, D]))]
        if kind == "decay":
            rhat = sb("rhat", [P, H, 3 * P])
            dist = sb("dist", [P, 3 * P])
            future = sb("future", [P, P])
            wh, vh, ev = sb("wh", [P, H]), sb("vh", [P, H]), sb("ev", [P, H])
            pairs += [(dist[:], w["distance"]), (future[:], w["future_neg"]),
                      (wh[:], w[f"{tag}_w"].rearrange("(a n) -> a n", a=1).to_broadcast([P, H])),
                      (vh[:], w[f"{tag}_v"].rearrange("(a n) -> a n", a=1).to_broadcast([P, H]))]
        normalise(c, tag + "_n", loads=pairs, **(norm or dict(src=c.x, dstT=c.xT)))
        if kind == "decay":
            sig = Signals(nc, tag + "_rh")
            with nc.Block() as block:
                @block.vector
                def _(dve):
                    ch = Chain(dve, sig("dve_chain"))
                    for h in range(H):
                        nc.vector.tensor_scalar(rhat[:, h, P:], dist[:, P:], wh[:, h:h + 1], -1.0, ALU.mult, ALU.mult).then_inc(sig("minus_wr"), 1)
                    dve.wait_ge(sig("exped"), 1)
                    nc.vector.tensor_scalar(ev[:], ev[:], 1.0, scale, ALU.add, ALU.mult).then_inc(sig("numerator"), 1)
                    for h in range(H):
                        dve.wait_ge(sig("exped"), h + 2)
                        ch.link(nc.vector.tensor_scalar(rhat[:, h, P:], rhat[:, h, P:], 1.0, None, ALU.add))
                        nc.vector.reciprocal(rhat[:, h, P:], rhat[:, h, P:]).then_inc(sig("inverse"), 1)

                @block.scalar
                def _(act):
                    nc.scalar.activation(ev[:], vh[:], ACT.Exp).then_inc(sig("exped"), 1)
                    for h in range(H):
                        act.wait_ge(sig("minus_wr"), h + 1)
                        nc.scalar.activation(rhat[:, h, P:], rhat[:, h, P:], ACT.Exp, bias=vh[:, h:h + 1]).then_inc(sig("exped"), 1)

                @block.gpsimd
                def _(pool):
                    pool.wait_ge(sig("numerator"), 1)
                    for h in range(H):
                        pool.wait_ge(sig("inverse"), h + 1)
                        by = lambda k: ev[:, h:h + 1].to_broadcast([P, k])
                        nc.gpsimd.tensor_tensor(rhat[:, h, 0:P], rhat[:, h, 2 * P:], by(P), ALU.mult).then_inc(sig("first_tile"), 1)
                        pool.wait_ge(sig("first_tile"), h + 1)
                        nc.gpsimd.tensor_tensor(rhat[:, h, P:], rhat[:, h, P:], by(2 * P), ALU.mult)
            sig.clear()
            sig.close()
        if twins == 2:
            sig = Signals(nc, tag + "_z")
            with nc.Block() as block:
                @block.gpsimd
                def _(pool):
                    for v_ in v:
                        nc.gpsimd.memset(v_[:], 0.0)
            sig.clear()
            sig.close()

        sig = Signals(nc, tag)
        with nc.Fori(0, B // ROWS) as turn:
            with nc.Block() as block:
                s_ring = Ring(sig, "s", c.banks[0:3])
                t_ring = Ring(sig, "t", c.banks[3:5])
                acc = c.banks[5:7]
                out_bank = c.banks[7]
                row_of = lambda r: turn * ROWS + r
                q_banks = MQ // 2
                k_banks = MQ * (NK // T) // 2
                v_banks = KT

                stages = []
                for r in range(ROWS):
                    stages += [("project", r)] if r == 0 else []
                    stages += [("attend", r)] + ([("project", r + 1)] if r + 1 < ROWS else []) + [("output", r)]

                def counts(project, attend, output):
                    before, at = 0, {}
                    for stage in stages:
                        at[stage] = before
                        before += {"project": project, "attend": attend, "output": output}[stage[0]]
                    return at

                t_at = counts(q_banks + v_banks, n, 0)
                s_at = counts(k_banks, n, 0)

                def source(i, r):
                    x_, c_ = xb[r % 2], cb[r % 2]
                    return (c_, i) if kind == "pairs" else (x_, i) if kind == "decay" else ((c_, i) if i < TB else (x_, i - TB))

                def parts(h):
                    p0 = h // twins * twins * rows
                    return p0 // P, h % twins * MQ + p0 // P, slice(p0 % P, p0 % P + twins * rows)

                @block.sync
                def _(sp):
                    for r in range(ROWS if kind != "decay" else 0):
                        if r >= 2:
                            sp.wait_ge(sig("bias"), r - 1)
                        if kind == "pairs":
                            sp.dma_start(mask[r % 2][:], w["mask_pairs"][row_of(r)]).then_inc(sig(f"mask{r % 2}"), 16)
                        if kind == "latent":
                            sp.dma_start(mask[r % 2][:, 0, :], w["mask_bool"][row_of(r)].to_broadcast([P, T])).then_inc(sig(f"mask{r % 2}"), 16)

                @block.tensor
                def _(pe):
                    def project(r):
                        pe.wait_ge(sig("sliced_x"), r + 1)
                        pe.wait_ge(sig("sliced_c"), r + 1)
                        for i in range(0, MQ, 2):
                            bank = t_ring.claim(pe)
                            for m in range(i, i + 2):
                                for k in range(KD):
                                    last = nc.tensor.matmul(bank[:, (m - i) * T:(m - i + 1) * T], wq[:, k, m * P:(m + 1) * P],
                                                            xb[r % 2][:, k, :], start=(k == 0), stop=(k == KD - 1))
                            t_ring.fill(last)
                        for i in range(0, MQ * (NK // T), 2):
                            bank = s_ring.claim(pe)
                            for j in (i, i + 1):
                                m, part = j % MQ, j // MQ
                                src = source(part * TB, r)[0]
                                for k in range(KD):
                                    last = nc.tensor.matmul(bank[:, (j - i) * T:(j - i + 1) * T], wk[:, k, m * P:(m + 1) * P],
                                                            src[:, k, :], start=(k == 0), stop=(k == KD - 1))
                            s_ring.fill(last)
                        for i in range(KT):
                            bank = t_ring.claim(pe)
                            src, j = source(i, r)
                            for k in range(KD):
                                last = nc.tensor.matmul(bank[:, 0:C], src[:, k, j * P:(j + 1) * P], wv[:, k, :],
                                                        start=(k == 0), stop=(k == KD - 1))
                            t_ring.fill(last)

                    def attend(r):
                        qT_, kT_, v_ = qT[r % 2], kT[r % 2], v[r % 2]
                        pe.wait_ge(t_ring.emptied, t_at["project", r] + q_banks)
                        pe.wait_ge(s_ring.emptied, s_at["project", r] + k_banks)
                        for i in range(n + LAG + 1):
                            if i < n:
                                h, segs = items[i]
                                m, mk, ps = parts(h)
                                bank = s_ring.claim(pe)
                                for t, at, nk in segs:
                                    last = nc.tensor.matmul(bank[:, at:at + nk], qT_[ps, m, t * P:(t + 1) * P], kT_[ps, mk, 0:nk],
                                                            start=True, stop=True)
                                s_ring.fill(last)
                            if LAG <= i < n + LAG:
                                j = i - LAG
                                bank = t_ring.claim(pe)
                                pe.wait_ge(sig("divided"), r * n + j + 1)
                                for b in range(W // P):
                                    last = nc.tensor.transpose(bank[:, b * P:(b + 1) * P], p_sb[(r * n + j) % LAG][:, b * P:(b + 1) * P], c.ident[:])
                                t_ring.fill(last)
                            if i > LAG:
                                j = i - LAG - 1
                                h, segs = items[j]
                                if j == 0 and r:
                                    pe.wait_ge(sig("cT"), TB * r)
                                pe.wait_ge(t_ring.emptied, t_at["attend", r] + j + 1)
                                e, u = h % twins, h // twins
                                rows_out, tile = slice(u % HT * DS, (u % HT + 1) * DS), u // HT
                                for t, at, nk in segs:
                                    for kt in range(nk // P):
                                        last = nc.tensor.matmul(acc[t][rows_out, tile * P:(tile + 1) * P], v_[:, kt, e * C + u * DS:e * C + (u + 1) * DS],
                                                                pT[(r * n + j) % 3][:, at + kt * P:at + (kt + 1) * P],
                                                                start=(e == 0 and kt == 0), stop=(e == twins - 1 and kt == nk // P - 1))
                                last.then_inc(sig("weighted"), 1)

                    def output(r):
                        if r:
                            pe.wait_ge(sig("out_read"), r)
                        pe.wait_ge(sig("cT"), TB * (r + 1))
                        for t in range(TB):
                            for k in range(KC):
                                last = nc.tensor.matmul(out_bank[:, t * D:(t + 1) * D], cT[:, k, t * P:(t + 1) * P], wo[:, k, :],
                                                        start=(k == 0), stop=(k == KC - 1))
                        last.then_inc(sig("projected"), 1)

                    for stage, r in stages:
                        {"project": project, "attend": attend, "output": output}[stage](r)

                @block.scalar
                def _(act):
                    def project(r):
                        nc.scalar.activation(xb[r % 2][:], c.xT[:, :, bass.ts(row_of(r), T)], ACT.Copy).then_inc(sig("sliced_x"), 1)
                        for i in range(0, MQ, 2):
                            bank = t_ring.take(act)
                            t_ring.empty(nc.scalar.activation(qT[r % 2][:, i:i + 2, :], bank[:].rearrange("p (m t) -> p m t", m=2), ACT.Copy))
                        for i in range(KT):
                            bank = t_ring.take(act)
                            for e in range(twins):
                                own = lambda a: a.rearrange("p (u e d) -> p u e d", e=twins, d=DV)[:, :, e, :]
                                last = nc.scalar.activation(own(v[r % 2][:, i, e * C:(e + 1) * C]), own(bank[:, 0:C]), ACT.Copy)
                            t_ring.empty(last)

                    def attend(r):
                        for i in range(n + BEHIND):
                            if i < n:
                                g = r * n + i
                                act.wait_ge(sig("max"), g + 1)
                                for e, (t, at, nk) in enumerate(items[i][1]):
                                    nc.scalar.activation(p_sb[g % LAG][:, at:at + nk], s_sb[g % 4][:, at:at + nk], ACT.Exp,
                                                         bias=nmax[r % 2][:, i, e:e + 1],
                                                         accum_out=rsum[r % 2][:, i, e:e + 1]).then_inc(sig("exp"), 1)
                            if i >= BEHIND:
                                g = r * n + i - BEHIND
                                if g >= 3:
                                    act.wait_ge(sig("weighted"), g - 2)
                                bank = t_ring.take(act)
                                t_ring.empty(nc.scalar.activation(pT[g % 3][:], bank[:, 0:W], ACT.Copy))

                    def output(r):
                        act.wait_ge(sig("weighted"), (r + 1) * n)
                        if r:
                            act.wait_ge(sig("projected"), r)
                        for t in range(TB):
                            nc.scalar.activation(cT[:, :, t * P:(t + 1) * P], acc[t][:, 0:C].rearrange("p (k t) -> p k t", k=KC),
                                                 ACT.Copy).then_inc(sig("cT"), 1)
                        if kind == "latent":
                            act.wait_ge(sig("var_eps"), r + 1)
                            nc.scalar.activation(rstd[:, :, 1], rstd[:, :, 0], ACT.Sqrt).then_inc(sig("std"), 1)

                    for stage, r in stages:
                        {"project": project, "attend": attend, "output": output}[stage](r)

                @block.gpsimd
                def _(pool):
                    for r in range(ROWS):
                        for i, (h, segs) in enumerate(items):
                            g = r * n + i
                            pool.wait_ge(sig("reciprocal"), g + 1)
                            if len({nk for _, _, nk in segs}) == 1:
                                both = p_sb[g % LAG][:].rearrange("p (e s) -> p e s", e=S)
                                last = nc.gpsimd.tensor_tensor(both, both, rsum[r % 2][:, i, :].unsqueeze(2).to_broadcast([P, S, NK]), ALU.mult)
                            else:
                                for e, (t, at, nk) in enumerate(segs):
                                    one = p_sb[g % LAG][:, at:at + nk]
                                    last = nc.gpsimd.tensor_tensor(one, one, rsum[r % 2][:, i, e:e + 1].to_broadcast([P, nk]), ALU.mult)
                            last.then_inc(sig("divided"), 1)

                @block.vector
                def _(dve):
                    ch = Chain(dve, sig("dve_chain"))
                    vec = nc.vector

                    def project(r):
                        src = c.ctxn if kind == "latent" else c.ctxT
                        vec.tensor_copy(cb[r % 2][:], src[:, :, bass.ts(row_of(r), T)]).then_inc(sig("sliced_c"), 1)
                        if kind != "decay":
                            dve.wait_ge(sig(f"mask{r % 2}"), 16 * (r // 2 + 1))
                        b_, m_ = bias[r % 2], mask[r % 2] if kind != "decay" else None
                        if kind == "pairs":
                            ch.link(vec.tensor_scalar(b_[:], m_[:], 0.0, -1.0, ALU.not_equal, ALU.add))
                            vec.tensor_scalar(b_[:], b_[:], 1e20 * scale, None, ALU.mult).then_inc(sig("bias"), 1)
                            dve.wait_ge(sig("bias"), r + 1)
                        if kind == "latent":
                            vec.memset(b_[:, :, T:NK], 0.0)
                            ch.link(vec.tensor_scalar(b_[:, :, 0:T], m_[:], 0.0, -1.0, ALU.not_equal, ALU.add))
                            vec.tensor_scalar(b_[:, :, 0:T], b_[:, :, 0:T], 3e38, None, ALU.mult).then_inc(sig("bias"), 1)
                            dve.wait_ge(sig("bias"), r + 1)
                        for i in range(0, MQ * (NK // T), 2):
                            bank = s_ring.take(dve)
                            m, part = i % MQ, i // MQ
                            feats = bank[:].rearrange("p (m t) -> p m t", m=2)
                            if twins == 1:
                                last = vec.tensor_copy(kT[r % 2][:, m:m + 2, part * T:(part + 1) * T], feats)
                            else:
                                for e in range(2):
                                    last = vec.tensor_scalar(kT[r % 2][:, e * MQ + m:e * MQ + m + 2, part * T:(part + 1) * T], feats,
                                                             twin[:, e:e + 1], None, ALU.mult)
                            s_ring.empty(last)

                    def attend(r):
                        def scale_mask(i):
                            h, g = items[i][0], r * n + i
                            bank = s_ring.take(dve)
                            if g >= 4:
                                dve.wait_ge(sig("exp"), S * (g - 3))
                            s = s_sb[g % 4]
                            if causal:
                                ins = vec.scalar_tensor_tensor(out=s[:], in0=bank[:, 0:W], scalar=0.0, in1=rhat[:, h, :],
                                                               op0=ALU.max, op1=ALU.mult)
                            else:
                                ins = vec.scalar_tensor_tensor(out=s[:], in0=bank[:, 0:W], scalar=scale,
                                                               in1=bias[r % 2][:].rearrange("p t s -> p (t s)"), op0=ALU.mult, op1=ALU.add)
                            s_ring.empty(ins)

                        def hide_future(i):
                            dve.wait_ge(s_ring.emptied, s_at["attend", r] + i + 1)
                            s = s_sb[(r * n + i) % 4]
                            for at in (0, 2 * P):
                                last = vec.tensor_tensor(s[:, at:at + P], s[:, at:at + P], future[:], ALU.add)
                            last.then_inc(sig("hidden"), 1)

                        def maximum(i):
                            g = r * n + i
                            if causal:
                                dve.wait_ge(sig("hidden"), g + 1)
                            else:
                                dve.wait_ge(s_ring.emptied, s_at["attend", r] + i + 1)
                            s, nm = s_sb[g % 4], nmax[r % 2]
                            if causal:
                                for e, (t, at, nk) in enumerate(items[i][1]):
                                    last = vec.tensor_reduce(nm[:, i, e:e + 1], s[:, at:at + nk], AX.X, ALU.max, negate=True)
                            else:
                                last = vec.tensor_reduce(nm[:, i, :], s[:].rearrange("p (e s) -> p e s", e=S), AX.X, ALU.max, negate=True)
                            last.then_inc(sig("max"), 1)

                        def reciprocal(i):
                            dve.wait_ge(sig("exp"), S * (r * n + i + 1))
                            rs = rsum[r % 2][:, i, :]
                            vec.reciprocal(rs, rs).then_inc(sig("reciprocal"), 1)

                        scale_mask(0)
                        for i in range(n + causal + 2):
                            if i >= causal + 2:
                                reciprocal(i - causal - 2)
                            if i + 1 < n:
                                scale_mask(i + 1)
                            if causal and i < n:
                                hide_future(i)
                            if causal <= i < n + causal:
                                maximum(i - causal)

                    def output(r):
                        xr = c.x[:, bass.ts(row_of(r), TB), :]
                        dve.wait_ge(sig("projected"), r + 1)
                        if r:
                            dve.wait_ge(sig("added"), r)
                        proj = out_bank[:].rearrange("p (t d) -> p t d", t=TB)
                        rowwise = lambda a: a[:].unsqueeze(1).to_broadcast([P, TB, D])
                        if kind == "latent":
                            for t in range(TB):
                                last = vec.bn_stats(stats[:, t, :], proj[:, t, :])
                            ch.link(last)
                            for t in range(TB):
                                last = vec.bn_aggr(mv[:, t, :], stats[:, t, :])
                            ch.link(last)
                            vec.tensor_scalar_add(rstd[:, :, 0], mv[:, :, 1], 1e-5).then_inc(sig("var_eps"), 1)
                            dve.wait_ge(sig("std"), r + 1)
                            ch.link(vec.reciprocal(rstd[:, :, 2], rstd[:, :, 1]))
                            for t in range(TB):
                                last = vec.tensor_scalar(y[:, t, :], proj[:, t, :], mv[:, t, 0:1], rstd[:, t, 2:3], ALU.subtract, ALU.mult)
                            last.then_inc(sig("out_read"), 1)
                            dve.wait_ge(sig("out_read"), r + 1)
                            ch.link(vec.tensor_tensor(y[:], y[:], rowwise(og), ALU.mult))
                            ch.link(vec.tensor_tensor(y[:], y[:], rowwise(ob), ALU.add))
                        else:
                            vec.tensor_tensor(y[:], proj, rowwise(bo), ALU.add).then_inc(sig("out_read"), 1)
                            dve.wait_ge(sig("out_read"), r + 1)
                        vec.tensor_tensor(xr, xr, y[:], ALU.add).then_inc(sig("added"), 1)

                    for stage, r in stages:
                        {"project": project, "attend": attend, "output": output}[stage](r)
            sig.clear()
        sig.close()


def layer1_attn(c):
    softmax_attention(c, "L1a", 16, 16, 2, 2, 16, "decay", 0.25)


def layer1_xattn(c):
    softmax_attention(c, "L1x", 16, 16, 2, 2, 16, "pairs", 0.25)


def layer2_xattn(c):
    normalise(c, "n2x", c.x, dstT=c.xT)
    plain_attention(c, "L2x", 1, 0, 2, 2, 256, "plain", 1.0 / 16.0)


def layer3_xattn(c):
    with ExitStack() as stack:
        sb = c.tiles(stack, "L3xn")
        c.ctxn = sb("ctxn", [P, KD, N])
        xn = sb("xn", [P, NT, D])
        affine = sb("affine", [P, 4, KD])
        c.load("L3xn_ld", [(affine[:], c.dram["L3x_ln"])])
        normalise(c, "n3x", c.x, dst=xn)
        normalise(c, "n3y", xn, dstT=c.xT, gain=affine[:, 0, :], shift=affine[:, 1, :])
        softmax_attention(c, "L3x", 8, 64, 4, 4, 64, "latent", 1.0 / 64.0,
                          norm=dict(src=c.ctx, dstT=c.ctxn, gain=affine[:, 2, :], shift=affine[:, 3, :]))


def layer1_ffn(c):
    nc, w = c.nc, c.dram
    I = 768
    MI = I // P
    QMAX = 32767.0
    normalise(c, "n1f", c.x, dstT=c.xT)
    with ExitStack() as stack:
        sb = c.tiles(stack, "L1f")
        up, gate = sb("up", [P, MI, N]), sb("gate", [P, MI, N])
        wT = {"up": sb("wT_up", [P, KD, I]), "gate": sb("wT_gate", [P, KD, I]), "down": sb("wT_down", [P, MI, D])}
        s = {n: sb("s_" + n, [P, 4]) for n in ("x", "up", "gate", "mix", "out")}

        def scale_of(ch, vec, t, factor=None):
            if factor is not None:
                ch.link(vec.tensor_tensor(t[:, 1:2], t[:, 0:1], factor, ALU.mult))
                ch.link(vec.tensor_scalar(t[:, 1:2], t[:, 1:2], 1.0 / QMAX, 1e-12, ALU.mult, ALU.max))
                ch.link(vec.reciprocal(t[:, 2:3], t[:, 1:2]))
                ch.link(vec.tensor_tensor(t[:, 3:4], t[:, 2:3], factor, ALU.mult))
            else:
                ch.link(vec.tensor_scalar(t[:, 1:2], t[:, 0:1], 1.0 / QMAX, 1e-12, ALU.mult, ALU.max))
                ch.link(vec.reciprocal(t[:, 2:3], t[:, 1:2]))
                ch.link(vec.tensor_copy(t[:, 3:4], t[:, 2:3]))

        def quantise(ch, vec, a, t, low=True):
            ch.link(vec.tensor_scalar(a, a, t[:, 3:4], ROUND, ALU.mult, ALU.add))
            ch.link(vec.tensor_scalar(a, a, -ROUND, QMAX, ALU.add, ALU.min))
            if low:
                ch.link(vec.tensor_scalar(a, a, -QMAX - 1.0, None, ALU.max))

        with ExitStack() as inner:
            sw = c.tiles(inner, "L1f")
            nat = {"up": sw("nat_up", [P, MI, D]), "gate": sw("nat_gate", [P, MI, D]), "down": sw("nat_down", [P, KD, I])}
            bs, binv = sw("block_scale", [P, 48]), sw("block_inv", [P, 48])
            c.load("L1f_ld", [(nat[n][:], w[f"L1f_{n}"]) for n in ("up", "gate", "down")])
            sig = Signals(nc, "L1f_w")
            with nc.Block() as block:
                order = ("up", "gate", "down")
                ring = Ring(sig, "wt", c.banks[0:4])

                @block.vector
                def _(dve):
                    ch = Chain(dve, sig("dve_chain"))
                    vec = nc.vector
                    for n in order:
                        a = nat[n][:].rearrange("p a b -> p (a b)").rearrange("p (g i) -> p g i", i=32)
                        wide = lambda t: t[:].unsqueeze(2).to_broadcast([P, 48, 32])
                        ch.link(vec.tensor_reduce(bs[:], a, AX.X, ALU.max, apply_absolute_value=True))
                        ch.link(vec.tensor_scalar(bs[:], bs[:], 1.0 / 7.0, 1e-12, ALU.mult, ALU.max))
                        ch.link(vec.reciprocal(binv[:], bs[:]))
                        ch.link(vec.tensor_tensor(a, a, wide(binv), ALU.mult))
                        ch.link(vec.tensor_scalar(a, a, ROUND, None, ALU.add))
                        ch.link(vec.tensor_scalar(a, a, -ROUND, 7.0, ALU.add, ALU.min))
                        ch.link(vec.tensor_scalar(a, a, -8.0, None, ALU.max))
                        ch.link(vec.tensor_tensor(a, a, wide(bs), ALU.mult))
                        vec.sem_inc(sig("dequantised"), 1)
                    vec.tensor_reduce(s["x"][:, 0:1], c.xT[:].rearrange("p k n -> p (k n)"), AX.X, ALU.max,
                                      apply_absolute_value=True).then_inc(sig("x_max"), 1)
                    dve.wait_ge(sig("x_all"), 1)
                    scale_of(ch, vec, s["x"])
                    quantise(ch, vec, c.xT[:], s["x"])

                @block.gpsimd
                def _(pool):
                    pool.wait_ge(sig("x_max"), 1)
                    nc.gpsimd.partition_all_reduce(s["x"][:, 0:1], s["x"][:, 0:1], P, bass.bass_isa.ReduceOp.max).then_inc(sig("x_all"), 1)

                @block.tensor
                def _(pe):
                    for q, n in enumerate(order):
                        pe.wait_ge(sig("dequantised"), q + 1)
                        outer, inner_ = (MI, KD) if n != "down" else (KD, MI)
                        for i in range(inner_):
                            for o0 in range(0, outer, 4):
                                bank = ring.claim(pe)
                                for o in range(o0, min(o0 + 4, outer)):
                                    last = nc.tensor.transpose(bank[:, (o - o0) * P:(o - o0 + 1) * P],
                                                               nat[n][:, o, i * P:(i + 1) * P], c.ident[:])
                                ring.fill(last)

                @block.scalar
                def _(act):
                    for n in order:
                        outer, inner_ = (MI, KD) if n != "down" else (KD, MI)
                        for i in range(inner_):
                            for o0 in range(0, outer, 4):
                                bank = ring.take(act)
                                cnt = min(4, outer - o0) * P
                                ring.empty(nc.scalar.activation(wT[n][:, i, o0 * P:o0 * P + cnt], bank[:, 0:cnt], ACT.Copy))
            sig.clear()
            sig.close()

        sig = Signals(nc, "L1f_u")
        with nc.Fori(0, NBLK) as t:
            with nc.Block() as block:
                u_ring = Ring(sig, "u", c.banks[0:4])
                g_ring = Ring(sig, "g", c.banks[4:8])

                @block.tensor
                def _(pe):
                    for m in range(MI):
                        for n, ring in (("up", u_ring), ("gate", g_ring)):
                            bank = ring.claim(pe)
                            for k in range(KD):
                                last = nc.tensor.matmul(bank[:], wT[n][:, k, m * P:(m + 1) * P], c.xT[:, k, bass.ts(t, BLK)],
                                                        start=(k == 0), stop=(k == KD - 1))
                            ring.fill(last)

                @block.scalar
                def _(act):
                    for m in range(MI):
                        bank = u_ring.take(act)
                        u_ring.empty(nc.scalar.activation(up[:, m, bass.ts(t, BLK)], bank[:], ACT.Copy, scale=s["x"][:, 1:2]))

                @block.vector
                def _(dve):
                    for m in range(MI):
                        bank = g_ring.take(dve)
                        g_ring.empty(nc.vector.tensor_scalar(gate[:, m, bass.ts(t, BLK)], bank[:], s["x"][:, 1:2], None, ALU.mult))
            sig.clear()
        sig.close()

        with ExitStack() as inner:
            sw = c.tiles(inner, "L1f")
            sg = [sw(f"sigmoid{i}", [P, N]) for i in range(2)]
            mx = sw("chunk_max", [P, 4, MI])
            sig = Signals(nc, "L1f_g")
            with nc.Block() as block:
                @block.vector
                def _(dve):
                    ch = Chain(dve, sig("dve_chain"))
                    vec = nc.vector
                    absmax = lambda o, a: vec.tensor_reduce(o, a, AX.X, ALU.max, apply_absolute_value=True)
                    for m in range(MI):
                        vec_last = absmax(mx[:, 0, m:m + 1], up[:, m, :])
                    ch.link(vec_last)
                    vec.tensor_reduce(s["up"][:, 0:1], mx[:, 0, :], AX.X, ALU.max).then_inc(sig("maxima"), 1)
                    for m in range(MI):
                        vec_last = absmax(mx[:, 1, m:m + 1], gate[:, m, :])
                    ch.link(vec_last)
                    vec.tensor_reduce(s["gate"][:, 0:1], mx[:, 1, :], AX.X, ALU.max).then_inc(sig("maxima"), 1)
                    dve.wait_ge(sig("reduced"), 1)
                    scale_of(ch, vec, s["up"])
                    vec.sem_inc(sig("up_scaled"), 1)
                    dve.wait_ge(sig("reduced"), 2)
                    scale_of(ch, vec, s["gate"])

                    def weigh(m):
                        dve.wait_ge(sig("sigmoid"), m + 1)
                        a = sg[m % 2][:]
                        ch.link(vec.tensor_scalar(a, a, 65536.0, ROUND, ALU.mult, ALU.add))
                        ch.link(vec.tensor_scalar(a, a, -ROUND, 65535.0, ALU.add, ALU.min))
                        ch.link(vec.scalar_tensor_tensor(out=gate[:, m, :], in0=a, scalar=0.0, in1=gate[:, m, :],
                                                         op0=ALU.max, op1=ALU.mult))
                        ch.link(absmax(mx[:, 2, m:m + 1], gate[:, m, :]))
                        vec.sem_inc(sig("weighed"), 1)

                    for m in range(MI):
                        quantise(ch, vec, gate[:, m, :], s["gate"])
                        vec.sem_inc(sig("gate_q"), 1)
                        if m:
                            weigh(m - 1)
                    weigh(MI - 1)
                    ch.link(vec.tensor_scalar(s["gate"][:, 0:1], s["gate"][:, 1:2], 1.0 / 65536.0, None, ALU.mult))
                    vec.tensor_reduce(s["mix"][:, 0:1], mx[:, 2, :], AX.X, ALU.max).then_inc(sig("maxima"), 1)
                    dve.wait_ge(sig("reduced"), 3)
                    scale_of(ch, vec, s["mix"], factor=s["gate"][:, 0:1])
                    ch.link(vec.tensor_tensor(s["up"][:, 0:1], s["up"][:, 1:2], s["mix"][:, 1:2], ALU.mult))
                    for m in range(MI):
                        quantise(ch, vec, gate[:, m, :], s["mix"], low=False)
                        dve.wait_ge(sig("up_q"), m + 1)
                        ch.link(vec.scalar_tensor_tensor(out=gate[:, m, :], in0=gate[:, m, :], scalar=-QMAX - 1.0, in1=up[:, m, :],
                                                         op0=ALU.max, op1=ALU.mult))
                        ch.link(absmax(mx[:, 3, m:m + 1], gate[:, m, :]))
                    vec.tensor_reduce(s["out"][:, 0:1], mx[:, 3, :], AX.X, ALU.max).then_inc(sig("maxima"), 1)
                    dve.wait_ge(sig("reduced"), 4)
                    scale_of(ch, vec, s["out"], factor=s["up"][:, 0:1])
                    for m in range(MI):
                        quantise(ch, vec, gate[:, m, :], s["out"])

                @block.gpsimd
                def _(pool):
                    for i, n in enumerate(("up", "gate")):
                        pool.wait_ge(sig("maxima"), i + 1)
                        nc.gpsimd.partition_all_reduce(s[n][:, 0:1], s[n][:, 0:1], P, bass.bass_isa.ReduceOp.max).then_inc(sig("reduced"), 1)
                    pool.wait_ge(sig("up_scaled"), 1)
                    for m in range(MI):
                        a = up[:, m, :]
                        nc.gpsimd.tensor_scalar(a, a, s["up"][:, 3:4], ROUND, ALU.mult, ALU.add).then_inc(sig("up_steps"), 1)
                        pool.wait_ge(sig("up_steps"), 3 * m + 1)
                        nc.gpsimd.tensor_scalar(a, a, -ROUND, QMAX, ALU.add, ALU.min).then_inc(sig("up_steps"), 1)
                        pool.wait_ge(sig("up_steps"), 3 * m + 2)
                        nc.gpsimd.tensor_scalar(a, a, -QMAX - 1.0, None, ALU.max).then_inc(sig("up_steps"), 1)
                        pool.wait_ge(sig("up_steps"), 3 * m + 3)
                        nc.gpsimd.sem_inc(sig("up_q"), 1)
                    for i, n in enumerate(("mix", "out")):
                        pool.wait_ge(sig("maxima"), i + 3)
                        nc.gpsimd.partition_all_reduce(s[n][:, 0:1], s[n][:, 0:1], P, bass.bass_isa.ReduceOp.max).then_inc(sig("reduced"), 1)

                @block.scalar
                def _(act):
                    for m in range(MI):
                        act.wait_ge(sig("gate_q"), m + 1)
                        if m >= 2:
                            act.wait_ge(sig("weighed"), m - 1)
                        nc.scalar.activation(sg[m % 2][:], gate[:, m, :], ACT.Sigmoid, scale=s["gate"][:, 1:2]).then_inc(sig("sigmoid"), 1)
            sig.clear()
            sig.close()

        sig = Signals(nc, "L1f_d")
        with nc.Block() as block:
            ring = Ring(sig, "y", c.banks)

            @block.tensor
            def _(pe):
                for t in range(0, NT, 2):
                    bank = ring.claim(pe)
                    for j in range(2):
                        for m in range(MI):
                            last = nc.tensor.matmul(bank[:, j * D:(j + 1) * D], gate[:, m, (t + j) * P:(t + j + 1) * P], wT["down"][:, m, :],
                                                    start=(m == 0), stop=(m == MI - 1))
                    ring.fill(last)

            @block.vector
            def _(dve):
                for t in range(0, NT, 2):
                    bank = ring.take(dve)
                    xs = c.x[:, t:t + 2, :].rearrange("p t d -> p (t d)")
                    ring.empty(nc.vector.scalar_tensor_tensor(out=xs, in0=bank[:], scalar=s["out"][:, 1:2], in1=xs,
                                                              op0=ALU.mult, op1=ALU.add))
        sig.clear()
        sig.close()


def layer2_attn(c):
    nc, w = c.nc, c.dram
    L, S = 64, 64
    START = (L - 1) // 2
    PAD = L - START - 1
    W = PAD + T + START + 1
    ON_TENSOR = list(range(0, 26))
    ON_VECTOR = [l for l in range(L) if l not in ON_TENSOR]
    normalise(c, "n2a", c.x, dstT=c.xT)
    with ExitStack() as stack:
        sb = c.tiles(stack, "L2a")
        taps = sb("taps", [P, KD, L])
        u = sb("u", [P, KD, B, W])
        with ExitStack() as inner:
            sw = c.tiles(inner, "L2a")
            cm, bm = sw("cm", [P, KD, S]), sw("bm", [P, KD, S])
            am, dvec, ldt = sw("am", [P, S]), sw("dvec", [P, KD]), sw("ldt", [P, KD])
            power, ones = sw("power", [P, L]), sw("ones", [P, P])
            la = sw("la", [P, L, S])
            ex = [sw(f"ex{k}", [P, L, S]) for k in range(KD)]
            c.load("L2a_ld", [(cm[:], w["L2a_c"]), (bm[:], w["L2a_b"]), (dvec[:], w["L2a_d"]), (ldt[:], w["L2a_ldt"]),
                              (power[:], w["iota64"]), (ones[:], w["tri_strict_ones"][:, 1, :]), (am[:], w["L2a_a"].rearrange("(a n) -> a n", a=1).to_broadcast([P, S]))])
            sig = Signals(nc, "L2a_k")
            with nc.Block() as block:
                @block.gpsimd
                def _(pool):
                    nc.gpsimd.memset(u[:], 0.0).then_inc(sig("zeroed"), 1)

                @block.tensor
                def _(pe):
                    for k in range(KD):
                        last = nc.tensor.matmul(c.banks[0][:, 0:S], ones[:], cm[:, k, :], start=(k == 0), stop=(k == KD - 1))
                    last.then_inc(sig("c_sum"), 1)

                @block.vector
                def _(dve):
                    ch = Chain(dve, sig("dve_chain"))
                    vec = nc.vector
                    vec.tensor_tensor(la[:], power[:].unsqueeze(2).to_broadcast([P, L, S]),
                                      am[:].unsqueeze(1).to_broadcast([P, L, S]), ALU.mult).then_inc(sig("exponents"), 1)
                    dve.wait_ge(sig("c_sum"), 1)
                    ch.link(vec.tensor_tensor(cm[:], c.banks[0][:, 0:S].unsqueeze(1).to_broadcast([P, KD, S]), bm[:], ALU.mult))
                    for k in range(KD):
                        dve.wait_ge(sig("powers"), k + 1)
                        ch.link(vec.tensor_tensor(ex[k][:], ex[k][:], cm[:, k, :].unsqueeze(1).to_broadcast([P, L, S]), ALU.mult))
                        ch.link(vec.tensor_reduce(taps[:, k, :], ex[k][:], AX.X, ALU.add))
                    vec.tensor_tensor(taps[:, :, START], taps[:, :, START], dvec[:], ALU.add)

                @block.scalar
                def _(act):
                    nc.scalar.activation(ldt[:], ldt[:], ACT.Exp).then_inc(sig("dt"), 1)
                    act.wait_ge(sig("dt"), 1)
                    act.wait_ge(sig("exponents"), 1)
                    for k in range(KD):
                        nc.scalar.activation(ex[k][:], la[:], ACT.Exp, scale=ldt[:, k:k + 1]).then_inc(sig("powers"), 1)
                    act.wait_ge(sig("zeroed"), 1)
                    for k in range(KD):
                        nc.scalar.activation(u[:, k, :, PAD:PAD + T], c.xT[:, k, :].rearrange("p (b t) -> p b t", b=B), ACT.Copy)
            sig.clear()
            sig.close()
        acc = sb("acc", [P, KD, B, T])
        diag = sb("diag", [P, KD, len(ON_TENSOR), P])
        sig = Signals(nc, "L2a")
        with nc.Block() as block:
            shifted = lambda k, l: u[:, k, :, PAD + START - l:PAD + START - l + T]
            y_ring_banks = c.banks

            @block.scalar
            def _(act):
                for k in range(KD):
                    for i, l in enumerate(ON_TENSOR):
                        nc.scalar.activation(diag[:, k, i, :], c.ident[:], ACT.Copy, scale=taps[:, k, l:l + 1]).then_inc(sig("diagonal"), 1)

            @block.tensor
            def _(pe):
                for k in range(KD):
                    for i, l in enumerate(ON_TENSOR):
                        pe.wait_ge(sig("diagonal"), k * len(ON_TENSOR) + i + 1)
                        for q in range(NBLK):
                            last = nc.tensor.matmul(c.banks[k * NBLK + q][:], diag[:, k, i, :],
                                                    shifted(k, l)[:, q * TB:(q + 1) * TB, :],
                                                    start=(i == 0), stop=(i == len(ON_TENSOR) - 1))
                    last.then_inc(sig("tensor_taps"), 1)
                pe.wait_ge(sig("summed"), 1)
                for t in range(0, NT, 2):
                    bank = c.banks[t // 2]
                    for j in range(2):
                        for k in range(KD):
                            tt = t + j
                            last = nc.tensor.transpose(bank[:, j * D + k * P:j * D + (k + 1) * P],
                                                       acc[:, k, tt // TB, (tt % TB) * P:(tt % TB + 1) * P], c.ident[:])
                    last.then_inc(sig("turned"), 1)

            @block.vector
            def _(dve):
                ch = Chain(dve, sig("dve_chain"))
                vec = nc.vector
                for k in range(KD):
                    for i, l in enumerate(ON_VECTOR):
                        if i == 0:
                            ch.link(vec.tensor_scalar(acc[:, k], shifted(k, l), taps[:, k, l:l + 1], None, ALU.mult))
                        else:
                            ch.link(vec.scalar_tensor_tensor(out=acc[:, k], in0=shifted(k, l), scalar=taps[:, k, l:l + 1], in1=acc[:, k],
                                                             op0=ALU.mult, op1=ALU.add))
                for k in range(KD):
                    dve.wait_ge(sig("tensor_taps"), k + 1)
                    for q in range(NBLK):
                        part = acc[:, k, q * TB:(q + 1) * TB, :].rearrange("p b t -> p (b t)")
                        last = vec.tensor_tensor(part, part, c.banks[k * NBLK + q][:], ALU.add)
                last.then_inc(sig("summed"), 1)
                for t in range(0, NT, 2):
                    dve.wait_ge(sig("turned"), t // 2 + 1)
                    xs = c.x[:, t:t + 2, :].rearrange("p t d -> p (t d)")
                    vec.tensor_tensor(xs, xs, c.banks[t // 2][:], ALU.add)
        sig.clear()
        sig.close()


def layer3_attn(c):
    nc, w = c.nc, c.dram
    H, DH = 16, 16
    with ExitStack() as stack:
        sb = c.tiles(stack, "L3a")
        xn = sb("xn", [P, NT, D])
        normalise(c, "n3a", c.x, dst=xn, dstT=c.xT)
        wqk, wv = sb("wqk", [P, KD, 2 * D]), sb("wv", [P, KD, D])
        bqk, bv, gamma, beta = sb("bqk", [P, 2 * D]), sb("bv", [P, D]), sb("gamma", [P, D]), sb("beta", [P, D])
        cos, sin = sb("cos", [P, TB, D]), sb("sin", [P, TB, D])
        ones, diag = sb("ones", [P, P]), sb("blockdiag", [P, P])
        xb = sb("xb", [P, KD, T])
        qk, rot, tmp = sb("qk", [P, TB, 2, D]), sb("rot", [P, TB, 2, D]), sb("tmp", [P, TB, 2, D])
        v = sb("v", [P, TB, D])
        kv = sb("kv", [P, KD, P])
        qrT = sb("qrT", [P, KD, T])
        z = sb("z", [P, TB, H])
        res = sb("res", [P, TB, D])
        stats, mv, rstd = sb("stats", [P, TB, 6]), sb("mv", [P, TB, 2]), sb("rstd", [P, TB, 3])
        row = lambda n: w[n].rearrange("(a n) -> a n", a=1)
        c.load("L3a_ld", [(wqk[:], w["L3a_wqk"]), (wv[:], w["L3a_wv"]), (bqk[:], row("L3a_bqk").to_broadcast([P, 2 * D])),
                          (bv[:], row("L3a_bv").to_broadcast([P, D])), (gamma[:], row("L3a_gamma").to_broadcast([P, D])),
                          (beta[:], row("L3a_beta").to_broadcast([P, D])), (cos[:], w["rope_cos"]), (sin[:], w["rope_sin"]),
                          (ones[:], w["tri_strict_ones"][:, 1, :]), (diag[:], w["blockdiag16"])])
        sig = Signals(nc, "L3a")
        with nc.Fori(0, B) as b:
            with nc.Block() as block:
                qk_bank, v_bank, sum_bank, kv_bank, turn_bank, out_bank = c.banks[0:2], c.banks[2], c.banks[3], c.banks[4], c.banks[5], c.banks[6]

                @block.scalar
                def _(act):
                    nc.scalar.activation(xb[:], c.xT[:, :, bass.ts(b, T)], ACT.Copy).then_inc(sig("sliced"), 1)
                    for t in range(TB):
                        act.wait_ge(sig("biased"), t + 1)
                        nc.scalar.activation(qk[:, t], qk[:, t], ACT.Gelu).then_inc(sig("gelu"), 1)
                    act.wait_ge(sig("turned"), 1)
                    nc.scalar.activation(qrT[:], turn_bank[:].rearrange("p (k t) -> p k t", k=KD), ACT.Copy).then_inc(sig("q_feat"), 1)
                    act.wait_ge(sig("var_eps"), 1)
                    nc.scalar.activation(rstd[:, :, 1], rstd[:, :, 0], ACT.Sqrt).then_inc(sig("std"), 1)

                @block.tensor
                def _(pe):
                    pe.wait_ge(sig("sliced"), 1)
                    for t in range(TB):
                        for k in range(KD):
                            last = nc.tensor.matmul(qk_bank[t][:], xb[:, k, t * P:(t + 1) * P], wqk[:, k, :], start=(k == 0), stop=(k == KD - 1))
                        last.then_inc(sig("qk"), 1)
                    for t in range(TB):
                        for k in range(KD):
                            last = nc.tensor.matmul(v_bank[:, t * D:(t + 1) * D], xb[:, k, t * P:(t + 1) * P], wv[:, k, :],
                                                    start=(k == 0), stop=(k == KD - 1))
                    last.then_inc(sig("v_raw"), 1)
                    pe.wait_ge(sig("shifted"), 1)
                    for t in range(TB):
                        last = nc.tensor.matmul(sum_bank[:, 0:D], ones[:], qk[:, t, 1, :], start=(t == 0), stop=(t == TB - 1))
                    last.then_inc(sig("k_sum"), 1)
                    pe.wait_ge(sig("rotated"), 1)
                    for m in range(KD):
                        for t in range(TB):
                            last = nc.tensor.transpose(turn_bank[:, m * T + t * P:m * T + (t + 1) * P], rot[:, t, 0, m * P:(m + 1) * P], c.ident[:])
                    last.then_inc(sig("turned"), 1)
                    for m in range(KD):
                        for t in range(TB):
                            last = nc.tensor.matmul(kv_bank[:, m * P:(m + 1) * P], rot[:, t, 1, m * P:(m + 1) * P],
                                                    v[:, t, m * P:(m + 1) * P], start=(t == 0), stop=(t == TB - 1))
                    last.then_inc(sig("kv"), 1)
                    pe.wait_ge(sig("q_feat"), 1)
                    pe.wait_ge(sig("kv_heads"), 1)
                    for t in range(TB):
                        for m in range(KD):
                            last = nc.tensor.matmul(out_bank[:, t * D + m * P:t * D + (m + 1) * P], qrT[:, m, t * P:(t + 1) * P], kv[:, m, :],
                                                    start=True, stop=True)
                    last.then_inc(sig("attended"), 1)

                @block.vector
                def _(dve):
                    ch = Chain(dve, sig("dve_chain"))
                    vec = nc.vector
                    for t in range(TB):
                        dve.wait_ge(sig("qk"), t + 1)
                        vec.tensor_tensor(qk[:, t].rearrange("p a d -> p (a d)"), qk_bank[t][:], bqk[:], ALU.add).then_inc(sig("biased"), 1)
                    dve.wait_ge(sig("v_raw"), 1)
                    vec.tensor_tensor(v[:], v_bank[:].rearrange("p (t d) -> p t d", t=TB), bv[:].unsqueeze(1).to_broadcast([P, TB, D]), ALU.add)
                    dve.wait_ge(sig("gelu"), TB)
                    vec.tensor_scalar(qk[:], qk[:], 0.21, None, ALU.add).then_inc(sig("shifted"), 1)
                    dve.wait_ge(sig("shifted"), 1)
                    for t in range(TB):
                        both = lambda a: a[:, t].unsqueeze(1).to_broadcast([P, 2, D])
                        even = lambda a: a.rearrange("p a (d two) -> p a d two", two=2)[:, :, :, 0]
                        odd = lambda a: a.rearrange("p a (d two) -> p a d two", two=2)[:, :, :, 1]
                        vec.tensor_tensor(even(tmp[:, t]), odd(qk[:, t]), even(both(sin)), ALU.mult)
                        vec.tensor_tensor(odd(tmp[:, t]), even(qk[:, t]), odd(both(sin)), ALU.mult)
                        ch.link(vec.tensor_tensor(rot[:, t], qk[:, t], both(cos), ALU.mult))
                    vec.tensor_tensor(rot[:], rot[:], tmp[:], ALU.add).then_inc(sig("rotated"), 1)
                    dve.wait_ge(sig("k_sum"), 1)
                    dve.wait_ge(sig("rotated"), 1)
                    ch.link(vec.tensor_tensor(tmp[:, :, 0, :], qk[:, :, 0, :], sum_bank[:, 0:D].unsqueeze(1).to_broadcast([P, TB, D]), ALU.mult))
                    for t in range(TB):
                        last = vec.tensor_reduce(z[:, t, :], tmp[:, t, 0, :].rearrange("p (h d) -> p h d", h=H), AX.X, ALU.add)
                    ch.link(last)
                    ch.link(vec.tensor_scalar(z[:], z[:], 1.0 / T, 1e-6, ALU.mult, ALU.add))
                    ch.link(vec.reciprocal(z[:], z[:]))
                    dve.wait_ge(sig("kv"), 1)
                    vec.tensor_tensor(kv[:], kv_bank[:, 0:T].rearrange("p (m e) -> p m e", m=KD),
                                      diag[:].unsqueeze(1).to_broadcast([P, KD, P]), ALU.mult).then_inc(sig("kv_heads"), 1)
                    dve.wait_ge(sig("attended"), 1)
                    for t in range(TB):
                        last = vec.tensor_tensor(res[:, t, :].rearrange("p (h d) -> p h d", h=H),
                                                 out_bank[:, t * D:(t + 1) * D].rearrange("p (h d) -> p h d", h=H),
                                                 z[:, t, :].unsqueeze(2).to_broadcast([P, H, DH]), ALU.mult)
                    ch.link(last)
                    ch.link(vec.tensor_tensor(res[:], res[:], xn[:, bass.ts(b, TB), :], ALU.add))
                    for t in range(TB):
                        last = vec.bn_stats(stats[:, t, :], res[:, t, :])
                    ch.link(last)
                    for t in range(TB):
                        last = vec.bn_aggr(mv[:, t, :], stats[:, t, :])
                    ch.link(last)
                    vec.tensor_scalar_add(rstd[:, :, 0], mv[:, :, 1], 1e-12).then_inc(sig("var_eps"), 1)
                    dve.wait_ge(sig("std"), 1)
                    ch.link(vec.reciprocal(rstd[:, :, 2], rstd[:, :, 1]))
                    for t in range(TB):
                        last = vec.tensor_scalar(res[:, t, :], res[:, t, :], mv[:, t, 0:1], rstd[:, t, 2:3], ALU.subtract, ALU.mult)
                    ch.link(last)
                    rowwise = lambda a: a[:].unsqueeze(1).to_broadcast([P, TB, D])
                    ch.link(vec.tensor_tensor(res[:], res[:], rowwise(gamma), ALU.mult))
                    ch.link(vec.tensor_tensor(res[:], res[:], rowwise(beta), ALU.add))
                    vec.tensor_tensor(c.x[:, bass.ts(b, TB), :], c.x[:, bass.ts(b, TB), :], res[:], ALU.add)
            sig.clear()
        sig.close()


def layer0_xattn(c):
    nc, w = c.nc, c.dram
    H, DH, NA, LAG = 16, 16, 4, 2
    with ExitStack() as stack:
        sb = c.tiles(stack, "L0x")
        wq, wv, wk, wo = (sb(n, [P, KD, D]) for n in ("wq", "wv", "wk", "wo"))
        bq, bv, bk, bo = sb("bq", [P, KD]), sb("bv", [P, KD]), sb("bk", [P, D]), sb("bo", [P, D])
        causal = sb("causal", [P, 3 * P])
        ones, twin = sb("ones", [P, P]), sb("twin", [P, 2])
        xb, cb = ([sb(f"{n}{i}", [P, KD, T]) for i in range(2)] for n in ("xb", "cb"))
        q = [sb(f"q{i}", [P, KD, T]) for i in range(2)]
        v = [sb(f"v{i}", [P, 2, KD, T]) for i in range(2)]
        k = [sb(f"k{i}", [P, TB, D]) for i in range(2)]
        k2 = [sb(f"k2{i}", [P, TB, 2, D]) for i in range(2)]
        eq, rq, ek, rk = sb("eq", [P, KD, T]), sb("rq", [P, KD, T]), sb("ek", [P, TB, D]), sb("rk", [P, TB, D])
        den = [sb(f"den{i}", [P, KD, T]) for i in range(2)]
        att = [sb(f"att{i}", [P, 3 * P]) for i in range(NA)]
        cT, y = sb("cT", [P, KD, T]), sb("y", [P, TB, D])
        row = lambda n: w[n].rearrange("(a n) -> a n", a=1)
        normalise(c, "n0x", c.x, dstT=c.xT, loads=[(wq[:], w["L0x_wq"]), (wv[:], w["L0x_wv"]), (wk[:], w["L0x_wk"]), (wo[:], w["L0x_wo"]),
                          (bq[:], w["L0x_bq"]), (bv[:], w["L0x_bv"]), (bk[:], row("L0x_bk").to_broadcast([P, D])),
                          (bo[:], row("L0x_bo").to_broadcast([P, D])), (causal[:], w["causal"]), (twin[:], w["twin"]),
                          (ones[:], w["tri_strict_ones"][:, 1, :])])
        sig = Signals(nc, "L0x_z")
        with nc.Block() as block:
            @block.gpsimd
            def _(pool):
                for k2_ in k2:
                    nc.gpsimd.memset(k2_[:], 0.0)
        sig.close()
        sig = Signals(nc, "L0x")
        with nc.Fori(0, B // ROWS) as turn:
            with nc.Block() as block:
                s_ring = Ring(sig, "s", c.banks[0:3])
                t_ring = Ring(sig, "t", c.banks[3:5])
                acc, out_bank = c.banks[5:7], c.banks[7]
                row_of = lambda r: turn * ROWS + r
                stages = []
                for r in range(ROWS):
                    stages += [("project", r)] if r == 0 else []
                    stages += [("attend", r)] + ([("project", r + 1)] if r + 1 < ROWS else []) + [("output", r)]
                s_at = lambda r: r * (H + 1) + 1

                @block.tensor
                def _(pe):
                    mm = nc.tensor.matmul

                    def project(r):
                        pe.wait_ge(sig("sliced"), 2 * (r + 1))
                        for ring, weights, src in ((t_ring, wq, xb[r % 2]), (s_ring, wv, cb[r % 2])):
                            bank = ring.claim(pe)
                            for m in range(KD):
                                for kd in range(KD):
                                    last = mm(bank[:, m * T:(m + 1) * T], weights[:, kd, m * P:(m + 1) * P], src[:, kd, :],
                                              start=(kd == 0), stop=(kd == KD - 1))
                            ring.fill(last)
                        bank = t_ring.claim(pe)
                        for t in range(TB):
                            for kd in range(KD):
                                last = mm(bank[:, t * D:(t + 1) * D], cb[r % 2][:, kd, t * P:(t + 1) * P], wk[:, kd, :],
                                          start=(kd == 0), stop=(kd == KD - 1))
                        t_ring.fill(last)

                    def attend(r):
                        q_, v_, k_, k2_ = q[r % 2], v[r % 2], k[r % 2], k2[r % 2]
                        pe.wait_ge(sig("q"), r + 1)
                        pe.wait_ge(s_ring.emptied, s_at(r))
                        for i in range(H + LAG):
                            if i < H:
                                bank = s_ring.claim(pe)
                                m, e, ps = i // 8, i % 2, slice(32 * (i % 8 // 2), 32 * (i % 8 // 2) + 32)
                                mm(bank[:, 0:T], v_[ps, e, m, 0:P], q_[ps, m, :], start=True, stop=True)
                                s_ring.fill(mm(bank[:, T:3 * P], v_[ps, e, m, P:T], q_[ps, m, P:T], start=True, stop=True))
                            if i == 1:
                                bank = t_ring.claim(pe)
                                pe.wait_ge(sig("k"), r + 1)
                                tri = causal[:, 0:P]
                                for m in range(KD):
                                    ks = slice(m * P, (m + 1) * P)
                                    mm(bank[:, m * T:m * T + P], k_[:, 0, ks], tri, start=True, stop=True)
                                    mm(bank[:, m * T + P:(m + 1) * T], k_[:, 0, ks], ones[:], start=True, stop=False)
                                    last = mm(bank[:, m * T + P:(m + 1) * T], k_[:, 1, ks], tri, start=False, stop=True)
                                t_ring.fill(last)
                            if i >= LAG:
                                h = i - LAG
                                e, u = h % 2, h // 2
                                if h == 0:
                                    pe.wait_ge(sig("k2"), r + 1)
                                    if r:
                                        pe.wait_ge(sig("cT"), TB * r)
                                pe.wait_ge(s_ring.emptied, s_at(r) + h + 1)
                                a, us = att[(r * H + h) % NA], slice(u * 32, (u + 1) * 32)
                                out = [acc[t][32 * (u % 4):32 * (u % 4) + 32, u // 4 * P:(u // 4 + 1) * P] for t in range(TB)]
                                mm(out[0], k2_[:, 0, e, us], a[:, 0:P], start=(e == 0), stop=(e == 1))
                                mm(out[1], k2_[:, 0, e, us], a[:, P:2 * P], start=(e == 0), stop=False)
                                mm(out[1], k2_[:, 1, e, us], a[:, 2 * P:3 * P], start=False, stop=(e == 1)).then_inc(sig("weighted"), 1)

                    def output(r):
                        if r:
                            pe.wait_ge(sig("out_read"), r)
                        pe.wait_ge(sig("cT"), TB * (r + 1))
                        for t in range(TB):
                            for kd in range(KD):
                                last = mm(out_bank[:, t * D:(t + 1) * D], cT[:, kd, t * P:(t + 1) * P], wo[:, kd, :],
                                          start=(kd == 0), stop=(kd == KD - 1))
                        last.then_inc(sig("projected"), 1)

                    for stage, r in stages:
                        {"project": project, "attend": attend, "output": output}[stage](r)

                @block.scalar
                def _(act):
                    for r in range(ROWS):
                        if r >= 2:
                            act.wait_ge(sig("k_raw"), r - 1)
                        nc.scalar.activation(xb[r % 2][:], c.xT[:, :, bass.ts(row_of(r), T)], ACT.Copy).then_inc(sig("sliced"), 1)
                        nc.scalar.activation(cb[r % 2][:], c.ctxT[:, :, bass.ts(row_of(r), T)], ACT.Copy).then_inc(sig("sliced"), 1)
                        act.wait_ge(sig("q_raw"), r + 1)
                        nc.scalar.activation(eq[:], eq[:], ACT.Exp).then_inc(sig("exp"), 1)
                        act.wait_ge(sig("k_min"), r + 1)
                        nc.scalar.activation(ek[:], ek[:], ACT.Exp).then_inc(sig("exp"), 1)

                @block.gpsimd
                def _(pool):
                    for r in range(ROWS):
                        pool.wait_ge(sig("exp"), 2 * r + 1)
                        nc.gpsimd.tensor_tensor(q[r % 2][:], rq[:], eq[:], ALU.add).then_inc(sig("q"), 1)
                        pool.wait_ge(sig("k"), r + 1)
                        for e in range(2):
                            own = lambda a: a.rearrange("p t (u e d) -> p t u e d", e=2, d=DH)[:, :, :, e, :]
                            last = nc.gpsimd.tensor_copy(own(k2[r % 2][:, :, e, :]), own(k[r % 2][:]))
                        last.then_inc(sig("k2"), 1)

                @block.vector
                def _(dve):
                    ch = Chain(dve, sig("dve_chain"))
                    vec = nc.vector
                    wide = lambda a: a[:].unsqueeze(1).to_broadcast([P, TB, D])

                    def project(r):
                        bank = t_ring.take(dve)
                        if r:
                            dve.wait_ge(sig("q"), r)
                        for m in range(KD):
                            cols = slice(m * T, (m + 1) * T)
                            vec.tensor_scalar(eq[:, m, :], bank[:, cols], bq[:, m:m + 1], 0.0, ALU.add, ALU.min)
                            last = vec.tensor_scalar(rq[:, m, :], bank[:, cols], bq[:, m:m + 1], 0.0, ALU.add, ALU.max)
                        t_ring.empty(last)
                        dve.wait_ge(t_ring.emptied, t_ring.n_out)
                        vec.sem_inc(sig("q_raw"), 1)
                        bank = s_ring.take(dve)
                        for m in range(KD):
                            for e in range(2):
                                last = vec.tensor_scalar(v[r % 2][:, e, m, :], bank[:, m * T:(m + 1) * T], bv[:, m:m + 1], twin[:, e:e + 1],
                                                         ALU.add, ALU.mult)
                        s_ring.empty(last)
                        bank = t_ring.take(dve)
                        t_ring.empty(vec.tensor_tensor(rk[:], bank[:].rearrange("p (t d) -> p t d", t=TB), wide(bk), ALU.add))
                        dve.wait_ge(t_ring.emptied, t_ring.n_out)
                        vec.sem_inc(sig("k_raw"), 1)
                        vec.tensor_scalar(ek[:], rk[:], 0.0, None, ALU.min).then_inc(sig("k_min"), 1)
                        dve.wait_ge(sig("exp"), 2 * (r + 1))
                        flat = lambda a: a[:].rearrange("p t d -> p (t d)")
                        vec.scalar_tensor_tensor(out=flat(k[r % 2]), in0=flat(rk), scalar=0.0, in1=flat(ek),
                                                 op0=ALU.max, op1=ALU.add).then_inc(sig("k"), 1)

                    def attend(r):
                        for h in range(H):
                            bank = s_ring.take(dve)
                            g = r * H + h
                            if g >= NA:
                                dve.wait_ge(sig("weighted"), g - NA + 1)
                            s_ring.empty(vec.tensor_tensor(att[g % NA][:], bank[:, 0:3 * P], causal[:], ALU.mult))
                            if h == 3:
                                bank, d = t_ring.take(dve), den[r % 2]
                                t_ring.empty(vec.tensor_tensor(d[:], q[r % 2][:], bank[:].rearrange("p (m t) -> p m t", m=KD), ALU.mult))
                                dve.wait_ge(t_ring.emptied, t_ring.n_out)
                                vec.tensor_scalar(d[:], d[:], 1e-6, None, ALU.add).then_inc(sig("den"), 1)
                                dve.wait_ge(sig("den"), r + 1)
                            if 4 <= h < 4 + KD:
                                d = den[r % 2][:, h - 4, :]
                                vec.reciprocal(d, d).then_inc(sig("inverse"), 1)

                    def output(r):
                        dve.wait_ge(sig("inverse"), KD * (r + 1))
                        dve.wait_ge(sig("weighted"), H * (r + 1))
                        for t in range(TB):
                            ts = slice(t * P, (t + 1) * P)
                            vec.tensor_tensor(cT[:, :, ts], acc[t][:, 0:D].rearrange("p (m t) -> p m t", m=KD), den[r % 2][:, :, ts],
                                              ALU.mult).then_inc(sig("cT"), 1)
                        dve.wait_ge(sig("projected"), r + 1)
                        if r:
                            dve.wait_ge(sig("added"), r)
                        vec.tensor_tensor(y[:], out_bank[:].rearrange("p (t d) -> p t d", t=TB), wide(bo), ALU.add).then_inc(sig("out_read"), 1)
                        dve.wait_ge(sig("out_read"), r + 1)
                        xr = c.x[:, bass.ts(row_of(r), TB), :]
                        vec.tensor_tensor(xr, xr, y[:], ALU.add).then_inc(sig("added"), 1)

                    for stage, r in stages:
                        {"project": project, "attend": attend, "output": output}[stage](r)
            sig.clear()
        sig.close()




def layer0_attn(c):
    nc, w = c.nc, c.dram
    H, HD, DI, KC = 32, 64, 2048, 4
    MH = H * 16 // P
    MX = 18
    NG, GC = 4, BLK
    xt = c.ctxT[:].rearrange("p k n -> p (k n)").rearrange("p (t e) -> p t e", t=TB)
    v = c.ctx[:].rearrange("p a d -> p (a d)").rearrange("p (t e) -> p t e", t=TB)
    yzT = c.ctx[:].rearrange("p a d -> p (a d)").rearrange("p (k t) -> p k t", t=T)
    with ExitStack() as stack:
        sb = c.tiles(stack, "L0a")
        wz, wx, wd = sb("wz", [P, KD, DI]), sb("wx", [P, KD, MX * P]), sb("wd", [P, 2, KD, MH * P])
        wout = sb("wout", [P, DI // P, D])
        normalise(c, "n0a", c.x, dst=c.ctx, dstT=c.xT, loads=[(wx[:], w["L0a_wx"]), (wd[:, 0], w["L0a_wdl"]), (wd[:, 1], w["L0a_wdt"]),
                                                              (wz[:], w["L0a_wz"]), (wout[:], w["L0a_wout"])])
        norm = sb("norm", [P, DI // P])
        bz, bx, bd = sb("bz", [P, DI]), sb("bx", [P, MX]), sb("bd", [P, 2, MH])
        conv = sb("conv", [P, MX, KC])
        lcol, nega, dtb = sb("lcol", [P, MH]), sb("nega", [P, MH]), sb("dtb", [P, MH])
        dh, bo = sb("dh", [P, H]), sb("bo", [P, D])
        pick = sb("pick", [P, 8, P])
        um, vm, tri, last_row = sb("um", [P, T]), sb("vm", [P, P]), sb("tri", [P, P]), sb("last_row", [P, P])
        ones = sb("ones", [P, P])
        row = lambda n: w[n].rearrange("(a n) -> a n", a=1)
        c.load("L0a_ld", [(norm[:], w["L0a_norm"]), (bz[:], row("L0a_bz").to_broadcast([P, DI])),
                          (bx[:], w["L0a_bx"]), (bd[:], w["L0a_bd"]), (conv[:], w["L0a_conv"]), (lcol[:], w["L0a_l"]),
                          (nega[:], w["L0a_alog"]), (dtb[:], w["L0a_dtb"]), (dh[:], row("L0a_d").to_broadcast([P, H])),
                          (bo[:], row("L0a_bo").to_broadcast([P, D])), (pick[:], w["L0a_pick"]), (um[:], w["L0a_u"]),
                          (vm[:], w["L0a_v"]), (tri[:], w["tri_strict_ones"][:, 0, :]), (last_row[:], w["last_row"]),
                          (ones[:], w["tri_strict_ones"][:, 1, :])])
        xb = sb("xb", [P, KD, T])
        xc = [sb(f"xc{i}", [P, 2, KC - 1 + T]) for i in range(3)]
        xf = [sb(f"xf{i}", [P, 2, T]) for i in range(3)]
        bc = sb("bc", [P, 2, T])
        pre, sp, ex1 = sb("pre", [P, 2, MH, T]), sb("sp", [P, 2, MH, T]), sb("soft", [P, 2, MH, T])
        gcT, g, R = sb("gcT", [P, MH, T]), ex1[:, 0], ex1[:, 1]
        dt, gc, lam0, lam8 = (sb(n, [P, TB, H]) for n in ("dt", "gc", "lam0", "lam8"))
        ngc, coef = sb("ngc", [P, TB, H]), sb("coef", [P, TB, H])
        sfac, tfac = sb("sfac", [P, H]), sb("tfac", [P, H])
        qkd, qko, qdiag = sb("qkd", [P, TB, P]), sb("qko", [P, P]), sb("qdiag", [P, TB])
        wv = sb("wv", [P, DI])
        dtmp = wv[:, 0:T].rearrange("p (t s) -> p t s", t=TB)
        ident16, never16 = sb("ident16", [P, P], BF16), sb("never16", [P, P], BF16)
        ru = [sb(f"ru{i}", [P, 2, T]) for i in range(2)]
        ex = [sb(f"ex{i}", [P, 2, T]) for i in range(2)]
        att = [sb(f"att{i}", [P, 2, T]) for i in range(2)]
        spare = pre[:].rearrange("p i m t -> p (i m t)")
        tmp, y = spare[:, 0:GC], spare[:, GC:2 * GC].rearrange("p (t d) -> p t d", t=TB)
        zb = [spare[:, 2 * GC:3 * GC], spare[:, 3 * GC:4 * GC]]
        ss = sb("ss", [P, TB, 4])

        sig = Signals(nc, "L0a_c")
        with nc.Block() as block:
            @block.scalar
            def _(act):
                nc.scalar.activation(nega[:], nega[:], ACT.Exp).then_inc(sig("a"), 1)

            @block.vector
            def _(dve):
                vec = nc.vector
                dve.wait_ge(sig("a"), 1)
                vec.tensor_scalar(nega[:], nega[:], -1.0, None, ALU.mult)
                vec.tensor_tensor(bd[:, 0, :], bd[:, 0, :], lcol[:], ALU.mult)
                vec.tensor_tensor(bd[:, 1, :], bd[:, 1, :], dtb[:], ALU.add)
                for i in range(3):
                    vec.memset(xc[i][:], 0.0)
                vec.tensor_copy(ident16[:], c.ident[:])
                vec.tensor_scalar(never16[:], tri[:], -1.0, 1e30, ALU.add, ALU.mult)
                for k in range(DI // P):
                    vec.tensor_scalar(wout[:, k, :], wout[:, k, :], norm[:, k:k + 1], None, ALU.mult)
        sig.clear()
        sig.close()

        sig = Signals(nc, "L0a")
        with nc.Fori(0, B) as b:
            with nc.Block() as block:
                ra = Ring(sig, "ra", c.banks[0:2])
                rv = Ring(sig, "rv", c.banks[2:4])
                rx = Ring(sig, "rx", c.banks[5:7])
                qk_bank, y_bank, off_bank = c.banks[4], c.banks[5:7], c.banks[7]
                across = (c.banks[7], c.banks[4])
                NPX = MX // 2
                NPH = H // 2
                A_EXP = 4 + NPX

                @block.tensor
                def _(pe):
                    mm, tp = nc.tensor.matmul, nc.tensor.transpose

                    def project(p):
                        bank = ra.claim(pe)
                        for j in range(2):
                            for k in range(KD):
                                last = mm(bank[:, j * T:(j + 1) * T], wx[:, k, (2 * p + j) * P:(2 * p + j + 1) * P], xb[:, k, :],
                                          start=(k == 0), stop=(k == KD - 1))
                        ra.fill(last)

                    def turn(p):
                        pe.wait_ge(sig("silu"), p + 1)
                        bank = rx.claim(pe)
                        for t in range(TB):
                            for j in range(2):
                                last = tp(bank[:, t * T + j * P:t * T + (j + 1) * P], xf[p % 3][:, j, t * P:(t + 1) * P], c.ident[:])
                        rx.fill(last)

                    pe.wait_ge(sig("sliced"), 1)
                    for i in range(2):
                        for m in range(0, MH, 2):
                            bank = ra.claim(pe)
                            for j in range(2):
                                for k in range(KD):
                                    last = mm(bank[:, j * T:(j + 1) * T], wd[:, i, k, (m + j) * P:(m + j + 1) * P], xb[:, k, :],
                                              start=(k == 0), stop=(k == KD - 1))
                            ra.fill(last)
                    for p in range(3):
                        project(p)
                    pe.wait_ge(sig("silu"), 1)
                    mm(qk_bank[:, 0:T], bc[:, 0, 0:P], bc[:, 1, :], start=True, stop=True)
                    mm(qk_bank[:, T:T + P], bc[:, 0, P:T], bc[:, 1, P:T], start=True, stop=True).then_inc(sig("qk"), 1)
                    for n, a in enumerate((sp[:, 1], sp[:, 0], gcT)):
                        pe.wait_ge(sig("rows"), (1, 1, 2)[n])
                        for t in range(TB):
                            bank = rv.claim(pe)
                            for m in range(MH):
                                last = tp(bank[:, m * P:(m + 1) * P], a[:, m, t * P:(t + 1) * P], c.ident[:])
                            rv.fill(last)
                    for p in range(3, NPX):
                        project(p)
                        turn(p - 2)
                    pe.wait_ge(sig("gc_tok"), 1)
                    mm(off_bank[:, 0:H], last_row[:], gc[:, 0, :], start=True, stop=True).then_inc(sig("total"), 1)
                    turn(NPX - 2)
                    turn(NPX - 1)
                    pe.wait_ge(sig("R"), 1)
                    for i in range(NPH + 2):
                        if i < NPH:
                            bank = rv.claim(pe)
                            for j in range(2):
                                h = 2 * i + j
                                last = mm(bank[:, j * T:(j + 1) * T], pick[:, h % 8, :], R[:, h // 8, :], start=True, stop=True)
                            rv.fill(last)
                        if 1 <= i <= NPH:
                            bank = ra.claim(pe)
                            pe.wait_ge(sig("ru"), i)
                            mm(bank[:], vm[:], ru[(i - 1) % 2][:].rearrange("p j t -> p (j t)"), start=True, stop=False)
                            ra.fill(mm(bank[:].rearrange("p (j t) -> p j t", t=P), ident16[:],
                                       never16[:].unsqueeze(1).to_broadcast([P, 4, P]), start=False, stop=True))
                        if i >= 2:
                            q = i - 2
                            if q % 4 == 0:
                                gi = q // 4
                                if gi == 0:
                                    pe.wait_ge(sig("wv"), 1)
                                if gi >= 2:
                                    pe.wait_ge(sig("across_used"), gi - 1)
                                mm(across[gi % 2][:], qko[:], wv[:, gi * GC:(gi + 1) * GC], start=True, stop=True)
                                if gi:
                                    pe.wait_ge(sig("y_used"), gi)
                            pe.wait_ge(sig("att"), q + 1)
                            for j in range(2):
                                h = 2 * q + j
                                for t in range(TB):
                                    last = mm(y_bank[t][:, (h % 8) * HD:(h % 8 + 1) * HD], att[q % 2][:, j, t * P:(t + 1) * P],
                                              v[:, t, h * HD:(h + 1) * HD], start=True, stop=True)
                            last.then_inc(sig("weighted"), 1)
                    for gi in range(NG):
                        for t in range(TB):
                            bank = rv.claim(pe)
                            for k in range(KD):
                                last = mm(bank[:], xb[:, k, t * P:(t + 1) * P], wz[:, k, gi * GC:(gi + 1) * GC], start=(k == 0), stop=(k == KD - 1))
                            rv.fill(last)
                    for k in range(0, DI // P, 2):
                        bank = ra.claim(pe)
                        pe.wait_ge(sig("gated"), 2 * (k // 4) + 2)
                        for j in range(2):
                            for t in range(TB):
                                last = tp(bank[:, j * T + t * P:j * T + (t + 1) * P], xt[:, t, (k + j) * P:(k + j + 1) * P], c.ident[:])
                        ra.fill(last)
                    pe.wait_ge(ra.emptied, A_EXP + NPH + DI // P // 2)
                    for t in range(TB):
                        for k in range(DI // P):
                            last = mm(off_bank[:, t * D:(t + 1) * D], yzT[:, k, t * P:(t + 1) * P], wout[:, k, :],
                                      start=(k == 0), stop=(k == DI // P - 1))
                    last.then_inc(sig("projected"), 1)

                @block.scalar
                def _(act):
                    a = nc.scalar.activation
                    ch = Chain(act, sig("act_chain"))

                    def biased(p):
                        bank = ra.take(act)
                        if p >= 3:
                            act.wait_ge(sig("conv"), 2 * (p - 2))
                        for j in range(2):
                            last = a(xc[p % 3][:, j, KC - 1:], bank[:, j * T:(j + 1) * T], ACT.Identity, bias=bx[:, 2 * p + j:2 * p + j + 1])
                        ra.empty(last)

                    def first_tap(p):
                        act.wait_ge(ra.emptied, 4 + p + 1)
                        if p >= 4:
                            act.wait_ge(rx.filled, p - 3)
                        elif p == 3:
                            act.wait_ge(sig("silu"), 1)
                        for j in range(2):
                            a(xf[p % 3][:, j, :], xc[p % 3][:, j, 0:T], ACT.Copy, scale=conv[:, 2 * p + j, 0:1]).then_inc(sig("tap"), 1)

                    def take_x(p):
                        bank = rx.take(act)
                        rx.empty(a(xt[:, :, (p - 1) * T:p * T], bank[:].rearrange("p (t e) -> p t e", t=TB), ACT.Copy))

                    def silu(p):
                        act.wait_ge(sig("conv"), 2 * p + 2)
                        a((bc if p == 0 else xf[p % 3])[:], xf[p % 3][:], ACT.Silu).then_inc(sig("silu"), 1)

                    a(xb[:], c.xT[:, :, bass.ts(b, T)], ACT.Copy).then_inc(sig("sliced"), 1)
                    for i in range(2):
                        for m in range(0, MH, 2):
                            bank = ra.take(act)
                            for j in range(2):
                                last = a(pre[:, i, m + j, :], bank[:, j * T:(j + 1) * T], ACT.Identity, bias=bd[:, i, m + j:m + j + 1],
                                         scale=lcol[:, m + j:m + j + 1] if i == 0 else 1.0)
                            ra.empty(last)
                    act.wait_ge(ra.emptied, 4)
                    ch.link(a(ex1[:], pre[:], ACT.Abs))
                    ch.link(a(ex1[:], ex1[:], ACT.Exp, scale=-1.0))
                    a(ex1[:], ex1[:], ACT.Ln, bias=1.0).then_inc(sig("log1p"), 1)
                    biased(0)
                    biased(1)
                    first_tap(0)
                    act.wait_ge(sig("lam_floor"), 1)
                    a(R, R, ACT.Ln).then_inc(sig("lnlam"), 1)
                    first_tap(1)
                    silu(0)
                    for p in range(2, NPX):
                        biased(p)
                        first_tap(p)
                        silu(p - 1)
                        if p >= 4:
                            take_x(p - 3)
                    silu(NPX - 1)
                    for p in range(NPX - 3, NPX):
                        take_x(p)
                    act.wait_ge(sig("total_diff"), 1)
                    a(sfac[:], sfac[:], ACT.Exp).then_inc(sig("factors"), 1)
                    a(tfac[:], tfac[:], ACT.Exp).then_inc(sig("factors"), 1)
                    for i in range(NPH):
                        bank = ra.take(act)
                        if i >= 2:
                            act.wait_ge(sig("att"), i - 1)
                        for j in range(2):
                            for t in range(TB):
                                last = a(ex[i % 2][:, j, t * P:(t + 1) * P], bank[:, j * T + t * P:j * T + (t + 1) * P], ACT.Exp,
                                         bias=ngc[:, t, 2 * i + j:2 * i + j + 1])
                        ra.empty(last)
                    for i in range(NG * TB):
                        act.wait_ge(sig("zb"), i + 1)
                        a(zb[i % 2], zb[i % 2], ACT.Silu).then_inc(sig("z_silu"), 1)
                    act.wait_ge(sig("gated"), NG * TB)
                    for k in range(0, DI // P, 2):
                        bank = ra.take(act)
                        ra.empty(a(yzT[:, k:k + 2, :], bank[:].rearrange("p (k t) -> p k t", k=2), ACT.Copy))
                    for t in range(TB):
                        a(wv[:], xt[:, t, :], ACT.Square, accum_out=ss[:, t, 0:1]).then_inc(sig("squares"), 1)
                        act.wait_ge(sig("squares"), t + 1)
                    act.wait_ge(sig("mean_sq"), 1)
                    a(ss[:, :, 2], ss[:, :, 1], ACT.Sqrt).then_inc(sig("rms"), 1)

                @block.gpsimd
                def _(pool):
                    tt = nc.gpsimd.tensor_tensor
                    by_head = lambda a, n: a.rearrange("p t (h d) -> p t h d", h=n)
                    pool.wait_ge(sig("capped"), 1)
                    pool.wait_ge(sig("rows"), 2)
                    tt(R, R, gcT[:], ALU.add).then_inc(sig("R"), 1)
                    for p in range(1, NPX):
                        pool.wait_ge(rx.emptied, p)
                        if p == 1:
                            pool.wait_ge(sig("gc_tok"), 1)
                            pool.wait_ge(sig("coef"), 1)
                        cs, hs = slice((p - 1) * T, p * T), slice((p - 1) * 4, p * 4)
                        tt(by_head(v[:, :, cs], 4), by_head(xt[:, :, cs], 4), dt[:, :, hs].unsqueeze(3).to_broadcast([P, TB, 4, HD]),
                           ALU.mult).then_inc(sig("v"), 1)
                    for p in range(1, NPX):
                        pool.wait_ge(sig("v"), p)
                        cs, hs = slice((p - 1) * T, p * T), slice((p - 1) * 4, p * 4)
                        tt(by_head(xt[:, :, cs], 4), by_head(xt[:, :, cs], 4), coef[:, :, hs].unsqueeze(3).to_broadcast([P, TB, 4, HD]),
                           ALU.mult).then_inc(sig("direct"), 1)
                    pool.wait_ge(sig("combined"), NG)
                    for n in range(NG * TB):
                        pool.wait_ge(sig("z_silu"), n + 1)
                        cs = slice(n // TB * GC, (n // TB + 1) * GC)
                        tt(xt[:, n % TB, cs], xt[:, n % TB, cs], zb[n % 2], ALU.mult).then_inc(sig("gated"), 1)

                @block.vector
                def _(dve):
                    ch = Chain(dve, sig("dve_chain"))
                    vec = nc.vector

                    def convolve(p):
                        for i in range(1, KC):
                            for j in range(2):
                                m = 2 * p + j
                                if i == 1:
                                    dve.wait_ge(sig("tap"), m + 1)
                                else:
                                    dve.wait_ge(sig("add_tap"), 4 * p + 2 * (i - 2) + j + 1)
                                vec.scalar_tensor_tensor(out=xf[p % 3][:, j, :], in0=xc[p % 3][:, j, i:i + T], scalar=conv[:, m, i:i + 1],
                                                         in1=xf[p % 3][:, j, :], op0=ALU.mult,
                                                         op1=ALU.add).then_inc(sig("conv" if i == KC - 1 else "add_tap"), 1)

                    dve.wait_ge(sig("log1p"), 1)
                    f = lambda a: a.rearrange("p i m t -> p (i m t)")
                    vec.scalar_tensor_tensor(out=f(sp[:]), in0=f(pre[:]), scalar=0.0, in1=f(ex1[:]), op0=ALU.max, op1=ALU.add).then_inc(sig("rows"), 1)
                    dve.wait_ge(sig("rows"), 1)
                    vec.tensor_scalar(R, sp[:, 0], 1e-9, None, ALU.max).then_inc(sig("lam_floor"), 1)
                    for m in range(MH):
                        last = vec.tensor_scalar(g[:, m, :], sp[:, 1, m, :], nega[:, m:m + 1], None, ALU.mult)
                    ch.link(last)
                    for m in range(MH):
                        for t in range(TB):
                            ts = slice(t * P, (t + 1) * P)
                            last = vec.tensor_tensor_scan(gcT[:, m, ts], ones[:], g[:, m, ts], 0.0, ALU.mult, ALU.add)
                    last.then_inc(sig("rows"), 1)
                    convolve(0)
                    convolve(1)
                    dve.wait_ge(sig("lnlam"), 1)
                    vec.tensor_tensor(R, R, pre[:, 0], ALU.min).then_inc(sig("capped"), 1)
                    convolve(2)
                    heads = lambda bank, j: bank[:].rearrange("p (h j) -> p h j", j=16)[:, :, j]
                    for t in range(TB):
                        bank = rv.take(dve)
                        rv.empty(vec.tensor_copy(dt[:, t, :], heads(bank, 0)))
                    for t in range(TB):
                        bank = rv.take(dve)
                        vec.tensor_copy(lam0[:, t, :], heads(bank, 0))
                        rv.empty(vec.tensor_copy(lam8[:, t, :], heads(bank, 8)))
                    for t in range(TB):
                        bank = rv.take(dve)
                        rv.empty(vec.tensor_copy(gc[:, t, :], heads(bank, 0)))
                    dve.wait_ge(rv.emptied, 6)
                    vec.sem_inc(sig("gc_tok"), 1)
                    vec.tensor_scalar(ngc[:], gc[:], -1.0, None, ALU.mult)
                    dve.wait_ge(sig("qk"), 1)
                    idw = c.ident[:]
                    vec.tensor_tensor(dtmp[:, 0, :], qk_bank[:, 0:P], idw, ALU.mult)
                    ch.link(vec.tensor_tensor(dtmp[:, 1, :], qk_bank[:, T:T + P], idw, ALU.mult))
                    ch.link(vec.tensor_reduce(qdiag[:], dtmp, AX.X, ALU.add))
                    vec.tensor_copy(qkd[:, 0, :], qk_bank[:, 0:P])
                    vec.tensor_copy(qkd[:, 1, :], qk_bank[:, T:T + P])
                    vec.tensor_copy(qko[:], qk_bank[:, P:T])
                    ch.link(vec.tensor_tensor(coef[:], dt[:], lam0[:], ALU.mult))
                    ch.link(vec.tensor_tensor(coef[:], coef[:], qdiag[:].unsqueeze(2).to_broadcast([P, TB, H]), ALU.mult))
                    vec.tensor_tensor(coef[:], coef[:], dh[:].unsqueeze(1).to_broadcast([P, TB, H]), ALU.add).then_inc(sig("coef"), 1)
                    for p in range(3, NPX):
                        convolve(p)
                    dve.wait_ge(sig("total"), 1)
                    vec.tensor_tensor(sfac[:], off_bank[:, 0:H], gc[:, 0, :], ALU.subtract)
                    vec.tensor_copy(tfac[:], gc[:, 1, :]).then_inc(sig("total_diff"), 1)
                    dve.wait_ge(sig("factors"), 2)
                    ch.link(vec.tensor_tensor(tfac[:], tfac[:], lam8[:, 1, :], ALU.mult))
                    dve.wait_ge(sig("v"), NPX - 1)
                    vec.tensor_tensor(wv[:].rearrange("p (h d) -> p h d", h=H), v[:, 0, :].rearrange("p (h d) -> p h d", h=H),
                                      sfac[:].unsqueeze(2).to_broadcast([P, H, HD]), ALU.mult).then_inc(sig("wv"), 1)

                    def combine(gi):
                        dve.wait_ge(sig("weighted"), 4 * gi + 4)
                        cs, hs = slice(gi * GC, (gi + 1) * GC), slice(gi * 8, gi * 8 + 8)
                        by_head = lambda a: a.rearrange("p (h d) -> p h d", h=8)
                        if gi == 0:
                            dve.wait_ge(sig("direct"), NPX - 1)
                        for t in range(TB):
                            last = vec.tensor_tensor(xt[:, t, cs], xt[:, t, cs], y_bank[t][:], ALU.add)
                        last.then_inc(sig("y_used"), 1)
                        vec.tensor_tensor(by_head(tmp), by_head(across[gi % 2][:]), tfac[:, hs].unsqueeze(2).to_broadcast([P, 8, HD]),
                                          ALU.mult).then_inc(sig("across_used"), 1)
                        dve.wait_ge(sig("y_used"), gi + 1)
                        dve.wait_ge(sig("across_used"), gi + 1)
                        vec.tensor_tensor(xt[:, 1, cs], xt[:, 1, cs], tmp, ALU.add).then_inc(sig("combined"), 1)

                    for i in range(NPH + 1):
                        if i < NPH:
                            bank = rv.take(dve)
                            if i >= 2:
                                dve.wait_ge(ra.filled, A_EXP + i - 1)
                            ins = vec.tensor_tensor(ru[i % 2][:], bank[:].rearrange("p (j t) -> p j t", j=2),
                                                    um[:].unsqueeze(1).to_broadcast([P, 2, T]), ALU.mult)
                            ins.then_inc(sig("ru"), 1)
                            dve.wait_ge(sig("ru"), i + 1)
                            vec.sem_inc(rv.emptied, 1)
                        if i >= 5 and i % 4 == 1:
                            combine(i // 4 - 1)
                        if i >= 1:
                            q = i - 1
                            dve.wait_ge(ra.emptied, A_EXP + q + 1)
                            if q >= 2:
                                dve.wait_ge(sig("weighted"), q - 1)
                            vec.tensor_tensor(att[q % 2][:], ex[q % 2][:], qkd[:].rearrange("p t s -> p (t s)").unsqueeze(1).to_broadcast([P, 2, T]),
                                              ALU.mult).then_inc(sig("att"), 1)
                    combine(NG - 1)
                    n = 0
                    for gi in range(NG):
                        for t in range(TB):
                            bank = rv.take(dve)
                            cs = slice(gi * GC, (gi + 1) * GC)
                            if n >= 2:
                                dve.wait_ge(sig("gated"), n - 1)
                            ins = vec.tensor_tensor(zb[n % 2], bank[:], bz[:, cs], ALU.add)
                            ins.then_inc(sig("zb"), 1)
                            dve.wait_ge(sig("zb"), n + 1)
                            vec.sem_inc(rv.emptied, 1)
                            n += 1
                    dve.wait_ge(sig("squares"), TB)
                    vec.tensor_scalar(ss[:, :, 1], ss[:, :, 0], 1.0 / DI, 1e-5, ALU.mult, ALU.add).then_inc(sig("mean_sq"), 1)
                    dve.wait_ge(sig("rms"), 1)
                    ch.link(vec.reciprocal(ss[:, :, 3], ss[:, :, 2]))
                    dve.wait_ge(sig("projected"), 1)
                    for t in range(TB):
                        last = vec.scalar_tensor_tensor(out=y[:, t, :], in0=off_bank[:, t * D:(t + 1) * D], scalar=ss[:, t, 3:4], in1=bo[:],
                                                        op0=ALU.mult, op1=ALU.add)
                    ch.link(last)
                    vec.tensor_tensor(c.x[:, bass.ts(b, TB), :], c.x[:, bass.ts(b, TB), :], y, ALU.add)
            sig.clear()
        sig.close()


def pack(inputs):
    i = {k: np.asarray(v) for k, v in inputs.items()}
    a = {}

    def rows(w):
        s = w.shape
        return np.ascontiguousarray(np.moveaxis(w.reshape(*s[:-2], s[-2] // P, P, s[-1]), -3, -2))

    def cols(v):
        return np.ascontiguousarray(np.swapaxes(v.reshape(*v.shape[:-1], v.shape[-1] // P, P), -1, -2))

    by_tile = lambda v: cols(v).transpose(1, 0, 2)
    tok = lambda v: np.ascontiguousarray(v.reshape(NT, P, D).transpose(1, 0, 2))
    tr = lambda v: np.swapaxes(v, -1, -2)
    a["x"], a["ctx"] = tok(i["x"]), tok(i["ctx_1024"])
    a["ident"] = np.eye(P, dtype=np.float32)
    a["iota8"] = np.broadcast_to(np.arange(8, dtype=np.float32), (P, 8)).copy()
    earlier = (np.arange(P)[:, None] < np.arange(P)[None, :]).astype(np.float32)
    a["tri_strict_ones"] = np.stack([earlier, np.ones((P, P), np.float32)], 1)

    def experts(tag, gate, ups, lins, downs):
        a[f"{tag}_gate"] = rows(gate)
        a[f"{tag}_up"] = rows(np.concatenate(ups))
        if lins:
            a[f"{tag}_lin"] = rows(np.concatenate(lins))
        a[f"{tag}_down"] = rows(np.concatenate(downs))

    halves = lambda w: w.reshape(2, 256, D)
    experts("L0f", i["L0_ffn_gate_w"].T, [tr(i["L0_ffn_w1"]), tr(halves(i["L0_ffn_ws1"]))],
            [tr(i["L0_ffn_w3"]), tr(halves(i["L0_ffn_ws3"]))],
            [tr(i["L0_ffn_w2"]), i["L0_ffn_ws2"].T.reshape(2, 256, D)])
    a["L0f_gate_b"] = i["L0_ffn_gate_b"]
    a["L0f_up_b"] = by_tile(np.concatenate([i["L0_ffn_b1"], i["L0_ffn_bs1"].reshape(2, 256)]))
    a["L0f_lin_b"] = by_tile(np.concatenate([i["L0_ffn_b3"], i["L0_ffn_bs3"].reshape(2, 256)]))
    a["L0f_down_b"] = np.concatenate([i["L0_ffn_b2"], i["L0_ffn_bs2"][None], np.zeros((1, D), np.float32)])
    w1 = i["L2_ffn_w1"].reshape(8, D, 2, 512).transpose(0, 2, 1, 3).reshape(16, D, 512)
    experts("L2f", i["L2_ffn_switch_w"], [w1], None, [i["L2_ffn_w2"].reshape(16, 512, D)])
    a["L2f_gate_b"] = i["L2_ffn_switch_b"]
    a["L2f_up_b"] = by_tile(i["L2_ffn_b1"].reshape(16, 512))
    a["L2f_down_b"] = np.stack([i["L2_ffn_b2"], np.zeros_like(i["L2_ffn_b2"])], 1).reshape(16, D)
    experts("L3f", i["L3_ffn_gate_w"].T, [tr(i["L3_ffn_we_gate"]), tr(halves(i["L3_ffn_ws_gate"]))],
            [tr(i["L3_ffn_we_up"]), tr(halves(i["L3_ffn_ws_up"]))],
            [tr(i["L3_ffn_we_down"]), i["L3_ffn_ws_down"].T.reshape(2, 256, D)])
    pack_attention(i, a, rows, cols, tr)
    return {k: np.ascontiguousarray(v) for k, v in a.items()}


def pack_attention(i, a, rows, cols, tr):
    t = np.arange(P)
    dist = np.abs(t[:, None] - t[None, :])
    dist1 = np.abs(P + t[:, None] - np.arange(T)[None, :])
    a["twin"] = (t[:, None] // 16 % 2 == np.arange(2)).astype(np.float32)
    a["distance"] = np.concatenate([dist, dist1], 1).astype(np.float32)
    a["future_neg"] = np.where(t[None, :] > t[:, None], -1e30, 0.0).astype(np.float32)
    a["L1a_wq"], a["L1a_wk"] = rows(i["L1_attn_Wq"]), rows(i["L1_attn_Wk"])
    a["L1a_wv"], a["L1a_wo"] = rows(i["L1_attn_Wv"]), rows(i["L1_attn_Wo"])
    a["L1a_bo"], a["L1a_w"], a["L1a_v"] = i["L1_attn_bo"], i["L1_attn_w"], i["L1_attn_v"]
    a["L1x_wq"], a["L1x_wk"] = rows(i["L1_xattn_Wq"].T), rows(i["L1_xattn_Wk"].T)
    a["L1x_wv"], a["L1x_wo"] = rows(i["L1_xattn_Wv"].T), rows(i["L1_xattn_Wo"].T)
    a["L1x_bo"] = i["L1_xattn_bo"]
    a["mask_pairs"] = i["mask_Bx1xSxS2_ik0"].reshape(B, TB, P, T).transpose(0, 2, 1, 3)
    a["mask_keys"] = i["mask_Bx1xS2_ik0"]
    a["mask_bool"] = i["mask_BxS2_bk1"].reshape(B, 1, T)
    a["L3x_wq"], a["L3x_wo"] = rows(i["L3_xattn_Wq"]), rows(i["L3_xattn_Wo"])
    a["L3x_wk"], a["L3x_wv"] = rows(i["L3_xattn_Wkv"][:, :512]), rows(i["L3_xattn_Wkv"][:, 512:])
    a["L3x_ln"] = np.stack([cols(i[f"L3_xattn_ln_{n}"]) for n in ("l_g", "l_b", "x_g", "x_b")], 1)
    a["L3x_og"], a["L3x_ob"] = i["L3_xattn_ln_o_g"], i["L3_xattn_ln_o_b"]
    for n in ("up", "gate", "down"):
        o, k = i[f"L1_ffn_w_{n}"].shape
        a[f"L1f_{n}"] = i[f"L1_ffn_w_{n}"].reshape(o // P, P, k).transpose(1, 0, 2)
    a["L2a_c"] = i["L2_attn_C"].reshape(KD, P, 64).transpose(1, 0, 2)
    a["L2a_b"] = i["L2_attn_B"].T.reshape(KD, P, 64).transpose(1, 0, 2)
    a["L2a_a"], a["L2a_d"], a["L2a_ldt"] = i["L2_attn_A"], cols(i["L2_attn_D"]), cols(i["L2_attn_log_dt"])
    a["iota64"] = np.broadcast_to(np.arange(64, dtype=np.float32), (P, 64))
    a["L3a_wqk"] = rows(np.concatenate([i["L3_attn_Wq"].T, i["L3_attn_Wk"].T], 1))
    a["L3a_wv"], a["L3a_bv"] = rows(i["L3_attn_Wv"].T), i["L3_attn_bv"]
    a["L3a_bqk"] = np.concatenate([i["L3_attn_bq"], i["L3_attn_bk"]])
    a["L3a_gamma"], a["L3a_beta"] = i["L3_attn_gamma"], i["L3_attn_beta"]
    freq = (1.0 / 10000.0 ** (np.arange(0, D, 2, dtype=np.float32) / D)).astype(np.float32)
    ang = np.arange(T, dtype=np.float32)[:, None] * freq
    paired = lambda e, o: np.stack([e, o], -1).reshape(TB, P, D).transpose(1, 0, 2).astype(np.float32)
    a["rope_cos"], a["rope_sin"] = paired(np.cos(ang), np.cos(ang)), paired(-np.sin(ang), np.sin(ang))
    a["blockdiag16"] = np.where(t[:, None] // 16 == t[None, :] // 16, 1.0 / T, 0.0).astype(np.float32)
    upto = (t[:, None] <= t[None, :]).astype(np.float32)
    a["causal"] = np.concatenate([upto, np.ones((P, P), np.float32), upto], 1)
    for n in ("q", "k", "v"):
        a[f"L0x_w{n}"], b = rows(i[f"L0_xattn_W{n}"]), i[f"L0_xattn_b{n}"]
        a[f"L0x_b{n}"] = b if n == "k" else cols(b)
    a["L0x_wo"], a["L0x_bo"] = rows(i["L0_xattn_Wo"]), i["L0_xattn_bo"]

    wi, bi = i["L0_attn_in_proj_w"], i["L0_attn_in_proj_b"]
    order = np.concatenate([np.arange(4096, 4352), np.arange(2048, 4096)])
    a["L0a_wz"], a["L0a_bz"] = rows(wi[:2048].T), bi[:2048]
    a["L0a_wx"], a["L0a_bx"] = rows(wi[order].T), cols(bi[order])
    a["L0a_conv"] = i["L0_attn_conv_w"][order - 2048].reshape(18, P, 4).transpose(1, 0, 2)
    padded = lambda m: np.concatenate([m.reshape(32, 15, -1), np.zeros((32, 1, m.size // 480), m.dtype)], 1).reshape(512, -1)
    per_head = lambda m: np.repeat(m, 16, axis=0)
    a["L0a_wdl"], a["L0a_wdt"] = rows(padded(wi[4384:]).T), rows(per_head(wi[4352:4384]).T)
    a["L0a_bd"] = np.stack([cols(padded(bi[4384:])[:, 0]), cols(per_head(bi[4352:4384]))], 1)
    a["L0a_l"] = cols(padded(i["L0_attn_L"].reshape(480))[:, 0])
    a["L0a_alog"], a["L0a_dtb"] = cols(per_head(i["L0_attn_A_log"])), cols(per_head(i["L0_attn_dt_bias"]))
    a["L0a_d"], a["L0a_norm"] = i["L0_attn_D"], cols(i["L0_attn_norm_w"])
    a["L0a_wout"], a["L0a_bo"] = rows(i["L0_attn_out_proj_w"].T), i["L0_attn_out_proj_b"]
    pick, u, v = np.zeros((P, 8, P), np.float32), np.zeros((P, P), np.float32), np.zeros((P, P), np.float32)
    n = 0
    for k in range(7):
        for j in range(P >> (k + 1)):
            start, half = j << (k + 1), 1 << k
            v[n, start:start + half] = 1.0
            u[n, start + half:start + 2 * half] = 1.0
            for h in range(8):
                pick[h * 16 + k + 1, h, n] = 1.0
            n += 1
    a["L0a_pick"], a["L0a_u"], a["L0a_v"] = pick, np.concatenate([u, u], 1), v
    last_row = np.zeros((P, P), np.float32)
    last_row[P - 1] = 1.0
    a["last_row"] = last_row


LAYERS = {1: layer0_attn, 2: layer0_xattn, 3: layer0_ffn, 4: layer1_attn, 5: layer1_xattn, 6: layer1_ffn, 7: layer2_attn, 8: layer2_xattn, 9: layer2_ffn, 10: layer3_attn, 11: layer3_xattn, 12: layer3_ffn}


def program(nc, dram, out, layers):
    with ExitStack() as ctx:
        c = Core(nc, ctx, dram)
        c.load("first", [(c.x[:], dram["x"]), (c.ident[:], dram["ident"])])
        if layers[0] == 1:
            layer0_attn(c)
            layers = layers[1:]
        c.load("context", [(c.ctx[:], dram["ctx"])])
        transpose_tokens(c, "ctxT", c.ctx, c.ctxT)
        for n in layers:
            LAYERS[n](c)
        sig = Signals(nc, "last")
        with nc.Block() as block:
            @block.sync
            def _(sp):
                sp.dma_start(out, c.x[:]).then_inc(sig("stored"), 16)
                sp.wait_ge(sig("stored"), 16)
        sig.close()


def kernel(**inputs):
    import concourse.bacc as bacc
    from concourse.bass_utils import run_bass_kernel_spmd

    arrays = pack(inputs)
    nc = bacc.Bacc("TRN2", target_bir_lowering=False, num_devices=1)
    dram = {k: nc.dram_tensor(f"in_{k}", v.shape, mybir.dt.from_np(v.dtype), kind="ExternalInput").ap()
            for k, v in arrays.items()}
    out = nc.dram_tensor("out_x", (P, NT, D), F32, kind="ExternalOutput").ap()
    program(nc, dram, out, sorted(LAYERS))
    r = run_bass_kernel_spmd(nc, [{f"in_{k}": v for k, v in arrays.items()}], core_ids=[0])
    got = r.results[0]["out_x"]
    return np.ascontiguousarray(got.transpose(1, 0, 2)).reshape(B, T, D)
```

```python
from contextlib import ExitStack

import numpy as np

import concourse.bass as bass
from concourse import mybir

P = 128
B, T, D = 8, 256, 256
N = B * T
NT = N // P
KD = D // P
TB = T // P
BLK = 512
NBLK = N // BLK

F32 = mybir.dt.float32
I32 = mybir.dt.int32
BF16 = mybir.dt.bfloat16
F32R = mybir.dt.float32r
U8 = mybir.dt.uint8
ACT = mybir.ActivationFunctionType
ALU = mybir.AluOpType
AX = mybir.AxisListType
ROWS = 4
ROUND = 12582912.0


class Signals:

    def __init__(self, nc, tag):
        self.nc, self.tag, self.ctx, self.by_name = nc, tag, ExitStack(), {}

    def __call__(self, name):
        if name not in self.by_name:
            self.by_name[name] = self.ctx.enter_context(self.nc.semaphore(f"{self.tag}_{name}"))
        return self.by_name[name]

    def clear(self):
        for s in self.by_name.values():
            self.nc.sync.sem_clear(s)
        self.nc.all_engine_barrier()

    def close(self):
        self.ctx.close()


class Ring:

    def __init__(self, sig, name, bufs):
        self.filled, self.emptied, self.bufs = sig(name + "_filled"), sig(name + "_emptied"), bufs
        self.n_in = self.n_out = 0

    def claim(self, eng):
        if self.n_in >= len(self.bufs):
            eng.wait_ge(self.emptied, self.n_in - len(self.bufs) + 1)
        self.n_in += 1
        return self.bufs[(self.n_in - 1) % len(self.bufs)]

    def fill(self, ins):
        ins.then_inc(self.filled, 1)

    def take(self, eng):
        self.n_out += 1
        eng.wait_ge(self.filled, self.n_out)
        return self.bufs[(self.n_out - 1) % len(self.bufs)]

    def empty(self, ins):
        ins.then_inc(self.emptied, 1)


class Chain:

    def __init__(self, eng, sem):
        self.eng, self.sem, self.n = eng, sem, 0

    def link(self, ins):
        self.n += 1
        ins.then_inc(self.sem, 1)
        self.eng.wait_ge(self.sem, self.n)


class Core:

    def __init__(self, nc, ctx, dram):
        self.nc, self.dram = nc, dram
        sb = lambda name, shape, dt=F32: ctx.enter_context(nc.sbuf_tensor(name, shape, dt))
        self.x = sb("x_res", [P, NT, D])
        self.ctx = sb("ctx_tok", [P, NT, D])
        self.ctxT = sb("ctx_feat", [P, KD, N])
        self.xT = sb("x_feat", [P, KD, N])
        self.ident = sb("ident", [P, P])
        self.banks = [ctx.enter_context(nc.psum_tensor(f"bank{i}", [P, BLK], F32)) for i in range(8)]

    def tiles(self, stack, tag):
        return lambda name, shape, dt=F32: stack.enter_context(self.nc.sbuf_tensor(f"{tag}_{name}", shape, dt))

    def load(self, tag, pairs):
        nc, sig = self.nc, Signals(self.nc, tag)
        with nc.Block() as block:

            @block.sync
            def _(sp):
                for dst, src in pairs[0::2]:
                    sp.dma_start(dst, src).then_inc(sig("loaded_sp"), 16)
                sp.wait_ge(sig("loaded_sp"), 16 * len(pairs[0::2]))

            @block.scalar
            def _(act):
                for dst, src in pairs[1::2]:
                    act.dma_start(dst, src).then_inc(sig("loaded_act"), 16)
                if len(pairs) > 1:
                    act.wait_ge(sig("loaded_act"), 16 * len(pairs[1::2]))
        sig.clear()
        sig.close()


def transpose_tokens(c, tag, src, dstT):
    nc = c.nc
    sig = Signals(nc, tag)
    with nc.Block() as block:
        ring = Ring(sig, "turned", c.banks)

        @block.tensor
        def _(pe):
            for n in range(NBLK):
                for k in range(KD):
                    bank = ring.claim(pe)
                    for j in range(4):
                        last = nc.tensor.transpose(bank[:, j * P:(j + 1) * P], src[:, 4 * n + j, k * P:(k + 1) * P], c.ident[:])
                    ring.fill(last)

        @block.scalar
        def _(act):
            for n in range(NBLK):
                for k in range(KD):
                    bank = ring.take(act)
                    ring.empty(nc.scalar.activation(dstT[:, k, n * BLK:(n + 1) * BLK], bank[:], ACT.Copy))
    sig.clear()
    sig.close()


def normalise(c, tag, src, dst=None, dstT=None, gain=None, shift=None, eps=1e-5, loads=()):
    nc = c.nc
    sig = Signals(nc, tag)
    with ExitStack() as stack:
        sb = c.tiles(stack, tag)
        stats = sb("stats", [P, NT, 6])
        mv = sb("mv", [P, NT, 2])
        rstd = sb("rstd", [P, NT, 3])
        xs = None if dst is not None else [sb(f"xs{i}", [P, 4, D]) for i in range(2)]
        rows_of = lambda n: dst[:, 4 * n:4 * n + 4, :] if dst is not None else xs[n % 2][:]
        with nc.Block() as block:
            @block.sync
            def _(sp):
                for to, come_from in loads:
                    sp.dma_start(to, come_from).then_inc(sig("loaded"), 16)
                if loads:
                    sp.wait_ge(sig("loaded"), 16 * len(loads))

            @block.vector
            def _(dve):
                for t in range(NT):
                    last = nc.vector.bn_stats(stats[:, t, :], src[:, t, :])
                last.then_inc(sig("stats"), 1)
                dve.wait_ge(sig("stats"), 1)
                for t in range(NT):
                    last = nc.vector.bn_aggr(mv[:, t, :], stats[:, t, :])
                last.then_inc(sig("mean_var"), 1)
                dve.wait_ge(sig("mean_var"), 1)
                nc.vector.tensor_scalar_add(rstd[:, :, 0], mv[:, :, 1], eps).then_inc(sig("var_eps"), 1)
                dve.wait_ge(sig("std"), 1)
                nc.vector.reciprocal(rstd[:, :, 2], rstd[:, :, 1]).then_inc(sig("rstd"), 1)
                dve.wait_ge(sig("rstd"), 1)
                for n in range(NBLK):
                    if dst is None and n >= 2:
                        dve.wait_ge(sig("transposed"), KD * (n - 1))
                    for j in range(4):
                        t = 4 * n + j
                        last = nc.vector.tensor_scalar(rows_of(n)[:, j, :], src[:, t, :], mv[:, t, 0:1], rstd[:, t, 2:3],
                                                       ALU.subtract, ALU.mult)
                    last.then_inc(sig("normed"), 1)

            @block.tensor
            def _(pe):
                if dstT is not None:
                    for n in range(NBLK):
                        pe.wait_ge(sig("normed"), n + 1)
                        for k in range(KD):
                            bank = c.banks[2 * n + k]
                            for j in range(4):
                                last = nc.tensor.transpose(bank[:, j * P:(j + 1) * P], rows_of(n)[:, j, k * P:(k + 1) * P], c.ident[:])
                            last.then_inc(sig("transposed"), 1)

            @block.scalar
            def _(act):
                act.wait_ge(sig("var_eps"), 1)
                nc.scalar.activation(rstd[:, :, 1], rstd[:, :, 0], ACT.Sqrt).then_inc(sig("std"), 1)
                if dstT is not None:
                    for n in range(NBLK):
                        for k in range(KD):
                            act.wait_ge(sig("transposed"), KD * n + k + 1)
                            out, bank = dstT[:, k, n * BLK:(n + 1) * BLK], c.banks[2 * n + k]
                            if gain is None:
                                nc.scalar.activation(out, bank[:], ACT.Copy)
                            else:
                                nc.scalar.activation(out, bank[:], ACT.Identity, bias=shift[:, k:k + 1], scale=gain[:, k:k + 1])
        sig.clear()
    sig.close()


def mixture(c, tag, n_routed, n_shared, M, gated, top, biases, renorm=False, capacity=None, parts=1, per_turn=2):
    nc = c.nc
    E = n_routed * parts + n_shared
    R = n_routed
    w = c.dram
    F = M * P
    act_fn = ACT.Silu if gated else ACT.Gelu_apprx_tanh
    with ExitStack() as stack:
        sb = c.tiles(stack, tag)
        comb = sb("comb", [P, E, NT])
        combT = sb("combT", [E, NT, P])
        down_b = sb("down_b", [E, D])
        xh, xl = sb("xh", [P, KD, N], F32R), sb("xl", [P, KD, N], F32R)
        b_all = sb("b_all", [P, 1 + gated, E, M])
        n_kinds = 2 + gated
        raw = [sb(f"raw{i}", [P, n_kinds, KD * F]) for i in range(2)]
        wh = [sb(f"wh{i}", [P, n_kinds, KD * F], F32R) for i in range(2)]
        wl = [sb(f"wl{i}", [P, n_kinds, KD * F], F32R) for i in range(2)]
        rising = lambda a, kind: a[:, kind, :].rearrange("p (k f) -> p k f", k=KD)
        falling = lambda a: a[:, n_kinds - 1, :].rearrange("p (m d) -> p m d", m=M)
        h = [sb(f"h{i}", [P, BLK]) for i in range(2)]
        hh = [sb(f"hh{i}", [P, M, BLK], F32R) for i in range(2)]
        hl = [sb(f"hl{i}", [P, M, BLK], F32R) for i in range(2)]
        silu = [sb(f"silu{i}", [P, BLK]) for i in range(2)] if gated else None
        comb_t = sb("comb_t", [P, per_turn, NT])
        bias_t = sb("bias_t", [P, 1 + gated, per_turn, M])
        kinds = ("up", "lin", "down") if gated else ("up", "down")

        def fetch(sp, i, e, sem):
            for j, kind in enumerate(kinds):
                sp.dma_start(raw[i][:, j, :], w[f"{tag}_{kind}"][e].rearrange("p a b -> p (a b)")).then_inc(sem, 16)

        def split(pool, i, high, sem, count=1):
            nc.gpsimd.tensor_copy(wh[i][:], raw[i][:]).then_inc(high, 1)
            pool.wait_ge(high, count)
            nc.gpsimd.tensor_tensor(wl[i][:], raw[i][:], wh[i][:].bitcast(F32), ALU.subtract).then_inc(sem, 1)

        with ExitStack() as inner:
            sc = c.tiles(inner, tag)
            gate = sc("gate", [P, KD, R])
            gate_b = sc("gate_b", [P, R])
            iota = sc("iota", [P, R])
            trist = sc("trist", [P, 2, P])
            pairs = [(gate[:], w[f"{tag}_gate"]), (iota[:], w["iota8"])]
            if biases:
                pairs += [(gate_b[:], w[f"{tag}_gate_b"].rearrange("(a n) -> a n", a=1).to_broadcast([P, R])),
                          (down_b[:], w[f"{tag}_down_b"]), (b_all[:, 0], w[f"{tag}_up_b"])]
                if gated:
                    pairs += [(b_all[:, 1], w[f"{tag}_lin_b"])]
            if capacity:
                pairs += [(trist[:], w["tri_strict_ones"])]
            normalise(c, tag + "_n", c.x, dstT=c.xT, loads=pairs)
            prob = sc("prob", [P, NT, R])
            tmp = sc("tmp", [P, NT, R])
            onehot = sc("onehot", [P, NT, R])
            assigned = sc("assigned", [P, NT, R])
            dense = sc("dense", [P, NT, R])
            count = sc("count", [P, NT, R])
            best = sc("best", [P, NT])
            wsum = sc("wsum", [P, NT])
            sig = Signals(nc, tag + "_gt")
            with nc.Block() as block:
                def bc(t2):
                    return t2[:].unsqueeze(2).to_broadcast([P, NT, R])

                def ie():
                    return iota[:].unsqueeze(1).to_broadcast([P, NT, R])

                logits = c.banks[0][:, 0:NT * R].rearrange("p (t e) -> p t e", t=NT)
                inside = c.banks[1][:, 0:NT * R].rearrange("p (t e) -> p t e", t=NT)
                totals = c.banks[2][:, 0:NT * R].rearrange("p (t e) -> p t e", t=NT)

                @block.tensor
                def _(pe):
                    for t in range(NT):
                        for k in range(KD):
                            last = nc.tensor.matmul(logits[:, t, :], c.xT[:, k, t * P:(t + 1) * P], gate[:, k, :],
                                                    start=(k == 0), stop=(k == KD - 1))
                    last.then_inc(sig("logits"), 1)
                    if capacity:
                        pe.wait_ge(sig("assigned"), 1)
                        nc.tensor.matmul(c.banks[1][:, 0:NT * R], trist[:, 0, :], assigned[:].rearrange("p t e -> p (t e)"),
                                         start=True, stop=True)
                        nc.tensor.matmul(c.banks[2][:, 0:NT * R], trist[:, 1, :], assigned[:].rearrange("p t e -> p (t e)"),
                                         start=True, stop=True).then_inc(sig("counted"), 1)
                    pe.wait_ge(sig("comb"), 1)
                    if biases:
                        for t in range(NT):
                            bank = c.banks[3 + t // 4]
                            last = nc.tensor.transpose(bank[0:E, (t % 4) * P:(t % 4 + 1) * P], comb[:, :, t], c.ident[:])
                        last.then_inc(sig("combT"), 1)

                @block.sync
                def _(sp):
                    fetch(sp, 0, 0, sig("raw0"))
                    fetch(sp, 1, 1, sig("raw1"))
                    sp.wait_ge(sig("raw1"), 16 * n_kinds)

                @block.gpsimd
                def _(pool):
                    pool.wait_ge(sig("raw0"), 16 * n_kinds)
                    split(pool, 0, sig("wh0"), sig("split0"))
                    for n in range(NBLK):
                        pool.wait_ge(sig("xh"), n + 1)
                        cols = slice(n * BLK, (n + 1) * BLK)
                        nc.gpsimd.tensor_tensor(xl[:, :, cols], c.xT[:, :, cols], xh[:, :, cols].bitcast(F32), ALU.subtract)

                @block.scalar
                def _(act):
                    for n in range(NBLK):
                        cols = slice(n * BLK, (n + 1) * BLK)
                        nc.scalar.activation(xh[:, :, cols], c.xT[:, :, cols], ACT.Copy).then_inc(sig("xh"), 1)
                    act.wait_ge(sig("centred"), 1)
                    nc.scalar.activation(prob[:], prob[:], ACT.Exp).then_inc(sig("exp"), 1)
                    if biases:
                        act.wait_ge(sig("combT"), 1)
                        for i in range(4):
                            nc.scalar.activation(combT[:, 4 * i:4 * i + 4, :].rearrange("e t p -> e (t p)"),
                                                 c.banks[3 + i][0:E, :], ACT.Copy)

                @block.vector
                def _(dve):
                    ch = Chain(dve, sig("dve_chain"))
                    v = nc.vector
                    dve.wait_ge(sig("logits"), 1)
                    if biases:
                        ch.link(v.tensor_tensor(prob[:], logits, gate_b[:].unsqueeze(1).to_broadcast([P, NT, R]), ALU.add))
                    else:
                        ch.link(v.tensor_copy(prob[:], logits))
                    ch.link(v.tensor_reduce(best[:], prob[:], AX.X, ALU.max))
                    v.tensor_tensor(prob[:], prob[:], bc(best), ALU.subtract).then_inc(sig("centred"), 1)
                    dve.wait_ge(sig("exp"), 1)
                    ch.link(v.tensor_reduce(wsum[:], prob[:], AX.X, ALU.add))
                    ch.link(v.reciprocal(wsum[:], wsum[:]))
                    ch.link(v.tensor_tensor(prob[:], prob[:], bc(wsum), ALU.mult))
                    ch.link(v.memset(assigned[:], 0.0))
                    ch.link(v.memset(dense[:], 0.0))
                    for r in range(top):
                        ch.link(v.tensor_reduce(best[:], prob[:], AX.X, ALU.max))
                        ch.link(v.tensor_tensor(onehot[:], prob[:], bc(best), ALU.is_equal))
                        ch.link(v.tensor_scalar(onehot[:], onehot[:], -64.0, 64.0, ALU.mult, ALU.add))
                        ch.link(v.tensor_tensor(onehot[:], onehot[:], ie(), ALU.add))
                        ch.link(v.tensor_reduce(wsum[:], onehot[:], AX.X, ALU.min))
                        ch.link(v.tensor_tensor(onehot[:], bc(wsum), ie(), ALU.is_equal))
                        ch.link(v.tensor_tensor(assigned[:], assigned[:], onehot[:], ALU.add))
                        ch.link(v.tensor_tensor(tmp[:], onehot[:], bc(best), ALU.mult))
                        ch.link(v.tensor_tensor(dense[:], dense[:], tmp[:], ALU.add))
                        if r + 1 < top:
                            ch.link(v.tensor_scalar(onehot[:], onehot[:], -2.0, None, ALU.mult))
                            ch.link(v.tensor_tensor(prob[:], prob[:], onehot[:], ALU.add))
                    if renorm:
                        ch.link(v.tensor_reduce(wsum[:], dense[:], AX.X, ALU.add))
                        ch.link(v.tensor_scalar_add(wsum[:], wsum[:], 1e-20))
                        ch.link(v.reciprocal(wsum[:], wsum[:]))
                        ch.link(v.tensor_tensor(dense[:], dense[:], bc(wsum), ALU.mult))
                    if capacity:
                        v.tensor_copy(tmp[:], assigned[:]).then_inc(sig("assigned"), 1)
                        dve.wait_ge(sig("counted"), 1)
                        ch.link(v.memset(count[:, 0, :], 0.0))
                        for t in range(1, NT):
                            ch.link(v.tensor_tensor(count[:, t, :], count[:, t - 1, :], totals[:, t - 1, :], ALU.add))
                        ch.link(v.tensor_tensor(count[:], count[:], inside, ALU.add))
                        ch.link(v.tensor_scalar(count[:], count[:], float(capacity), None, ALU.is_lt))
                        ch.link(v.tensor_tensor(dense[:], dense[:], count[:], ALU.mult))
                    if n_shared:
                        ch.link(v.memset(comb[:, R * parts:E, :], 1.0))
                    for part in range(parts):
                        last = v.tensor_copy(comb[:, 0:R * parts, :].rearrange("p (e u) t -> p t e u", u=parts)[:, :, :, part], dense[:])
                    last.then_inc(sig("comb"), 1)
            sig.clear()
            sig.close()
        if biases:
            sig = Signals(nc, tag + "_ob")
            with nc.Block() as block:
                ring = Ring(sig, "bias", c.banks[0:4])

                @block.tensor
                def _(pe):
                    for t in range(NT):
                        ring.fill(nc.tensor.matmul(ring.claim(pe)[:, 0:D], combT[:, t, :], down_b[:], start=True, stop=True))

                @block.vector
                def _(dve):
                    for t in range(NT):
                        bank = ring.take(dve)
                        ring.empty(nc.vector.tensor_tensor(c.x[:, t, :], bank[:, 0:D], c.x[:, t, :], ALU.add))
            sig.clear()
            sig.close()
        sig = Signals(nc, tag + "_ex")
        steps = [(i, n) for i in range(per_turn) for n in range(NBLK)]
        passes = ((0, 0), (0, 1), (1, 0))

        def turn(group, more):
            n_split = per_turn if more else per_turn - 1
            with nc.Block() as block:
                up_ring = Ring(sig, "up", c.banks[0:3])
                lin_ring = Ring(sig, "lin", c.banks[3:5])
                out_ring = Ring(sig, "out", c.banks[5:8])

                @block.sync
                def _(sp):
                    for i in range(2, per_turn + 2 if more else per_turn):
                        if i > 2:
                            sp.wait_ge(sig("split"), i - 2)
                        fetch(sp, i % 2, group * per_turn + i, sig(f"raw{i % 2}"))
                    if more:
                        sp.wait_ge(sig("raw1"), 16 * n_kinds * (per_turn // 2))

                @block.tensor
                def _(pe):
                    def rise(i, n):
                        if i and n == 0:
                            pe.wait_ge(sig("split"), i)
                        for m in range(M):
                            for kind, ring in enumerate((up_ring, lin_ring) if gated else (up_ring,)):
                                bank = ring.claim(pe)
                                for k in range(KD):
                                    for a, b in passes:
                                        last = nc.tensor.matmul(bank[:], rising((wh, wl)[a][i % 2], kind)[:, k, m * P:(m + 1) * P],
                                                                (xh, xl)[b][:, k, n * BLK:(n + 1) * BLK],
                                                                start=(k == 0 and (a, b) == passes[0]),
                                                                stop=(k == KD - 1 and (a, b) == passes[-1]))
                                ring.fill(last)

                    def fall(s):
                        i, n = steps[s]
                        pe.wait_ge(sig("hl"), M * (s + 1))
                        for half in range(2):
                            bank = out_ring.claim(pe)
                            for j in range(2):
                                tok = (2 * half + j) * P
                                for m in range(M):
                                    for a, b in passes:
                                        last = nc.tensor.matmul(bank[:, j * D:(j + 1) * D], (hh, hl)[a][s % 2][:, m, tok:tok + P],
                                                                falling((wh, wl)[b][i % 2])[:, m, :],
                                                                start=(m == 0 and (a, b) == passes[0]),
                                                                stop=(m == M - 1 and (a, b) == passes[-1]))
                            out_ring.fill(last)

                    for s, (i, n) in enumerate(steps):
                        rise(i, n)
                        if s:
                            fall(s - 1)
                    fall(len(steps) - 1)

                @block.scalar
                def _(act):
                    if biases:
                        act.wait_ge(sig("bias_t"), 1)
                    for s, (i, n) in enumerate(steps):
                        for m in range(M):
                            q = s * M + m
                            if q >= 2:
                                act.wait_ge(lin_ring.emptied if gated else sig("hl"), q - 1)
                            bank = up_ring.take(act)
                            up_ring.empty(nc.scalar.activation((silu if gated else h)[q % 2][:], bank[:], act_fn,
                                                               bias=bias_t[:, 0, i, m:m + 1] if biases else 0.0))

                @block.gpsimd
                def _(pool):
                    for s in range(len(steps)):
                        for m in range(M):
                            q = s * M + m
                            pool.wait_ge(sig("hh"), q + 1)
                            nc.gpsimd.tensor_tensor(hl[s % 2][:, m, :], h[q % 2][:], hh[s % 2][:, m, :].bitcast(F32),
                                                    ALU.subtract).then_inc(sig("hl"), 1)
                        i, n = steps[s]
                        if n == min(i, 1) and i < n_split:
                            if i:
                                pool.wait_ge(sig(f"raw{(i + 1) % 2}"), 16 * n_kinds * ((i + 1) // 2))
                                pool.wait_ge(out_ring.filled, 2 * NBLK * i)
                            split(pool, (i + 1) % 2, sig("high"), sig("split"), i + 1)

                @block.vector
                def _(dve):
                    if biases:
                        nc.vector.tensor_copy(bias_t[:], b_all[:, :, bass.ts(group, per_turn), :]).then_inc(sig("bias_t"), 1)
                        dve.wait_ge(sig("bias_t"), 1)
                    nc.vector.tensor_copy(comb_t[:], comb[:, bass.ts(group, per_turn), :]).then_inc(sig("comb_t"), 1)
                    dve.wait_ge(sig("comb_t"), 1)

                    def high(s):
                        i, n = steps[s]
                        for m in range(M):
                            q = s * M + m
                            if gated:
                                dve.wait_ge(up_ring.emptied, q + 1)
                                if q >= 2:
                                    dve.wait_ge(sig("hl"), q - 1)
                                bank = lin_ring.take(dve)
                                lin_ring.empty(nc.vector.scalar_tensor_tensor(out=h[q % 2][:], in0=bank[:],
                                                                              scalar=bias_t[:, 1, i, m:m + 1] if biases else 0.0,
                                                                              in1=silu[q % 2][:], op0=ALU.add, op1=ALU.mult))
                                dve.wait_ge(lin_ring.emptied, q + 1)
                            else:
                                dve.wait_ge(up_ring.emptied, q + 1)
                            if s >= 2 and m == 0:
                                dve.wait_ge(out_ring.filled, 2 * (s - 1))
                            nc.vector.tensor_copy(hh[s % 2][:, m, :], h[q % 2][:]).then_inc(sig("hh"), 1)

                    def add_out(s):
                        i, n = steps[s]
                        for half in range(2):
                            bank = out_ring.take(dve)
                            if s and half == 0:
                                dve.wait_ge(out_ring.emptied, 2 * s)
                            for j in range(2):
                                t = 4 * n + 2 * half + j
                                last = nc.vector.scalar_tensor_tensor(out=c.x[:, t, :], in0=bank[:, j * D:(j + 1) * D],
                                                                      scalar=comb_t[:, i, t:t + 1], in1=c.x[:, t, :],
                                                                      op0=ALU.mult, op1=ALU.add)
                            out_ring.empty(last)

                    for s in range(len(steps)):
                        high(s)
                        if s:
                            add_out(s - 1)
                    add_out(len(steps) - 1)
            sig.clear()

        with nc.Fori(0, E // per_turn - 1) as group:
            turn(group, more=True)
        turn(E // per_turn - 1, more=False)
        sig.close()


def layer0_ffn(c):
    mixture(c, "L0f", 8, 2, 2, gated=True, top=2, biases=True)


def layer2_ffn(c):
    mixture(c, "L2f", 8, 0, 4, gated=False, top=1, biases=True, parts=2, per_turn=4)


def layer3_ffn(c):
    mixture(c, "L3f", 8, 2, 2, gated=True, top=2, biases=False, renorm=True, capacity=640)

def softmax_attention(c, tag, H, rows, MQ, KT, DV, kind, scale, norm=None):
    nc, w = c.nc, c.dram
    NK, C = KT * P, H * DV
    causal = kind == "decay"
    twins = 2 if rows == 16 else 1
    DS = DV * twins
    HT = P // DS
    KC = C // P
    if causal:
        items = [(h, [(0, 0, P), (1, P, 2 * P)]) for h in range(H)]
    elif NK == T:
        items = [(h, [(0, 0, NK), (1, NK, NK)]) for h in range(H)]
    else:
        items = [(h, [(t, 0, NK)]) for h in range(H) for t in range(TB)]
    n, S = len(items), len(items[0][1])
    W = sum(nk for _, _, nk in items[0][1])
    LAG = 4 + twins
    BEHIND = LAG - 2 - causal
    with ExitStack() as stack:
        sb = c.tiles(stack, tag)
        xb = [sb(f"xb{i}", [P, KD, T]) for i in range(2)]
        cb = [sb(f"cb{i}", [P, KD, T]) for i in range(2)]
        qT = [sb(f"qT{i}", [P, MQ, T]) for i in range(2)]
        kT = [sb(f"kT{i}", [P, twins * MQ, NK]) for i in range(2)]
        v = [sb(f"v{i}", [P, KT, twins * C]) for i in range(2)]
        s_sb = [sb(f"s{i}", [P, W]) for i in range(4)]
        p_sb = [sb(f"p{i}", [P, W]) for i in range(LAG)]
        pT = [sb(f"pT{i}", [P, W]) for i in range(3)]
        nmax = [sb(f"nmax{i}", [P, n, S]) for i in range(2)]
        rsum = [sb(f"rsum{i}", [P, n, S]) for i in range(2)]
        bias = [sb(f"bias{i}", [P, TB if kind == "pairs" else 1, NK]) for i in range(2)]
        pairs = []
        wq, wk = sb("wq", [P, KD, MQ * P]), sb("wk", [P, KD, MQ * P])
        wv, wo = sb("wv", [P, KD, C]), sb("wo", [P, KC, D])
        cT = sb("cT", [P, KC, T])
        bo = sb("bo", [P, D])
        y = sb("y", [P, TB, D])
        pairs += [(wq[:], w[f"{tag}_wq"]), (wk[:], w[f"{tag}_wk"]), (wv[:], w[f"{tag}_wv"]), (wo[:], w[f"{tag}_wo"])]
        if twins == 2:
            twin = sb("twin", [P, 2])
            pairs += [(twin[:], w["twin"])]
        if kind != "latent":
            pairs += [(bo[:], w[f"{tag}_bo"].rearrange("(a n) -> a n", a=1).to_broadcast([P, D]))]
        if kind == "pairs":
            mask = [sb(f"mask{i}", [P, TB, NK], I32) for i in range(2)]
        if kind == "latent":
            mask = [sb(f"mask{i}", [P, 1, T], U8) for i in range(2)]
            og, ob = sb("og", [P, D]), sb("ob", [P, D])
            stats, mv, rstd = sb("stats", [P, TB, 6]), sb("mv", [P, TB, 2]), sb("rstd", [P, TB, 3])
            pairs += [(og[:], w[f"{tag}_og"].rearrange("(a n) -> a n", a=1).to_broadcast([P, D])),
                      (ob[:], w[f"{tag}_ob"].rearrange("(a n) -> a n", a=1).to_broadcast([P, D]))]
        if kind == "decay":
            rhat = sb("rhat", [P, H, 3 * P])
            dist = sb("dist", [P, 3 * P])
            future = sb("future", [P, P])
            wh, vh, ev = sb("wh", [P, H]), sb("vh", [P, H]), sb("ev", [P, H])
            pairs += [(dist[:], w["distance"]), (future[:], w["future_neg"]),
                      (wh[:], w[f"{tag}_w"].rearrange("(a n) -> a n", a=1).to_broadcast([P, H])),
                      (vh[:], w[f"{tag}_v"].rearrange("(a n) -> a n", a=1).to_broadcast([P, H]))]
        normalise(c, tag + "_n", loads=pairs, **(norm or dict(src=c.x, dstT=c.xT)))
        if kind == "decay":
            sig = Signals(nc, tag + "_rh")
            with nc.Block() as block:
                @block.vector
                def _(dve):
                    ch = Chain(dve, sig("dve_chain"))
                    for h in range(H):
                        nc.vector.tensor_scalar(rhat[:, h, P:], dist[:, P:], wh[:, h:h + 1], -1.0, ALU.mult, ALU.mult).then_inc(sig("minus_wr"), 1)
                    dve.wait_ge(sig("exped"), 1)
                    nc.vector.tensor_scalar(ev[:], ev[:], 1.0, scale, ALU.add, ALU.mult).then_inc(sig("numerator"), 1)
                    for h in range(H):
                        dve.wait_ge(sig("exped"), h + 2)
                        ch.link(nc.vector.tensor_scalar(rhat[:, h, P:], rhat[:, h, P:], 1.0, None, ALU.add))
                        nc.vector.reciprocal(rhat[:, h, P:], rhat[:, h, P:]).then_inc(sig("inverse"), 1)

                @block.scalar
                def _(act):
                    nc.scalar.activation(ev[:], vh[:], ACT.Exp).then_inc(sig("exped"), 1)
                    for h in range(H):
                        act.wait_ge(sig("minus_wr"), h + 1)
                        nc.scalar.activation(rhat[:, h, P:], rhat[:, h, P:], ACT.Exp, bias=vh[:, h:h + 1]).then_inc(sig("exped"), 1)

                @block.gpsimd
                def _(pool):
                    pool.wait_ge(sig("numerator"), 1)
                    for h in range(H):
                        pool.wait_ge(sig("inverse"), h + 1)
                        by = lambda k: ev[:, h:h + 1].to_broadcast([P, k])
                        nc.gpsimd.tensor_tensor(rhat[:, h, 0:P], rhat[:, h, 2 * P:], by(P), ALU.mult).then_inc(sig("first_tile"), 1)
                        pool.wait_ge(sig("first_tile"), h + 1)
                        nc.gpsimd.tensor_tensor(rhat[:, h, P:], rhat[:, h, P:], by(2 * P), ALU.mult)
            sig.clear()
            sig.close()
        if twins == 2:
            sig = Signals(nc, tag + "_z")
            with nc.Block() as block:
                @block.gpsimd
                def _(pool):
                    for v_ in v:
                        nc.gpsimd.memset(v_[:], 0.0)
            sig.clear()
            sig.close()

        sig = Signals(nc, tag)
        with nc.Fori(0, B // ROWS) as turn:
            with nc.Block() as block:
                s_ring = Ring(sig, "s", c.banks[0:3])
                t_ring = Ring(sig, "t", c.banks[3:5])
                acc = c.banks[5:7]
                out_bank = c.banks[7]
                row_of = lambda r: turn * ROWS + r
                q_banks = MQ // 2
                k_banks = MQ * (NK // T) // 2
                v_banks = KT

                total = ROWS * n
                t_bufs = q_banks + v_banks

                def t_projection(r):
                    return max(0, r * n - LAG) + t_bufs * r

                def t_item(g):
                    return g + t_bufs * min(ROWS, (g + LAG) // n + 1)

                def s_item(g):
                    return g + k_banks * (g // n + 1)

                def source(i, r):
                    x_, c_ = xb[r % 2], cb[r % 2]
                    return (c_, i) if kind == "pairs" else (x_, i) if kind == "decay" else ((c_, i) if i < TB else (x_, i - TB))

                def parts(h):
                    p0 = h // twins * twins * rows
                    return p0 // P, h % twins * MQ + p0 // P, slice(p0 % P, p0 % P + twins * rows)

                @block.sync
                def _(sp):
                    for r in range(ROWS if kind != "decay" else 0):
                        if r >= 2:
                            sp.wait_ge(sig("bias"), r - 1)
                        if kind == "pairs":
                            sp.dma_start(mask[r % 2][:], w["mask_pairs"][row_of(r)]).then_inc(sig(f"mask{r % 2}"), 16)
                        if kind == "latent":
                            sp.dma_start(mask[r % 2][:, 0, :], w["mask_bool"][row_of(r)].to_broadcast([P, T])).then_inc(sig(f"mask{r % 2}"), 16)

                @block.tensor
                def _(pe):
                    def project(r):
                        pe.wait_ge(sig("sliced_x"), r + 1)
                        pe.wait_ge(sig("sliced_c"), r + 1)
                        for i in range(0, MQ, 2):
                            bank = t_ring.claim(pe)
                            for m in range(i, i + 2):
                                for k in range(KD):
                                    last = nc.tensor.matmul(bank[:, (m - i) * T:(m - i + 1) * T], wq[:, k, m * P:(m + 1) * P],
                                                            xb[r % 2][:, k, :], start=(k == 0), stop=(k == KD - 1))
                            t_ring.fill(last)
                        for i in range(0, MQ * (NK // T), 2):
                            bank = s_ring.claim(pe)
                            for j in (i, i + 1):
                                m, part = j % MQ, j // MQ
                                src = source(part * TB, r)[0]
                                for k in range(KD):
                                    last = nc.tensor.matmul(bank[:, (j - i) * T:(j - i + 1) * T], wk[:, k, m * P:(m + 1) * P],
                                                            src[:, k, :], start=(k == 0), stop=(k == KD - 1))
                            s_ring.fill(last)
                        for i in range(KT):
                            bank = t_ring.claim(pe)
                            src, j = source(i, r)
                            for k in range(KD):
                                last = nc.tensor.matmul(bank[:, 0:C], src[:, k, j * P:(j + 1) * P], wv[:, k, :],
                                                        start=(k == 0), stop=(k == KD - 1))
                            t_ring.fill(last)

                    def output(r):
                        if r:
                            pe.wait_ge(sig("out_read"), r)
                        pe.wait_ge(sig("cT"), TB * (r + 1))
                        for t in range(TB):
                            for k in range(KC):
                                last = nc.tensor.matmul(out_bank[:, t * D:(t + 1) * D], cT[:, k, t * P:(t + 1) * P], wo[:, k, :],
                                                        start=(k == 0), stop=(k == KC - 1))
                        last.then_inc(sig("projected"), 1)

                    for g in range(total + LAG + 1):
                        if g < total:
                            r, i = divmod(g, n)
                            if i == 0:
                                project(r)
                                pe.wait_ge(t_ring.emptied, t_projection(r) + q_banks)
                                pe.wait_ge(s_ring.emptied, s_item(g))
                            h, segs = items[i]
                            m, mk, ps = parts(h)
                            bank = s_ring.claim(pe)
                            for t, at, nk in segs:
                                last = nc.tensor.matmul(bank[:, at:at + nk], qT[r % 2][ps, m, t * P:(t + 1) * P], kT[r % 2][ps, mk, 0:nk],
                                                        start=True, stop=True)
                            s_ring.fill(last)
                        if LAG <= g < total + LAG:
                            j = g - LAG
                            bank = t_ring.claim(pe)
                            pe.wait_ge(sig("divided"), j + 1)
                            for b in range(W // P):
                                last = nc.tensor.transpose(bank[:, b * P:(b + 1) * P], p_sb[j % LAG][:, b * P:(b + 1) * P], c.ident[:])
                            t_ring.fill(last)
                        r, i = divmod(g - LAG - 2, n)
                        if r >= 1 and i == 0 and r <= ROWS - 1:
                            output(r - 1)
                        if g > LAG:
                            j = g - LAG - 1
                            r, i = divmod(j, n)
                            h, segs = items[i]
                            if i == 0 and r:
                                pe.wait_ge(sig("cT"), TB * r)
                            pe.wait_ge(t_ring.emptied, t_item(j) + 1)
                            e, u = h % twins, h // twins
                            rows_out, tile = slice(u % HT * DS, (u % HT + 1) * DS), u // HT
                            for t, at, nk in segs:
                                for kt in range(nk // P):
                                    last = nc.tensor.matmul(acc[t][rows_out, tile * P:(tile + 1) * P],
                                                            v[r % 2][:, kt, e * C + u * DS:e * C + (u + 1) * DS],
                                                            pT[j % 3][:, at + kt * P:at + (kt + 1) * P],
                                                            start=(e == 0 and kt == 0), stop=(e == twins - 1 and kt == nk // P - 1))
                            last.then_inc(sig("weighted"), 1)
                    output(ROWS - 1)

                @block.scalar
                def _(act):
                    def slice_x(r):
                        nc.scalar.activation(xb[r % 2][:], c.xT[:, :, bass.ts(row_of(r), T)], ACT.Copy).then_inc(sig("sliced_x"), 1)

                    def project(r):
                        for i in range(0, MQ, 2):
                            bank = t_ring.take(act)
                            t_ring.empty(nc.scalar.activation(qT[r % 2][:, i:i + 2, :], bank[:].rearrange("p (m t) -> p m t", m=2), ACT.Copy))
                        for i in range(KT):
                            bank = t_ring.take(act)
                            for e in range(twins):
                                own = lambda a: a.rearrange("p (u e d) -> p u e d", e=twins, d=DV)[:, :, e, :]
                                last = nc.scalar.activation(own(v[r % 2][:, i, e * C:(e + 1) * C]), own(bank[:, 0:C]), ACT.Copy)
                            t_ring.empty(last)

                    def output(r):
                        act.wait_ge(sig("weighted"), (r + 1) * n)
                        if r:
                            act.wait_ge(sig("projected"), r)
                        for t in range(TB):
                            nc.scalar.activation(cT[:, :, t * P:(t + 1) * P], acc[t][:, 0:C].rearrange("p (k t) -> p k t", k=KC),
                                                 ACT.Copy).then_inc(sig("cT"), 1)

                    def root(r):
                        if kind == "latent":
                            act.wait_ge(sig("var_eps"), r + 1)
                            nc.scalar.activation(rstd[:, :, 1], rstd[:, :, 0], ACT.Sqrt).then_inc(sig("std"), 1)

                    slice_x(0)
                    project(0)
                    for g in range(total + BEHIND):
                        r, i = divmod(g, n)
                        if i == 2 and r + 1 < ROWS:
                            slice_x(r + 1)
                        if i == BEHIND + 1 and r and g < total:
                            output(r - 1)
                        if i == LAG + 2 and r and g < total:
                            root(r - 1)
                        if g < total:
                            act.wait_ge(sig("max"), g + 1)
                            for e, (t, at, nk) in enumerate(items[i][1]):
                                nc.scalar.activation(p_sb[g % LAG][:, at:at + nk], s_sb[g % 4][:, at:at + nk], ACT.Exp,
                                                     bias=nmax[r % 2][:, i, e:e + 1],
                                                     accum_out=rsum[r % 2][:, i, e:e + 1]).then_inc(sig("exp"), 1)
                        if g >= BEHIND:
                            j = g - BEHIND
                            if (j + LAG) % n == 0 and (j + LAG) // n < ROWS:
                                project((j + LAG) // n)
                            if j >= 3:
                                act.wait_ge(sig("weighted"), j - 2)
                            bank = t_ring.take(act)
                            t_ring.empty(nc.scalar.activation(pT[j % 3][:], bank[:, 0:W], ACT.Copy))
                    output(ROWS - 1)
                    root(ROWS - 1)

                @block.gpsimd
                def _(pool):
                    for r in range(ROWS):
                        for i, (h, segs) in enumerate(items):
                            g = r * n + i
                            pool.wait_ge(sig("reciprocal"), g + 1)
                            if len({nk for _, _, nk in segs}) == 1:
                                both = p_sb[g % LAG][:].rearrange("p (e s) -> p e s", e=S)
                                last = nc.gpsimd.tensor_tensor(both, both, rsum[r % 2][:, i, :].unsqueeze(2).to_broadcast([P, S, NK]), ALU.mult)
                            else:
                                for e, (t, at, nk) in enumerate(segs):
                                    one = p_sb[g % LAG][:, at:at + nk]
                                    last = nc.gpsimd.tensor_tensor(one, one, rsum[r % 2][:, i, e:e + 1].to_broadcast([P, nk]), ALU.mult)
                            last.then_inc(sig("divided"), 1)

                @block.vector
                def _(dve):
                    ch = Chain(dve, sig("dve_chain"))
                    vec = nc.vector

                    def slice_c(r):
                        src = c.ctxn if kind == "latent" else c.ctxT
                        vec.tensor_copy(cb[r % 2][:], src[:, :, bass.ts(row_of(r), T)]).then_inc(sig("sliced_c"), 1)

                    def project(r):
                        if kind != "decay":
                            dve.wait_ge(sig(f"mask{r % 2}"), 16 * (r // 2 + 1))
                        b_, m_ = bias[r % 2], mask[r % 2] if kind != "decay" else None
                        if kind == "pairs":
                            ch.link(vec.tensor_scalar(b_[:], m_[:], 0.0, -1.0, ALU.not_equal, ALU.add))
                            vec.tensor_scalar(b_[:], b_[:], 1e20 * scale, None, ALU.mult).then_inc(sig("bias"), 1)
                            dve.wait_ge(sig("bias"), r + 1)
                        if kind == "latent":
                            vec.memset(b_[:, :, T:NK], 0.0)
                            ch.link(vec.tensor_scalar(b_[:, :, 0:T], m_[:], 0.0, -1.0, ALU.not_equal, ALU.add))
                            vec.tensor_scalar(b_[:, :, 0:T], b_[:, :, 0:T], 3e38, None, ALU.mult).then_inc(sig("bias"), 1)
                            dve.wait_ge(sig("bias"), r + 1)
                        for i in range(0, MQ * (NK // T), 2):
                            bank = s_ring.take(dve)
                            m, part = i % MQ, i // MQ
                            feats = bank[:].rearrange("p (m t) -> p m t", m=2)
                            if twins == 1:
                                last = vec.tensor_copy(kT[r % 2][:, m:m + 2, part * T:(part + 1) * T], feats)
                            else:
                                for e in range(2):
                                    last = vec.tensor_scalar(kT[r % 2][:, e * MQ + m:e * MQ + m + 2, part * T:(part + 1) * T], feats,
                                                             twin[:, e:e + 1], None, ALU.mult)
                            s_ring.empty(last)

                    def scale_mask(g):
                        r, i = divmod(g, n)
                        bank = s_ring.take(dve)
                        if g >= 4:
                            dve.wait_ge(sig("exp"), S * (g - 3))
                        s = s_sb[g % 4]
                        if causal:
                            ins = vec.scalar_tensor_tensor(out=s[:], in0=bank[:, 0:W], scalar=0.0, in1=rhat[:, items[i][0], :],
                                                           op0=ALU.max, op1=ALU.mult)
                        else:
                            ins = vec.scalar_tensor_tensor(out=s[:], in0=bank[:, 0:W], scalar=scale,
                                                           in1=bias[r % 2][:].rearrange("p t s -> p (t s)"), op0=ALU.mult, op1=ALU.add)
                        s_ring.empty(ins)

                    def hide_future(g):
                        dve.wait_ge(s_ring.emptied, s_item(g) + 1)
                        s = s_sb[g % 4]
                        for at in (0, 2 * P):
                            last = vec.tensor_tensor(s[:, at:at + P], s[:, at:at + P], future[:], ALU.add)
                        last.then_inc(sig("hidden"), 1)

                    def maximum(g):
                        r, i = divmod(g, n)
                        if causal:
                            dve.wait_ge(sig("hidden"), g + 1)
                        else:
                            dve.wait_ge(s_ring.emptied, s_item(g) + 1)
                        s, nm = s_sb[g % 4], nmax[r % 2]
                        if causal:
                            for e, (t, at, nk) in enumerate(items[i][1]):
                                last = vec.tensor_reduce(nm[:, i, e:e + 1], s[:, at:at + nk], AX.X, ALU.max, negate=True)
                        else:
                            last = vec.tensor_reduce(nm[:, i, :], s[:].rearrange("p (e s) -> p e s", e=S), AX.X, ALU.max, negate=True)
                        last.then_inc(sig("max"), 1)

                    def reciprocal(g):
                        r, i = divmod(g, n)
                        dve.wait_ge(sig("exp"), S * (g + 1))
                        rs = rsum[r % 2][:, i, :]
                        vec.reciprocal(rs, rs).then_inc(sig("reciprocal"), 1)

                    def output(r):
                        xr = c.x[:, bass.ts(row_of(r), TB), :]
                        dve.wait_ge(sig("projected"), r + 1)
                        if r:
                            dve.wait_ge(sig("added"), r)
                        proj = out_bank[:].rearrange("p (t d) -> p t d", t=TB)
                        rowwise = lambda a: a[:].unsqueeze(1).to_broadcast([P, TB, D])
                        if kind == "latent":
                            for t in range(TB):
                                last = vec.bn_stats(stats[:, t, :], proj[:, t, :])
                            ch.link(last)
                            for t in range(TB):
                                last = vec.bn_aggr(mv[:, t, :], stats[:, t, :])
                            ch.link(last)
                            vec.tensor_scalar_add(rstd[:, :, 0], mv[:, :, 1], 1e-5).then_inc(sig("var_eps"), 1)
                            dve.wait_ge(sig("std"), r + 1)
                            ch.link(vec.reciprocal(rstd[:, :, 2], rstd[:, :, 1]))
                            for t in range(TB):
                                last = vec.tensor_scalar(y[:, t, :], proj[:, t, :], mv[:, t, 0:1], rstd[:, t, 2:3], ALU.subtract, ALU.mult)
                            last.then_inc(sig("out_read"), 1)
                            dve.wait_ge(sig("out_read"), r + 1)
                            ch.link(vec.tensor_tensor(y[:], y[:], rowwise(og), ALU.mult))
                            ch.link(vec.tensor_tensor(y[:], y[:], rowwise(ob), ALU.add))
                        else:
                            vec.tensor_tensor(y[:], proj, rowwise(bo), ALU.add).then_inc(sig("out_read"), 1)
                            dve.wait_ge(sig("out_read"), r + 1)
                        vec.tensor_tensor(xr, xr, y[:], ALU.add).then_inc(sig("added"), 1)

                    slice_c(0)
                    project(0)
                    scale_mask(0)
                    for g in range(total + causal + 2):
                        r, i = divmod(g, n)
                        if i == 2 and r + 1 < ROWS:
                            slice_c(r + 1)
                        if i == LAG + 3 and r and g < total:
                            output(r - 1)
                        if g >= causal + 2:
                            reciprocal(g - causal - 2)
                        if g + 1 < total:
                            if i == n - 1:
                                project(r + 1)
                            scale_mask(g + 1)
                        if causal and g < total:
                            hide_future(g)
                        if causal <= g < total + causal:
                            maximum(g - causal)
                    output(ROWS - 1)
            sig.clear()
        sig.close()


def layer1_attn(c):
    softmax_attention(c, "L1a", 16, 16, 2, 2, 16, "decay", 0.25)


def layer1_xattn(c):
    softmax_attention(c, "L1x", 16, 16, 2, 2, 16, "pairs", 0.25)


def layer2_xattn(c):
    nc, w = c.nc, c.dram
    normalise(c, "n2x", c.x, dstT=c.xT)
    with ExitStack() as stack:
        sb = c.tiles(stack, "L2x")
        xb, cb, v = ([sb(f"{n}{i}", [P, TB, D]) for i in range(k)] for n, k in (("xb", 3), ("cb", 2), ("v", 3)))
        mask = [sb(f"mask{i}", [P, T], I32) for i in range(2)]
        bias = [sb(f"bias{i}", [P, T]) for i in range(2)]
        scores, prob, probT = ([sb(f"{n}{i}", [P, T]) for i in range(3)] for n in ("scores", "prob", "probT"))
        nmax, rsum = sb("nmax", [P, TB * ROWS]), sb("rsum", [P, TB * ROWS])
        y = [sb(f"y{i}", [P, D]) for i in range(2)]
        sig = Signals(nc, "L2x")
        with nc.Fori(0, B // ROWS) as turn:
            with nc.Block() as block:
                s_ring = Ring(sig, "s", c.banks[0:3])
                t_ring = Ring(sig, "t", c.banks[3:5])
                o_ring = Ring(sig, "o", c.banks[5:8])
                row_of = lambda r: turn * ROWS + r
                items = [(r, t) for r in range(ROWS) for t in range(TB)]
                n = len(items)

                @block.sync
                def _(sp):
                    for r in range(ROWS):
                        if r >= 2:
                            sp.wait_ge(sig("bias"), r - 1)
                        sp.dma_start(mask[r % 2][:], w["mask_keys"][row_of(r)].to_broadcast([P, T])).then_inc(sig(f"mask{r % 2}"), 16)

                @block.tensor
                def _(pe):
                    for i in range(n + 3):
                        if i < n:
                            r, t = items[i]
                            pe.wait_ge(sig("sliced_x"), r + 1)
                            pe.wait_ge(sig("sliced_c"), r + 1)
                            bank = s_ring.claim(pe)
                            for k in range(KD):
                                last = nc.tensor.matmul(bank[:, 0:T], xb[r % 3][:, k, t * P:(t + 1) * P], cb[r % 2][:, k, :],
                                                        start=(k == 0), stop=(k == KD - 1))
                            s_ring.fill(last)
                        if 2 <= i < n + 2:
                            j = i - 2
                            bank = t_ring.claim(pe)
                            pe.wait_ge(sig("exp"), j + 1)
                            for k in range(TB):
                                last = nc.tensor.transpose(bank[:, k * P:(k + 1) * P], prob[j % 3][:, k * P:(k + 1) * P], c.ident[:])
                            t_ring.fill(last)
                        if i >= 3:
                            j = i - 3
                            bank = o_ring.claim(pe)
                            pe.wait_ge(t_ring.emptied, j + 1)
                            pe.wait_ge(sig("sliced_v"), items[j][0] + 1)
                            for k in range(TB):
                                last = nc.tensor.matmul(bank[:, 0:D], probT[j % 3][:, k * P:(k + 1) * P], v[items[j][0] % 3][:, k, :],
                                                        start=(k == 0), stop=(k == TB - 1))
                            o_ring.fill(last)

                @block.scalar
                def _(act):
                    def slice_row(r):
                        if r >= 3:
                            act.wait_ge(o_ring.filled, TB * (r - 2))
                        nc.scalar.activation(xb[r % 3][:], c.xT[:, :, bass.ts(row_of(r), T)], ACT.Copy).then_inc(sig("sliced_x"), 1)
                        nc.scalar.activation(v[r % 3][:], c.ctx[:, bass.ts(row_of(r), TB), :], ACT.Copy).then_inc(sig("sliced_v"), 1)

                    slice_row(0)
                    for i in range(n + 1):
                        if i % TB == 0 and i // TB + 1 < ROWS:
                            slice_row(i // TB + 1)
                        if i < n:
                            act.wait_ge(sig("max"), i + 1)
                            nc.scalar.activation(prob[i % 3][:], scores[i % 3][:], ACT.Exp, bias=nmax[:, i:i + 1],
                                                 accum_out=rsum[:, i:i + 1]).then_inc(sig("exp"), 1)
                        if i >= 1:
                            j = i - 1
                            if j >= 3:
                                act.wait_ge(o_ring.filled, j - 2)
                            bank = t_ring.take(act)
                            t_ring.empty(nc.scalar.activation(probT[j % 3][:], bank[:, 0:T], ACT.Copy))

                @block.vector
                def _(dve):
                    ch = Chain(dve, sig("dve_chain"))
                    vec = nc.vector

                    def add(i):
                        r, t = items[i]
                        bank = o_ring.take(dve)
                        ch.link(vec.reciprocal(rsum[:, i:i + 1], rsum[:, i:i + 1]))
                        o_ring.empty(vec.tensor_scalar(y[i % 2][:], bank[:, 0:D], rsum[:, i:i + 1], None, ALU.mult))
                        dve.wait_ge(o_ring.emptied, i + 1)
                        xr = c.x[:, bass.ts(row_of(r) * TB + t, 1), :].rearrange("p a d -> p (a d)")
                        vec.tensor_tensor(xr, xr, y[i % 2][:], ALU.add).then_inc(sig("added"), 1)

                    for i, (r, t) in enumerate(items):
                        if t == 0:
                            if r >= 2:
                                dve.wait_ge(s_ring.filled, TB * (r - 1))
                            vec.tensor_copy(cb[r % 2][:], c.ctxT[:, :, bass.ts(row_of(r), T)]).then_inc(sig("sliced_c"), 1)
                            dve.wait_ge(sig(f"mask{r % 2}"), 16 * (r // 2 + 1))
                            vec.tensor_scalar(bias[r % 2][:], mask[r % 2][:], -1e9, None, ALU.mult).then_inc(sig("bias"), 1)
                            dve.wait_ge(sig("bias"), r + 1)
                        bank = s_ring.take(dve)
                        if i >= 3:
                            dve.wait_ge(sig("exp"), i - 2)
                        s_ring.empty(vec.scalar_tensor_tensor(out=scores[i % 3][:], in0=bank[:, 0:T], scalar=1.0 / 16.0, in1=bias[r % 2][:],
                                                              op0=ALU.mult, op1=ALU.add))
                        dve.wait_ge(s_ring.emptied, i + 1)
                        vec.tensor_reduce(nmax[:, i:i + 1], scores[i % 3][:], AX.X, ALU.max, negate=True).then_inc(sig("max"), 1)
                        if i >= 3:
                            if i >= 5:
                                dve.wait_ge(sig("added"), i - 4)
                            add(i - 3)
                    for i in range(n - 3, n):
                        dve.wait_ge(sig("added"), i - 1)
                        add(i)
            sig.clear()
        sig.close()


def layer3_xattn(c):
    with ExitStack() as stack:
        sb = c.tiles(stack, "L3xn")
        c.ctxn = sb("ctxn", [P, KD, N])
        xn = sb("xn", [P, NT, D])
        affine = sb("affine", [P, 4, KD])
        c.load("L3xn_ld", [(affine[:], c.dram["L3x_ln"])])
        normalise(c, "n3x", c.x, dst=xn)
        normalise(c, "n3y", xn, dstT=c.xT, gain=affine[:, 0, :], shift=affine[:, 1, :])
        softmax_attention(c, "L3x", 8, 64, 4, 4, 64, "latent", 1.0 / 64.0,
                          norm=dict(src=c.ctx, dstT=c.ctxn, gain=affine[:, 2, :], shift=affine[:, 3, :]))


def layer1_ffn(c):
    nc, w = c.nc, c.dram
    I = 768
    MI = I // P
    QMAX = 32767.0
    with ExitStack() as stack:
        sb = c.tiles(stack, "L1f")
        up, gate = sb("up", [P, MI, N]), sb("gate", [P, MI, N])
        wT = {"up": sb("wT_up", [P, KD, I]), "gate": sb("wT_gate", [P, KD, I]), "down": sb("wT_down", [P, MI, D])}
        turn_max, all_max = sb("turn_max", [P, 2, MI]), sb("all_max", [P, NBLK * 2 * MI])
        s = {n: sb("s_" + n, [P, 4]) for n in ("x", "up", "gate", "mix", "out")}

        def scale_of(ch, vec, t, factor=None):
            if factor is not None:
                ch.link(vec.tensor_tensor(t[:, 1:2], t[:, 0:1], factor, ALU.mult))
                ch.link(vec.tensor_scalar(t[:, 1:2], t[:, 1:2], 1.0 / QMAX, 1e-12, ALU.mult, ALU.max))
                ch.link(vec.reciprocal(t[:, 2:3], t[:, 1:2]))
                ch.link(vec.tensor_tensor(t[:, 3:4], t[:, 2:3], factor, ALU.mult))
            else:
                ch.link(vec.tensor_scalar(t[:, 1:2], t[:, 0:1], 1.0 / QMAX, 1e-12, ALU.mult, ALU.max))
                ch.link(vec.reciprocal(t[:, 2:3], t[:, 1:2]))
                ch.link(vec.tensor_copy(t[:, 3:4], t[:, 2:3]))

        def quantise(ch, vec, a, t, low=True):
            ch.link(vec.tensor_scalar(a, a, t[:, 3:4], ROUND, ALU.mult, ALU.add))
            ch.link(vec.tensor_scalar(a, a, -ROUND, QMAX, ALU.add, ALU.min))
            if low:
                ch.link(vec.tensor_scalar(a, a, -QMAX - 1.0, None, ALU.max))

        with ExitStack() as inner:
            sw = c.tiles(inner, "L1f")
            nat = {"up": sw("nat_up", [P, MI, D]), "gate": sw("nat_gate", [P, MI, D]), "down": sw("nat_down", [P, KD, I])}
            bs, binv = sw("block_scale", [P, 48]), sw("block_inv", [P, 48])
            normalise(c, "n1f", c.x, dstT=c.xT, loads=[(nat[n][:], w[f"L1f_{n}"]) for n in ("up", "gate", "down")])
            sig = Signals(nc, "L1f_w")
            with nc.Block() as block:
                order = ("up", "gate", "down")
                ring = Ring(sig, "wt", c.banks[0:4])

                @block.vector
                def _(dve):
                    ch = Chain(dve, sig("dve_chain"))
                    vec = nc.vector
                    for n in order:
                        a = nat[n][:].rearrange("p a b -> p (a b)").rearrange("p (g i) -> p g i", i=32)
                        wide = lambda t: t[:].unsqueeze(2).to_broadcast([P, 48, 32])
                        ch.link(vec.tensor_reduce(bs[:], a, AX.X, ALU.max, apply_absolute_value=True))
                        ch.link(vec.tensor_scalar(bs[:], bs[:], 1.0 / 7.0, 1e-12, ALU.mult, ALU.max))
                        ch.link(vec.reciprocal(binv[:], bs[:]))
                        ch.link(vec.tensor_tensor(a, a, wide(binv), ALU.mult))
                        ch.link(vec.tensor_scalar(a, a, ROUND, None, ALU.add))
                        ch.link(vec.tensor_scalar(a, a, -ROUND, 7.0, ALU.add, ALU.min))
                        ch.link(vec.tensor_scalar(a, a, -8.0, None, ALU.max))
                        ch.link(vec.tensor_tensor(a, a, wide(bs), ALU.mult))
                        vec.sem_inc(sig("dequantised"), 1)
                    vec.tensor_reduce(s["x"][:, 0:1], c.xT[:].rearrange("p k n -> p (k n)"), AX.X, ALU.max,
                                      apply_absolute_value=True).then_inc(sig("x_max"), 1)
                    dve.wait_ge(sig("x_all"), 1)
                    scale_of(ch, vec, s["x"])
                    quantise(ch, vec, c.xT[:], s["x"])

                @block.gpsimd
                def _(pool):
                    pool.wait_ge(sig("x_max"), 1)
                    nc.gpsimd.partition_all_reduce(s["x"][:, 0:1], s["x"][:, 0:1], P, bass.bass_isa.ReduceOp.max).then_inc(sig("x_all"), 1)

                @block.tensor
                def _(pe):
                    for q, n in enumerate(order):
                        pe.wait_ge(sig("dequantised"), q + 1)
                        outer, inner_ = (MI, KD) if n != "down" else (KD, MI)
                        for i in range(inner_):
                            for o0 in range(0, outer, 4):
                                bank = ring.claim(pe)
                                for o in range(o0, min(o0 + 4, outer)):
                                    last = nc.tensor.transpose(bank[:, (o - o0) * P:(o - o0 + 1) * P],
                                                               nat[n][:, o, i * P:(i + 1) * P], c.ident[:])
                                ring.fill(last)

                @block.scalar
                def _(act):
                    for n in order:
                        outer, inner_ = (MI, KD) if n != "down" else (KD, MI)
                        for i in range(inner_):
                            for o0 in range(0, outer, 4):
                                bank = ring.take(act)
                                cnt = min(4, outer - o0) * P
                                ring.empty(nc.scalar.activation(wT[n][:, i, o0 * P:o0 * P + cnt], bank[:, 0:cnt], ACT.Copy))
            sig.clear()
            sig.close()

        sig = Signals(nc, "L1f_u")
        with nc.Fori(0, NBLK) as t:
            with nc.Block() as block:
                u_ring = Ring(sig, "u", c.banks[0:4])
                g_ring = Ring(sig, "g", c.banks[4:8])

                @block.tensor
                def _(pe):
                    for m in range(MI):
                        for n, ring in (("up", u_ring), ("gate", g_ring)):
                            bank = ring.claim(pe)
                            for k in range(KD):
                                last = nc.tensor.matmul(bank[:], wT[n][:, k, m * P:(m + 1) * P], c.xT[:, k, bass.ts(t, BLK)],
                                                        start=(k == 0), stop=(k == KD - 1))
                            ring.fill(last)

                @block.scalar
                def _(act):
                    for m in range(MI):
                        bank = u_ring.take(act)
                        act.wait_ge(sig("u_max"), m + 1)
                        u_ring.empty(nc.scalar.activation(up[:, m, bass.ts(t, BLK)], bank[:], ACT.Copy, scale=s["x"][:, 1:2]))

                @block.vector
                def _(dve):
                    for m in range(MI):
                        bank = u_ring.bufs[m % 4]
                        dve.wait_ge(u_ring.filled, m + 1)
                        nc.vector.tensor_reduce(turn_max[:, 0, m:m + 1], bank[:], AX.X, ALU.max,
                                                apply_absolute_value=True).then_inc(sig("u_max"), 1)
                        bank = g_ring.take(dve)
                        nc.vector.tensor_reduce(turn_max[:, 1, m:m + 1], bank[:], AX.X, ALU.max, apply_absolute_value=True).then_inc(sig("g_max"), 1)
                        g_ring.empty(nc.vector.tensor_scalar(gate[:, m, bass.ts(t, BLK)], bank[:], s["x"][:, 1:2], None, ALU.mult))
                    dve.wait_ge(sig("g_max"), MI)
                    dve.wait_ge(sig("u_max"), MI)
                    nc.vector.tensor_copy(all_max[:, bass.ts(t, 2 * MI)], turn_max[:].rearrange("p a m -> p (a m)"))
            sig.clear()
        sig.close()

        with ExitStack() as inner:
            sw = c.tiles(inner, "L1f")
            sg = [sw(f"sigmoid{i}", [P, N]) for i in range(2)]
            mx = sw("chunk_max", [P, 2, MI])
            sig = Signals(nc, "L1f_g")
            with nc.Block() as block:
                @block.vector
                def _(dve):
                    ch = Chain(dve, sig("dve_chain"))
                    vec = nc.vector
                    absmax = lambda o, a: vec.tensor_reduce(o, a, AX.X, ALU.max, apply_absolute_value=True)
                    for i, n in enumerate(("up", "gate")):
                        of_n = all_max[:].rearrange("p (t a m) -> p a t m", a=2, m=MI)[:, i]
                        ch.link(vec.tensor_reduce(s[n][:, 0:1], of_n, AX.XY, ALU.max))
                        vec.tensor_scalar(s[n][:, 0:1], s[n][:, 0:1], s["x"][:, 1:2], None, ALU.mult).then_inc(sig("maxima"), 1)
                    dve.wait_ge(sig("reduced"), 1)
                    scale_of(ch, vec, s["up"])
                    vec.sem_inc(sig("up_scaled"), 1)
                    dve.wait_ge(sig("reduced"), 2)
                    scale_of(ch, vec, s["gate"])

                    def weigh(m):
                        dve.wait_ge(sig("sigmoid"), m + 1)
                        a = sg[m % 2][:]
                        ch.link(vec.tensor_scalar(a, a, 65536.0, ROUND, ALU.mult, ALU.add))
                        ch.link(vec.tensor_scalar(a, a, -ROUND, 65535.0, ALU.add, ALU.min))
                        ch.link(vec.scalar_tensor_tensor(out=gate[:, m, :], in0=a, scalar=0.0, in1=gate[:, m, :],
                                                         op0=ALU.max, op1=ALU.mult))
                        ch.link(absmax(mx[:, 0, m:m + 1], gate[:, m, :]))
                        vec.sem_inc(sig("weighed"), 1)

                    for m in range(MI):
                        quantise(ch, vec, gate[:, m, :], s["gate"])
                        vec.sem_inc(sig("gate_q"), 1)
                        if m:
                            weigh(m - 1)
                    weigh(MI - 1)
                    ch.link(vec.tensor_scalar(s["gate"][:, 0:1], s["gate"][:, 1:2], 1.0 / 65536.0, None, ALU.mult))
                    vec.tensor_reduce(s["mix"][:, 0:1], mx[:, 0, :], AX.X, ALU.max).then_inc(sig("maxima"), 1)
                    dve.wait_ge(sig("reduced"), 3)
                    scale_of(ch, vec, s["mix"], factor=s["gate"][:, 0:1])
                    ch.link(vec.tensor_tensor(s["up"][:, 0:1], s["up"][:, 1:2], s["mix"][:, 1:2], ALU.mult))
                    for m in range(MI):
                        quantise(ch, vec, gate[:, m, :], s["mix"], low=False)
                        dve.wait_ge(sig("up_q"), m + 1)
                        ch.link(vec.scalar_tensor_tensor(out=gate[:, m, :], in0=gate[:, m, :], scalar=-QMAX - 1.0, in1=up[:, m, :],
                                                         op0=ALU.max, op1=ALU.mult))
                        ch.link(absmax(mx[:, 1, m:m + 1], gate[:, m, :]))
                    vec.tensor_reduce(s["out"][:, 0:1], mx[:, 1, :], AX.X, ALU.max).then_inc(sig("maxima"), 1)
                    dve.wait_ge(sig("reduced"), 4)
                    scale_of(ch, vec, s["out"], factor=s["up"][:, 0:1])

                @block.gpsimd
                def _(pool):
                    for i, n in enumerate(("up", "gate")):
                        pool.wait_ge(sig("maxima"), i + 1)
                        nc.gpsimd.partition_all_reduce(s[n][:, 0:1], s[n][:, 0:1], P, bass.bass_isa.ReduceOp.max).then_inc(sig("reduced"), 1)
                    pool.wait_ge(sig("up_scaled"), 1)
                    for m in range(MI):
                        a = up[:, m, :]
                        nc.gpsimd.tensor_scalar(a, a, s["up"][:, 3:4], ROUND, ALU.mult, ALU.add).then_inc(sig("up_steps"), 1)
                        pool.wait_ge(sig("up_steps"), 3 * m + 1)
                        nc.gpsimd.tensor_scalar(a, a, -ROUND, QMAX, ALU.add, ALU.min).then_inc(sig("up_steps"), 1)
                        pool.wait_ge(sig("up_steps"), 3 * m + 2)
                        nc.gpsimd.tensor_scalar(a, a, -QMAX - 1.0, None, ALU.max).then_inc(sig("up_steps"), 1)
                        pool.wait_ge(sig("up_steps"), 3 * m + 3)
                        nc.gpsimd.sem_inc(sig("up_q"), 1)
                    for i, n in enumerate(("mix", "out")):
                        pool.wait_ge(sig("maxima"), i + 3)
                        nc.gpsimd.partition_all_reduce(s[n][:, 0:1], s[n][:, 0:1], P, bass.bass_isa.ReduceOp.max).then_inc(sig("reduced"), 1)

                @block.scalar
                def _(act):
                    for m in range(MI):
                        act.wait_ge(sig("gate_q"), m + 1)
                        if m >= 2:
                            act.wait_ge(sig("weighed"), m - 1)
                        nc.scalar.activation(sg[m % 2][:], gate[:, m, :], ACT.Sigmoid, scale=s["gate"][:, 1:2]).then_inc(sig("sigmoid"), 1)
            sig.clear()
            sig.close()

        sig = Signals(nc, "L1f_d")
        with nc.Block() as block:
            ring = Ring(sig, "y", c.banks)

            @block.tensor
            def _(pe):
                for t in range(0, NT, 2):
                    pe.wait_ge(sig("out_q"), t // 4 + 1)
                    bank = ring.claim(pe)
                    for j in range(2):
                        for m in range(MI):
                            last = nc.tensor.matmul(bank[:, j * D:(j + 1) * D], gate[:, m, (t + j) * P:(t + j + 1) * P], wT["down"][:, m, :],
                                                    start=(m == 0), stop=(m == MI - 1))
                    ring.fill(last)

            @block.vector
            def _(dve):
                ch = Chain(dve, sig("dve_chain"))
                for n in range(NBLK):
                    quantise(ch, nc.vector, gate[:, :, n * BLK:(n + 1) * BLK], s["out"])
                    nc.vector.sem_inc(sig("out_q"), 1)
                for t in range(0, NT, 2):
                    bank = ring.take(dve)
                    xs = c.x[:, t:t + 2, :].rearrange("p t d -> p (t d)")
                    ring.empty(nc.vector.scalar_tensor_tensor(out=xs, in0=bank[:], scalar=s["out"][:, 1:2], in1=xs,
                                                              op0=ALU.mult, op1=ALU.add))
        sig.clear()
        sig.close()


def layer2_attn(c):
    nc, w = c.nc, c.dram
    L, S = 64, 64
    START = (L - 1) // 2
    PAD = L - START - 1
    W = PAD + T + START + 1
    ON_TENSOR, ON_VECTOR, ON_GPSIMD = (list(range(*r)) for r in ((0, 20), (20, 49), (49, L)))
    with ExitStack() as stack:
        sb = c.tiles(stack, "L2a")
        taps = sb("taps", [P, KD, L])
        u = sb("u", [P, KD, B, W])
        with ExitStack() as inner:
            sw = c.tiles(inner, "L2a")
            cm, bm = sw("cm", [P, KD, S]), sw("bm", [P, KD, S])
            am, dvec, ldt = sw("am", [P, S]), sw("dvec", [P, KD]), sw("ldt", [P, KD])
            power, ones = sw("power", [P, L]), sw("ones", [P, P])
            la = sw("la", [P, L, S])
            ex = [sw(f"ex{k}", [P, L, S]) for k in range(KD)]
            normalise(c, "n2a", c.x, dstT=c.xT, loads=[(cm[:], w["L2a_c"]), (bm[:], w["L2a_b"]), (dvec[:], w["L2a_d"]), (ldt[:], w["L2a_ldt"]),
                              (power[:], w["iota64"]), (ones[:], w["tri_strict_ones"][:, 1, :]), (am[:], w["L2a_a"].rearrange("(a n) -> a n", a=1).to_broadcast([P, S]))])
            sig = Signals(nc, "L2a_k")
            with nc.Block() as block:
                @block.gpsimd
                def _(pool):
                    nc.gpsimd.memset(u[:], 0.0).then_inc(sig("zeroed"), 1)

                @block.tensor
                def _(pe):
                    for k in range(KD):
                        last = nc.tensor.matmul(c.banks[0][:, 0:S], ones[:], cm[:, k, :], start=(k == 0), stop=(k == KD - 1))
                    last.then_inc(sig("c_sum"), 1)

                @block.vector
                def _(dve):
                    ch = Chain(dve, sig("dve_chain"))
                    vec = nc.vector
                    vec.tensor_tensor(la[:], power[:].unsqueeze(2).to_broadcast([P, L, S]),
                                      am[:].unsqueeze(1).to_broadcast([P, L, S]), ALU.mult).then_inc(sig("exponents"), 1)
                    dve.wait_ge(sig("c_sum"), 1)
                    ch.link(vec.tensor_tensor(cm[:], c.banks[0][:, 0:S].unsqueeze(1).to_broadcast([P, KD, S]), bm[:], ALU.mult))
                    for k in range(KD):
                        dve.wait_ge(sig("powers"), k + 1)
                        ch.link(vec.tensor_tensor(ex[k][:], ex[k][:], cm[:, k, :].unsqueeze(1).to_broadcast([P, L, S]), ALU.mult))
                        ch.link(vec.tensor_reduce(taps[:, k, :], ex[k][:], AX.X, ALU.add))
                    vec.tensor_tensor(taps[:, :, START], taps[:, :, START], dvec[:], ALU.add)

                @block.scalar
                def _(act):
                    nc.scalar.activation(ldt[:], ldt[:], ACT.Exp).then_inc(sig("dt"), 1)
                    act.wait_ge(sig("dt"), 1)
                    act.wait_ge(sig("exponents"), 1)
                    for k in range(KD):
                        nc.scalar.activation(ex[k][:], la[:], ACT.Exp, scale=ldt[:, k:k + 1]).then_inc(sig("powers"), 1)
                    act.wait_ge(sig("zeroed"), 1)
                    for k in range(KD):
                        nc.scalar.activation(u[:, k, :, PAD:PAD + T], c.xT[:, k, :].rearrange("p (b t) -> p b t", b=B), ACT.Copy)
            sig.clear()
            sig.close()
        acc = sb("acc", [P, KD, B, T])
        acc_g = c.xT[:].rearrange("p k (b t) -> p k b t", b=B)
        product = [sb(f"product{i}", [P, B, T]) for i in range(2)]
        diag = sb("diag", [P, KD, len(ON_TENSOR), P])
        sig = Signals(nc, "L2a")
        with nc.Block() as block:
            shifted = lambda k, l: u[:, k, :, PAD + START - l:PAD + START - l + T]

            @block.scalar
            def _(act):
                for k in range(KD):
                    for i, l in enumerate(ON_TENSOR):
                        nc.scalar.activation(diag[:, k, i, :], c.ident[:], ACT.Copy, scale=taps[:, k, l:l + 1]).then_inc(sig("diagonal"), 1)
                n = 0
                for k in range(KD):
                    for i, l in enumerate(ON_GPSIMD):
                        if i == 0:
                            nc.scalar.activation(acc_g[:, k], shifted(k, l), ACT.Copy, scale=taps[:, k, l:l + 1]).then_inc(sig("first_product"), 1)
                            continue
                        if n >= 2:
                            act.wait_ge(sig("added"), n - 1)
                        nc.scalar.activation(product[n % 2][:], shifted(k, l), ACT.Copy, scale=taps[:, k, l:l + 1]).then_inc(sig("product"), 1)
                        n += 1

            @block.gpsimd
            def _(pool):
                n = 0
                for k in range(KD):
                    pool.wait_ge(sig("first_product"), k + 1)
                    for l in ON_GPSIMD[1:]:
                        pool.wait_ge(sig("product"), n + 1)
                        nc.gpsimd.tensor_tensor(acc_g[:, k], acc_g[:, k], product[n % 2][:], ALU.add).then_inc(sig("added"), 1)
                        n += 1
                        pool.wait_ge(sig("added"), n)

            @block.tensor
            def _(pe):
                for k in range(KD):
                    for i, l in enumerate(ON_TENSOR):
                        pe.wait_ge(sig("diagonal"), k * len(ON_TENSOR) + i + 1)
                        for q in range(NBLK):
                            last = nc.tensor.matmul(c.banks[k * NBLK + q][:], diag[:, k, i, :],
                                                    shifted(k, l)[:, q * TB:(q + 1) * TB, :],
                                                    start=(i == 0), stop=(i == len(ON_TENSOR) - 1))
                    last.then_inc(sig("tensor_taps"), 1)
                pe.wait_ge(sig("summed"), 1)
                for t in range(0, NT, 2):
                    bank = c.banks[t // 2]
                    for j in range(2):
                        for k in range(KD):
                            tt = t + j
                            last = nc.tensor.transpose(bank[:, j * D + k * P:j * D + (k + 1) * P],
                                                       acc[:, k, tt // TB, (tt % TB) * P:(tt % TB + 1) * P], c.ident[:])
                    last.then_inc(sig("turned"), 1)

            @block.vector
            def _(dve):
                ch = Chain(dve, sig("dve_chain"))
                vec = nc.vector
                for k in range(KD):
                    for i, l in enumerate(ON_VECTOR):
                        if i == 0:
                            ch.link(vec.tensor_scalar(acc[:, k], shifted(k, l), taps[:, k, l:l + 1], None, ALU.mult))
                        else:
                            ch.link(vec.scalar_tensor_tensor(out=acc[:, k], in0=shifted(k, l), scalar=taps[:, k, l:l + 1], in1=acc[:, k],
                                                             op0=ALU.mult, op1=ALU.add))
                for k in range(KD):
                    dve.wait_ge(sig("added"), (k + 1) * (len(ON_GPSIMD) - 1))
                    ch.link(vec.tensor_tensor(acc[:, k], acc[:, k], acc_g[:, k], ALU.add))
                    dve.wait_ge(sig("tensor_taps"), k + 1)
                    for q in range(NBLK):
                        part = acc[:, k, q * TB:(q + 1) * TB, :].rearrange("p b t -> p (b t)")
                        last = vec.tensor_tensor(part, part, c.banks[k * NBLK + q][:], ALU.add)
                last.then_inc(sig("summed"), 1)
                for t in range(0, NT, 2):
                    dve.wait_ge(sig("turned"), t // 2 + 1)
                    xs = c.x[:, t:t + 2, :].rearrange("p t d -> p (t d)")
                    vec.tensor_tensor(xs, xs, c.banks[t // 2][:], ALU.add)
        sig.clear()
        sig.close()


def layer3_attn(c):
    nc, w = c.nc, c.dram
    H, DH = 16, 16
    with ExitStack() as stack:
        sb = c.tiles(stack, "L3a")
        xn = sb("xn", [P, NT, D])
        wqk, wv = sb("wqk", [P, KD, 2 * D]), sb("wv", [P, KD, D])
        bqk, bv, gamma, beta = sb("bqk", [P, 2 * D]), sb("bv", [P, D]), sb("gamma", [P, D]), sb("beta", [P, D])
        cos, sin = sb("cos", [P, TB, D]), sb("sin", [P, TB, D])
        ones, diag = sb("ones", [P, P]), sb("blockdiag", [P, P])
        pair = lambda name, shape: [sb(f"{name}{r}", shape) for r in range(2)]
        xb_r = pair("xb", [P, KD, T])
        qk_r, rot_r, tmp_r = (pair(n, [P, TB, 2, D]) for n in ("qk", "rot", "tmp"))
        v_r, res_r = pair("v", [P, TB, D]), pair("res", [P, TB, D])
        kv_r, qrT_r, z_r = pair("kv", [P, KD, P]), pair("qrT", [P, KD, T]), pair("z", [P, TB, H])
        stats_r, mv_r, rstd_r = pair("stats", [P, TB, 6]), pair("mv", [P, TB, 2]), pair("rstd", [P, TB, 3])
        row = lambda n: w[n].rearrange("(a n) -> a n", a=1)
        normalise(c, "n3a", c.x, dst=xn, dstT=c.xT, loads=[(wqk[:], w["L3a_wqk"]), (wv[:], w["L3a_wv"]), (bqk[:], row("L3a_bqk").to_broadcast([P, 2 * D])),
                          (bv[:], row("L3a_bv").to_broadcast([P, D])), (gamma[:], row("L3a_gamma").to_broadcast([P, D])),
                          (beta[:], row("L3a_beta").to_broadcast([P, D])), (cos[:], w["rope_cos"]), (sin[:], w["rope_sin"]),
                          (ones[:], w["tri_strict_ones"][:, 1, :]), (diag[:], w["blockdiag16"])])
        sig = Signals(nc, "L3a")
        with nc.Fori(0, B // 2) as turn:
            with nc.Block() as block:
                def bank_of(r, what):
                    return c.banks[4 * r + {"qk0": 0, "turned": 0, "qk1": 1, "out": 1, "v": 2, "kv": 2, "sum": 3}[what]]

                @block.scalar
                def _(act):
                    for r in range(2):
                        nc.scalar.activation(xb_r[r][:], c.xT[:, :, bass.ts(turn * 2 + r, T)], ACT.Copy).then_inc(sig(f"sliced{r}"), 1)
                    for r in range(2):
                        qk = qk_r[r]
                        for t in range(TB):
                            act.wait_ge(sig(f"biased{r}"), t + 1)
                            nc.scalar.activation(qk[:, t], qk[:, t], ACT.Gelu).then_inc(sig(f"gelu{r}"), 1)
                    for r in range(2):
                        act.wait_ge(sig(f"turned{r}"), 1)
                        nc.scalar.activation(qrT_r[r][:], bank_of(r, "turned")[:].rearrange("p (k t) -> p k t", k=KD), ACT.Copy).then_inc(sig(f"q_feat{r}"), 1)
                    for r in range(2):
                        act.wait_ge(sig(f"var_eps{r}"), 1)
                        nc.scalar.activation(rstd_r[r][:, :, 1], rstd_r[r][:, :, 0], ACT.Sqrt).then_inc(sig(f"std{r}"), 1)

                @block.tensor
                def _(pe):
                    for r in range(2):
                        xb = xb_r[r]
                        pe.wait_ge(sig(f"sliced{r}"), 1)
                        for t in range(TB):
                            for k in range(KD):
                                last = nc.tensor.matmul(bank_of(r, f"qk{t}")[:], xb[:, k, t * P:(t + 1) * P], wqk[:, k, :], start=(k == 0), stop=(k == KD - 1))
                            last.then_inc(sig(f"qk{r}"), 1)
                        for t in range(TB):
                            for k in range(KD):
                                last = nc.tensor.matmul(bank_of(r, "v")[:, t * D:(t + 1) * D], xb[:, k, t * P:(t + 1) * P], wv[:, k, :],
                                                        start=(k == 0), stop=(k == KD - 1))
                        last.then_inc(sig(f"v_raw{r}"), 1)
                    for r in range(2):
                        qk, rot, v = qk_r[r], rot_r[r], v_r[r]
                        pe.wait_ge(sig(f"shifted{r}"), 1)
                        for t in range(TB):
                            last = nc.tensor.matmul(bank_of(r, "sum")[:, 0:D], ones[:], qk[:, t, 1, :], start=(t == 0), stop=(t == TB - 1))
                        last.then_inc(sig(f"k_sum{r}"), 1)
                        pe.wait_ge(sig(f"rotated{r}"), 1)
                        for m in range(KD):
                            for t in range(TB):
                                last = nc.tensor.transpose(bank_of(r, "turned")[:, m * T + t * P:m * T + (t + 1) * P], rot[:, t, 0, m * P:(m + 1) * P], c.ident[:])
                        last.then_inc(sig(f"turned{r}"), 1)
                        pe.wait_ge(sig(f"v{r}"), 1)
                        for m in range(KD):
                            for t in range(TB):
                                last = nc.tensor.matmul(bank_of(r, "kv")[:, m * P:(m + 1) * P], rot[:, t, 1, m * P:(m + 1) * P],
                                                        v[:, t, m * P:(m + 1) * P], start=(t == 0), stop=(t == TB - 1))
                        last.then_inc(sig(f"kv{r}"), 1)
                    for r in range(2):
                        pe.wait_ge(sig(f"q_feat{r}"), 1)
                        pe.wait_ge(sig(f"kv_heads{r}"), 1)
                        for t in range(TB):
                            for m in range(KD):
                                last = nc.tensor.matmul(bank_of(r, "out")[:, t * D + m * P:t * D + (m + 1) * P], qrT_r[r][:, m, t * P:(t + 1) * P],
                                                        kv_r[r][:, m, :], start=True, stop=True)
                        last.then_inc(sig(f"attended{r}"), 1)

                @block.vector
                def _(dve):
                    ch = Chain(dve, sig("dve_chain"))
                    vec = nc.vector
                    for r in range(2):
                        qk = qk_r[r]
                        for t in range(TB):
                            dve.wait_ge(sig(f"qk{r}"), t + 1)
                            vec.tensor_tensor(qk[:, t].rearrange("p a d -> p (a d)"), bank_of(r, f"qk{t}")[:], bqk[:], ALU.add).then_inc(sig(f"biased{r}"), 1)
                        dve.wait_ge(sig(f"v_raw{r}"), 1)
                        vec.tensor_tensor(v_r[r][:], bank_of(r, "v")[:].rearrange("p (t d) -> p t d", t=TB), bv[:].unsqueeze(1).to_broadcast([P, TB, D]),
                                          ALU.add).then_inc(sig(f"v{r}"), 1)
                    for r in range(2):
                        qk, rot, tmp, z = qk_r[r], rot_r[r], tmp_r[r], z_r[r]
                        dve.wait_ge(sig(f"gelu{r}"), TB)
                        vec.tensor_scalar(qk[:], qk[:], 0.21, None, ALU.add).then_inc(sig(f"shifted{r}"), 1)
                        dve.wait_ge(sig(f"shifted{r}"), 1)
                        for t in range(TB):
                            both = lambda a: a[:, t].unsqueeze(1).to_broadcast([P, 2, D])
                            even = lambda a: a.rearrange("p a (d two) -> p a d two", two=2)[:, :, :, 0]
                            odd = lambda a: a.rearrange("p a (d two) -> p a d two", two=2)[:, :, :, 1]
                            vec.tensor_tensor(even(tmp[:, t]), odd(qk[:, t]), even(both(sin)), ALU.mult)
                            vec.tensor_tensor(odd(tmp[:, t]), even(qk[:, t]), odd(both(sin)), ALU.mult)
                            ch.link(vec.tensor_tensor(rot[:, t], qk[:, t], both(cos), ALU.mult))
                        vec.tensor_tensor(rot[:], rot[:], tmp[:], ALU.add).then_inc(sig(f"rotated{r}"), 1)
                        dve.wait_ge(sig(f"k_sum{r}"), 1)
                        dve.wait_ge(sig(f"rotated{r}"), 1)
                        ch.link(vec.tensor_tensor(tmp[:, :, 0, :], qk[:, :, 0, :], bank_of(r, "sum")[:, 0:D].unsqueeze(1).to_broadcast([P, TB, D]), ALU.mult))
                        for t in range(TB):
                            last = vec.tensor_reduce(z[:, t, :], tmp[:, t, 0, :].rearrange("p (h d) -> p h d", h=H), AX.X, ALU.add)
                        ch.link(last)
                        ch.link(vec.tensor_scalar(z[:], z[:], 1.0 / T, 1e-6, ALU.mult, ALU.add))
                        ch.link(vec.reciprocal(z[:], z[:]))
                    for r in range(2):
                        dve.wait_ge(sig(f"kv{r}"), 1)
                        vec.tensor_tensor(kv_r[r][:], bank_of(r, "kv")[:, 0:D].rearrange("p (m e) -> p m e", m=KD),
                                          diag[:].unsqueeze(1).to_broadcast([P, KD, P]), ALU.mult).then_inc(sig(f"kv_heads{r}"), 1)
                    for r in range(2):
                        res, z, stats, mv, rstd = res_r[r], z_r[r], stats_r[r], mv_r[r], rstd_r[r]
                        dve.wait_ge(sig(f"attended{r}"), 1)
                        for t in range(TB):
                            last = vec.tensor_tensor(res[:, t, :].rearrange("p (h d) -> p h d", h=H),
                                                     bank_of(r, "out")[:, t * D:(t + 1) * D].rearrange("p (h d) -> p h d", h=H),
                                                     z[:, t, :].unsqueeze(2).to_broadcast([P, H, DH]), ALU.mult)
                        ch.link(last)
                        ch.link(vec.tensor_tensor(res[:], res[:], xn[:, bass.ts(turn * 2 + r, TB), :], ALU.add))
                        for t in range(TB):
                            last = vec.bn_stats(stats[:, t, :], res[:, t, :])
                        ch.link(last)
                        for t in range(TB):
                            last = vec.bn_aggr(mv[:, t, :], stats[:, t, :])
                        ch.link(last)
                        vec.tensor_scalar_add(rstd[:, :, 0], mv[:, :, 1], 1e-12).then_inc(sig(f"var_eps{r}"), 1)
                    for r in range(2):
                        res, mv, rstd = res_r[r], mv_r[r], rstd_r[r]
                        dve.wait_ge(sig(f"std{r}"), 1)
                        ch.link(vec.reciprocal(rstd[:, :, 2], rstd[:, :, 1]))
                        for t in range(TB):
                            last = vec.tensor_scalar(res[:, t, :], res[:, t, :], mv[:, t, 0:1], rstd[:, t, 2:3], ALU.subtract, ALU.mult)
                        ch.link(last)
                        rowwise = lambda a: a[:].unsqueeze(1).to_broadcast([P, TB, D])
                        xr = c.x[:, bass.ts(turn * 2 + r, TB), :]
                        ch.link(vec.tensor_tensor(res[:], res[:], rowwise(gamma), ALU.mult))
                        ch.link(vec.tensor_tensor(res[:], res[:], rowwise(beta), ALU.add))
                        vec.tensor_tensor(xr, xr, res[:], ALU.add)
            sig.clear()
        sig.close()




def layer0_xattn(c):
    nc, w = c.nc, c.dram
    H, DH, NA, LAG = 16, 16, 4, 2
    with ExitStack() as stack:
        sb = c.tiles(stack, "L0x")
        wq, wv, wk, wo = (sb(n, [P, KD, D]) for n in ("wq", "wv", "wk", "wo"))
        bq, bv, bk, bo = sb("bq", [P, KD]), sb("bv", [P, KD]), sb("bk", [P, D]), sb("bo", [P, D])
        causal = sb("causal", [P, 3 * P])
        ones, twin = sb("ones", [P, P]), sb("twin", [P, 2])
        xb, cb = ([sb(f"{n}{i}", [P, KD, T]) for i in range(2)] for n in ("xb", "cb"))
        q = [sb(f"q{i}", [P, KD, T]) for i in range(2)]
        v = [sb(f"v{i}", [P, 2, KD, T]) for i in range(2)]
        k = [sb(f"k{i}", [P, TB, D]) for i in range(2)]
        k2 = [sb(f"k2{i}", [P, TB, 2, D]) for i in range(2)]
        eq, rq, ek, rk = sb("eq", [P, KD, T]), sb("rq", [P, KD, T]), sb("ek", [P, TB, D]), sb("rk", [P, TB, D])
        den = [sb(f"den{i}", [P, KD, T]) for i in range(2)]
        att = [sb(f"att{i}", [P, 3 * P]) for i in range(NA)]
        cT, y = sb("cT", [P, KD, T]), sb("y", [P, TB, D])
        row = lambda n: w[n].rearrange("(a n) -> a n", a=1)
        normalise(c, "n0x", c.x, dstT=c.xT, loads=[(wq[:], w["L0x_wq"]), (wv[:], w["L0x_wv"]), (wk[:], w["L0x_wk"]), (wo[:], w["L0x_wo"]),
                          (bq[:], w["L0x_bq"]), (bv[:], w["L0x_bv"]), (bk[:], row("L0x_bk").to_broadcast([P, D])),
                          (bo[:], row("L0x_bo").to_broadcast([P, D])), (causal[:], w["causal"]), (twin[:], w["twin"]),
                          (ones[:], w["tri_strict_ones"][:, 1, :])])
        sig = Signals(nc, "L0x_z")
        with nc.Block() as block:
            @block.gpsimd
            def _(pool):
                for k2_ in k2:
                    nc.gpsimd.memset(k2_[:], 0.0)
        sig.close()
        sig = Signals(nc, "L0x")
        with nc.Fori(0, B // ROWS) as turn:
            with nc.Block() as block:
                s_ring = Ring(sig, "s", c.banks[0:3])
                t_ring = Ring(sig, "t", c.banks[3:5])
                acc, out_bank = c.banks[5:7], c.banks[7]
                row_of = lambda r: turn * ROWS + r
                total, MID = ROWS * H, H // 2

                def s_item(g):
                    return g + min(ROWS, (g + MID) // H + 1)

                @block.tensor
                def _(pe):
                    mm = nc.tensor.matmul

                    def project(r):
                        pe.wait_ge(sig("sliced"), 2 * (r + 1))
                        for ring, weights, src in ((t_ring, wq, xb[r % 2]), (s_ring, wv, cb[r % 2])):
                            bank = ring.claim(pe)
                            for m in range(KD):
                                for kd in range(KD):
                                    last = mm(bank[:, m * T:(m + 1) * T], weights[:, kd, m * P:(m + 1) * P], src[:, kd, :],
                                              start=(kd == 0), stop=(kd == KD - 1))
                            ring.fill(last)
                        bank = t_ring.claim(pe)
                        for t in range(TB):
                            for kd in range(KD):
                                last = mm(bank[:, t * D:(t + 1) * D], cb[r % 2][:, kd, t * P:(t + 1) * P], wk[:, kd, :],
                                          start=(kd == 0), stop=(kd == KD - 1))
                        t_ring.fill(last)

                    def output(r):
                        if r:
                            pe.wait_ge(sig("out_read"), r)
                        pe.wait_ge(sig("cT"), TB * (r + 1))
                        for t in range(TB):
                            for kd in range(KD):
                                last = mm(out_bank[:, t * D:(t + 1) * D], cT[:, kd, t * P:(t + 1) * P], wo[:, kd, :],
                                          start=(kd == 0), stop=(kd == KD - 1))
                        last.then_inc(sig("projected"), 1)

                    project(0)
                    for g in range(total + LAG):
                        r, i = divmod(g, H)
                        if g < total:
                            if i == MID and r + 1 < ROWS:
                                project(r + 1)
                            if i == 0:
                                pe.wait_ge(sig("q"), r + 1)
                                pe.wait_ge(s_ring.emptied, max(0, r * H - MID) + r + 1)
                            bank = s_ring.claim(pe)
                            q_, v_ = q[r % 2], v[r % 2]
                            m, e, ps = i // 8, i % 2, slice(32 * (i % 8 // 2), 32 * (i % 8 // 2) + 32)
                            mm(bank[:, 0:T], v_[ps, e, m, 0:P], q_[ps, m, :], start=True, stop=True)
                            s_ring.fill(mm(bank[:, T:3 * P], v_[ps, e, m, P:T], q_[ps, m, P:T], start=True, stop=True))
                        if i == 1 and r < ROWS:
                            bank = t_ring.claim(pe)
                            pe.wait_ge(sig("k"), r + 1)
                            tri, k_ = causal[:, 0:P], k[r % 2]
                            for m in range(KD):
                                ks = slice(m * P, (m + 1) * P)
                                mm(bank[:, m * T:m * T + P], k_[:, 0, ks], tri, start=True, stop=True)
                                mm(bank[:, m * T + P:(m + 1) * T], k_[:, 0, ks], ones[:], start=True, stop=False)
                                last = mm(bank[:, m * T + P:(m + 1) * T], k_[:, 1, ks], tri, start=False, stop=True)
                            t_ring.fill(last)
                        if r and i == LAG + 2 and r < ROWS:
                            output(r - 1)
                        if g >= LAG:
                            j = g - LAG
                            r, h = divmod(j, H)
                            e, u, k2_ = h % 2, h // 2, k2[r % 2]
                            if h == 0:
                                pe.wait_ge(sig("k2"), r + 1)
                                if r:
                                    pe.wait_ge(sig("cT"), TB * r)
                            pe.wait_ge(s_ring.emptied, s_item(j) + 1)
                            a, us = att[j % NA], slice(u * 32, (u + 1) * 32)
                            out = [acc[t][32 * (u % 4):32 * (u % 4) + 32, u // 4 * P:(u // 4 + 1) * P] for t in range(TB)]
                            mm(out[0], k2_[:, 0, e, us], a[:, 0:P], start=(e == 0), stop=(e == 1))
                            mm(out[1], k2_[:, 0, e, us], a[:, P:2 * P], start=(e == 0), stop=False)
                            mm(out[1], k2_[:, 1, e, us], a[:, 2 * P:3 * P], start=False, stop=(e == 1)).then_inc(sig("weighted"), 1)
                    output(ROWS - 1)

                @block.scalar
                def _(act):
                    for r in range(ROWS):
                        if r >= 2:
                            act.wait_ge(sig("k_raw"), r - 1)
                        nc.scalar.activation(xb[r % 2][:], c.xT[:, :, bass.ts(row_of(r), T)], ACT.Copy).then_inc(sig("sliced"), 1)
                        nc.scalar.activation(cb[r % 2][:], c.ctxT[:, :, bass.ts(row_of(r), T)], ACT.Copy).then_inc(sig("sliced"), 1)
                        act.wait_ge(sig("q_raw"), r + 1)
                        nc.scalar.activation(eq[:], eq[:], ACT.Exp).then_inc(sig("exp"), 1)
                        act.wait_ge(sig("k_min"), r + 1)
                        nc.scalar.activation(ek[:], ek[:], ACT.Exp).then_inc(sig("exp"), 1)

                @block.gpsimd
                def _(pool):
                    for r in range(ROWS):
                        pool.wait_ge(sig("exp"), 2 * r + 1)
                        nc.gpsimd.tensor_tensor(q[r % 2][:], rq[:], eq[:], ALU.add).then_inc(sig("q"), 1)
                        pool.wait_ge(sig("k"), r + 1)
                        for e in range(2):
                            own = lambda a: a.rearrange("p t (u e d) -> p t u e d", e=2, d=DH)[:, :, :, e, :]
                            last = nc.gpsimd.tensor_copy(own(k2[r % 2][:, :, e, :]), own(k[r % 2][:]))
                        last.then_inc(sig("k2"), 1)

                @block.vector
                def _(dve):
                    vec = nc.vector
                    wide = lambda a: a[:].unsqueeze(1).to_broadcast([P, TB, D])

                    def project(r):
                        bank = t_ring.take(dve)
                        if r:
                            dve.wait_ge(sig("q"), r)
                        for m in range(KD):
                            cols = slice(m * T, (m + 1) * T)
                            vec.tensor_scalar(eq[:, m, :], bank[:, cols], bq[:, m:m + 1], 0.0, ALU.add, ALU.min)
                            last = vec.tensor_scalar(rq[:, m, :], bank[:, cols], bq[:, m:m + 1], 0.0, ALU.add, ALU.max)
                        t_ring.empty(last)
                        dve.wait_ge(t_ring.emptied, t_ring.n_out)
                        vec.sem_inc(sig("q_raw"), 1)
                        bank = s_ring.take(dve)
                        for m in range(KD):
                            for e in range(2):
                                last = vec.tensor_scalar(v[r % 2][:, e, m, :], bank[:, m * T:(m + 1) * T], bv[:, m:m + 1], twin[:, e:e + 1],
                                                         ALU.add, ALU.mult)
                        s_ring.empty(last)
                        bank = t_ring.take(dve)
                        t_ring.empty(vec.tensor_tensor(rk[:], bank[:].rearrange("p (t d) -> p t d", t=TB), wide(bk), ALU.add))
                        dve.wait_ge(t_ring.emptied, t_ring.n_out)
                        vec.sem_inc(sig("k_raw"), 1)
                        vec.tensor_scalar(ek[:], rk[:], 0.0, None, ALU.min).then_inc(sig("k_min"), 1)
                        dve.wait_ge(sig("exp"), 2 * (r + 1))
                        flat = lambda a: a[:].rearrange("p t d -> p (t d)")
                        vec.scalar_tensor_tensor(out=flat(k[r % 2]), in0=flat(rk), scalar=0.0, in1=flat(ek),
                                                 op0=ALU.max, op1=ALU.add).then_inc(sig("k"), 1)

                    def divide(r):
                        dve.wait_ge(sig("inverse"), KD * (r + 1))
                        dve.wait_ge(sig("weighted"), H * (r + 1))
                        for t in range(TB):
                            ts = slice(t * P, (t + 1) * P)
                            vec.tensor_tensor(cT[:, :, ts], acc[t][:, 0:D].rearrange("p (m t) -> p m t", m=KD), den[r % 2][:, :, ts],
                                              ALU.mult).then_inc(sig("cT"), 1)

                    def add(r):
                        dve.wait_ge(sig("projected"), r + 1)
                        if r:
                            dve.wait_ge(sig("added"), r)
                        vec.tensor_tensor(y[:], out_bank[:].rearrange("p (t d) -> p t d", t=TB), wide(bo), ALU.add).then_inc(sig("out_read"), 1)
                        dve.wait_ge(sig("out_read"), r + 1)
                        xr = c.x[:, bass.ts(row_of(r), TB), :]
                        vec.tensor_tensor(xr, xr, y[:], ALU.add).then_inc(sig("added"), 1)

                    project(0)
                    for g in range(total):
                        r, h = divmod(g, H)
                        if h == MID and r + 1 < ROWS:
                            project(r + 1)
                        bank = s_ring.take(dve)
                        if g >= NA:
                            dve.wait_ge(sig("weighted"), g - NA + 1)
                        s_ring.empty(vec.tensor_tensor(att[g % NA][:], bank[:, 0:3 * P], causal[:], ALU.mult))
                        if h == LAG and r:
                            divide(r - 1)
                        if h == 3:
                            bank, d = t_ring.take(dve), den[r % 2]
                            t_ring.empty(vec.tensor_tensor(d[:], q[r % 2][:], bank[:].rearrange("p (m t) -> p m t", m=KD), ALU.mult))
                            dve.wait_ge(t_ring.emptied, t_ring.n_out)
                            vec.tensor_scalar(d[:], d[:], 1e-6, None, ALU.add).then_inc(sig("den"), 1)
                            dve.wait_ge(sig("den"), r + 1)
                        if 4 <= h < 4 + KD:
                            d = den[r % 2][:, h - 4, :]
                            vec.reciprocal(d, d).then_inc(sig("inverse"), 1)
                        if h == 6 and r:
                            add(r - 1)
                    divide(ROWS - 1)
                    add(ROWS - 1)
            sig.clear()
        sig.close()




def layer0_attn(c):
    nc, w = c.nc, c.dram
    H, HD, DI, KC = 32, 64, 2048, 4
    MH = H * 16 // P
    MX = 18
    NG, GC = 4, BLK
    xt = c.ctxT[:].rearrange("p k n -> p (k n)").rearrange("p (t e) -> p t e", t=TB)
    v = c.ctx[:].rearrange("p a d -> p (a d)").rearrange("p (t e) -> p t e", t=TB)
    yzT = c.ctx[:].rearrange("p a d -> p (a d)").rearrange("p (k t) -> p k t", t=T)
    with ExitStack() as stack:
        sb = c.tiles(stack, "L0a")
        wz, wx, wd = sb("wz", [P, KD, DI]), sb("wx", [P, KD, MX * P]), sb("wd", [P, 2, KD, MH * P])
        wout = sb("wout", [P, DI // P, D])
        normalise(c, "n0a", c.x, dst=c.ctx, dstT=c.xT, loads=[(wx[:], w["L0a_wx"]), (wd[:, 0], w["L0a_wdl"]), (wd[:, 1], w["L0a_wdt"]),
                                                              (wz[:], w["L0a_wz"]), (wout[:], w["L0a_wout"])])
        norm = sb("norm", [P, DI // P])
        bz, bx, bd = sb("bz", [P, DI]), sb("bx", [P, MX]), sb("bd", [P, 2, MH])
        conv = sb("conv", [P, MX, KC])
        lcol, nega, dtb = sb("lcol", [P, MH]), sb("nega", [P, MH]), sb("dtb", [P, MH])
        dh, bo = sb("dh", [P, H]), sb("bo", [P, D])
        pick = sb("pick", [P, 8, P])
        um, vm, tri, last_row = sb("um", [P, T]), sb("vm", [P, P]), sb("tri", [P, P]), sb("last_row", [P, P])
        ones = sb("ones", [P, P])
        row = lambda n: w[n].rearrange("(a n) -> a n", a=1)
        c.load("L0a_ld", [(norm[:], w["L0a_norm"]), (bz[:], row("L0a_bz").to_broadcast([P, DI])),
                          (bx[:], w["L0a_bx"]), (bd[:], w["L0a_bd"]), (conv[:], w["L0a_conv"]), (lcol[:], w["L0a_l"]),
                          (nega[:], w["L0a_alog"]), (dtb[:], w["L0a_dtb"]), (dh[:], row("L0a_d").to_broadcast([P, H])),
                          (bo[:], row("L0a_bo").to_broadcast([P, D])), (pick[:], w["L0a_pick"]), (um[:], w["L0a_u"]),
                          (vm[:], w["L0a_v"]), (tri[:], w["tri_strict_ones"][:, 0, :]), (last_row[:], w["last_row"]),
                          (ones[:], w["tri_strict_ones"][:, 1, :])])
        xb = sb("xb", [P, KD, T])
        xc = [sb(f"xc{i}", [P, 2, KC - 1 + T]) for i in range(3)]
        xf = [sb(f"xf{i}", [P, 2, T]) for i in range(3)]
        bc = sb("bc", [P, 2, T])
        pre, sp, ex1 = sb("pre", [P, 2, MH, T]), sb("sp", [P, 2, MH, T]), sb("soft", [P, 2, MH, T])
        gcT, g, R = sb("gcT", [P, MH, T]), ex1[:, 0], ex1[:, 1]
        dt, gc, lam0, lam8 = (sb(n, [P, TB, H]) for n in ("dt", "gc", "lam0", "lam8"))
        ngc, coef = sb("ngc", [P, TB, H]), sb("coef", [P, TB, H])
        sfac, tfac = sb("sfac", [P, H]), sb("tfac", [P, H])
        qkd, qko, qdiag = sb("qkd", [P, TB, P]), sb("qko", [P, P]), sb("qdiag", [P, TB])
        wv = sb("wv", [P, DI])
        dtmp = wv[:, 0:T].rearrange("p (t s) -> p t s", t=TB)
        ident16, never16 = sb("ident16", [P, P], BF16), sb("never16", [P, P], BF16)
        ru = [sb(f"ru{i}", [P, 2, T]) for i in range(2)]
        ex = [sb(f"ex{i}", [P, 2, T]) for i in range(2)]
        att = [sb(f"att{i}", [P, 2, T]) for i in range(2)]
        spare = pre[:].rearrange("p i m t -> p (i m t)")
        tmp, y = spare[:, 0:GC], spare[:, GC:2 * GC].rearrange("p (t d) -> p t d", t=TB)
        zb = [spare[:, 2 * GC:3 * GC], spare[:, 3 * GC:4 * GC]]
        ss = sb("ss", [P, TB, 4])

        sig = Signals(nc, "L0a_c")
        with nc.Block() as block:
            @block.scalar
            def _(act):
                nc.scalar.activation(nega[:], nega[:], ACT.Exp).then_inc(sig("a"), 1)

            @block.vector
            def _(dve):
                vec = nc.vector
                dve.wait_ge(sig("a"), 1)
                vec.tensor_scalar(nega[:], nega[:], -1.0, None, ALU.mult)
                vec.tensor_tensor(bd[:, 0, :], bd[:, 0, :], lcol[:], ALU.mult)
                vec.tensor_tensor(bd[:, 1, :], bd[:, 1, :], dtb[:], ALU.add)
                for i in range(3):
                    vec.memset(xc[i][:], 0.0)
                vec.tensor_copy(ident16[:], c.ident[:])
                vec.tensor_scalar(never16[:], tri[:], -1.0, 1e30, ALU.add, ALU.mult)
                for k in range(DI // P):
                    vec.tensor_scalar(wout[:, k, :], wout[:, k, :], norm[:, k:k + 1], None, ALU.mult)
        sig.clear()
        sig.close()

        sig = Signals(nc, "L0a")
        with nc.Fori(0, B) as b:
            with nc.Block() as block:
                ra = Ring(sig, "ra", c.banks[0:2])
                rv = Ring(sig, "rv", c.banks[2:4])
                rx = Ring(sig, "rx", c.banks[5:7])
                qk_bank, y_bank, off_bank = c.banks[4], c.banks[5:7], c.banks[7]
                across = (c.banks[7], c.banks[4])
                NPX = MX // 2
                NPH = H // 2
                A_EXP = 4 + NPX

                @block.tensor
                def _(pe):
                    mm, tp = nc.tensor.matmul, nc.tensor.transpose

                    def project(p):
                        bank = ra.claim(pe)
                        for j in range(2):
                            for k in range(KD):
                                last = mm(bank[:, j * T:(j + 1) * T], wx[:, k, (2 * p + j) * P:(2 * p + j + 1) * P], xb[:, k, :],
                                          start=(k == 0), stop=(k == KD - 1))
                        ra.fill(last)

                    def turn(p):
                        pe.wait_ge(sig("silu"), p + 1)
                        bank = rx.claim(pe)
                        for t in range(TB):
                            for j in range(2):
                                last = tp(bank[:, t * T + j * P:t * T + (j + 1) * P], xf[p % 3][:, j, t * P:(t + 1) * P], c.ident[:])
                        rx.fill(last)

                    pe.wait_ge(sig("sliced"), 1)
                    for i in range(2):
                        for m in range(0, MH, 2):
                            bank = ra.claim(pe)
                            for j in range(2):
                                for k in range(KD):
                                    last = mm(bank[:, j * T:(j + 1) * T], wd[:, i, k, (m + j) * P:(m + j + 1) * P], xb[:, k, :],
                                              start=(k == 0), stop=(k == KD - 1))
                            ra.fill(last)
                    for p in range(3):
                        project(p)
                    pe.wait_ge(sig("silu"), 1)
                    mm(qk_bank[:, 0:T], bc[:, 0, 0:P], bc[:, 1, :], start=True, stop=True)
                    mm(qk_bank[:, T:T + P], bc[:, 0, P:T], bc[:, 1, P:T], start=True, stop=True).then_inc(sig("qk"), 1)
                    for n, a in enumerate((sp[:, 1], sp[:, 0], gcT)):
                        pe.wait_ge(sig("rows"), (2, 2, 3)[n])
                        for t in range(TB):
                            bank = rv.claim(pe)
                            for m in range(MH):
                                last = tp(bank[:, m * P:(m + 1) * P], a[:, m, t * P:(t + 1) * P], c.ident[:])
                            rv.fill(last)
                    for p in range(3, NPX):
                        project(p)
                        turn(p - 2)
                    pe.wait_ge(sig("gc_tok"), 1)
                    mm(off_bank[:, 0:H], last_row[:], gc[:, 0, :], start=True, stop=True).then_inc(sig("total"), 1)
                    turn(NPX - 2)
                    turn(NPX - 1)
                    pe.wait_ge(sig("R"), 1)
                    for i in range(NPH + 2):
                        if i < NPH:
                            bank = rv.claim(pe)
                            for j in range(2):
                                h = 2 * i + j
                                last = mm(bank[:, j * T:(j + 1) * T], pick[:, h % 8, :], R[:, h // 8, :], start=True, stop=True)
                            rv.fill(last)
                        if 1 <= i <= NPH:
                            bank = ra.claim(pe)
                            pe.wait_ge(sig("ru"), i)
                            mm(bank[:], vm[:], ru[(i - 1) % 2][:].rearrange("p j t -> p (j t)"), start=True, stop=False)
                            ra.fill(mm(bank[:].rearrange("p (j t) -> p j t", t=P), ident16[:],
                                       never16[:].unsqueeze(1).to_broadcast([P, 4, P]), start=False, stop=True))
                        if i >= 2:
                            q = i - 2
                            if q % 4 == 0:
                                gi = q // 4
                                pe.wait_ge(sig("wv"), gi + 1)
                                if gi >= 2:
                                    pe.wait_ge(sig("across_used"), gi - 1)
                                mm(across[gi % 2][:], qko[:], wv[:, gi * GC:(gi + 1) * GC], start=True, stop=True)
                                if gi:
                                    pe.wait_ge(sig("y_used"), gi)
                            pe.wait_ge(sig("att"), q + 1)
                            for j in range(2):
                                h = 2 * q + j
                                for t in range(TB):
                                    last = mm(y_bank[t][:, (h % 8) * HD:(h % 8 + 1) * HD], att[q % 2][:, j, t * P:(t + 1) * P],
                                              v[:, t, h * HD:(h + 1) * HD], start=True, stop=True)
                            last.then_inc(sig("weighted"), 1)
                    for gi in range(NG):
                        for t in range(TB):
                            bank = rv.claim(pe)
                            for k in range(KD):
                                last = mm(bank[:], xb[:, k, t * P:(t + 1) * P], wz[:, k, gi * GC:(gi + 1) * GC], start=(k == 0), stop=(k == KD - 1))
                            rv.fill(last)
                    for k in range(0, DI // P, 2):
                        bank = ra.claim(pe)
                        pe.wait_ge(sig("gated"), 2 * (k // 4) + 2)
                        for j in range(2):
                            for t in range(TB):
                                last = tp(bank[:, j * T + t * P:j * T + (t + 1) * P], xt[:, t, (k + j) * P:(k + j + 1) * P], c.ident[:])
                        ra.fill(last)
                    pe.wait_ge(ra.emptied, A_EXP + NPH + DI // P // 2)
                    for t in range(TB):
                        for k in range(DI // P):
                            last = mm(off_bank[:, t * D:(t + 1) * D], yzT[:, k, t * P:(t + 1) * P], wout[:, k, :],
                                      start=(k == 0), stop=(k == DI // P - 1))
                    last.then_inc(sig("projected"), 1)

                @block.scalar
                def _(act):
                    a = nc.scalar.activation

                    def biased(p):
                        bank = ra.take(act)
                        if p >= 3:
                            act.wait_ge(sig("conv"), 2 * (p - 2))
                        for j in range(2):
                            last = a(xc[p % 3][:, j, KC - 1:], bank[:, j * T:(j + 1) * T], ACT.Identity, bias=bx[:, 2 * p + j:2 * p + j + 1])
                        ra.empty(last)

                    def first_tap(p):
                        act.wait_ge(ra.emptied, 4 + p + 1)
                        if p >= 4:
                            act.wait_ge(rx.filled, p - 3)
                        elif p == 3:
                            act.wait_ge(sig("silu"), 1)
                        for j in range(2):
                            a(xf[p % 3][:, j, :], xc[p % 3][:, j, 0:T], ACT.Copy, scale=conv[:, 2 * p + j, 0:1]).then_inc(sig("tap"), 1)

                    def take_x(p):
                        bank = rx.take(act)
                        rx.empty(a(xt[:, :, (p - 1) * T:p * T], bank[:].rearrange("p (t e) -> p t e", t=TB), ACT.Copy))

                    def silu(p):
                        act.wait_ge(sig("conv"), 2 * p + 2)
                        a((bc if p == 0 else xf[p % 3])[:], xf[p % 3][:], ACT.Silu).then_inc(sig("silu"), 1)

                    a(xb[:], c.xT[:, :, bass.ts(b, T)], ACT.Copy).then_inc(sig("sliced"), 1)
                    for i in range(2):
                        for m in range(0, MH, 2):
                            bank = ra.take(act)
                            for j in range(2):
                                last = a(pre[:, i, m + j, :], bank[:, j * T:(j + 1) * T], ACT.Identity, bias=bd[:, i, m + j:m + j + 1],
                                         scale=lcol[:, m + j:m + j + 1] if i == 0 else 1.0)
                            ra.empty(last)
                    for i in range(2):
                        act.wait_ge(sig("magnitude"), i + 1)
                        a(ex1[:, i], ex1[:, i], ACT.Exp, scale=-1.0).then_inc(sig("exp"), 1)
                    for i in range(2):
                        act.wait_ge(sig("exp"), i + 1)
                        a(ex1[:, i], ex1[:, i], ACT.Ln, bias=1.0).then_inc(sig("log1p"), 1)
                    biased(0)
                    biased(1)
                    first_tap(0)
                    act.wait_ge(sig("lam_floor"), 1)
                    a(R, R, ACT.Ln).then_inc(sig("lnlam"), 1)
                    first_tap(1)
                    silu(0)
                    for p in range(2, NPX):
                        biased(p)
                        first_tap(p)
                        silu(p - 1)
                        if p >= 4:
                            take_x(p - 3)
                    silu(NPX - 1)
                    for p in range(NPX - 3, NPX):
                        take_x(p)
                    act.wait_ge(sig("total_diff"), 1)
                    a(sfac[:], sfac[:], ACT.Exp).then_inc(sig("factors"), 1)
                    a(tfac[:], tfac[:], ACT.Exp).then_inc(sig("factors"), 1)
                    for i in range(NPH):
                        bank = ra.take(act)
                        if i >= 2:
                            act.wait_ge(sig("att"), i - 1)
                        for j in range(2):
                            for t in range(TB):
                                last = a(ex[i % 2][:, j, t * P:(t + 1) * P], bank[:, j * T + t * P:j * T + (t + 1) * P], ACT.Exp,
                                         bias=ngc[:, t, 2 * i + j:2 * i + j + 1])
                        ra.empty(last)
                    for i in range(NG * TB):
                        act.wait_ge(sig("zb"), i + 1)
                        a(zb[i % 2], zb[i % 2], ACT.Silu).then_inc(sig("z_silu"), 1)
                    act.wait_ge(sig("gated"), NG * TB)
                    for k in range(0, DI // P, 2):
                        bank = ra.take(act)
                        ra.empty(a(yzT[:, k:k + 2, :], bank[:].rearrange("p (k t) -> p k t", k=2), ACT.Copy))
                    for t in range(TB):
                        a(wv[:], xt[:, t, :], ACT.Square, accum_out=ss[:, t, 0:1]).then_inc(sig("squares"), 1)
                        act.wait_ge(sig("squares"), t + 1)
                    act.wait_ge(sig("mean_sq"), 1)
                    a(ss[:, :, 2], ss[:, :, 1], ACT.Sqrt).then_inc(sig("rms"), 1)

                @block.gpsimd
                def _(pool):
                    tt = nc.gpsimd.tensor_tensor
                    by_head = lambda a, n: a.rearrange("p t (h d) -> p t h d", h=n)
                    pool.wait_ge(sig("capped"), 1)
                    pool.wait_ge(sig("rows"), 3)
                    tt(R, R, gcT[:], ALU.add).then_inc(sig("R"), 1)
                    for p in range(1, NPX):
                        pool.wait_ge(rx.emptied, p)
                        if p == 1:
                            pool.wait_ge(sig("gc_tok"), 1)
                            pool.wait_ge(sig("coef"), 1)
                        cs, hs = slice((p - 1) * T, p * T), slice((p - 1) * 4, p * 4)
                        tt(by_head(v[:, :, cs], 4), by_head(xt[:, :, cs], 4), dt[:, :, hs].unsqueeze(3).to_broadcast([P, TB, 4, HD]),
                           ALU.mult).then_inc(sig("v"), 1)
                    for p in range(1, NPX):
                        pool.wait_ge(sig("v"), p)
                        cs, hs = slice((p - 1) * T, p * T), slice((p - 1) * 4, p * 4)
                        tt(by_head(xt[:, :, cs], 4), by_head(xt[:, :, cs], 4), coef[:, :, hs].unsqueeze(3).to_broadcast([P, TB, 4, HD]),
                           ALU.mult).then_inc(sig("direct"), 1)
                    pool.wait_ge(sig("combined"), NG)
                    for n in range(NG * TB):
                        pool.wait_ge(sig("z_silu"), n + 1)
                        cs = slice(n // TB * GC, (n // TB + 1) * GC)
                        tt(xt[:, n % TB, cs], xt[:, n % TB, cs], zb[n % 2], ALU.mult).then_inc(sig("gated"), 1)

                @block.vector
                def _(dve):
                    ch = Chain(dve, sig("dve_chain"))
                    vec = nc.vector

                    def convolve(p):
                        for i in range(1, KC):
                            for j in range(2):
                                m = 2 * p + j
                                if i == 1:
                                    dve.wait_ge(sig("tap"), m + 1)
                                else:
                                    dve.wait_ge(sig("add_tap"), 4 * p + 2 * (i - 2) + j + 1)
                                vec.scalar_tensor_tensor(out=xf[p % 3][:, j, :], in0=xc[p % 3][:, j, i:i + T], scalar=conv[:, m, i:i + 1],
                                                         in1=xf[p % 3][:, j, :], op0=ALU.mult,
                                                         op1=ALU.add).then_inc(sig("conv" if i == KC - 1 else "add_tap"), 1)

                    f = lambda a: a.rearrange("p m t -> p (m t)")
                    for i in range(2):
                        dve.wait_ge(ra.emptied, 2 * (i + 1))
                        vec.scalar_tensor_tensor(out=f(ex1[:, i]), in0=f(pre[:, i]), scalar=-1.0, in1=f(pre[:, i]),
                                                 op0=ALU.mult, op1=ALU.max).then_inc(sig("magnitude"), 1)
                    for i in range(2):
                        dve.wait_ge(sig("log1p"), i + 1)
                        vec.scalar_tensor_tensor(out=f(sp[:, i]), in0=f(pre[:, i]), scalar=0.0, in1=f(ex1[:, i]),
                                                 op0=ALU.max, op1=ALU.add).then_inc(sig("rows"), 1)
                    dve.wait_ge(sig("rows"), 2)
                    vec.tensor_scalar(R, sp[:, 0], 1e-9, None, ALU.max).then_inc(sig("lam_floor"), 1)
                    for m in range(MH):
                        last = vec.tensor_scalar(g[:, m, :], sp[:, 1, m, :], nega[:, m:m + 1], None, ALU.mult)
                    ch.link(last)
                    for m in range(MH):
                        for t in range(TB):
                            ts = slice(t * P, (t + 1) * P)
                            last = vec.tensor_tensor_scan(gcT[:, m, ts], ones[:], g[:, m, ts], 0.0, ALU.mult, ALU.add)
                    last.then_inc(sig("rows"), 1)
                    convolve(0)
                    convolve(1)
                    dve.wait_ge(sig("lnlam"), 1)
                    vec.tensor_tensor(R, R, pre[:, 0], ALU.min).then_inc(sig("capped"), 1)
                    convolve(2)
                    heads = lambda bank, j: bank[:].rearrange("p (h j) -> p h j", j=16)[:, :, j]
                    for t in range(TB):
                        bank = rv.take(dve)
                        rv.empty(vec.tensor_copy(dt[:, t, :], heads(bank, 0)))
                    for t in range(TB):
                        bank = rv.take(dve)
                        vec.tensor_copy(lam0[:, t, :], heads(bank, 0))
                        rv.empty(vec.tensor_copy(lam8[:, t, :], heads(bank, 8)))
                    for t in range(TB):
                        bank = rv.take(dve)
                        rv.empty(vec.tensor_copy(gc[:, t, :], heads(bank, 0)))
                    dve.wait_ge(rv.emptied, 6)
                    vec.sem_inc(sig("gc_tok"), 1)
                    vec.tensor_scalar(ngc[:], gc[:], -1.0, None, ALU.mult)
                    dve.wait_ge(sig("qk"), 1)
                    idw = c.ident[:]
                    vec.tensor_tensor(dtmp[:, 0, :], qk_bank[:, 0:P], idw, ALU.mult)
                    ch.link(vec.tensor_tensor(dtmp[:, 1, :], qk_bank[:, T:T + P], idw, ALU.mult))
                    ch.link(vec.tensor_reduce(qdiag[:], dtmp, AX.X, ALU.add))
                    vec.tensor_copy(qkd[:, 0, :], qk_bank[:, 0:P])
                    vec.tensor_copy(qkd[:, 1, :], qk_bank[:, T:T + P])
                    vec.tensor_copy(qko[:], qk_bank[:, P:T])
                    ch.link(vec.tensor_tensor(coef[:], dt[:], lam0[:], ALU.mult))
                    ch.link(vec.tensor_tensor(coef[:], coef[:], qdiag[:].unsqueeze(2).to_broadcast([P, TB, H]), ALU.mult))
                    vec.tensor_tensor(coef[:], coef[:], dh[:].unsqueeze(1).to_broadcast([P, TB, H]), ALU.add).then_inc(sig("coef"), 1)
                    for p in range(3, NPX):
                        convolve(p)
                    dve.wait_ge(sig("total"), 1)
                    vec.tensor_tensor(sfac[:], off_bank[:, 0:H], gc[:, 0, :], ALU.subtract)
                    vec.tensor_copy(tfac[:], gc[:, 1, :]).then_inc(sig("total_diff"), 1)
                    dve.wait_ge(sig("factors"), 2)
                    ch.link(vec.tensor_tensor(tfac[:], tfac[:], lam8[:, 1, :], ALU.mult))

                    def decay_v(gi):
                        dve.wait_ge(sig("v"), 2 * gi + 2)
                        cs, hs = slice(gi * GC, (gi + 1) * GC), slice(gi * 8, gi * 8 + 8)
                        vec.tensor_tensor(wv[:, cs].rearrange("p (h d) -> p h d", h=8), v[:, 0, cs].rearrange("p (h d) -> p h d", h=8),
                                          sfac[:, hs].unsqueeze(2).to_broadcast([P, 8, HD]), ALU.mult).then_inc(sig("wv"), 1)

                    def combine(gi):
                        dve.wait_ge(sig("weighted"), 4 * gi + 4)
                        cs, hs = slice(gi * GC, (gi + 1) * GC), slice(gi * 8, gi * 8 + 8)
                        by_head = lambda a: a.rearrange("p (h d) -> p h d", h=8)
                        if gi == 0:
                            dve.wait_ge(sig("direct"), NPX - 1)
                        for t in range(TB):
                            last = vec.tensor_tensor(xt[:, t, cs], xt[:, t, cs], y_bank[t][:], ALU.add)
                        last.then_inc(sig("y_used"), 1)
                        vec.tensor_tensor(by_head(tmp), by_head(across[gi % 2][:]), tfac[:, hs].unsqueeze(2).to_broadcast([P, 8, HD]),
                                          ALU.mult).then_inc(sig("across_used"), 1)
                        dve.wait_ge(sig("y_used"), gi + 1)
                        dve.wait_ge(sig("across_used"), gi + 1)
                        vec.tensor_tensor(xt[:, 1, cs], xt[:, 1, cs], tmp, ALU.add).then_inc(sig("combined"), 1)

                    for i in range(NPH + 1):
                        if i % 4 == 1 and i < NPH:
                            decay_v(i // 4)
                        if i < NPH:
                            bank = rv.take(dve)
                            if i >= 2:
                                dve.wait_ge(ra.filled, A_EXP + i - 1)
                            ins = vec.tensor_tensor(ru[i % 2][:], bank[:].rearrange("p (j t) -> p j t", j=2),
                                                    um[:].unsqueeze(1).to_broadcast([P, 2, T]), ALU.mult)
                            ins.then_inc(sig("ru"), 1)
                            dve.wait_ge(sig("ru"), i + 1)
                            vec.sem_inc(rv.emptied, 1)
                        if i >= 5 and i % 4 == 1:
                            combine(i // 4 - 1)
                        if i >= 1:
                            q = i - 1
                            dve.wait_ge(ra.emptied, A_EXP + q + 1)
                            if q >= 2:
                                dve.wait_ge(sig("weighted"), q - 1)
                            vec.tensor_tensor(att[q % 2][:], ex[q % 2][:], qkd[:].rearrange("p t s -> p (t s)").unsqueeze(1).to_broadcast([P, 2, T]),
                                              ALU.mult).then_inc(sig("att"), 1)
                    combine(NG - 1)
                    n = 0
                    for gi in range(NG):
                        for t in range(TB):
                            bank = rv.take(dve)
                            cs = slice(gi * GC, (gi + 1) * GC)
                            if n >= 2:
                                dve.wait_ge(sig("gated"), n - 1)
                            ins = vec.tensor_tensor(zb[n % 2], bank[:], bz[:, cs], ALU.add)
                            ins.then_inc(sig("zb"), 1)
                            dve.wait_ge(sig("zb"), n + 1)
                            vec.sem_inc(rv.emptied, 1)
                            n += 1
                    dve.wait_ge(sig("squares"), TB)
                    vec.tensor_scalar(ss[:, :, 1], ss[:, :, 0], 1.0 / DI, 1e-5, ALU.mult, ALU.add).then_inc(sig("mean_sq"), 1)
                    dve.wait_ge(sig("rms"), 1)
                    ch.link(vec.reciprocal(ss[:, :, 3], ss[:, :, 2]))
                    dve.wait_ge(sig("projected"), 1)
                    for t in range(TB):
                        last = vec.scalar_tensor_tensor(out=y[:, t, :], in0=off_bank[:, t * D:(t + 1) * D], scalar=ss[:, t, 3:4], in1=bo[:],
                                                        op0=ALU.mult, op1=ALU.add)
                    ch.link(last)
                    vec.tensor_tensor(c.x[:, bass.ts(b, TB), :], c.x[:, bass.ts(b, TB), :], y, ALU.add)
            sig.clear()
        sig.close()


def pack(inputs):
    i = {k: np.asarray(v) for k, v in inputs.items()}
    a = {}

    def rows(w):
        s = w.shape
        return np.ascontiguousarray(np.moveaxis(w.reshape(*s[:-2], s[-2] // P, P, s[-1]), -3, -2))

    def cols(v):
        return np.ascontiguousarray(np.swapaxes(v.reshape(*v.shape[:-1], v.shape[-1] // P, P), -1, -2))

    by_tile = lambda v: cols(v).transpose(1, 0, 2)
    tok = lambda v: np.ascontiguousarray(v.reshape(NT, P, D).transpose(1, 0, 2))
    tr = lambda v: np.swapaxes(v, -1, -2)
    a["x"], a["ctx"] = tok(i["x"]), tok(i["ctx_1024"])
    a["ident"] = np.eye(P, dtype=np.float32)
    a["iota8"] = np.broadcast_to(np.arange(8, dtype=np.float32), (P, 8)).copy()
    earlier = (np.arange(P)[:, None] < np.arange(P)[None, :]).astype(np.float32)
    a["tri_strict_ones"] = np.stack([earlier, np.ones((P, P), np.float32)], 1)

    def experts(tag, gate, ups, lins, downs):
        a[f"{tag}_gate"] = rows(gate)
        a[f"{tag}_up"] = rows(np.concatenate(ups))
        if lins:
            a[f"{tag}_lin"] = rows(np.concatenate(lins))
        a[f"{tag}_down"] = rows(np.concatenate(downs))

    halves = lambda w: w.reshape(2, 256, D)
    experts("L0f", i["L0_ffn_gate_w"].T, [tr(i["L0_ffn_w1"]), tr(halves(i["L0_ffn_ws1"]))],
            [tr(i["L0_ffn_w3"]), tr(halves(i["L0_ffn_ws3"]))],
            [tr(i["L0_ffn_w2"]), i["L0_ffn_ws2"].T.reshape(2, 256, D)])
    a["L0f_gate_b"] = i["L0_ffn_gate_b"]
    a["L0f_up_b"] = by_tile(np.concatenate([i["L0_ffn_b1"], i["L0_ffn_bs1"].reshape(2, 256)]))
    a["L0f_lin_b"] = by_tile(np.concatenate([i["L0_ffn_b3"], i["L0_ffn_bs3"].reshape(2, 256)]))
    a["L0f_down_b"] = np.concatenate([i["L0_ffn_b2"], i["L0_ffn_bs2"][None], np.zeros((1, D), np.float32)])
    w1 = i["L2_ffn_w1"].reshape(8, D, 2, 512).transpose(0, 2, 1, 3).reshape(16, D, 512)
    experts("L2f", i["L2_ffn_switch_w"], [w1], None, [i["L2_ffn_w2"].reshape(16, 512, D)])
    a["L2f_gate_b"] = i["L2_ffn_switch_b"]
    a["L2f_up_b"] = by_tile(i["L2_ffn_b1"].reshape(16, 512))
    a["L2f_down_b"] = np.stack([i["L2_ffn_b2"], np.zeros_like(i["L2_ffn_b2"])], 1).reshape(16, D)
    experts("L3f", i["L3_ffn_gate_w"].T, [tr(i["L3_ffn_we_gate"]), tr(halves(i["L3_ffn_ws_gate"]))],
            [tr(i["L3_ffn_we_up"]), tr(halves(i["L3_ffn_ws_up"]))],
            [tr(i["L3_ffn_we_down"]), i["L3_ffn_ws_down"].T.reshape(2, 256, D)])
    pack_attention(i, a, rows, cols, tr)
    return {k: np.ascontiguousarray(v) for k, v in a.items()}


def pack_attention(i, a, rows, cols, tr):
    t = np.arange(P)
    dist = np.abs(t[:, None] - t[None, :])
    dist1 = np.abs(P + t[:, None] - np.arange(T)[None, :])
    a["twin"] = (t[:, None] // 16 % 2 == np.arange(2)).astype(np.float32)
    a["distance"] = np.concatenate([dist, dist1], 1).astype(np.float32)
    a["future_neg"] = np.where(t[None, :] > t[:, None], -1e30, 0.0).astype(np.float32)
    a["L1a_wq"], a["L1a_wk"] = rows(i["L1_attn_Wq"]), rows(i["L1_attn_Wk"])
    a["L1a_wv"], a["L1a_wo"] = rows(i["L1_attn_Wv"]), rows(i["L1_attn_Wo"])
    a["L1a_bo"], a["L1a_w"], a["L1a_v"] = i["L1_attn_bo"], i["L1_attn_w"], i["L1_attn_v"]
    a["L1x_wq"], a["L1x_wk"] = rows(i["L1_xattn_Wq"].T), rows(i["L1_xattn_Wk"].T)
    a["L1x_wv"], a["L1x_wo"] = rows(i["L1_xattn_Wv"].T), rows(i["L1_xattn_Wo"].T)
    a["L1x_bo"] = i["L1_xattn_bo"]
    a["mask_pairs"] = i["mask_Bx1xSxS2_ik0"].reshape(B, TB, P, T).transpose(0, 2, 1, 3)
    a["mask_keys"] = i["mask_Bx1xS2_ik0"]
    a["mask_bool"] = i["mask_BxS2_bk1"].reshape(B, 1, T)
    a["L3x_wq"], a["L3x_wo"] = rows(i["L3_xattn_Wq"]), rows(i["L3_xattn_Wo"])
    a["L3x_wk"], a["L3x_wv"] = rows(i["L3_xattn_Wkv"][:, :512]), rows(i["L3_xattn_Wkv"][:, 512:])
    a["L3x_ln"] = np.stack([cols(i[f"L3_xattn_ln_{n}"]) for n in ("l_g", "l_b", "x_g", "x_b")], 1)
    a["L3x_og"], a["L3x_ob"] = i["L3_xattn_ln_o_g"], i["L3_xattn_ln_o_b"]
    for n in ("up", "gate", "down"):
        o, k = i[f"L1_ffn_w_{n}"].shape
        a[f"L1f_{n}"] = i[f"L1_ffn_w_{n}"].reshape(o // P, P, k).transpose(1, 0, 2)
    a["L2a_c"] = i["L2_attn_C"].reshape(KD, P, 64).transpose(1, 0, 2)
    a["L2a_b"] = i["L2_attn_B"].T.reshape(KD, P, 64).transpose(1, 0, 2)
    a["L2a_a"], a["L2a_d"], a["L2a_ldt"] = i["L2_attn_A"], cols(i["L2_attn_D"]), cols(i["L2_attn_log_dt"])
    a["iota64"] = np.broadcast_to(np.arange(64, dtype=np.float32), (P, 64))
    a["L3a_wqk"] = rows(np.concatenate([i["L3_attn_Wq"].T, i["L3_attn_Wk"].T], 1))
    a["L3a_wv"], a["L3a_bv"] = rows(i["L3_attn_Wv"].T), i["L3_attn_bv"]
    a["L3a_bqk"] = np.concatenate([i["L3_attn_bq"], i["L3_attn_bk"]])
    a["L3a_gamma"], a["L3a_beta"] = i["L3_attn_gamma"], i["L3_attn_beta"]
    freq = (1.0 / 10000.0 ** (np.arange(0, D, 2, dtype=np.float32) / D)).astype(np.float32)
    ang = np.arange(T, dtype=np.float32)[:, None] * freq
    paired = lambda e, o: np.stack([e, o], -1).reshape(TB, P, D).transpose(1, 0, 2).astype(np.float32)
    a["rope_cos"], a["rope_sin"] = paired(np.cos(ang), np.cos(ang)), paired(-np.sin(ang), np.sin(ang))
    a["blockdiag16"] = np.where(t[:, None] // 16 == t[None, :] // 16, 1.0 / T, 0.0).astype(np.float32)
    upto = (t[:, None] <= t[None, :]).astype(np.float32)
    a["causal"] = np.concatenate([upto, np.ones((P, P), np.float32), upto], 1)
    for n in ("q", "k", "v"):
        a[f"L0x_w{n}"], b = rows(i[f"L0_xattn_W{n}"]), i[f"L0_xattn_b{n}"]
        a[f"L0x_b{n}"] = b if n == "k" else cols(b)
    a["L0x_wo"], a["L0x_bo"] = rows(i["L0_xattn_Wo"]), i["L0_xattn_bo"]

    wi, bi = i["L0_attn_in_proj_w"], i["L0_attn_in_proj_b"]
    order = np.concatenate([np.arange(4096, 4352), np.arange(2048, 4096)])
    a["L0a_wz"], a["L0a_bz"] = rows(wi[:2048].T), bi[:2048]
    a["L0a_wx"], a["L0a_bx"] = rows(wi[order].T), cols(bi[order])
    a["L0a_conv"] = i["L0_attn_conv_w"][order - 2048].reshape(18, P, 4).transpose(1, 0, 2)
    padded = lambda m: np.concatenate([m.reshape(32, 15, -1), np.zeros((32, 1, m.size // 480), m.dtype)], 1).reshape(512, -1)
    per_head = lambda m: np.repeat(m, 16, axis=0)
    a["L0a_wdl"], a["L0a_wdt"] = rows(padded(wi[4384:]).T), rows(per_head(wi[4352:4384]).T)
    a["L0a_bd"] = np.stack([cols(padded(bi[4384:])[:, 0]), cols(per_head(bi[4352:4384]))], 1)
    a["L0a_l"] = cols(padded(i["L0_attn_L"].reshape(480))[:, 0])
    a["L0a_alog"], a["L0a_dtb"] = cols(per_head(i["L0_attn_A_log"])), cols(per_head(i["L0_attn_dt_bias"]))
    a["L0a_d"], a["L0a_norm"] = i["L0_attn_D"], cols(i["L0_attn_norm_w"])
    a["L0a_wout"], a["L0a_bo"] = rows(i["L0_attn_out_proj_w"].T), i["L0_attn_out_proj_b"]
    pick, u, v = np.zeros((P, 8, P), np.float32), np.zeros((P, P), np.float32), np.zeros((P, P), np.float32)
    n = 0
    for k in range(7):
        for j in range(P >> (k + 1)):
            start, half = j << (k + 1), 1 << k
            v[n, start:start + half] = 1.0
            u[n, start + half:start + 2 * half] = 1.0
            for h in range(8):
                pick[h * 16 + k + 1, h, n] = 1.0
            n += 1
    a["L0a_pick"], a["L0a_u"], a["L0a_v"] = pick, np.concatenate([u, u], 1), v
    last_row = np.zeros((P, P), np.float32)
    last_row[P - 1] = 1.0
    a["last_row"] = last_row


LAYERS = {1: layer0_attn, 2: layer0_xattn, 3: layer0_ffn, 4: layer1_attn, 5: layer1_xattn, 6: layer1_ffn, 7: layer2_attn, 8: layer2_xattn, 9: layer2_ffn, 10: layer3_attn, 11: layer3_xattn, 12: layer3_ffn}


def program(nc, dram, out, layers):
    with ExitStack() as ctx:
        c = Core(nc, ctx, dram)
        c.load("first", [(c.x[:], dram["x"]), (c.ident[:], dram["ident"])])
        if layers[0] == 1:
            layer0_attn(c)
            layers = layers[1:]
        c.load("context", [(c.ctx[:], dram["ctx"])])
        transpose_tokens(c, "ctxT", c.ctx, c.ctxT)
        for n in layers:
            LAYERS[n](c)
        sig = Signals(nc, "last")
        with nc.Block() as block:
            @block.sync
            def _(sp):
                sp.dma_start(out, c.x[:]).then_inc(sig("stored"), 16)
                sp.wait_ge(sig("stored"), 16)
        sig.close()


def kernel(**inputs):
    import concourse.bacc as bacc
    from concourse.bass_utils import run_bass_kernel_spmd

    arrays = pack(inputs)
    nc = bacc.Bacc("TRN2", target_bir_lowering=False, num_devices=1)
    dram = {k: nc.dram_tensor(f"in_{k}", v.shape, mybir.dt.from_np(v.dtype), kind="ExternalInput").ap()
            for k, v in arrays.items()}
    out = nc.dram_tensor("out_x", (P, NT, D), F32, kind="ExternalOutput").ap()
    program(nc, dram, out, sorted(LAYERS))
    r = run_bass_kernel_spmd(nc, [{f"in_{k}": v for k, v in arrays.items()}], core_ids=[0])
    got = r.results[0]["out_x"]
    return np.ascontiguousarray(got.transpose(1, 0, 2)).reshape(B, T, D)
```
